# Optimizing a Trainium2 kernel written in Bass

```python
import numpy as np
import jax
import jax.numpy as jnp

def _softmax(x, axis=-1):
    return jax.nn.softmax(x, axis=axis)

def _gelu(x):
    return jax.nn.gelu(x, approximate=True)

def _silu(x):
    return jax.nn.silu(x)

def _sigmoid(x):
    return jax.nn.sigmoid(x)

def _layernorm(x, axis=-1, eps=1e-05):
    m = jnp.mean(x, axis=axis, keepdims=True)
    v = jnp.var(x, axis=axis, keepdims=True)
    return (x - m) / jnp.sqrt(v + eps)

def _scatter_add(tgt, idx, src, axis=0):
    return tgt.at[idx].add(src)

def _segment_sum(src, seg, n):
    return jax.ops.segment_sum(src, seg, n)
kernel_name = 'mk_early_fusion_embed_d4_tok_img768_r4_4ba24c'

def setup_inputs(seed: int=0):
    np.random.seed(seed)
    _w = jnp.asarray

    def _rec_inputs():
        import jax
        import jax.numpy as jnp
        _rk = jax.random.key(seed)
        x = -0.000596345 + 1.00056 * jax.random.normal(jax.random.fold_in(_rk, 1), (2, 3, 64, 64), jnp.float32)
        x_txt = jax.random.randint(jax.random.fold_in(_rk, 51), (2, 77), 0, 30522, jnp.int32)
        mask_BS_i1_0 = jnp.where(jnp.ones((2, 77), dtype=bool), 1, 0).astype(jnp.int32)
        return (x, x_txt, mask_BS_i1_0)
    x, x_txt, mask_BS_i1_0 = _rec_inputs()

    def _L0_tok_setup():
        import jax, jax.numpy as jnp
        import numpy as np
        B = 16
        IMG = 64
        CH = 3
        EMBED = 64
        GP = 16
        PRE = [1, 2, 4]
        N_LEVELS = 3
        FUSED = EMBED * N_LEVELS

        def hilbert_flat_indices(n):
            t = np.arange(n * n, dtype=np.int64)
            x = np.zeros(n * n, dtype=np.int64)
            y = np.zeros(n * n, dtype=np.int64)
            s = 1
            while s < n:
                rx = 1 & t // 2
                ry = 1 & (t ^ rx)
                swap = ry == 0
                flip = swap & (rx == 1)
                x = np.where(flip, s - 1 - x, x)
                y = np.where(flip, s - 1 - y, y)
                x2 = np.where(swap, y, x)
                y2 = np.where(swap, x, y)
                x, y = (x2, y2)
                x = x + s * rx
                y = y + s * ry
                t = t // 4
                s *= 2
            return y * n + x

        def _level(x, idx, W, b, p, gp):
            Bsz, C, H, _ = x.shape
            h = H // p
            t = x.reshape(Bsz, C, h, p, h, p).transpose(0, 2, 4, 3, 5, 1).reshape(Bsz, h * h, p * p * C)
            t = t[:, idx]
            t = t.reshape(Bsz, h * h // gp, gp * p * p * C)
            return t @ W.T + b

        def _interp_linear(x, n_out):
            L = x.shape[1]
            pos = (jnp.arange(n_out, dtype=jnp.float32) + 0.5) * (L / n_out) - 0.5
            pos = jnp.clip(pos, 0.0, L - 1)
            i0 = jnp.floor(pos).astype(jnp.int32)
            i1 = jnp.minimum(i0 + 1, L - 1)
            w = (pos - i0).astype(x.dtype)
            return x[:, i0] * (1.0 - w)[None, :, None] + x[:, i1] * w[None, :, None]
        key = jax.random.key(seed)
        ks = jax.random.split(key, 9)
        inp = {'x': jax.random.normal(ks[0], (B, CH, IMG, IMG), jnp.float32)}
        for i, p in enumerate(PRE):
            din = CH * p * p * GP
            inp[f'W{i}'] = jax.random.normal(ks[1 + 2 * i], (EMBED, din), jnp.float32) * din ** (-0.5)
            inp[f'b{i}'] = jax.random.normal(ks[2 + 2 * i], (EMBED,), jnp.float32) * 0.02
        inp['Wf'] = jax.random.normal(ks[7], (FUSED, FUSED), jnp.float32) * FUSED ** (-0.5)
        inp['bf'] = jax.random.normal(ks[8], (FUSED,), jnp.float32) * 0.02
        for i, p in enumerate(PRE):
            inp[f'idx{i}'] = jnp.asarray(hilbert_flat_indices(IMG // p), jnp.int32)
        return inp
    _L0_tok_all = _L0_tok_setup()
    _L0_tok_in = {k: v for k, v in _L0_tok_all.items() if k in ('W0', 'b0', 'W1', 'b1', 'W2', 'b2', 'Wf', 'bf', 'idx0', 'idx1', 'idx2')}
    del _L0_tok_all

    def _L0_txt_setup():
        import jax, jax.numpy as jnp
        import numpy as np
        B, S, H, V, P, T = (64, 128, 192, 30522, 128, 2)
        LN_EPS = 1e-12

        def _conv3(x, w):
            xp = jnp.pad(x, [(0, 0)] * (x.ndim - 1) + [(1, 1)])
            return w[0] * xp[..., :-2] + w[1] * xp[..., 1:-1] + w[2] * xp[..., 2:]
        key = jax.random.key(seed)
        ks = jax.random.split(key, 7)
        return {'input_ids': jax.random.randint(ks[0], (B, S), 0, V), 'token_type_ids': jax.random.randint(ks[1], (B, S), 0, T), 'word_emb': jax.random.normal(ks[2], (V, H), dtype=jnp.float32) * 0.02, 'pos_emb': jax.random.normal(ks[3], (P, H), dtype=jnp.float32) * 0.02, 'type_emb': jax.random.normal(ks[4], (T, H), dtype=jnp.float32) * 0.02, 'conv_w': jax.random.normal(ks[5], (2, 3), dtype=jnp.float32) * 0.2, 'conv_b': jax.random.normal(ks[6], (1,), dtype=jnp.float32) * 0.02, 'residual_weight': jnp.float32(0.5), 'ln_gamma': jnp.ones((H,), dtype=jnp.float32), 'ln_beta': jnp.zeros((H,), dtype=jnp.float32)}
    _L0_txt_all = _L0_txt_setup()
    _L0_txt_in = {k: v for k, v in _L0_txt_all.items() if k in ('word_emb', 'pos_emb', 'type_emb', 'conv_w', 'conv_b', 'residual_weight', 'ln_gamma', 'ln_beta')}
    del _L0_txt_all

    def _L0_attn_setup():
        import jax, jax.numpy as jnp
        import numpy as np
        EPS = 1e-06

        def _ln(x, g, b):
            mu = x.mean(-1, keepdims=True)
            var = ((x - mu) ** 2).mean(-1, keepdims=True)
            return (x - mu) * jax.lax.rsqrt(var + EPS) * g + b

        def _ln_l2_grad(z, target, g, b):
            d = z.shape[-1]
            mu = z.mean(-1, keepdims=True)
            var = ((z - mu) ** 2).mean(-1, keepdims=True)
            std = jnp.sqrt(var + EPS)
            zh = (z - mu) / std
            go = zh * g + b - target
            gxh = go * g
            return (d * gxh - gxh.sum(-1, keepdims=True) - zh * (gxh * zh).sum(-1, keepdims=True)) / (d * std)

        def _forward(x, W_down, b_down, Wq, Wk, Wv, Wo, W1, b1, ttt_g, ttt_b, lr_w, lr_b, post_g, post_b, norm_g, norm_b, W_up, b_up):
            B, S, D = x.shape
            A = W_down.shape[1]
            H, hd, _ = W1.shape
            h = jax.nn.silu(x @ W_down + b_down)
            xq = (h @ Wq).reshape(B, S, H, hd)
            xk = (h @ Wk).reshape(B, S, H, hd)
            xv = (h @ Wv).reshape(B, S, H, hd)
            eta = jax.nn.sigmoid(h @ lr_w + lr_b) / hd
            W1_0 = jnp.broadcast_to(W1, (B, H, hd, hd))
            b1_0 = jnp.broadcast_to(b1, (B, H, 1, hd))
            xs = (xq.transpose(1, 0, 2, 3), xk.transpose(1, 0, 2, 3), xv.transpose(1, 0, 2, 3), eta.transpose(1, 0, 2))

            def step(carry, ins):
                W, bb = carry
                q, k, v, e = ins
                Z = jnp.einsum('bhd,bhde->bhe', k, W) + bb[:, :, 0, :]
                g = _ln_l2_grad(Z, v - k, ttt_g, ttt_b)
                e4 = e[:, :, None, None]
                Wn = W - e4 * (k[..., :, None] * g[..., None, :])
                bn = bb - e4 * g[:, :, None, :]
                Zq = jnp.einsum('bhd,bhde->bhe', q, Wn) + bn[:, :, 0, :]
                out = q + _ln(Zq, ttt_g, ttt_b)
                return ((Wn, bn), out)
            _, ys = jax.lax.scan(step, (W1_0, b1_0), xs)
            t = ys.transpose(1, 0, 2, 3).reshape(B, S, A)
            t = _ln(t, post_g, post_b) @ Wo
            out = _ln(t, norm_g, norm_b)
            return out @ W_up + b_up
        key = jax.random.key(seed)
        ks = jax.random.split(key, 12)
        B, S, D, A, H = (4, 256, 192, 192, 3)
        hd = A // H
        s = 0.02
        return {'x': jax.random.normal(ks[0], (B, S, D), jnp.float32), 'W_down': jax.random.normal(ks[1], (D, A), jnp.float32) * s, 'b_down': jnp.zeros((A,), jnp.float32), 'Wq': jax.random.normal(ks[2], (A, A), jnp.float32) * s, 'Wk': jax.random.normal(ks[3], (A, A), jnp.float32) * s, 'Wv': jax.random.normal(ks[4], (A, A), jnp.float32) * s, 'Wo': jax.random.normal(ks[5], (A, A), jnp.float32) * s, 'W1': jax.random.normal(ks[6], (H, hd, hd), jnp.float32) * s, 'b1': jnp.zeros((H, 1, hd), jnp.float32), 'ttt_g': jnp.ones((H, hd), jnp.float32), 'ttt_b': jnp.zeros((H, hd), jnp.float32), 'lr_w': jax.random.normal(ks[7], (A, H), jnp.float32) * s, 'lr_b': jnp.zeros((H,), jnp.float32), 'post_g': jnp.ones((A,), jnp.float32), 'post_b': jnp.zeros((A,), jnp.float32), 'norm_g': jnp.ones((A,), jnp.float32), 'norm_b': jnp.zeros((A,), jnp.float32), 'W_up': jax.random.normal(ks[8], (A, D), jnp.float32) * s, 'b_up': jnp.zeros((D,), jnp.float32)}
    _L0_attn_all = _L0_attn_setup()
    _L0_attn_in = {k: v for k, v in _L0_attn_all.items() if k in ('W_down', 'b_down', 'Wq', 'Wk', 'Wv', 'Wo', 'W1', 'b1', 'ttt_g', 'ttt_b', 'lr_w', 'lr_b', 'post_g', 'post_b', 'norm_g', 'norm_b', 'W_up', 'b_up')}
    del _L0_attn_all

    def _L0_ffn_setup():
        import jax, jax.numpy as jnp
        import numpy as np
        E = 16
        K = 4
        H = 192
        I = 384
        LIMIT = 7.0
        ALPHA = 1.702
        EPS = 1e-05

        def rmsnorm(x, scale):
            xf = x.astype(jnp.float32)
            inv = jax.lax.rsqrt(jnp.mean(xf * xf, axis=-1, keepdims=True) + EPS)
            return (xf * inv).astype(x.dtype) * scale

        def swiglu(x, limit=LIMIT, alpha=ALPHA):
            x_glu = x[..., ::2]
            x_lin = x[..., 1::2]
            x_glu = jnp.minimum(x_glu, limit)
            x_lin = jnp.clip(x_lin, -limit, limit)
            return x_glu * jax.nn.sigmoid(alpha * x_glu) * (x_lin + 1.0)
        key = jax.random.key(seed)
        ks = jax.random.split(key, 7)
        s = 0.02
        return {'x': jax.random.normal(ks[0], (2, 256, H), dtype=jnp.float32), 'norm_scale': jnp.ones((H,), dtype=jnp.float32), 'gate_w': jax.random.normal(ks[1], (E, H), dtype=jnp.float32) * s, 'gate_b': jnp.zeros((E,), dtype=jnp.float32), 'mlp1_w': jax.random.normal(ks[2], (E, 2 * I, H), dtype=jnp.float32) * s, 'mlp1_b': jax.random.normal(ks[3], (E, 2 * I), dtype=jnp.float32) * s, 'mlp2_w': jax.random.normal(ks[4], (E, H, I), dtype=jnp.float32) * s, 'mlp2_b': jax.random.normal(ks[5], (E, H), dtype=jnp.float32) * s}
    _L0_ffn_all = _L0_ffn_setup()
    _L0_ffn_in = {k: v for k, v in _L0_ffn_all.items() if k in ('norm_scale', 'gate_w', 'gate_b', 'mlp1_w', 'mlp1_b', 'mlp2_w', 'mlp2_b')}
    del _L0_ffn_all

    def _L1_attn_setup():
        import jax, jax.numpy as jnp
        import numpy as np
        NUM_HEADS = 12

        def _l2_norm(t):
            return t / jnp.linalg.norm(t, axis=-2, keepdims=True)

        def _reference_tuple_inner(x, w_qkv, w_proj, b_proj):
            B, N, C = x.shape
            H = NUM_HEADS
            D = C // H
            qkv = (x @ w_qkv).reshape(B, N, 3, H, D).transpose(2, 0, 3, 1, 4)
            q, k, v = (qkv[0], qkv[1], qkv[2])
            q = _l2_norm(q)
            kT = _l2_norm(k).transpose(0, 1, 3, 2)
            sum_k = kT.sum(axis=-1)
            D_inv = 1.0 / (N + jnp.einsum('bhnd,bhd->bhd', q, sum_k))
            attn_matrix = jnp.einsum('bhnd,bhdn->bhdn', q, kT) * D_inv[..., None]
            matrix = jnp.einsum('bhnd,bhdn->bdhn', v, kT)
            y = jnp.einsum('bdhn,bhdn->bhnd', matrix, attn_matrix)
            y = y.transpose(0, 2, 1, 3).reshape(B, N, C)
            out = y @ w_proj + b_proj
            return (out, attn_matrix)
        key = jax.random.key(seed)
        k1, k2, k3 = jax.random.split(key, 3)
        B, N, C = (64, 256, 192)
        x = jax.random.normal(k1, (B, N, C), dtype=jnp.float32)
        w_qkv = jax.random.normal(k2, (C, 3 * C), dtype=jnp.float32) * 0.02
        w_proj = jax.random.normal(k3, (C, C), dtype=jnp.float32) * 0.02
        b_proj = jnp.zeros((C,), dtype=jnp.float32)
        return {'x': x, 'w_qkv': w_qkv, 'w_proj': w_proj, 'b_proj': b_proj}
    _L1_attn_all = _L1_attn_setup()
    _L1_attn_in = {k: v for k, v in _L1_attn_all.items() if k in ('w_qkv', 'w_proj', 'b_proj')}
    del _L1_attn_all

    def _L1_ffn_setup():
        import jax, jax.numpy as jnp
        import numpy as np
        B, T, E = (2, 256, 192)
        H = 768
        N_EXP = 4
        key = jax.random.key(seed)
        ks = jax.random.split(key, 8)
        s_e = 1.0 / np.sqrt(E)
        s_h = 1.0 / np.sqrt(H)
        return {'x': jax.random.normal(ks[0], (B, T, E), dtype=jnp.float32), 'Wg': jax.random.uniform(ks[1], (E, N_EXP), minval=-s_e, maxval=s_e, dtype=jnp.float32), 'bg': jax.random.uniform(ks[2], (N_EXP,), minval=-s_e, maxval=s_e, dtype=jnp.float32), 'W1': jax.random.uniform(ks[3], (N_EXP, E, H), minval=-s_e, maxval=s_e, dtype=jnp.float32), 'b1': jax.random.uniform(ks[4], (N_EXP, H), minval=-s_e, maxval=s_e, dtype=jnp.float32), 'W2': jax.random.uniform(ks[5], (N_EXP, H, E), minval=-s_h, maxval=s_h, dtype=jnp.float32), 'b2': jax.random.uniform(ks[6], (N_EXP, E), minval=-s_h, maxval=s_h, dtype=jnp.float32)}
    _L1_ffn_all = _L1_ffn_setup()
    _L1_ffn_in = {k: v for k, v in _L1_ffn_all.items() if k in ('Wg', 'bg', 'W1', 'b1', 'W2', 'b2')}
    del _L1_ffn_all

    def _L2_attn_setup():
        import jax, jax.numpy as jnp
        import numpy as np
        QMIN, QMAX = (-128.0, 127.0)
        BITS_S = 4
        NUM_HEADS = 12

        def fake_quant(x, scale):
            return jnp.clip(jnp.round(x / scale), QMIN, QMAX) * scale

        def int_softmax(x, scale):
            c0, c1, c2 = (0.35815147, 0.96963238, 1.0)
            b_int = jnp.floor(c1 / c0 / scale)
            c_int = jnp.floor(c2 / c0 / scale ** 2)
            x_int = x / scale
            x_int = x_int - jnp.max(x_int, axis=-1, keepdims=True)
            x0 = -0.6931
            n = 30
            x0_int = jnp.floor(x0 / scale)
            x_int = jnp.maximum(x_int, n * x0_int)
            q = jnp.floor(x_int / x0_int)
            r = x_int - x0_int * q
            z = r * (r + b_int) + c_int
            exp_int = jnp.maximum(jnp.floor(z * 2.0 ** (n - q)), 0.0)
            exp_int_sum = jnp.sum(exp_int, axis=-1, keepdims=True)
            return (exp_int, exp_int_sum)

        def log_round(x):
            big = jnp.floor(jnp.log2(x))
            return jnp.where(x - 2.0 ** big >= 2.0 ** (big - 1.0), big + 1.0, big)

        def _sym_scale(t):
            return jnp.max(jnp.abs(t)) / QMAX
        key = jax.random.key(seed)
        k1, k2, k3 = jax.random.split(key, 3)
        B, N, C, H = (64, 197, 192, NUM_HEADS)
        D = C // H
        x = jax.random.normal(k1, (B, N, C), dtype=jnp.float32)
        qkv_w = jax.random.normal(k2, (3 * C, C), dtype=jnp.float32) * 0.02
        qkv_b = jnp.zeros((3 * C,), dtype=jnp.float32)
        proj_w = jax.random.normal(k3, (C, C), dtype=jnp.float32) * 0.02
        proj_b = jnp.zeros((C,), dtype=jnp.float32)
        w_qkv_scale = _sym_scale(qkv_w)
        w_proj_scale = _sym_scale(proj_w)
        h = x @ qkv_w.T + qkv_b
        a1_scale = _sym_scale(h)
        qkv = h.reshape(B, N, 3, H, D).transpose(2, 0, 3, 1, 4)
        q, k, v = (qkv[0], qkv[1], qkv[2])
        attn = jnp.einsum('bhnd,bhmd->bhnm', q, k) * D ** (-0.5)
        attn_scale = _sym_scale(attn)
        ctx = jnp.einsum('bhnm,bhmd->bhnd', jax.nn.softmax(attn, axis=-1), v)
        ctx = ctx.transpose(0, 2, 1, 3).reshape(B, N, C)
        a2_scale = _sym_scale(ctx)
        a3_scale = _sym_scale(ctx @ proj_w.T + proj_b)
        return {'x': x, 'qkv_w': qkv_w, 'qkv_b': qkv_b, 'proj_w': proj_w, 'proj_b': proj_b, 'w_qkv_scale': w_qkv_scale, 'a1_scale': a1_scale, 'attn_scale': attn_scale, 'a2_scale': a2_scale, 'w_proj_scale': w_proj_scale, 'a3_scale': a3_scale}
    _L2_attn_all = _L2_attn_setup()
    _L2_attn_in = {k: v for k, v in _L2_attn_all.items() if k in ('qkv_w', 'qkv_b', 'proj_w', 'proj_b', 'w_qkv_scale', 'a1_scale', 'attn_scale', 'a2_scale', 'w_proj_scale', 'a3_scale')}
    del _L2_attn_all

    def _L2_ffn_setup():
        import jax, jax.numpy as jnp
        import numpy as np
        E = 8
        TOP_K = 2
        CAP_RATIO = 1.2
        key = jax.random.key(seed)
        k1, k2, k3, k4 = jax.random.split(key, 4)
        B, L, D, H = (2, 512, 192, 512)
        x = jax.random.normal(k1, (B, L, D), dtype=jnp.float32)
        Wg = jax.random.normal(k2, (D, E), dtype=jnp.float32) * 0.02
        W1 = jax.random.normal(k3, (E, D, 2 * H), dtype=jnp.float32) * 0.02
        W2 = jax.random.normal(k4, (E, H, D), dtype=jnp.float32) * 0.02
        return {'x': x, 'Wg': Wg, 'W1': W1, 'W2': W2}
    _L2_ffn_all = _L2_ffn_setup()
    _L2_ffn_in = {k: v for k, v in _L2_ffn_all.items() if k in ('Wg', 'W1', 'W2')}
    del _L2_ffn_all

    def _L3_attn_setup():
        import jax, jax.numpy as jnp
        import numpy as np
        EPS = 1e-05

        def _ste(y, x):
            return x + jax.lax.stop_gradient(y - x)

        def _absmean_quant(x):
            s = jnp.mean(jnp.abs(x)) + EPS
            u = x / s
            q = _ste(jnp.round(jnp.clip(u, -1.0, 1.0)), u)
            return (q, s)

        def _ternary_weight(w):
            s = jnp.mean(jnp.abs(w)) + EPS
            u = w / s
            return _ste(jnp.round(jnp.clip(u, -1.0, 1.0)), u) * s

        def _l1norm(x):
            return x / (jnp.sum(jnp.abs(x), axis=-1, keepdims=True) + EPS)
        key = jax.random.key(seed)
        k1, k2 = jax.random.split(key)
        B, N, C = (16, 1025, 192)
        x = jax.random.normal(k1, (B, N, C), dtype=jnp.float32)
        w_qkv = jax.random.normal(k2, (3 * C, C), dtype=jnp.float32) * 0.02
        return {'x': x, 'w_qkv': w_qkv}
    _L3_attn_all = _L3_attn_setup()
    _L3_attn_in = {k: v for k, v in _L3_attn_all.items() if k in ('w_qkv',)}
    del _L3_attn_all

    def _L3_ffn_setup():
        import jax, jax.numpy as jnp
        import numpy as np
        SEQ, BATCH, EMBED = (256, 2, 192)
        E = 16
        FFN_H = 384
        K_SHARED = 1
        K_ROUTE = 3
        LN_EPS = 1e-05
        NEG_INF = -1000000000.0
        key = jax.random.key(seed)
        ks = jax.random.split(key, 4)
        x = jax.random.normal(ks[0], (SEQ, BATCH, EMBED), dtype=jnp.float32)
        gate_w = jax.random.normal(ks[1], (EMBED, E), dtype=jnp.float32) * 0.02
        gate_b = jnp.zeros((E,), jnp.float32)
        fc1_w = jax.random.normal(ks[2], (E, EMBED, FFN_H), dtype=jnp.float32) * 0.02
        fc1_b = jnp.zeros((E, FFN_H), jnp.float32)
        ln_w = jnp.ones((E, FFN_H), jnp.float32)
        ln_b = jnp.zeros((E, FFN_H), jnp.float32)
        fc2_w = jax.random.normal(ks[3], (E, FFN_H, EMBED), dtype=jnp.float32) * 0.02
        fc2_b = jnp.zeros((E, EMBED), jnp.float32)
        return {'x': x, 'gate_w': gate_w, 'gate_b': gate_b, 'fc1_w': fc1_w, 'fc1_b': fc1_b, 'ln_w': ln_w, 'ln_b': ln_b, 'fc2_w': fc2_w, 'fc2_b': fc2_b}
    _L3_ffn_all = _L3_ffn_setup()
    _L3_ffn_in = {k: v for k, v in _L3_ffn_all.items() if k in ('gate_w', 'gate_b', 'fc1_w', 'fc1_b', 'ln_w', 'ln_b', 'fc2_w', 'fc2_b')}
    del _L3_ffn_all
    return {'x': x, 'x_txt': x_txt, 'mask_BS_i1_0': mask_BS_i1_0, 'L0_tok_W0': _L0_tok_in['W0'], 'L0_tok_b0': _L0_tok_in['b0'], 'L0_tok_W1': _L0_tok_in['W1'], 'L0_tok_b1': _L0_tok_in['b1'], 'L0_tok_W2': _L0_tok_in['W2'], 'L0_tok_b2': _L0_tok_in['b2'], 'L0_tok_Wf': _L0_tok_in['Wf'], 'L0_tok_bf': _L0_tok_in['bf'], 'L0_tok_idx0': _L0_tok_in['idx0'], 'L0_tok_idx1': _L0_tok_in['idx1'], 'L0_tok_idx2': _L0_tok_in['idx2'], 'L0_txt_word_emb': _L0_txt_in['word_emb'], 'L0_txt_pos_emb': _L0_txt_in['pos_emb'], 'L0_txt_type_emb': _L0_txt_in['type_emb'], 'L0_txt_conv_w': _L0_txt_in['conv_w'], 'L0_txt_conv_b': _L0_txt_in['conv_b'], 'L0_txt_residual_weight': _L0_txt_in['residual_weight'], 'L0_txt_ln_gamma': _L0_txt_in['ln_gamma'], 'L0_txt_ln_beta': _L0_txt_in['ln_beta'], 'L0_attn_W_down': _L0_attn_in['W_down'], 'L0_attn_b_down': _L0_attn_in['b_down'], 'L0_attn_Wq': _L0_attn_in['Wq'], 'L0_attn_Wk': _L0_attn_in['Wk'], 'L0_attn_Wv': _L0_attn_in['Wv'], 'L0_attn_Wo': _L0_attn_in['Wo'], 'L0_attn_W1': _L0_attn_in['W1'], 'L0_attn_b1': _L0_attn_in['b1'], 'L0_attn_ttt_g': _L0_attn_in['ttt_g'], 'L0_attn_ttt_b': _L0_attn_in['ttt_b'], 'L0_attn_lr_w': _L0_attn_in['lr_w'], 'L0_attn_lr_b': _L0_attn_in['lr_b'], 'L0_attn_post_g': _L0_attn_in['post_g'], 'L0_attn_post_b': _L0_attn_in['post_b'], 'L0_attn_norm_g': _L0_attn_in['norm_g'], 'L0_attn_norm_b': _L0_attn_in['norm_b'], 'L0_attn_W_up': _L0_attn_in['W_up'], 'L0_attn_b_up': _L0_attn_in['b_up'], 'L0_ffn_norm_scale': _L0_ffn_in['norm_scale'], 'L0_ffn_gate_w': _L0_ffn_in['gate_w'], 'L0_ffn_gate_b': _L0_ffn_in['gate_b'], 'L0_ffn_mlp1_w': _L0_ffn_in['mlp1_w'], 'L0_ffn_mlp1_b': _L0_ffn_in['mlp1_b'], 'L0_ffn_mlp2_w': _L0_ffn_in['mlp2_w'], 'L0_ffn_mlp2_b': _L0_ffn_in['mlp2_b'], 'L1_attn_w_qkv': _L1_attn_in['w_qkv'], 'L1_attn_w_proj': _L1_attn_in['w_proj'], 'L1_attn_b_proj': _L1_attn_in['b_proj'], 'L1_ffn_Wg': _L1_ffn_in['Wg'], 'L1_ffn_bg': _L1_ffn_in['bg'], 'L1_ffn_W1': _L1_ffn_in['W1'], 'L1_ffn_b1': _L1_ffn_in['b1'], 'L1_ffn_W2': _L1_ffn_in['W2'], 'L1_ffn_b2': _L1_ffn_in['b2'], 'L2_attn_qkv_w': _L2_attn_in['qkv_w'], 'L2_attn_qkv_b': _L2_attn_in['qkv_b'], 'L2_attn_proj_w': _L2_attn_in['proj_w'], 'L2_attn_proj_b': _L2_attn_in['proj_b'], 'L2_attn_w_qkv_scale': _L2_attn_in['w_qkv_scale'], 'L2_attn_a1_scale': _L2_attn_in['a1_scale'], 'L2_attn_attn_scale': _L2_attn_in['attn_scale'], 'L2_attn_a2_scale': _L2_attn_in['a2_scale'], 'L2_attn_w_proj_scale': _L2_attn_in['w_proj_scale'], 'L2_attn_a3_scale': _L2_attn_in['a3_scale'], 'L2_ffn_Wg': _L2_ffn_in['Wg'], 'L2_ffn_W1': _L2_ffn_in['W1'], 'L2_ffn_W2': _L2_ffn_in['W2'], 'L3_attn_w_qkv': _L3_attn_in['w_qkv'], 'L3_ffn_gate_w': _L3_ffn_in['gate_w'], 'L3_ffn_gate_b': _L3_ffn_in['gate_b'], 'L3_ffn_fc1_w': _L3_ffn_in['fc1_w'], 'L3_ffn_fc1_b': _L3_ffn_in['fc1_b'], 'L3_ffn_ln_w': _L3_ffn_in['ln_w'], 'L3_ffn_ln_b': _L3_ffn_in['ln_b'], 'L3_ffn_fc2_w': _L3_ffn_in['fc2_w'], 'L3_ffn_fc2_b': _L3_ffn_in['fc2_b']}

def reference(x, x_txt, mask_BS_i1_0, L0_tok_W0, L0_tok_b0, L0_tok_W1, L0_tok_b1, L0_tok_W2, L0_tok_b2, L0_tok_Wf, L0_tok_bf, L0_tok_idx0, L0_tok_idx1, L0_tok_idx2, L0_txt_word_emb, L0_txt_pos_emb, L0_txt_type_emb, L0_txt_conv_w, L0_txt_conv_b, L0_txt_residual_weight, L0_txt_ln_gamma, L0_txt_ln_beta, L0_attn_W_down, L0_attn_b_down, L0_attn_Wq, L0_attn_Wk, L0_attn_Wv, L0_attn_Wo, L0_attn_W1, L0_attn_b1, L0_attn_ttt_g, L0_attn_ttt_b, L0_attn_lr_w, L0_attn_lr_b, L0_attn_post_g, L0_attn_post_b, L0_attn_norm_g, L0_attn_norm_b, L0_attn_W_up, L0_attn_b_up, L0_ffn_norm_scale, L0_ffn_gate_w, L0_ffn_gate_b, L0_ffn_mlp1_w, L0_ffn_mlp1_b, L0_ffn_mlp2_w, L0_ffn_mlp2_b, L1_attn_w_qkv, L1_attn_w_proj, L1_attn_b_proj, L1_ffn_Wg, L1_ffn_bg, L1_ffn_W1, L1_ffn_b1, L1_ffn_W2, L1_ffn_b2, L2_attn_qkv_w, L2_attn_qkv_b, L2_attn_proj_w, L2_attn_proj_b, L2_attn_w_qkv_scale, L2_attn_a1_scale, L2_attn_attn_scale, L2_attn_a2_scale, L2_attn_w_proj_scale, L2_attn_a3_scale, L2_ffn_Wg, L2_ffn_W1, L2_ffn_W2, L3_attn_w_qkv, L3_ffn_gate_w, L3_ffn_gate_b, L3_ffn_fc1_w, L3_ffn_fc1_b, L3_ffn_ln_w, L3_ffn_ln_b, L3_ffn_fc2_w, L3_ffn_fc2_b):
    import jax
    import jax.numpy as jnp

    def _L0_tok_ref(x, W0, b0, W1, b1, W2, b2, Wf, bf, idx0, idx1, idx2):
        import jax, jax.numpy as jnp
        import numpy as np
        B = 16
        IMG = 64
        CH = 3
        EMBED = 64
        GP = 16
        PRE = [1, 2, 4]
        N_LEVELS = 3
        FUSED = EMBED * N_LEVELS

        def hilbert_flat_indices(n):
            t = np.arange(n * n, dtype=np.int64)
            x = np.zeros(n * n, dtype=np.int64)
            y = np.zeros(n * n, dtype=np.int64)
            s = 1
            while s < n:
                rx = 1 & t // 2
                ry = 1 & (t ^ rx)
                swap = ry == 0
                flip = swap & (rx == 1)
                x = np.where(flip, s - 1 - x, x)
                y = np.where(flip, s - 1 - y, y)
                x2 = np.where(swap, y, x)
                y2 = np.where(swap, x, y)
                x, y = (x2, y2)
                x = x + s * rx
                y = y + s * ry
                t = t // 4
                s *= 2
            return y * n + x

        def _level(x, idx, W, b, p, gp):
            Bsz, C, H, _ = x.shape
            h = H // p
            t = x.reshape(Bsz, C, h, p, h, p).transpose(0, 2, 4, 3, 5, 1).reshape(Bsz, h * h, p * p * C)
            t = t[:, idx]
            t = t.reshape(Bsz, h * h // gp, gp * p * p * C)
            return t @ W.T + b

        def _interp_linear(x, n_out):
            L = x.shape[1]
            pos = (jnp.arange(n_out, dtype=jnp.float32) + 0.5) * (L / n_out) - 0.5
            pos = jnp.clip(pos, 0.0, L - 1)
            i0 = jnp.floor(pos).astype(jnp.int32)
            i1 = jnp.minimum(i0 + 1, L - 1)
            w = (pos - i0).astype(x.dtype)
            return x[:, i0] * (1.0 - w)[None, :, None] + x[:, i1] * w[None, :, None]
        Ws = [(idx0, W0, b0, PRE[0]), (idx1, W1, b1, PRE[1]), (idx2, W2, b2, PRE[2])]
        outs = [_level(x, idx, W, b, p, GP) for idx, W, b, p in Ws]
        n_tokens = outs[0].shape[1]
        outs = [outs[0]] + [_interp_linear(o, n_tokens) for o in outs[1:]]
        y = jnp.concatenate(outs, axis=-1)
        return y @ Wf.T + bf

    def _L0_txt_ref(input_ids, token_type_ids, word_emb, pos_emb, type_emb, conv_w, conv_b, residual_weight, ln_gamma, ln_beta):
        import jax, jax.numpy as jnp
        import numpy as np
        B, S, H, V, P, T = (64, 128, 192, 30522, 128, 2)
        LN_EPS = 1e-12

        def _conv3(x, w):
            xp = jnp.pad(x, [(0, 0)] * (x.ndim - 1) + [(1, 1)])
            return w[0] * xp[..., :-2] + w[1] * xp[..., 1:-1] + w[2] * xp[..., 2:]
        seq_len = input_ids.shape[1]
        we = word_emb[input_ids]
        pe = pos_emb[jnp.arange(seq_len)][None, :, :]
        te = type_emb[token_type_ids]
        conv_out = _conv3(we, conv_w[0]) + _conv3(pe, conv_w[1]) + conv_b[0]
        simple_sum = we + pe
        emb = (1.0 - residual_weight) * simple_sum + residual_weight * conv_out + te
        mu = jnp.mean(emb, axis=-1, keepdims=True)
        var = jnp.mean(jnp.square(emb - mu), axis=-1, keepdims=True)
        normed = (emb - mu) * jax.lax.rsqrt(var + LN_EPS)
        return normed * ln_gamma + ln_beta

    def _L0_attn_ref(x, W_down, b_down, Wq, Wk, Wv, Wo, W1, b1, ttt_g, ttt_b, lr_w, lr_b, post_g, post_b, norm_g, norm_b, W_up, b_up):
        import jax, jax.numpy as jnp
        import numpy as np
        EPS = 1e-06

        def _ln(x, g, b):
            mu = x.mean(-1, keepdims=True)
            var = ((x - mu) ** 2).mean(-1, keepdims=True)
            return (x - mu) * jax.lax.rsqrt(var + EPS) * g + b

        def _ln_l2_grad(z, target, g, b):
            d = z.shape[-1]
            mu = z.mean(-1, keepdims=True)
            var = ((z - mu) ** 2).mean(-1, keepdims=True)
            std = jnp.sqrt(var + EPS)
            zh = (z - mu) / std
            go = zh * g + b - target
            gxh = go * g
            return (d * gxh - gxh.sum(-1, keepdims=True) - zh * (gxh * zh).sum(-1, keepdims=True)) / (d * std)

        def _forward(x, W_down, b_down, Wq, Wk, Wv, Wo, W1, b1, ttt_g, ttt_b, lr_w, lr_b, post_g, post_b, norm_g, norm_b, W_up, b_up):
            B, S, D = x.shape
            A = W_down.shape[1]
            H, hd, _ = W1.shape
            h = jax.nn.silu(x @ W_down + b_down)
            xq = (h @ Wq).reshape(B, S, H, hd)
            xk = (h @ Wk).reshape(B, S, H, hd)
            xv = (h @ Wv).reshape(B, S, H, hd)
            eta = jax.nn.sigmoid(h @ lr_w + lr_b) / hd
            W1_0 = jnp.broadcast_to(W1, (B, H, hd, hd))
            b1_0 = jnp.broadcast_to(b1, (B, H, 1, hd))
            xs = (xq.transpose(1, 0, 2, 3), xk.transpose(1, 0, 2, 3), xv.transpose(1, 0, 2, 3), eta.transpose(1, 0, 2))

            def step(carry, ins):
                W, bb = carry
                q, k, v, e = ins
                Z = jnp.einsum('bhd,bhde->bhe', k, W) + bb[:, :, 0, :]
                g = _ln_l2_grad(Z, v - k, ttt_g, ttt_b)
                e4 = e[:, :, None, None]
                Wn = W - e4 * (k[..., :, None] * g[..., None, :])
                bn = bb - e4 * g[:, :, None, :]
                Zq = jnp.einsum('bhd,bhde->bhe', q, Wn) + bn[:, :, 0, :]
                out = q + _ln(Zq, ttt_g, ttt_b)
                return ((Wn, bn), out)
            _, ys = jax.lax.scan(step, (W1_0, b1_0), xs)
            t = ys.transpose(1, 0, 2, 3).reshape(B, S, A)
            t = _ln(t, post_g, post_b) @ Wo
            out = _ln(t, norm_g, norm_b)
            return out @ W_up + b_up
        return _forward(x, W_down, b_down, Wq, Wk, Wv, Wo, W1, b1, ttt_g, ttt_b, lr_w, lr_b, post_g, post_b, norm_g, norm_b, W_up, b_up)

    def _L0_ffn_ref(x, norm_scale, gate_w, gate_b, mlp1_w, mlp1_b, mlp2_w, mlp2_b):
        import jax, jax.numpy as jnp
        import numpy as np
        E = 16
        K = 4
        H = 192
        I = 384
        LIMIT = 7.0
        ALPHA = 1.702
        EPS = 1e-05

        def rmsnorm(x, scale):
            xf = x.astype(jnp.float32)
            inv = jax.lax.rsqrt(jnp.mean(xf * xf, axis=-1, keepdims=True) + EPS)
            return (xf * inv).astype(x.dtype) * scale

        def swiglu(x, limit=LIMIT, alpha=ALPHA):
            x_glu = x[..., ::2]
            x_lin = x[..., 1::2]
            x_glu = jnp.minimum(x_glu, limit)
            x_lin = jnp.clip(x_lin, -limit, limit)
            return x_glu * jax.nn.sigmoid(alpha * x_glu) * (x_lin + 1.0)
        B, T, _ = x.shape
        t = rmsnorm(x, norm_scale)
        g = jnp.einsum('bth,eh->bte', t, gate_w) + gate_b
        top_vals, top_idx = jax.lax.top_k(g, K)
        route_w = jax.nn.softmax(top_vals, axis=-1)
        t_flat = t.reshape(B * T, H)
        idx_flat = top_idx.reshape(B * T, K)
        w_flat = route_w.reshape(B * T, K)
        onehot = jax.nn.one_hot(idx_flat, E, dtype=t_flat.dtype)
        comb = jnp.einsum('nke,nk->ne', onehot, w_flat)
        h = jnp.einsum('nh,ech->nec', t_flat, mlp1_w) + mlp1_b
        a = swiglu(h)
        y = jnp.einsum('nec,ehc->neh', a, mlp2_w) + mlp2_b
        out_flat = jnp.einsum('neh,ne->nh', y, comb)
        return x + out_flat.reshape(B, T, H)

    def _L1_attn_ref(x, w_qkv, w_proj, b_proj):
        import jax, jax.numpy as jnp
        import numpy as np
        NUM_HEADS = 12

        def _l2_norm(t):
            return t / jnp.linalg.norm(t, axis=-2, keepdims=True)

        def _reference_tuple_inner(x, w_qkv, w_proj, b_proj):
            B, N, C = x.shape
            H = NUM_HEADS
            D = C // H
            qkv = (x @ w_qkv).reshape(B, N, 3, H, D).transpose(2, 0, 3, 1, 4)
            q, k, v = (qkv[0], qkv[1], qkv[2])
            q = _l2_norm(q)
            kT = _l2_norm(k).transpose(0, 1, 3, 2)
            sum_k = kT.sum(axis=-1)
            D_inv = 1.0 / (N + jnp.einsum('bhnd,bhd->bhd', q, sum_k))
            attn_matrix = jnp.einsum('bhnd,bhdn->bhdn', q, kT) * D_inv[..., None]
            matrix = jnp.einsum('bhnd,bhdn->bdhn', v, kT)
            y = jnp.einsum('bdhn,bhdn->bhnd', matrix, attn_matrix)
            y = y.transpose(0, 2, 1, 3).reshape(B, N, C)
            out = y @ w_proj + b_proj
            return (out, attn_matrix)
        return _reference_tuple_inner(x, w_qkv, w_proj, b_proj)[0]

    def _L1_ffn_ref(x, Wg, bg, W1, b1, W2, b2):
        import jax, jax.numpy as jnp
        import numpy as np
        B, T, E = (2, 256, 192)
        H = 768
        N_EXP = 4
        gate_logits = jnp.einsum('bte,en->btn', x, Wg) + bg
        top = jnp.argmax(gate_logits, axis=-1)
        h = jax.nn.gelu(jnp.einsum('bte,neh->nbth', x, W1) + b1[:, None, None, :], approximate=False)
        y = jnp.einsum('nbth,nhe->nbte', h, W2) + b2[:, None, None, :]
        onehot = jax.nn.one_hot(top, N_EXP, dtype=x.dtype)
        out = jnp.einsum('nbte,btn->bte', y, onehot)
        return out

    def _L2_attn_ref(x, qkv_w, qkv_b, proj_w, proj_b, w_qkv_scale, a1_scale, attn_scale, a2_scale, w_proj_scale, a3_scale):
        import jax, jax.numpy as jnp
        import numpy as np
        QMIN, QMAX = (-128.0, 127.0)
        BITS_S = 4
        NUM_HEADS = 12

        def fake_quant(x, scale):
            return jnp.clip(jnp.round(x / scale), QMIN, QMAX) * scale

        def int_softmax(x, scale):
            c0, c1, c2 = (0.35815147, 0.96963238, 1.0)
            b_int = jnp.floor(c1 / c0 / scale)
            c_int = jnp.floor(c2 / c0 / scale ** 2)
            x_int = x / scale
            x_int = x_int - jnp.max(x_int, axis=-1, keepdims=True)
            x0 = -0.6931
            n = 30
            x0_int = jnp.floor(x0 / scale)
            x_int = jnp.maximum(x_int, n * x0_int)
            q = jnp.floor(x_int / x0_int)
            r = x_int - x0_int * q
            z = r * (r + b_int) + c_int
            exp_int = jnp.maximum(jnp.floor(z * 2.0 ** (n - q)), 0.0)
            exp_int_sum = jnp.sum(exp_int, axis=-1, keepdims=True)
            return (exp_int, exp_int_sum)

        def log_round(x):
            big = jnp.floor(jnp.log2(x))
            return jnp.where(x - 2.0 ** big >= 2.0 ** (big - 1.0), big + 1.0, big)

        def _sym_scale(t):
            return jnp.max(jnp.abs(t)) / QMAX
        B, N, C = x.shape
        H = NUM_HEADS
        D = C // H
        h = x @ fake_quant(qkv_w, w_qkv_scale).T + qkv_b
        h = fake_quant(h, a1_scale)
        qkv = h.reshape(B, N, 3, H, D).transpose(2, 0, 3, 1, 4)
        q, k, v = (qkv[0], qkv[1], qkv[2])
        attn = jnp.einsum('bhnd,bhmd->bhnm', q, k) * D ** (-0.5)
        attn = fake_quant(attn, attn_scale)
        exp_int, exp_int_sum = int_softmax(attn, attn_scale)
        softmax_out = jnp.round(exp_int_sum / exp_int)
        rounds = log_round(softmax_out)
        mask = rounds >= 2.0 ** BITS_S
        qlog = jnp.clip(rounds, 0.0, 2.0 ** BITS_S - 1.0)
        p = jnp.where(mask, 0.0, 2.0 ** (-qlog))
        out = jnp.einsum('bhnm,bhmd->bhnd', p, v)
        out = out.transpose(0, 2, 1, 3).reshape(B, N, C)
        out = fake_quant(out, a2_scale)
        out = out @ fake_quant(proj_w, w_proj_scale).T + proj_b
        out = fake_quant(out, a3_scale)
        return out

    def _L2_ffn_ref(x, Wg, W1, W2):
        import jax, jax.numpy as jnp
        import numpy as np
        E = 8
        TOP_K = 2
        CAP_RATIO = 1.2
        B, L, D = x.shape
        H = W2.shape[1]
        xf = x.reshape(-1, D)
        N = xf.shape[0]
        capacity = int(CAP_RATIO * N / E)
        logits = xf @ Wg
        scores, idx = jax.lax.top_k(logits, TOP_K)
        weights = jax.nn.softmax(scores, axis=-1)
        xpad = jnp.concatenate([xf, jnp.zeros((1, D), xf.dtype)], axis=0)
        wpad_zero = jnp.zeros((1,), weights.dtype)
        out = jnp.zeros((N, D), x.dtype)
        for k in range(TOP_K):
            ik = idx[:, k]
            onehot = ik[:, None] == jnp.arange(E)[None, :]
            pos = jnp.cumsum(onehot, axis=0) - 1
            posk = jnp.take_along_axis(pos, ik[:, None], axis=1)[:, 0]
            keep = posk < capacity
            buf = jnp.full((E, capacity), N, dtype=jnp.int32)
            buf = buf.at[ik, posk].set(jnp.arange(N, dtype=jnp.int32), mode='drop')
            xg = xpad[buf]
            h = jnp.einsum('ecd,edh->ech', xg, W1)
            act = h[..., :H] * jax.nn.silu(h[..., H:])
            ye = jnp.einsum('ech,ehd->ecd', act, W2)
            wk = jnp.where(keep, weights[:, k], 0.0)
            w_buf = jnp.concatenate([wk, wpad_zero])[buf]
            out = out.at[buf.reshape(-1)].add((w_buf[..., None] * ye).reshape(E * capacity, D), mode='drop')
        return out.reshape(B, L, D)

    def _L3_attn_ref(x, w_qkv):
        import jax, jax.numpy as jnp
        import numpy as np
        EPS = 1e-05

        def _ste(y, x):
            return x + jax.lax.stop_gradient(y - x)

        def _absmean_quant(x):
            s = jnp.mean(jnp.abs(x)) + EPS
            u = x / s
            q = _ste(jnp.round(jnp.clip(u, -1.0, 1.0)), u)
            return (q, s)

        def _ternary_weight(w):
            s = jnp.mean(jnp.abs(w)) + EPS
            u = w / s
            return _ste(jnp.round(jnp.clip(u, -1.0, 1.0)), u) * s

        def _l1norm(x):
            return x / (jnp.sum(jnp.abs(x), axis=-1, keepdims=True) + EPS)
        B, N, C = x.shape
        H = 12
        D = C // H
        scale = D ** (-0.5)
        wq = _ternary_weight(w_qkv)
        qkv = jnp.einsum('bnc,oc->bno', x, wq)
        qkv = qkv.reshape(B, N, 3, H, D).transpose(2, 0, 3, 1, 4)
        q, k, v = (qkv[0], qkv[1], qkv[2])
        q_q, q_s = _absmean_quant(_l1norm(q))
        k_q, k_s = _absmean_quant(_l1norm(k))
        v_q, v_s = _absmean_quant(_l1norm(v))
        attn = jnp.einsum('bhnd,bhmd->bhnm', q_q, k_q) * scale
        attn = attn * q_s * k_s
        attn_q, qk_s = _absmean_quant(attn)
        out = jnp.einsum('bhnm,bhmd->bhnd', attn_q, v_q)
        out = out.transpose(0, 2, 1, 3).reshape(B, N, C)
        return out * qk_s * v_s

    def _L3_ffn_ref(x, gate_w, gate_b, fc1_w, fc1_b, ln_w, ln_b, fc2_w, fc2_b):
        import jax, jax.numpy as jnp
        import numpy as np
        SEQ, BATCH, EMBED = (256, 2, 192)
        E = 16
        FFN_H = 384
        K_SHARED = 1
        K_ROUTE = 3
        LN_EPS = 1e-05
        NEG_INF = -1000000000.0
        S, B, D = x.shape
        T = S * B
        xf = x.reshape(T, D)
        scores = xf @ gate_w + gate_b
        scores = scores.at[:, :K_SHARED].set(NEG_INF)
        probs = jax.nn.softmax(scores, axis=-1)
        topv, topi = jax.lax.top_k(probs, K_ROUTE)
        combine = jnp.zeros((T, E), xf.dtype)
        combine = combine.at[jnp.arange(T)[:, None], topi].add(topv)
        combine = combine.at[:, :K_SHARED].add(1.0)
        h = jnp.einsum('td,edh->eth', xf, fc1_w) + fc1_b[:, None, :]
        h = jax.nn.gelu(h, approximate=False)
        mu = h.mean(-1, keepdims=True)
        var = h.var(-1, keepdims=True)
        h = (h - mu) * jax.lax.rsqrt(var + LN_EPS) * ln_w[:, None, :] + ln_b[:, None, :]
        y = jnp.einsum('eth,ehd->etd', h, fc2_w) + fc2_b[:, None, :]
        out = jnp.einsum('te,etd->td', combine, y)
        return out.reshape(S, B, D)
    h = _L0_tok_ref(x, L0_tok_W0, L0_tok_b0, L0_tok_W1, L0_tok_b1, L0_tok_W2, L0_tok_b2, L0_tok_Wf, L0_tok_bf, L0_tok_idx0, L0_tok_idx1, L0_tok_idx2)
    h = jnp.concatenate([h, _L0_txt_ref(x_txt, mask_BS_i1_0, L0_txt_word_emb, L0_txt_pos_emb, L0_txt_type_emb, L0_txt_conv_w, L0_txt_conv_b, L0_txt_residual_weight, L0_txt_ln_gamma, L0_txt_ln_beta)], axis=1)
    h = h + _L0_attn_ref(_layernorm(h, axis=-1), L0_attn_W_down, L0_attn_b_down, L0_attn_Wq, L0_attn_Wk, L0_attn_Wv, L0_attn_Wo, L0_attn_W1, L0_attn_b1, L0_attn_ttt_g, L0_attn_ttt_b, L0_attn_lr_w, L0_attn_lr_b, L0_attn_post_g, L0_attn_post_b, L0_attn_norm_g, L0_attn_norm_b, L0_attn_W_up, L0_attn_b_up)
    h = h + _L0_ffn_ref(_layernorm(h, axis=-1), L0_ffn_norm_scale, L0_ffn_gate_w, L0_ffn_gate_b, L0_ffn_mlp1_w, L0_ffn_mlp1_b, L0_ffn_mlp2_w, L0_ffn_mlp2_b)
    h = h + _L1_attn_ref(_layernorm(h, axis=-1), L1_attn_w_qkv, L1_attn_w_proj, L1_attn_b_proj)
    h = h + _L1_ffn_ref(_layernorm(h, axis=-1), L1_ffn_Wg, L1_ffn_bg, L1_ffn_W1, L1_ffn_b1, L1_ffn_W2, L1_ffn_b2)
    h = h + _L2_attn_ref(_layernorm(h, axis=-1), L2_attn_qkv_w, L2_attn_qkv_b, L2_attn_proj_w, L2_attn_proj_b, L2_attn_w_qkv_scale, L2_attn_a1_scale, L2_attn_attn_scale, L2_attn_a2_scale, L2_attn_w_proj_scale, L2_attn_a3_scale)
    h = h + _L2_ffn_ref(_layernorm(h, axis=-1), L2_ffn_Wg, L2_ffn_W1, L2_ffn_W2)
    h = h + _L3_attn_ref(_layernorm(h, axis=-1), L3_attn_w_qkv)
    h = h + _L3_ffn_ref(_layernorm(h, axis=-1), L3_ffn_gate_w, L3_ffn_gate_b, L3_ffn_fc1_w, L3_ffn_fc1_b, L3_ffn_ln_w, L3_ffn_ln_b, L3_ffn_fc2_w, L3_ffn_fc2_b)
    return h

_drawn_inputs = setup_inputs


def setup_inputs(seed=0):
    import zlib

    import numpy as np

    out = dict(_drawn_inputs(seed))
    spreads = {'L0_txt_ln_gamma': (1.0, 0.2),
     'L0_txt_ln_beta': (0.0, 0.1),
     'L0_attn_b_down': (0.0, 0.272),
     'L0_attn_b1': (0.0, 0.1),
     'L0_attn_ttt_g': (1.0, 0.2),
     'L0_attn_ttt_b': (0.0, 0.1),
     'L0_attn_lr_b': (0.0, 0.8),
     'L0_attn_post_g': (1.0, 0.2),
     'L0_attn_post_b': (0.0, 0.1),
     'L0_attn_norm_g': (1.0, 0.2),
     'L0_attn_norm_b': (0.0, 0.1),
     'L0_attn_b_up': (0.0, 0.1),
     'L0_ffn_norm_scale': (1.0, 0.6),
     'L0_ffn_gate_b': (0.0, 0.745),
     'L1_attn_b_proj': (0.0, 0.1),
     'L2_attn_qkv_b': (0.0, 0.8),
     'L2_attn_proj_b': (0.0, 0.576),
     'L3_ffn_gate_b': (0.0, 2.0),
     'L3_ffn_fc1_b': (0.0, 0.568),
     'L3_ffn_ln_w': (1.0, 0.6),
     'L3_ffn_ln_b': (0.0, 1.742),
     'L3_ffn_fc2_b': (0.0, 0.749)}
    factors = {'L0_tok_b0': 4.265,
     'L0_tok_b1': 4.286,
     'L0_tok_b2': 4.153,
     'L0_attn_lr_w': 8.0,
     'L0_ffn_gate_w': 3.375,
     'L0_ffn_mlp1_w': 2.868,
     'L0_ffn_mlp1_b': 8.0,
     'L0_ffn_mlp2_w': 2.986,
     'L0_ffn_mlp2_b': 7.988,
     'L1_attn_w_qkv': 200.0,
     'L1_attn_w_proj': 200.0,
     'L1_ffn_b1': 7.255,
     'L1_ffn_b2': 5.038,
     'L2_attn_qkv_w': 8.0,
     'L2_attn_proj_w': 8.0,
     'L2_ffn_Wg': 8.0,
     'L2_ffn_W1': 8.0,
     'L2_ffn_W2': 8.0,
     'L3_attn_w_qkv': 200.0,
     'L3_ffn_gate_w': 8.0}
    for name, (base, spread) in spreads.items():
        noise = np.random.default_rng([zlib.crc32(name.encode()), seed]).standard_normal(out[name].shape)
        drawn = base * np.exp(spread * noise) if base else spread * noise
        out[name] = jnp.asarray(drawn.astype(out[name].dtype))
    for name, factor in factors.items():
        out[name] = (out[name] * factor).astype(out[name].dtype)
    return out
```

```python
from contextlib import ExitStack, contextmanager

import numpy as np

import concourse.bass as bass
from concourse import mybir

F32 = mybir.dt.float32
BF16 = mybir.dt.bfloat16
I32 = mybir.dt.int32
U32 = mybir.dt.uint32
ALU = mybir.AluOpType
ACT = mybir.ActivationFunctionType
AX = mybir.AxisListType

B = 2
IMG_TOK, TXT_TOK = 256, 77
S = IMG_TOK + TXT_TOK
D = 192
R = 111
NT = B * S // R
TPB = S // R
KC = 96
ROUND = 1.5 * 2.0 ** 23


class Steps:

    def __init__(self, eng, sem):
        self.eng, self.sem, self.n = eng, sem, 0

    def __call__(self, ins):
        self.n += 1
        ins.then_inc(self.sem, 1)
        self.eng.wait_ge(self.sem, self.n)

    def start(self, ins):
        self.n += 1
        ins.then_inc(self.sem, 1)

    def wait(self):
        self.eng.wait_ge(self.sem, self.n)


@contextmanager
def stage(nc, *names):
    with ExitStack() as c:
        sems = [c.enter_context(nc.semaphore(n)) for n in names]
        with nc.Block(no_gpsimd_drain=True) as block:
            yield (block, *sems)
        nums = sorted(s.num for s in sems)
        first = nums[0]
        for n, after in zip(nums, nums[1:] + [None]):
            if after != n + 1:
                nc.gpsimd.sem_clear(range(first, n + 1))
                first = after
        nc.all_engine_barrier(sem_only=True)


def bcast(ap, parts):
    return bass.AP(tensor=ap.tensor, offset=ap.offset, ap=[[0, parts]] + [list(x) for x in ap.ap])


class Chip:

    def __init__(self, nc, ctx):
        self.nc, self.ctx = nc, ctx
        self.h = self.sb("h", [R, NT, D])
        self.xn = self.sb("xn", [R, NT, D])
        self.xt = self.sb("xt", [KC + 1, 2, B * S])
        self.ident = self.sb("ident", [128, 128])
        self.ones = self.sb("ones", [128, 128])
        self.stats = self.sb("stats", [R, NT, 6])
        self.mv = self.sb("mv", [R, NT, 2])
        self.rstd = self.sb("rstd", [R, NT, 1])
        self.neg_half = self.sb("neg_half", [128, 8])
        self.ps = ctx.enter_context(nc.psum_tensor("ps", [128, 8, 512], F32))

    def sb(self, name, shape, dt=F32, ctx=None):
        return (ctx or self.ctx).enter_context(self.nc.sbuf_tensor(name, shape, dt))


def constants(nc, k):
    with stage(nc, "filled", "selected") as (block, filled, selected):
        @block.gpsimd
        def _(pool):
            nc.gpsimd.memset(k.ident[:, :], 0.0).then_inc(filled, 1)
            nc.gpsimd.memset(k.ones[:, :], 1.0).then_inc(filled, 1)
            nc.gpsimd.memset(k.neg_half[:, :], -0.5).then_inc(filled, 1)
            nc.gpsimd.memset(k.xt[:, :, :], 1.0).then_inc(filled, 1)
            pool.wait_ge(filled, 4)
            nc.gpsimd.affine_select(out=k.ident[:, :], in_=k.ident[:, :], compare_op=ALU.not_equal, fill=1.0,
                                    base=0, pattern=[[-1, 128]], channel_multiplier=1).then_inc(selected, 1)
            pool.wait_ge(selected, 1)


def normalise(nc, k, src, dst, eps, gain=None, shift=None):
    with stage(nc, "dve_done", "aggregated", "rstd_eps", "rstd_ready") as (block, dve_done, aggregated, rstd_eps, rstd_ready):
        @block.vector
        def _(dve):
            step = Steps(dve, dve_done)
            for t in range(NT):
                step.start(nc.vector.bn_stats(k.stats[:, t, :], src[:, t, :]))
            step.wait()
            for t in range(NT):
                nc.vector.bn_aggr(k.mv[:, t, :], k.stats[:, t, :]).then_inc(aggregated, 1)
            dve.wait_ge(aggregated, NT)
            dve.wait_ge(rstd_ready, 1)
            for t in range(NT):
                step.start(nc.vector.tensor_scalar(dst[:, t, :], src[:, t, :], k.mv[:, t, 0:1], k.rstd[:, t, 0:1],
                                                   ALU.subtract, ALU.mult))
            step.wait()
            if gain is not None:
                step(nc.vector.tensor_tensor(dst[:, :, :], dst[:, :, :], gain.unsqueeze(1).broadcast_to([R, NT, D]), ALU.mult))
                step(nc.vector.tensor_tensor(dst[:, :, :], dst[:, :, :], shift.unsqueeze(1).broadcast_to([R, NT, D]), ALU.add))

        @block.gpsimd
        def _(pool):
            pool.wait_ge(aggregated, NT)
            nc.gpsimd.tensor_scalar(k.rstd[:, :, :], k.mv[:, :, 1:2], eps, None, ALU.add).then_inc(rstd_eps, 1)
            pool.wait_ge(rstd_eps, 1)
            nc.gpsimd.tensor_tensor(k.rstd[:, :, 0], k.rstd[:, :, 0], k.neg_half[0:R, 0:NT], ALU.pow).then_inc(rstd_ready, 1)


def to_columns(nc, k, src, dst):
    with stage(nc, "bank_ready", "act_copied", "dve_copied") as (block, bank_ready, act_copied, dve_copied):
        banks = [(b, c) for b in range(B) for c in range(2)]

        @block.tensor
        def _(pe):
            for n, (b, c) in enumerate(banks):
                for j in range(TPB):
                    ins = nc.tensor.transpose(k.ps[0:KC, n, j * R:(j + 1) * R], src[:, b * TPB + j, c * KC:(c + 1) * KC],
                                              k.ident[0:R, 0:R])
                ins.then_inc(bank_ready, 1)

        @block.scalar
        def _(act):
            for n in (0, 2):
                b, c = banks[n]
                act.wait_ge(bank_ready, n + 1)
                nc.scalar.copy(dst[0:KC, c, b * S:(b + 1) * S], k.ps[0:KC, n, 0:S]).then_inc(act_copied, 1)
            act.wait_ge(act_copied, 2)

        @block.vector
        def _(dve):
            for n in (1, 3):
                b, c = banks[n]
                dve.wait_ge(bank_ready, n + 1)
                nc.vector.tensor_copy(dst[0:KC, c, b * S:(b + 1) * S], k.ps[0:KC, n, 0:S]).then_inc(dve_copied, 1)
            dve.wait_ge(dve_copied, 2)


def to_rows(nc, k, src, dst):
    with stage(nc, "tile_ready", "dve_copied") as (block, tile_ready, dve_copied):
        @block.tensor
        def _(pe):
            for t in range(NT):
                for c in range(2):
                    ins = nc.tensor.transpose(k.ps[0:R, t, c * KC:(c + 1) * KC], src[0:KC, c, t * R:(t + 1) * R],
                                              k.ident[0:KC, 0:KC])
                ins.then_inc(tile_ready, 1)

        @block.vector
        def _(dve):
            for t in range(NT):
                dve.wait_ge(tile_ready, t + 1)
                nc.vector.tensor_copy(dst[:, t, :], k.ps[0:R, t, 0:D]).then_inc(dve_copied, 1)
            dve.wait_ge(dve_copied, NT)


def interpolation(n_in, n_out):
    pos = np.clip((np.arange(n_out, dtype=np.float32) + 0.5) * (n_in / n_out) - 0.5, 0.0, n_in - 1).astype(np.float32)
    i0 = np.floor(pos).astype(np.int32)
    w = (pos - i0).astype(np.float32)
    m = np.zeros((n_in, n_out), np.float32)
    m[i0, np.arange(n_out)] += np.float32(1.0) - w
    m[np.minimum(i0 + 1, n_in - 1), np.arange(n_out)] += w
    return m
PATCHES = 16
LEVELS = [(1, 256), (2, 64), (4, 16)]
EMB = 64


def embed(nc, k, a):
    with ExitStack() as c:
        idx = [k.sb(f"idx{n}", [min(tok, 128), max(tok // 128, 1), PATCHES], I32, c) for n, (_, tok) in enumerate(LEVELS)]
        width = [B * p * p * 3 for p, _ in LEVELS]
        got = [k.sb(f"got{n}", [min(tok, 128), max(tok // 128, 1), PATCHES, w], F32, c)
               for n, ((_, tok), w) in enumerate(zip(LEVELS, width))]
        feat = [k.sb(f"feat{n}", [min(tok, 128), max(tok // 128, 1), B, PATCHES * w // B], F32, c)
                for n, ((_, tok), w) in enumerate(zip(LEVELS, width))]
        din = [PATCHES * w // B for w in width]
        kw = [min(d, KC) for d in din]
        nk = [d // w for d, w in zip(din, kw)]
        wt = [k.sb(f"tokw{n}", [kw[n], nk[n], EMB], F32, c) for n in range(3)]
        bias0 = k.sb("tok_bias0", [EMB, 1], F32, c)
        bias = [None] + [k.sb(f"tok_bias{n}", [1, EMB], F32, c) for n in (1, 2)]
        wf = k.sb("tok_wf", [EMB, 3, D], F32, c)
        bf = k.sb("tok_bf", [KC, 2], F32, c)
        inter = [None] + [k.sb(f"inter{n}", [LEVELS[n][1], IMG_TOK], F32, c) for n in (1, 2)]
        ft = [k.sb("ft0", [48, B, 256], F32, c), k.sb("ft1", [KC, B, 2, 64], F32, c), k.sb("ft2", [KC, B, 8, 16], F32, c)]
        lev = [None, k.sb("lev1", [64, B, EMB], F32, c), k.sb("lev2", [16, B, EMB], F32, c)]
        yt = k.sb("yt", [EMB, 3, B * IMG_TOK], F32, c)
        ids = k.sb("ids", [TXT_TOK, B], I32, c)
        typ = k.sb("typ", [TXT_TOK, B], I32, c)
        we = k.sb("we", [TXT_TOK, B, D], F32, c)
        te = k.sb("te", [TXT_TOK, B, D], F32, c)
        pe_ = k.sb("pos", [TXT_TOK, D], F32, c)
        wpad = k.sb("wpad", [TXT_TOK, B, D + 2], F32, c)
        ppad = k.sb("ppad", [TXT_TOK, B, D + 2], F32, c)
        cw = k.sb("conv_w", [TXT_TOK, 8], F32, c)
        gamma = k.sb("txt_gamma", [TXT_TOK, D], F32, c)
        beta = k.sb("txt_beta", [TXT_TOK, D], F32, c)
        conv = k.sb("conv", [TXT_TOK, B, D], F32, c)
        emb = k.sb("emb", [TXT_TOK, B, D], F32, c)
        one_minus = k.sb("one_minus", [TXT_TOK, 1], F32, c)
        st = k.sb("txt_stats", [TXT_TOK, B, 6], F32, c)
        mv = k.sb("txt_mv", [TXT_TOK, B, 2], F32, c)
        rs = k.sb("txt_rstd", [TXT_TOK, B], F32, c)
        N_SMALL = 21

        gathered = [k.ctx.enter_context(nc.semaphore(f"gathered{n}")) for n in range(3)]
        txt_gathered = k.ctx.enter_context(nc.semaphore("txt_gathered"))
        with stage(nc, "idx_in", "small_in", "feat_done", "feat_t", "ft_done", "mm_done",
                   "evac", "dve_done", "var_ready", "rstd_ready", "ready", "pool_done") as \
                (block, idx_in, small_in, feat_done, feat_t, ft_done, mm_done,
                 evac, dve_done, var_ready, rstd_ready, ready, pool_done):
            @block.sync
            def _(sp):
                for n, (_, tok) in enumerate(LEVELS):
                    sp.dma_start(idx[n][:, :, :], a[f"L0_tok_idx{n}"].rearrange("(t p g) -> p t g", g=PATCHES, p=min(tok, 128))
                                 ).then_inc(idx_in, 16)
                sp.dma_start(ids[:, :], a["x_txt"]).then_inc(idx_in, 16)
                sp.dma_start(typ[:, :], a["mask_BS_i1_0"]).then_inc(idx_in, 16)
                for n in range(3):
                    sp.dma_start(wt[n][:, :, :], a[f"L0_tok_W{n}"].rearrange("(c p) e -> p c e", p=kw[n])).then_inc(small_in, 16)
                sp.dma_start(bias0[:, :], a["L0_tok_b0"].unsqueeze(1)).then_inc(small_in, 16)
                for n in (1, 2):
                    sp.dma_start(bias[n][:, :], a[f"L0_tok_b{n}"].unsqueeze(0)).then_inc(small_in, 16)
                    sp.dma_start(inter[n][:, :], a[f"inter{n}"]).then_inc(small_in, 16)
                sp.dma_start(wf[:, :, :], a["L0_tok_Wf"].rearrange("(l p) e -> p l e", p=EMB)).then_inc(small_in, 16)
                sp.dma_start(bf[:, :], a["L0_tok_bf"]).then_inc(small_in, 16)

            @block.scalar
            def _(act):
                act.dma_start(pe_[:, :], a["L0_txt_pos_emb"][0:TXT_TOK, :]).then_inc(small_in, 16)
                act.dma_start(cw[:, 0:6], bcast(a["L0_txt_conv_w"].rearrange("a b -> (a b)"), TXT_TOK)).then_inc(small_in, 16)
                act.dma_start(cw[:, 6:7], bcast(a["L0_txt_conv_b"], TXT_TOK)).then_inc(small_in, 16)
                act.dma_start(cw[:, 7:8], bcast(a["L0_txt_residual_weight"], TXT_TOK)).then_inc(small_in, 16)
                act.dma_start(gamma[:, :], bcast(a["L0_txt_ln_gamma"], TXT_TOK)).then_inc(small_in, 16)
                act.dma_start(beta[:, :], bcast(a["L0_txt_ln_beta"], TXT_TOK)).then_inc(small_in, 16)
                act.wait_ge(small_in, 16 * 16)

            @block.gpsimd
            def _(pool):
                pool.wait_ge(idx_in, 16 * 5)
                for b in range(B):
                    for dst, table, at in ((we, "L0_txt_word_emb", ids), (te, "L0_txt_type_emb", typ)):
                        pool.indirect_dma_start(dst[:, b, :], None, a[table], bass.IndirectOffsetOnAxis(ap=at[:, b:b + 1], axis=0)
                                                ).then_inc(txt_gathered, 16)
                for n, (_, tok) in enumerate(LEVELS):
                    for t in range(max(tok // 128, 1)):
                        for g in range(PATCHES):
                            pool.indirect_dma_start(got[n][:, t, g, :], None, a[f"pix{n}"],
                                                    bass.IndirectOffsetOnAxis(ap=idx[n][:, t, g:g + 1], axis=0)
                                                    ).then_inc(gathered[n], 16)
                pool.wait_ge(var_ready, 1)
                nc.gpsimd.tensor_tensor(rs[:, :], rs[:, :], k.neg_half[0:TXT_TOK, 0:B], ALU.pow).then_inc(rstd_ready, 1)


            @block.vector
            def _(dve):
                step = Steps(dve, dve_done)
                step.start(nc.vector.memset(wpad[:, :, :], 0.0))
                step(nc.vector.memset(ppad[:, :, :], 0.0))
                dve.wait_ge(small_in, 16 * 16)
                dve.wait_ge(txt_gathered, 16 * 4)
                for b in range(B):
                    step.start(nc.vector.tensor_copy(wpad[:, b, 1:D + 1], we[:, b, :]))
                    step.start(nc.vector.tensor_copy(ppad[:, b, 1:D + 1], pe_[:, :]))
                step(nc.vector.tensor_scalar(one_minus[:, :], cw[:, 7:8], -1.0, 1.0, ALU.mult, ALU.add))
                step(nc.vector.tensor_scalar(conv[:, :, :], wpad[:, :, 0:D], cw[:, 0:1], cw[:, 6:7], ALU.mult, ALU.add))
                for pad, first, taps in ((wpad, 0, (1, 2)), (ppad, 3, (0, 1, 2))):
                    for tap in taps:
                        step(nc.vector.scalar_tensor_tensor(conv[:, :, :], pad[:, :, tap:tap + D], cw[:, first + tap:first + tap + 1],
                                                            conv[:, :, :], ALU.mult, ALU.add))
                step(nc.vector.tensor_tensor(emb[:, :, :], wpad[:, :, 1:D + 1], ppad[:, :, 1:D + 1], ALU.add))
                step(nc.vector.scalar_tensor_tensor(emb[:, :, :], emb[:, :, :], one_minus[:, 0:1], te[:, :, :], ALU.mult, ALU.add))
                step(nc.vector.scalar_tensor_tensor(emb[:, :, :], conv[:, :, :], cw[:, 7:8], emb[:, :, :], ALU.mult, ALU.add))
                for b in range(B):
                    step(nc.vector.bn_stats(st[:, b, :], emb[:, b, :]))
                    step(nc.vector.bn_aggr(mv[:, b, :], st[:, b, :]))
                nc.vector.tensor_scalar(rs[:, :], mv[:, :, 1], 1e-12, None, ALU.add).then_inc(var_ready, 1)
                dve.wait_ge(rstd_ready, 1)
                for b in range(B):
                    step(nc.vector.tensor_scalar(emb[:, b, :], emb[:, b, :], mv[:, b, 0:1], rs[:, b:b + 1], ALU.subtract, ALU.mult))
                    step(nc.vector.tensor_tensor(emb[:, b, :], emb[:, b, :], gamma[:, :], ALU.mult))
                    nc.vector.tensor_tensor(emb[:, b, :], emb[:, b, :], beta[:, :], ALU.add).then_inc(feat_done, 1)
                for n, (_, tok) in enumerate(LEVELS):
                    dve.wait_ge(gathered[n], 16 * PATCHES * max(tok // 128, 1))
                    f = width[n] // B
                    for t in range(max(tok // 128, 1)):
                        for b in range(B):
                            nc.vector.tensor_copy(feat[n][:, t, b, :].rearrange("p (g f) -> p g f", f=f),
                                                  got[n][:, t, :, b * f:(b + 1) * f]).then_inc(feat_done, 1)
                dve.wait_ge(feat_t, 1)
                step.start(nc.vector.tensor_copy(k.xt[0:KC, 0, :].rearrange("p (b s) -> p b s", b=B)[:, :, IMG_TOK:S],
                                                 k.ps[0:KC, 0, 0:B * TXT_TOK].rearrange("p (b s) -> p b s", b=B)))
                step.start(nc.vector.tensor_copy(k.xt[0:KC, 1, :].rearrange("p (b s) -> p b s", b=B)[:, :, IMG_TOK:S],
                                                 k.ps[0:KC, 1, 0:B * TXT_TOK].rearrange("p (b s) -> p b s", b=B)))
                dve.wait_ge(feat_t, 2)
                nc.vector.tensor_copy(ft[0][:, :, :], k.ps[0:48, 2, :].rearrange("p (b s) -> p b s", b=B)).then_inc(ft_done, 1)
                dve.wait_ge(feat_t, 3)
                nc.vector.tensor_copy(ft[1][:, :, :, :], k.ps[0:KC, 3, 0:256].rearrange("p (b c s) -> p b c s", b=B, c=2)).then_inc(ft_done, 1)
                dve.wait_ge(feat_t, 4)
                nc.vector.tensor_copy(ft[2][:, :, :, :], k.ps[0:KC, 4, 0:256].rearrange("p (b c s) -> p b c s", b=B, c=8)).then_inc(ft_done, 1)
                dve.wait_ge(mm_done, 1)
                nc.vector.tensor_scalar(yt[:, 0, :], k.ps[0:EMB, 5, :], bias0[:, 0:1], None, ALU.add).then_inc(evac, 1)
                dve.wait_ge(mm_done, 2)
                nc.vector.tensor_copy(lev[1][:, :, :], k.ps[0:64, 6, 0:B * EMB].rearrange("p (b e) -> p b e", b=B)).then_inc(evac, 1)
                dve.wait_ge(mm_done, 3)
                nc.vector.tensor_copy(lev[2][:, :, :], k.ps[0:16, 7, 0:B * EMB].rearrange("p (b e) -> p b e", b=B)).then_inc(evac, 1)
                for n in (1, 2):
                    dve.wait_ge(mm_done, 3 + n)
                    nc.vector.tensor_copy(yt[:, n, :], k.ps[0:EMB, n + 1, :]).then_inc(evac, 1)
                for ch in range(2):
                    dve.wait_ge(mm_done, 6 + ch)
                    step.start(nc.vector.tensor_scalar(k.xt[0:KC, ch, :].rearrange("p (b s) -> p b s", b=B)[:, :, 0:IMG_TOK],
                                                       k.ps[0:KC, ch, :].rearrange("p (b s) -> p b s", b=B), bf[:, ch:ch + 1], None, ALU.add))
                step.wait()

            @block.tensor
            def _(pe):
                mm, tr = nc.tensor.matmul, nc.tensor.transpose
                pe.wait_ge(feat_done, 2)
                for ch in range(2):
                    for b in range(B):
                        ins = tr(k.ps[0:KC, ch, b * TXT_TOK:(b + 1) * TXT_TOK], emb[:, b, ch * KC:(ch + 1) * KC], k.ident[0:TXT_TOK, 0:TXT_TOK])
                ins.then_inc(feat_t, 1)
                pe.wait_ge(feat_done, 2 + 4)
                for b in range(B):
                    for t in range(2):
                        ins = tr(k.ps[0:48, 2, b * 256 + t * 128:b * 256 + (t + 1) * 128], feat[0][:, t, b, :], k.ident[:, :])
                ins.then_inc(feat_t, 1)
                pe.wait_ge(feat_done, 2 + 6)
                for b in range(B):
                    for ch in range(2):
                        ins = tr(k.ps[0:KC, 3, (b * 2 + ch) * 64:(b * 2 + ch + 1) * 64], feat[1][:, 0, b, ch * KC:(ch + 1) * KC], k.ident[0:64, 0:64])
                ins.then_inc(feat_t, 1)
                pe.wait_ge(feat_done, 2 + 8)
                for b in range(B):
                    for ch in range(8):
                        ins = tr(k.ps[0:KC, 4, (b * 8 + ch) * 16:(b * 8 + ch + 1) * 16], feat[2][:, 0, b, ch * KC:(ch + 1) * KC], k.ident[0:16, 0:16])
                ins.then_inc(feat_t, 1)
                pe.wait_ge(small_in, 16 * 16)
                pe.wait_ge(ft_done, 1)
                mm(k.ps[0:EMB, 5, :], wt[0][:, 0, :], ft[0][:, :, :].rearrange("p b s -> p (b s)"), start=True, stop=True).then_inc(mm_done, 1)
                for n in (1, 2):
                    pe.wait_ge(ft_done, n + 1)
                    tok = LEVELS[n][1]
                    for b in range(B):
                        for ch in range(nk[n]):
                            mm(k.ps[0:tok, 5 + n, b * EMB:(b + 1) * EMB], ft[n][:, b, ch, :], wt[n][:, ch, :], start=(ch == 0), stop=False)
                        ins = mm(k.ps[0:tok, 5 + n, b * EMB:(b + 1) * EMB], k.ones[0:1, 0:tok], bias[n][:, :], start=False, stop=True)
                    ins.then_inc(mm_done, 1)
                for n in (1, 2):
                    pe.wait_ge(evac, 1 + n)
                    for b in range(B):
                        ins = mm(k.ps[0:EMB, n + 1, b * IMG_TOK:(b + 1) * IMG_TOK], lev[n][:, b, :], inter[n][:, :], start=True, stop=True)
                    ins.then_inc(mm_done, 1)
                pe.wait_ge(evac, 5)
                pe.wait_ge(dve_done, 21)
                for ch in range(2):
                    for n in range(3):
                        ins = mm(k.ps[0:KC, ch, :], wf[:, n, ch * KC:(ch + 1) * KC], yt[:, n, :], start=(n == 0), stop=(n == 2))
                    ins.then_inc(mm_done, 1)
    to_rows(nc, k, k.xt, k.h)


def project(nc, k, w, dst=None, add_to=None):
    kk = w.shape[0]
    with stage(nc, "tile_ready", "dve_done") as (block, tile_ready, dve_done):
        @block.tensor
        def _(pe):
            for t in range(NT):
                nc.tensor.matmul(k.ps[0:R, t, 0:D], k.xt[0:KC, 0, t * R:(t + 1) * R], w[0:KC, 0, :], start=True, stop=False)
                nc.tensor.matmul(k.ps[0:R, t, 0:D], k.xt[0:kk, 1, t * R:(t + 1) * R], w[0:kk, 1, :], start=False, stop=True
                                 ).then_inc(tile_ready, 1)

        @block.vector
        def _(dve):
            for t in range(NT):
                dve.wait_ge(tile_ready, t + 1)
                if dst is not None:
                    nc.vector.tensor_copy(dst[:, t, :], k.ps[0:R, t, 0:D]).then_inc(dve_done, 1)
                else:
                    nc.vector.tensor_tensor(add_to[:, t, :], k.ps[0:R, t, 0:D], add_to[:, t, :], ALU.add).then_inc(dve_done, 1)
            dve.wait_ge(dve_done, NT)


NH0, HD = 3, 64
NJ = B * NH0
C = 21
NCH = -(-S // C)
SP = NCH * C
RJ = NJ * C
LAST = S - (NCH - 1) * C


def ttt_constants():
    j, t = np.divmod(np.arange(RJ), C)
    same = j[:, None] == j[None, :]
    return {"ttt_before": -(same & (t[:, None] < t[None, :])).astype(np.float32),
            "ttt_upto": -(same & (t[:, None] <= t[None, :])).astype(np.float32),
            "ttt_member": -(j[:, None] == np.arange(NJ)[None, :]).astype(np.float32)}


def ttt_attention(nc, k, a):
    with ExitStack() as c:
        w_down = k.sb("w_down", [KC, 2, D], F32, c)
        b_down = k.sb("b_down", [KC, 2], F32, c)
        hid = k.sb("hid", [KC + 1, 2, B, SP], F32, c)
        w_row = k.sb("w_row", [KC + 1, 2, NH0, 3 * HD + 1], F32, c)
        w_out = k.sb("w_out", [KC, 2, D], F32, c)
        w_up = k.sb("w_up", [KC + 1, 2, D], F32, c)
        post = k.sb("post", [R, 4, D], F32, c)
        g_row = k.sb("g_row", [RJ, HD], F32, c)
        g2_row = k.sb("g2_row", [RJ, HD], F32, c)
        b_row = k.sb("b_row", [RJ, HD], F32, c)
        before = k.sb("before", [RJ, RJ], F32, c)
        upto = k.sb("upto", [RJ, RJ], F32, c)
        member = k.sb("member", [RJ, NJ], F32, c)
        state = k.sb("state", [HD + 1, NJ, HD], F32, c)
        s_mean = k.sb("s_mean", [HD + 1, NJ], F32, c)
        hm = k.sb("hm", [KC + 1, NH0, 2, RJ], F32, c)
        kt = k.sb("kt", [HD + 1, 2, RJ], F32, c)
        ktm = k.sb("ktm", [HD + 1, 2, NJ, RJ], F32, c)
        k_aug = k.sb("k_aug", [RJ, HD + 1], F32, c)
        q_rows = k.sb("q_rows", [RJ, HD], F32, c)
        eta = k.sb("eta", [RJ, 1], F32, c)
        tgt = k.sb("tgt", [RJ, HD], F32, c)
        t_mean = k.sb("t_mean", [RJ, 1], F32, c)
        inner = k.sb("inner", [RJ, RJ], F32, c)
        inner_q = k.sb("inner_q", [RJ, RJ], F32, c)
        z0 = k.sb("z0", [RJ, HD], F32, c)
        pg = k.sb("pg", [RJ, HD], F32, c)
        y = k.sb("y", [RJ, HD], F32, c)
        zs = k.sb("zs", [RJ, HD], F32, c)
        tr = k.sb("tr", [RJ, HD], F32, c)
        junk = k.sb("junk", [RJ, HD], F32, c)
        junk2 = k.sb("junk2", [RJ, HD], F32, c)
        grad = k.sb("grad", [RJ, HD + 1], F32, c)
        gradc = k.sb("gradc", [RJ, HD], F32, c)
        sc = k.sb("sc", [RJ, 16], F32, c)
        eg = k.sb("eg", [RJ, NJ, HD], F32, c)
        outr = k.sb("outr", [RJ, HD], F32, c)
        st6 = k.sb("ttt_st6", [RJ, 6], F32, c)
        mv = k.sb("ttt_mv", [RJ, 2], F32, c)
        rq = k.sb("ttt_rq", [RJ, 1], F32, c)
        out_d = nc.dram_tensor("ttt_rows", [B, C + SP, D], F32).ap()
        v, r2, rstd, a1, a2, u, s2, yn, m64r2 = (sc[:, n:n + 1] for n in range(9))

        normalise(nc, k, k.h, k.xn, 1e-5)
        to_columns(nc, k, k.xn, k.xt)
        N_LOADS = 10 + 4 * NJ + 3 + 1
        with stage(nc, "loaded", "filled", "bank_ready", "act_done", "dve_done") as (block, loaded, filled, bank_ready, act_done, dve_done):
            @block.sync
            def _(sp):
                sp.dma_start(w_down[:, :, :], a["L0_attn_W_down"].rearrange("(c p) n -> p c n", p=KC)).then_inc(loaded, 16)
                sp.dma_start(b_down[:, :], a["L0_attn_b_down"]).then_inc(loaded, 16)
                sp.dma_start(w_row[0:KC, :, :, :], a["ttt_w_row"].rearrange("(c p) h n -> p c h n", p=KC)).then_inc(loaded, 16)
                sp.dma_start(w_out[:, :, :], a["L0_attn_Wo"].rearrange("(c p) n -> p c n", p=KC)).then_inc(loaded, 16)
                sp.dma_start(w_up[0:KC, :, :], a["L0_attn_W_up"].rearrange("(c p) n -> p c n", p=KC)).then_inc(loaded, 16)
                sp.dma_start(w_up[KC:KC + 1, 1, :], a["L0_attn_b_up"].unsqueeze(0)).then_inc(loaded, 16)
                for n, name in enumerate(("post_g", "post_b", "norm_g", "norm_b")):
                    sp.dma_start(post[:, n, :], bcast(a["L0_attn_" + name], R)).then_inc(loaded, 16)
                for j in range(NJ):
                    sp.dma_start(g_row[j * C:(j + 1) * C, :], bcast(a["L0_attn_ttt_g"][j % NH0], C)).then_inc(loaded, 16)
                    sp.dma_start(b_row[j * C:(j + 1) * C, :], bcast(a["L0_attn_ttt_b"][j % NH0], C)).then_inc(loaded, 16)
                    sp.dma_start(state[0:HD, j, :], a["L0_attn_W1"][j % NH0]).then_inc(loaded, 16)
                    sp.dma_start(state[HD:HD + 1, j, :], a["L0_attn_b1"][j % NH0]).then_inc(loaded, 16)
                sp.dma_start(before[:, :], a["ttt_before"]).then_inc(loaded, 16)
                sp.dma_start(upto[:, :], a["ttt_upto"]).then_inc(loaded, 16)
                sp.dma_start(member[:, :], a["ttt_member"]).then_inc(loaded, 16)
                sp.wait_ge(filled, 1)
                sp.dma_start(w_row[KC:KC + 1, 1, :, 3 * HD:3 * HD + 1], a["L0_attn_lr_b"].unsqueeze(0).unsqueeze(2), allow_slow_non_contiguous=True).then_inc(loaded, 16)
                sp.wait_ge(loaded, 16 * N_LOADS)

            @block.gpsimd
            def _(pool):
                step = Steps(pool, filled)
                step(nc.gpsimd.memset(w_row[KC:KC + 1, :, :, :], 0.0))
                step(nc.gpsimd.memset(hid[:, :, :, S:SP], 0.0))
                step(nc.gpsimd.memset(hid[KC:KC + 1, :, :, :], 1.0))
                step(nc.gpsimd.memset(hm[:, :, :, :], 0.0))
                step(nc.gpsimd.memset(kt[HD:HD + 1, :, :], 1.0))
                step(nc.gpsimd.memset(ktm[:, :, :, :], 0.0))
                step(nc.gpsimd.memset(k_aug[:, HD:HD + 1], 1.0))
                step(nc.gpsimd.memset(outr[:, :], 0.0))

            @block.tensor
            def _(pe):
                pe.wait_ge(loaded, 16 * N_LOADS)
                for b in range(B):
                    for m in range(2):
                        for kc in range(2):
                            ins = nc.tensor.matmul(k.ps[0:KC, 2 * b + m, 0:S], w_down[:, kc, m * KC:(m + 1) * KC],
                                                   k.xt[0:KC, kc, b * S:(b + 1) * S], start=(kc == 0), stop=(kc == 1))
                        ins.then_inc(bank_ready, 1)

            @block.scalar
            def _(act):
                for n in range(2 * B):
                    act.wait_ge(bank_ready, n + 1)
                    nc.scalar.activation(hid[0:KC, n % 2, n // 2, 0:S], k.ps[0:KC, n, 0:S], ACT.Silu,
                                         bias=b_down[:, n % 2:n % 2 + 1]).then_inc(act_done, 1)
                act.wait_ge(act_done, 2 * B)

            @block.vector
            def _(dve):
                step = Steps(dve, dve_done)
                dve.wait_ge(loaded, 16 * N_LOADS)
                dve.wait_ge(filled, 8)
                step.start(nc.vector.scalar_tensor_tensor(g2_row[:, :], g_row[:, :], -1.0 / HD, g_row[:, :], ALU.mult, ALU.mult))
                step(nc.vector.tensor_reduce(s_mean[:, :], state[:, :, :], AX.X, ALU.add))
                step(nc.vector.tensor_scalar(s_mean[:, :], s_mean[:, :], 1.0 / HD, None, ALU.mult))
                step(nc.vector.tensor_tensor(state[:, :, :], state[:, :, :], s_mean[:, :].unsqueeze(2).broadcast_to([HD + 1, NJ, HD]), ALU.subtract))
                for n in range(2):
                    own = ktm[HD:HD + 1, n, :, :].rearrange("p j r -> p (j r)")
                    for j in range(NJ):
                        step.start(nc.vector.memset(own[:, j * (RJ + C):j * (RJ + C) + C], 1.0))
                step.wait()

        def chunk(first_token, prev_row, sweeps):
            eg_done = 8 + 9 * sweeps - 1 + 3
            with stage(nc, "picked", "proj", "pool_done", "dve_copied", "grams", "act_done", "z_ready", "r2_ready", "rstd_ready",
                       "tr_ready", "m64_ready", "grad_ready", "dve_done", "q_var", "q_rstd", "stored", "states") as \
                    (block, picked, proj, pool_done, dve_copied, grams, act_done, z_ready, r2_ready, rstd_ready,
                     tr_ready, m64_ready, grad_ready, dve_done, q_var, q_rstd, stored, states):
                rows, cols_k, cols_q, gram_b, z0_b, zq_b = (k.ps[:, n, :] for n in range(6))
                z_bank = k.ps[0:RJ, 6, 0:HD + 1]

                @block.sync
                def _(sp):
                    for b in range(B):
                        dst = out_d[b, bass.ds(prev_row, C), :].rearrange("t (h e) -> h t e", h=NH0)
                        for h in range(NH0):
                            j = b * NH0 + h
                            sp.dma_start(dst[h], outr[j * C:(j + 1) * C, :]).then_inc(stored, 16)
                    sp.wait_ge(stored, 16 * NJ)

                @block.gpsimd
                def _(pool):
                    for h in range(NH0):
                        dst = hm[:, h, :, :].rearrange("p c (b r) -> p c b r", b=B)[:, :, :, h * C:(h + 1) * C]
                        nc.gpsimd.tensor_copy(dst[:, 0], hid[:, 0, :, bass.ds(first_token, C)]).then_inc(picked, 1)
                        nc.gpsimd.tensor_copy(dst[:, 1], hid[:, 1, :, bass.ds(first_token, C)]).then_inc(picked, 1)
                    for i in range(sweeps):
                        pool.wait_ge(r2_ready, i + 1)
                        if i:
                            pool.wait_ge(grad_ready, i)
                        nc.gpsimd.tensor_scalar(m64r2, r2, -float(HD), None, ALU.mult).then_inc(m64_ready, 1)
                    pool.wait_ge(q_var, 1)
                    nc.gpsimd.tensor_tensor(rq[:, :], mv[:, 1:2], k.neg_half[0:RJ, 0:1], ALU.pow).then_inc(q_rstd, 1)

                @block.tensor
                def _(pe):
                    mm = nc.tensor.matmul
                    pe.wait_ge(picked, 2 * NH0)
                    for h in range(NH0):
                        for kc in range(2):
                            kk = KC + kc
                            ins = mm(rows[0:RJ, 0:3 * HD + 1], hm[0:kk, h, kc, :], w_row[0:kk, kc, h, :],
                                     start=(h == 0 and kc == 0), stop=(h == NH0 - 1 and kc == 1))
                    ins.then_inc(proj, 1)
                    for bank, at in ((cols_k, 0), (cols_q, 2 * HD)):
                        for h in range(NH0):
                            own = slice(h * C, (h + 1) * C)
                            for kc in range(2):
                                ins = mm(bank[0:HD, 0:RJ].rearrange("p (b r) -> p b r", b=B)[:, :, own], w_row[0:KC, kc, h, at:at + HD],
                                         hm[0:KC, h, kc, :].rearrange("p (b r) -> p b r", b=B)[:, :, own],
                                         start=(kc == 0), stop=(kc == 1))
                        ins.then_inc(proj, 1)
                    pe.wait_ge(dve_copied, 2)
                    mm(gram_b[0:RJ, 0:RJ], kt[:, 0, :], kt[:, 0, :], start=True, stop=True).then_inc(grams, 1)
                    mm(gram_b[0:RJ, RJ:2 * RJ], kt[:, 0, :], kt[:, 1, :], start=True, stop=True).then_inc(grams, 1)
                    pe.wait_ge(dve_copied, 4)
                    for j in range(NJ):
                        ins = mm(z0_b[0:RJ, 0:HD], ktm[:, 0, j, :], state[:, j, :], start=(j == 0), stop=(j == NJ - 1))
                    ins.then_inc(grams, 1)
                    for j in range(NJ):
                        ins = mm(zq_b[0:RJ, 0:HD], ktm[:, 1, j, :], state[:, j, :], start=(j == 0), stop=False)
                    for i in range(1, sweeps):
                        pe.wait_ge(grad_ready, i)
                        mm(z_bank, inner[:, :], grad[:, :], start=True, stop=True).then_inc(z_ready, 1)
                    pe.wait_ge(dve_done, eg_done)
                    mm(zq_b[0:RJ, 0:HD], inner_q[:, :], gradc[:, :], start=False, stop=True).then_inc(states, 1)
                    mm(rows[0:HD + 1, 0:NJ * HD], k_aug[:, :], eg[:, :, :].rearrange("p j e -> p (j e)"), start=True, stop=True
                       ).then_inc(states, 1)

                @block.scalar
                def _(act):
                    act.wait_ge(proj, 1)
                    nc.scalar.activation(eta[:, :], rows[0:RJ, 3 * HD:3 * HD + 1], ACT.Sigmoid).then_inc(act_done, 1)
                    nc.scalar.copy(q_rows[:, :], rows[0:RJ, 2 * HD:3 * HD]).then_inc(act_done, 1)
                    nc.scalar.copy(k_aug[:, 0:HD], rows[0:RJ, 0:HD]).then_inc(act_done, 1)
                    for i in range(sweeps):
                        act.wait_ge(r2_ready, i + 1)
                        nc.scalar.activation(rstd, r2, ACT.Sqrt).then_inc(rstd_ready, 1)
                        act.wait_ge(rstd_ready, i + 1)
                        nc.scalar.activation(tr[:, :], tgt[:, :], ACT.Copy, scale=rstd).then_inc(tr_ready, 1)

                @block.vector
                def _(dve):
                    step = Steps(dve, dve_done)
                    V = nc.vector
                    for n, bank in enumerate((cols_k, cols_q)):
                        dve.wait_ge(proj, 2 + n)
                        V.tensor_copy(kt[0:HD, n, :], bank[0:HD, 0:RJ]).then_inc(dve_copied, 1)
                    for n, bank in enumerate((cols_k, cols_q)):
                        own = bass.AP(tensor=ktm[0:HD, n, :, :].tensor, offset=ktm[0:HD, n, :, :].offset,
                                      ap=[list(ktm[0:HD, n, :, :].ap[0]), [RJ + C, NJ], [1, C]])
                        V.tensor_copy(own, bank[0:HD, 0:RJ].rearrange("p (j t) -> p j t", j=NJ)).then_inc(dve_copied, 1)
                    dve.wait_ge(act_done, 3)
                    step(V.tensor_tensor(tgt[:, :], k_aug[:, 0:HD], rows[0:RJ, HD:2 * HD], ALU.subtract))
                    step(V.tensor_tensor(tgt[:, :], tgt[:, :], b_row[:, :], ALU.add))
                    step(V.tensor_tensor_reduce(tgt[:, :], tgt[:, :], g_row[:, :], 1.0, 0.0, ALU.mult, ALU.add, t_mean[:, :]))
                    step(V.tensor_scalar(t_mean[:, :], t_mean[:, :], 1.0 / HD, None, ALU.mult))
                    step(V.tensor_scalar(tgt[:, :], tgt[:, :], t_mean[:, 0:1], None, ALU.subtract))
                    step(V.tensor_scalar(eta[:, :], eta[:, :], 1.0 / HD, None, ALU.mult))
                    dve.wait_ge(grams, 2)
                    step.start(V.scalar_tensor_tensor(inner[:, :], gram_b[0:RJ, 0:RJ], eta[:, 0:1], before[:, :], ALU.mult, ALU.mult))
                    step.start(V.scalar_tensor_tensor(inner_q[:, :], gram_b[0:RJ, RJ:2 * RJ], eta[:, 0:1], upto[:, :], ALU.mult, ALU.mult))
                    step.wait()
                    dve.wait_ge(grams, 3)
                    V.tensor_copy(z0[:, :], z0_b[0:RJ, 0:HD]).then_inc(dve_copied, 1)
                    dve.wait_ge(dve_copied, 5)
                    for i in range(sweeps):
                        z = zs[:, :] if i else z0[:, :]
                        if i:
                            dve.wait_ge(z_ready, i)
                            step(V.scalar_tensor_tensor(z, z_bank[:, 0:HD], z_bank[:, HD:HD + 1], z0[:, :], ALU.add, ALU.add))
                        step.start(V.tensor_tensor_reduce(junk[:, :], z, z, 1.0 / HD, 1e-6, ALU.mult, ALU.add, v))
                        step.start(V.tensor_tensor(pg[:, :], z, g2_row[:, :], ALU.mult))
                        step.start(V.tensor_tensor_reduce(y[:, :], z, tgt[:, :], 1.0 / HD ** 2, 0.0, ALU.mult, ALU.add, a1))
                        dve.wait_ge(dve_done, step.n - 2)
                        V.reciprocal(r2, v).then_inc(r2_ready, 1)
                        dve.wait_ge(dve_done, step.n - 1)
                        step.start(V.tensor_tensor_reduce(junk2[:, :], z, pg[:, :], -1.0 / HD, 0.0, ALU.mult, ALU.add, a2))
                        step.wait()
                        dve.wait_ge(r2_ready, i + 1)
                        step(V.tensor_scalar(u, a2, r2, None, ALU.mult))
                        dve.wait_ge(rstd_ready, i + 1)
                        step(V.scalar_tensor_tensor(s2, a1, rstd, u, ALU.mult, ALU.add))
                        step(V.scalar_tensor_tensor(y[:, :], z, s2, pg[:, :], ALU.mult, ALU.add, accum_out=yn))
                        dve.wait_ge(tr_ready, i + 1)
                        dve.wait_ge(m64_ready, i + 1)
                        step.start(V.scalar_tensor_tensor(grad[:, 0:HD], y[:, :], m64r2, tr[:, :], ALU.mult, ALU.add))
                        V.tensor_scalar(grad[:, HD:HD + 1], yn, r2, None, ALU.mult).then_inc(grad_ready, 1)
                    dve.wait_ge(grad_ready, sweeps)
                    step.wait()
                    step(V.tensor_scalar(gradc[:, :], grad[:, 0:HD], grad[:, HD:HD + 1], None, ALU.add))
                    step(V.tensor_scalar(y[:, :], gradc[:, :], eta[:, 0:1], None, ALU.mult))
                    step(V.tensor_tensor(eg[:, :, :], y[:, :].unsqueeze(1).broadcast_to([RJ, NJ, HD]),
                                         member[:, :].unsqueeze(2).broadcast_to([RJ, NJ, HD]), ALU.mult))
                    assert step.n == eg_done
                    dve.wait_ge(states, 1)
                    step(V.bn_stats(st6[:, :], zq_b[0:RJ, 0:HD]))
                    step(V.bn_aggr(mv[:, :], st6[:, :]))
                    V.tensor_scalar(mv[:, 1:2], mv[:, 1:2], 1e-6, None, ALU.add).then_inc(q_var, 1)
                    dve.wait_ge(q_rstd, 1)
                    step(V.tensor_scalar(y[:, :], zq_b[0:RJ, 0:HD], mv[:, 0:1], rq[:, 0:1], ALU.subtract, ALU.mult))
                    step(V.tensor_tensor(y[:, :], y[:, :], g_row[:, :], ALU.mult))
                    step(V.tensor_tensor(y[:, :], y[:, :], b_row[:, :], ALU.add))
                    dve.wait_ge(stored, 16 * NJ)
                    step(V.tensor_tensor(outr[:, :], y[:, :], q_rows[:, :], ALU.add))
                    dve.wait_ge(states, 2)
                    step(V.tensor_tensor(state[:, :, :], state[:, :, :], rows[0:HD + 1, 0:NJ * HD].rearrange("p (j e) -> p j e", j=NJ), ALU.add))

        with nc.Fori(0, NCH - 1) as i:
            chunk(i * C, i * C, C)
        chunk((NCH - 1) * C, (NCH - 1) * C, LAST)
        with stage(nc, "stored", "back") as (block, stored, back):
            @block.sync
            def _(sp):
                for b in range(B):
                    dst = out_d[b, NCH * C:(NCH + 1) * C, :].rearrange("t (h e) -> h t e", h=NH0)
                    for h in range(NH0):
                        j = b * NH0 + h
                        sp.dma_start(dst[h], outr[j * C:(j + 1) * C, :]).then_inc(stored, 16)
                sp.wait_ge(stored, 16 * NJ)
                for b in range(B):
                    sp.dma_start(k.xn[:, b * TPB:(b + 1) * TPB, :], out_d[b, C:C + S, :].rearrange("(j p) d -> p j d", p=R)).then_inc(back, 16)
                sp.wait_ge(back, 16 * B)
        normalise(nc, k, k.xn, k.xn, 1e-6, post[:, 0, :], post[:, 1, :])
        to_columns(nc, k, k.xn, k.xt)
        project(nc, k, w_out, dst=k.xn)
        normalise(nc, k, k.xn, k.xn, 1e-6, post[:, 2, :], post[:, 3, :])
        to_columns(nc, k, k.xn, k.xt)
        project(nc, k, w_up, add_to=k.h)


GROUP = 4


class Experts:

    def __init__(self, name, n, f1, hid, w1, b1, w2):
        self.name, self.n, self.f1, self.hid, self.w1, self.b1, self.w2 = name, n, f1, hid, w1, b1, w2
        self.hc = hid // 128
        self.loads = 2 + (b1 is not None)


FFN = [Experts("swiglu", 16, 768, 384, "L0_ffn_mlp1_w", "L0_ffn_mlp1_b", "L0_ffn_mlp2_w"),
       Experts("gelu", 4, 768, 768, "L1_ffn_W1", "L1_ffn_b1", "L1_ffn_W2"),
       Experts("silu", 8, 1024, 512, "L2_ffn_W1", None, "L2_ffn_W2"),
       Experts("gelu_norm", 16, 384, 384, "L3_ffn_fc1_w", "L3_ffn_fc1_b", "L3_ffn_fc2_w")]


def weight_buffers(k):
    k.w1 = [k.sb(f"w1_{n}", [KC + 1, 2, 1024]) for n in range(GROUP)]
    k.w2 = [k.sb(f"w2_{n}", [128, 6, D]) for n in range(GROUP)]
    k.gate = k.sb("gate", [R, NT, 16])
    k.w_in = [k.ctx.enter_context(k.nc.semaphore(f"w_in{n}")) for n in range(GROUP)]


def load_expert(eng, k, a, ffn, n, e):
    eng.dma_start(k.w1[n][0:KC, :, 0:ffn.f1], a[ffn.w1][bass.ds(e, 1)].rearrange("o (c p) f -> p (o c) f", p=KC)).then_inc(k.w_in[n], 16)
    if ffn.b1 is not None:
        eng.dma_start(k.w1[n][KC:KC + 1, 1, 0:ffn.f1], a[ffn.b1][bass.ds(e, 1), :]).then_inc(k.w_in[n], 16)
    eng.dma_start(k.w2[n][:, 0:ffn.hc, :], a[ffn.w2][bass.ds(e, 1)].rearrange("o (c p) d -> p (o c) d", p=128)).then_inc(k.w_in[n], 16)


def first_experts(nc, k, a):
    with nc.Block(no_gpsimd_drain=True) as block:
        @block.sync
        def _(sp):
            for n in range(GROUP):
                load_expert(sp, k, a, FFN[0], n, n)


def router(nc, k, a, kind, n_exp, w_name, b_name, top):
    P = f"L{kind}_"
    PAD, TAKEN, NEVER = -1.0e38, -3.0e38, 3.0e38
    with ExitStack() as c:
        gw = k.sb(P + "gw", [KC + 1, 2, n_exp], F32, c)
        lg = k.sb(P + "lg", [R, NT, 16], F32, c)
        top8 = k.sb(P + "top8", [R, NT, 8], F32, c)
        best = k.sb(P + "best", [R, NT, 8], F32, c)
        mr = k.sb(P + "mr", [R, NT, 16], F32, c)
        mask = k.sb(P + "mask", [R, NT, 16], F32, c)
        mask0 = k.sb(P + "mask0", [R, NT, 16], F32, c)
        ex = k.sb(P + "ex", [R, NT, 16], F32, c)
        tot = k.sb(P + "tot", [R, NT], F32, c)
        wk = k.sb(P + "wk", [R, NT, 2], F32, c)
        pos = k.sb(P + "pos", [R, NT, 2, 8], F32, c)
        both = k.sb(P + "both", [R, NT, 2, 8], F32, c)
        tri = k.sb(P + "tri", [R, R], F32, c)
        capacity = int(1.2 * B * S / 8)
        with stage(nc, P + "gw_in", P + "logits", P + "dve_done", P + "act_in", P + "act_out", P + "onehot", P + "counted", P + "tri_ready") as \
                (block, gw_in, logits, dve_done, act_in, act_out, onehot, counted, tri_ready):
            n_loads = 2 if b_name else 1

            @block.sync
            def _(sp):
                sp.dma_start(gw[0:KC, :, :], a[w_name].rearrange("(c p) e -> p c e", p=KC)).then_inc(gw_in, 16)
                if b_name:
                    sp.dma_start(gw[KC:KC + 1, 1, :], a[b_name].unsqueeze(0)).then_inc(gw_in, 16)

            @block.gpsimd
            def _(pool):
                if kind == 2:
                    nc.gpsimd.memset(tri[:, :], 1.0).then_inc(tri_ready, 1)
                    pool.wait_ge(tri_ready, 1)
                    nc.gpsimd.affine_select(out=tri[:, :], in_=tri[:, :], compare_op=ALU.is_ge, fill=0.0, base=0,
                                            pattern=[[1, R]], channel_multiplier=-1).then_inc(tri_ready, 1)

            @block.tensor
            def _(pe):
                pe.wait_ge(gw_in, 16 * n_loads)
                kk = KC + (b_name is not None)
                for t in range(NT):
                    own = k.ps[0:R, 0, t * n_exp:(t + 1) * n_exp]
                    nc.tensor.matmul(own, k.xt[0:KC, 0, t * R:(t + 1) * R], gw[0:KC, 0, :], start=True, stop=False)
                    ins = nc.tensor.matmul(own, k.xt[0:kk, 1, t * R:(t + 1) * R], gw[0:kk, 1, :], start=False, stop=True)
                ins.then_inc(logits, 1)
                if kind == 2:
                    pe.wait_ge(tri_ready, 2)
                    pe.wait_ge(onehot, 1)
                    for t in range(NT):
                        for s in range(t + 1):
                            ins = nc.tensor.matmul(k.ps[0:R, 1, t * 16:(t + 1) * 16], tri[:, :] if s == t else k.ones[0:R, 0:R],
                                                   both[:, s, :, :].rearrange("p k e -> p (k e)"), start=(s == 0), stop=(s == t))
                    ins.then_inc(counted, 1)

            @block.scalar
            def _(act):
                if kind == 0 or kind == 3:
                    act.wait_ge(act_in, 1)
                    nc.scalar.activation(ex[:, :, :], lg[:, :, :], ACT.Exp).then_inc(act_out, 1)
                if kind == 2:
                    act.wait_ge(act_in, 1)
                    nc.scalar.activation(wk[:, :, 1], wk[:, :, 0], ACT.Exp).then_inc(act_out, 1)

            @block.vector
            def _(dve):
                V = nc.vector
                step = Steps(dve, dve_done)

                def choose(values, n, out):
                    for t in range(NT):
                        step.start(V.max(top8[:, t, :], values[:, t, :]))
                    step.wait()
                    step(V.tensor_copy(best[:, :, :], top8[:, :, :]))
                    step(V.memset(best[:, :, n:8], NEVER))
                    for t in range(NT):
                        step(V.match_replace(mr[:, t, :], best[:, t, :], values[:, t, :], TAKEN))
                    step(V.tensor_scalar(out[:, :, :], mr[:, :, :], 2.0 * PAD, None, ALU.is_lt))

                step(V.memset(lg[:, :, :], PAD))
                dve.wait_ge(logits, 1)
                step(V.tensor_copy(lg[:, :, 0:n_exp], k.ps[0:R, 0, 0:NT * n_exp].rearrange("p (t e) -> p t e", t=NT)))
                if kind == 0:
                    choose(lg, top, mask)
                    V.tensor_tensor(lg[:, :, :], lg[:, :, :], top8[:, :, 0:1].broadcast_to([R, NT, 16]), ALU.subtract).then_inc(act_in, 1)
                    dve.wait_ge(act_out, 1)
                    step(V.tensor_tensor(ex[:, :, :], ex[:, :, :], mask[:, :, :], ALU.mult))
                    step(V.tensor_reduce(tot[:, :], ex[:, :, :], AX.X, ALU.add))
                    step(V.reciprocal(tot[:, :], tot[:, :]))
                    step(V.tensor_tensor(k.gate[:, :, :], ex[:, :, :], tot[:, :].unsqueeze(2).broadcast_to([R, NT, 16]), ALU.mult))
                elif kind == 1:
                    choose(lg, top, k.gate)
                elif kind == 2:
                    choose(lg, 2, mask)
                    choose(lg, 1, mask0)
                    step.start(V.tensor_copy(both[:, :, 0, :], mask0[:, :, 0:8]))
                    V.tensor_tensor(both[:, :, 1, :], mask[:, :, 0:8], mask0[:, :, 0:8], ALU.subtract).then_inc(onehot, 1)
                    V.tensor_tensor(wk[:, :, 0], top8[:, :, 1], top8[:, :, 0], ALU.subtract).then_inc(act_in, 1)
                    dve.wait_ge(act_out, 1)
                    step(V.tensor_scalar(tot[:, :], wk[:, :, 1], 1.0, None, ALU.add))
                    step(V.reciprocal(wk[:, :, 0], tot[:, :]))
                    step(V.tensor_tensor(wk[:, :, 1], wk[:, :, 1], wk[:, :, 0], ALU.mult))
                    dve.wait_ge(counted, 1)
                    step(V.tensor_scalar(pos[:, :, :, :], k.ps[0:R, 1, 0:NT * 16].rearrange("p (t k e) -> p t k e", t=NT, k=2),
                                         float(capacity), None, ALU.is_le))
                    dve.wait_ge(onehot, 1)
                    step(V.tensor_tensor(pos[:, :, :, :], pos[:, :, :, :], both[:, :, :, :], ALU.mult))
                    step(V.tensor_tensor(pos[:, :, :, :], pos[:, :, :, :], wk[:, :, :].unsqueeze(3).broadcast_to([R, NT, 2, 8]), ALU.mult))
                    step(V.tensor_tensor(k.gate[:, :, 0:8], pos[:, :, 0, :], pos[:, :, 1, :], ALU.add))
                else:
                    step(V.memset(lg[:, :, 0:1], -1.0e9))
                    step(V.tensor_reduce(tot[:, :], lg[:, :, :], AX.X, ALU.max))
                    V.tensor_tensor(lg[:, :, :], lg[:, :, :], tot[:, :].unsqueeze(2).broadcast_to([R, NT, 16]), ALU.subtract).then_inc(act_in, 1)
                    dve.wait_ge(act_out, 1)
                    step(V.tensor_reduce(tot[:, :], ex[:, :, :], AX.X, ALU.add))
                    step(V.reciprocal(tot[:, :], tot[:, :]))
                    step(V.tensor_tensor(ex[:, :, :], ex[:, :, :], tot[:, :].unsqueeze(2).broadcast_to([R, NT, 16]), ALU.mult))
                    choose(ex, top, mask)
                    step(V.tensor_tensor(k.gate[:, :, :], ex[:, :, :], mask[:, :, :], ALU.mult))
                    step(V.tensor_scalar(k.gate[:, :, 0:1], k.gate[:, :, 0:1], 1.0, None, ALU.add))


def run_experts(nc, k, a, ffn, following):
    with ExitStack() as c:
        hT = [k.sb(f"{ffn.name}_hT{n}", [128, ffn.hc, B * S], F32, c) for n in range(2)]
        ga = [k.sb(f"{ffn.name}_ga{n}", [128, S], F32, c) for n in range(2)]
        li = [k.sb(f"{ffn.name}_li{n}", [128, S], F32, c) for n in range(2)]
        sg = [k.sb(f"{ffn.name}_sg{n}", [128, S], F32, c) for n in range(2)]
        paired = ffn.name != "gelu"
        per = ffn.hc * B
        ring = 2 if paired else 4

        def group(first, last):
            with stage(nc, "unit_ready", "bank_free", "clipped", "gate_act", "dve_done", "unit_done", "y_ready", "y_added") as \
                    (block, unit_ready, bank_free, clipped, gate_act, dve_done, unit_done, y_ready, y_added):
                def units(n):
                    return [(n * per + m, m // B, m % B) for m in range(per)]

                def bank(u, which):
                    return k.ps[:, (u % ring) * (2 if paired else 1) + which, 0:S]

                @block.sync
                def _(sp):
                    for n in range(GROUP):
                        if last and following is None:
                            break
                        sp.wait_ge(y_added, NT * (n + 1))
                        sp.sem_clear(k.w_in[n])
                        if last:
                            load_expert(sp, k, a, following, n, n)
                        else:
                            load_expert(sp, k, a, ffn, n, first + (GROUP + n))

                @block.tensor
                def _(pe):
                    mm = nc.tensor.matmul

                    def up(n):
                        pe.wait_ge(k.w_in[n], 16 * ffn.loads)
                        kk = KC + (ffn.b1 is not None)
                        for u, j, b in units(n):
                            if u >= ring:
                                pe.wait_ge(bank_free if ffn.name == "swiglu" else unit_done, u - ring + 1)
                            for which in range(2 if paired else 1):
                                f = (j + which * ffn.hc) * 128
                                mm(bank(u, which), k.w1[n][0:KC, 0, f:f + 128], k.xt[0:KC, 0, b * S:(b + 1) * S], start=True, stop=False)
                                ins = mm(bank(u, which), k.w1[n][0:kk, 1, f:f + 128], k.xt[0:kk, 1, b * S:(b + 1) * S], start=False, stop=True)
                            ins.then_inc(unit_ready, 1)

                    def down(n):
                        pe.wait_ge(unit_done, per * (n + 1))
                        for t in range(NT):
                            m = NT * n + t
                            if m >= 3:
                                pe.wait_ge(y_added, m - 2)
                            for j in range(ffn.hc):
                                ins = mm(k.ps[0:R, 4 + m % 3, 0:D], hT[n % 2][:, j, t * R:(t + 1) * R], k.w2[n][:, j, :],
                                         start=(j == 0), stop=(j == ffn.hc - 1))
                            ins.then_inc(y_ready, 1)

                    up(0)
                    for n in range(GROUP):
                        if n + 1 < GROUP:
                            up(n + 1)
                        down(n)

                @block.scalar
                def _(act):
                    for n in range(GROUP):
                        for u, j, b in units(n):
                            if ffn.name == "swiglu":
                                act.wait_ge(clipped, u + 1)
                                nc.scalar.activation(sg[u % 2][:, :], ga[u % 2][:, :], ACT.Sigmoid, scale=1.702).then_inc(gate_act, 1)
                            elif ffn.name == "silu":
                                act.wait_ge(unit_ready, u + 1)
                                if u >= 2:
                                    act.wait_ge(unit_done, u - 1)
                                nc.scalar.activation(sg[u % 2][:, :], bank(u, 1), ACT.Silu).then_inc(gate_act, 1)
                            else:
                                act.wait_ge(unit_ready, u + 1)
                                nc.scalar.activation(hT[n % 2][:, j, b * S:(b + 1) * S], bank(u, 0), ACT.Gelu).then_inc(unit_done, 1)

                @block.vector
                def _(dve):
                    V = nc.vector
                    step = Steps(dve, dve_done)

                    def add(n):
                        for t in range(NT):
                            dve.wait_ge(y_ready, NT * n + t + 1)
                            ins = V.scalar_tensor_tensor(k.h[:, t, :], k.ps[0:R, 4 + (NT * n + t) % 3, 0:D], k.gate[:, t, bass.ds(first + n, 1)],
                                                         k.h[:, t, :], ALU.mult, ALU.add)
                            ins.then_inc(y_added, 1)
                        dve.wait_ge(y_added, NT * (n + 1))

                    for n in range(GROUP):
                        for u, j, b in units(n):
                            out = hT[n % 2][:, j, b * S:(b + 1) * S]
                            if ffn.name == "swiglu":
                                dve.wait_ge(unit_ready, u + 1)
                                V.tensor_scalar(ga[u % 2][:, :], bank(u, 0), 7.0, None, ALU.min).then_inc(clipped, 1)
                                V.tensor_scalar(li[u % 2][:, :], bank(u, 1), 7.0, -7.0, ALU.min, ALU.max).then_inc(bank_free, 1)
                                dve.wait_ge(bank_free, u + 1)
                                step(V.scalar_tensor_tensor(li[u % 2][:, :], li[u % 2][:, :], 1.0, ga[u % 2][:, :], ALU.add, ALU.mult))
                                dve.wait_ge(gate_act, u + 1)
                                V.tensor_tensor(out, li[u % 2][:, :], sg[u % 2][:, :], ALU.mult).then_inc(unit_done, 1)
                            elif ffn.name == "silu":
                                dve.wait_ge(gate_act, u + 1)
                                V.tensor_tensor(out, bank(u, 0), sg[u % 2][:, :], ALU.mult).then_inc(unit_done, 1)
                        if n:
                            add(n - 1)
                    add(GROUP - 1)

        if ffn.n > GROUP:
            with nc.Fori(0, ffn.n // GROUP - 1) as g:
                group(g * GROUP, False)
        group(ffn.n - GROUP, True)


def gated_bias(nc, k, n_exp, b2):
    with ExitStack() as c:
        gt = k.sb(f"gate_t{n_exp}_{nc.next_id()}", [16, B * S], F32, c)
        with stage(nc, "turned", "copied", "tile_ready", "dve_done") as (block, turned, copied, tile_ready, dve_done):
            @block.tensor
            def _(pe):
                for t in range(NT):
                    ins = nc.tensor.transpose(k.ps[0:n_exp, t // 3, (t % 3) * R:(t % 3 + 1) * R], k.gate[:, t, 0:n_exp], k.ident[0:R, 0:R])
                    if t % 3 == 2:
                        ins.then_inc(turned, 1)
                for t in range(NT):
                    pe.wait_ge(copied, t // 3 + 1)
                    nc.tensor.matmul(k.ps[0:R, 2 + t, 0:D], gt[0:n_exp, t * R:(t + 1) * R], b2[0:n_exp, :], start=True, stop=True
                                     ).then_inc(tile_ready, 1)

            @block.vector
            def _(dve):
                for b in range(B):
                    dve.wait_ge(turned, b + 1)
                    nc.vector.tensor_copy(gt[0:n_exp, b * S:(b + 1) * S], k.ps[0:n_exp, b, 0:S]).then_inc(copied, 1)
                for t in range(NT):
                    dve.wait_ge(tile_ready, t + 1)
                    nc.vector.tensor_tensor(k.h[:, t, :], k.ps[0:R, 2 + t, 0:D], k.h[:, t, :], ALU.add).then_inc(dve_done, 1)
                dve.wait_ge(dve_done, NT)


def swiglu_layer(nc, k, a):
    normalise(nc, k, k.h, k.xn, 1e-5)
    with ExitStack() as c:
        scale = k.sb("rms_scale", [R, D], F32, c)
        t_ = k.sb("rms_t", [R, NT, D], F32, c)
        junk = k.sb("rms_junk", [R, NT, D], F32, c)
        ms = k.sb("rms_ms", [R, NT], F32, c)
        b2 = k.sb("swiglu_b2", [16, D], F32, c)
        with stage(nc, "loaded", "ms_ready", "rms_ready", "dve_done") as (block, loaded, ms_ready, rms_ready, dve_done):
            @block.sync
            def _(sp):
                sp.dma_start(scale[:, :], bcast(a["L0_ffn_norm_scale"], R)).then_inc(loaded, 16)
                sp.dma_start(b2[:, :], a["L0_ffn_mlp2_b"]).then_inc(loaded, 16)
                sp.wait_ge(loaded, 32)

            @block.gpsimd
            def _(pool):
                pool.wait_ge(ms_ready, NT)
                nc.gpsimd.tensor_tensor(k.rstd[:, :, 0], ms[:, :], k.neg_half[0:R, 0:NT], ALU.pow).then_inc(rms_ready, 1)

            @block.vector
            def _(dve):
                step = Steps(dve, dve_done)
                for t in range(NT):
                    nc.vector.tensor_tensor_reduce(junk[:, t, :], k.xn[:, t, :], k.xn[:, t, :], 1.0 / D, 1e-5, ALU.mult, ALU.add,
                                                   ms[:, t:t + 1]).then_inc(ms_ready, 1)
                step.start(nc.vector.tensor_tensor(k.h[:, :, :], k.h[:, :, :], k.xn[:, :, :], ALU.add))
                dve.wait_ge(rms_ready, 1)
                dve.wait_ge(loaded, 32)
                for t in range(NT):
                    step.start(nc.vector.scalar_tensor_tensor(t_[:, t, :], k.xn[:, t, :], k.rstd[:, t, 0:1], scale[:, :], ALU.mult, ALU.mult))
                step.wait()
        to_columns(nc, k, t_, k.xt)
        router(nc, k, a, 0, 16, "L0_ffn_gate_w", "L0_ffn_gate_b", 4)
        run_experts(nc, k, a, FFN[0], FFN[1])
        gated_bias(nc, k, 16, b2)


def gelu_layer(nc, k, a):
    normalise(nc, k, k.h, k.xn, 1e-5)
    to_columns(nc, k, k.xn, k.xt)
    with ExitStack() as c:
        b2 = k.sb("gelu_b2", [4, D], F32, c)
        with stage(nc, "loaded") as (block, loaded):
            @block.sync
            def _(sp):
                sp.dma_start(b2[:, :], a["L1_ffn_b2"]).then_inc(loaded, 16)
                sp.wait_ge(loaded, 16)
        router(nc, k, a, 1, 4, "L1_ffn_Wg", "L1_ffn_bg", 1)
        run_experts(nc, k, a, FFN[1], FFN[2])
        gated_bias(nc, k, 4, b2)


def silu_layer(nc, k, a):
    normalise(nc, k, k.h, k.xn, 1e-5)
    to_columns(nc, k, k.xn, k.xt)
    router(nc, k, a, 2, 8, "L2_ffn_Wg", None, 2)
    run_experts(nc, k, a, FFN[2], FFN[3])


def channel_attention(nc, k, a):
    normalise(nc, k, k.h, k.xn, 1e-5)
    to_columns(nc, k, k.xn, k.xt)
    with ExitStack() as c:
        w = k.sb("ca_w", [KC, 2, 3 * D], F32, c)
        wp = k.sb("ca_wp", [KC + 1, 2, D], F32, c)
        qkv = [k.sb("ca_" + n, [KC, 4, S], F32, c) for n in "qkv"]
        junk = k.sb("ca_junk", [KC, S], F32, c)
        tmp = k.sb("ca_tmp", [KC, 4, S], F32, c)
        sums = k.sb("ca_sums", [KC, 2, 4], F32, c)
        ssq = k.sb("ca_ssq", [KC, 2, 4], F32, c)
        coef = k.sb("ca_coef", [KC, 4], F32, c)
        prod = k.sb("ca_prod", [KC, 4], F32, c)
        with stage(nc, "loaded", "unit_ready", "act_done", "dve_done", "rnorm", "copied") as \
                (block, loaded, unit_ready, act_done, dve_done, rnorm, copied):
            parts = [(cb, i) for cb in range(4) for i in range(3)]

            @block.sync
            def _(sp):
                sp.dma_start(w[:, :, :], a["L1_attn_w_qkv"].rearrange("(c p) n -> p c n", p=KC)).then_inc(loaded, 16)
                sp.dma_start(wp[0:KC, :, :], a["L1_attn_w_proj"].rearrange("(c p) n -> p c n", p=KC)).then_inc(loaded, 16)
                sp.dma_start(wp[KC:KC + 1, 1, :], a["L1_attn_b_proj"].unsqueeze(0)).then_inc(loaded, 16)

            @block.tensor
            def _(pe):
                pe.wait_ge(loaded, 48)
                for cb in range(4):
                    m, b = cb // 2, cb % 2
                    for i in range(3):
                        bank = (cb % 2) * 3 + i
                        if cb >= 2:
                            if i < 2:
                                pe.wait_ge(act_done, 4 * (cb - 2) + 2 * i + 2)
                            else:
                                pe.wait_ge(copied, cb - 1)
                        for kc in range(2):
                            ins = nc.tensor.matmul(k.ps[0:KC, bank, 0:S], w[:, kc, i * D + m * KC:i * D + (m + 1) * KC],
                                                   k.xt[0:KC, kc, b * S:(b + 1) * S], start=(kc == 0), stop=(kc == 1))
                        ins.then_inc(unit_ready, 1)

            @block.scalar
            def _(act):
                for cb in range(4):
                    for i in range(2):
                        bank = k.ps[0:KC, (cb % 2) * 3 + i, 0:S]
                        act.wait_ge(unit_ready, 3 * cb + i + 1)
                        nc.scalar.activation(qkv[i][:, cb, :], bank, ACT.Copy, accum_out=sums[:, i, cb:cb + 1]).then_inc(act_done, 1)
                        n = 4 * cb + 2 * i
                        if n:
                            act.wait_ge(act_done, n)
                        nc.scalar.activation(junk[:, :], bank, ACT.Square, accum_out=ssq[:, i, cb:cb + 1]).then_inc(act_done, 1)

            @block.gpsimd
            def _(pool):
                pool.wait_ge(act_done, 16)
                nc.gpsimd.tensor_tensor(ssq[:, :, :].rearrange("p i c -> p (i c)"), ssq[:, :, :].rearrange("p i c -> p (i c)"),
                                        k.neg_half[0:KC, 0:8], ALU.pow).then_inc(rnorm, 1)

            @block.vector
            def _(dve):
                V = nc.vector
                step = Steps(dve, dve_done)
                for cb in range(4):
                    dve.wait_ge(unit_ready, 3 * cb + 3)
                    V.tensor_copy(qkv[2][:, cb, :], k.ps[0:KC, (cb % 2) * 3 + 2, 0:S]).then_inc(copied, 1)
                dve.wait_ge(copied, 4)
                dve.wait_ge(rnorm, 1)
                step(V.tensor_tensor(sums[:, :, :], sums[:, :, :], ssq[:, :, :], ALU.mult))
                step(V.tensor_tensor(prod[:, :], sums[:, 0, :], sums[:, 1, :], ALU.mult))
                step(V.tensor_scalar(prod[:, :], prod[:, :], float(S), None, ALU.add))
                step(V.reciprocal(prod[:, :], prod[:, :]))
                step(V.tensor_tensor(coef[:, :], prod[:, :], ssq[:, 0, :], ALU.mult))
                for cb in range(4):
                    step.start(V.scalar_tensor_tensor(tmp[:, cb, :], qkv[1][:, cb, :], ssq[:, 1, cb:cb + 1], qkv[0][:, cb, :], ALU.mult, ALU.mult))
                step.wait()
                for cb in range(4):
                    step.start(V.scalar_tensor_tensor(tmp[:, cb, :], qkv[1][:, cb, :], ssq[:, 1, cb:cb + 1], tmp[:, cb, :], ALU.mult, ALU.mult))
                step.wait()
                for cb in range(4):
                    step.start(V.scalar_tensor_tensor(k.xt[0:KC, cb // 2, (cb % 2) * S:(cb % 2 + 1) * S], qkv[2][:, cb, :],
                                                      coef[:, cb:cb + 1], tmp[:, cb, :], ALU.mult, ALU.mult))
                step.wait()
        project(nc, k, wp, add_to=k.h)


NHEAD, HW = 12, 16
HG = 3
NHG = NHEAD // HG
RP = R + 1
QMIN, QMAX = -128.0, 127.0


def head_rows(h):
    return slice(32 * (h % 4), 32 * (h % 4) + HW), h // 4


def quantised_attention(nc, k, a):
    normalise(nc, k, k.h, k.xn, 1e-5)
    to_columns(nc, k, k.xn, k.xt)
    with ExitStack() as c:
        raw = k.sb("qa_raw", [KC, 2, 3 * D], F32, c)
        bias_raw = k.sb("qa_bias", [KC + 1, 3 * D], F32, c)
        praw = k.sb("qa_praw", [KC, 2, D], F32, c)
        wqk = k.sb("qa_wqk", [KC + 1, 2, 2, NHEAD, 32], F32, c)
        wv = k.sb("qa_wv", [KC + 1, 2, D], F32, c)
        wp = k.sb("qa_wp", [KC + 1, 2, D], F32, c)
        qk_t = k.sb("qa_qkt", [128, 2, B, 3, S], BF16, c)
        qk_b = k.sb("qa_qkb", [128, 2, 3, S], BF16, c)
        v_q = k.sb("qa_v", [R, NT, D], BF16, c)
        v_b = k.sb("qa_vb", [R, TPB, D], BF16, c)
        id16 = k.sb("qa_id", [128, 128], BF16, c)
        sc = k.sb("qa_scales", [128, 6], F32, c)
        inv = k.sb("qa_inv", [128, 6], F32, c)
        cc = k.sb("qa_cc", [128, 16], F32, c)
        rnd = k.sb("qa_round", [128, 1], F32, c)
        tmp = k.sb("qa_tmp", [128, 2, 3 * D], F32, c)
        W_S, A1, ATT, A2, WP_S, A3 = range(6)
        logit, negx0, invx0, off, b_int, c_int, lowest, ctx_s = (cc[:, n:n + 1] for n in range(8))

        def floor(V, step, x):
            y = tmp[:, 0, 0:1]
            step(V.tensor_scalar(y, x, ROUND, ROUND, ALU.add, ALU.subtract))
            step(V.tensor_tensor(tmp[:, 0, 1:2], y, x, ALU.is_gt))
            step(V.tensor_tensor(x, y, tmp[:, 0, 1:2], ALU.subtract))

        with stage(nc, "loaded", "filled", "dve_done", "unit_ready", "act_done", "bank_free", "w_ready", "consts") as \
                (block, loaded, filled, dve_done, unit_ready, act_done, bank_free, w_ready, consts):
            @block.sync
            def _(sp):
                sp.dma_start(sc[:, :], bcast(a["qa_scales"], 128)).then_inc(loaded, 16)
                sp.dma_start(raw[:, :, :], a["L2_attn_qkv_w"].rearrange("(c p) n -> p c n", p=KC)).then_inc(loaded, 16)
                sp.dma_start(praw[:, :, :], a["L2_attn_proj_w"].rearrange("(c p) n -> p c n", p=KC)).then_inc(loaded, 16)
                sp.dma_start(bias_raw[KC:KC + 1, :], a["L2_attn_qkv_b"].unsqueeze(0)).then_inc(loaded, 16)
                sp.dma_start(wp[KC:KC + 1, 1, :], a["L2_attn_proj_b"].unsqueeze(0)).then_inc(loaded, 16)
                sp.dma_start(wv[KC:KC + 1, 1, :], a["L2_attn_qkv_b"][2 * D:3 * D].unsqueeze(0)).then_inc(loaded, 16)

            @block.gpsimd
            def _(pool):
                step = Steps(pool, filled)
                step(nc.gpsimd.memset(wqk[:, :, :, :, :], 0.0))
                step(nc.gpsimd.memset(rnd[:, :], ROUND))
                step(nc.gpsimd.tensor_copy(id16[:, :], k.ident[:, :]))

            units = [("qk", b, w, g) for b in range(B) for w in range(2) for g in range(3)] + [("v", t, 0, 0) for t in range(NT)]

            @block.tensor
            def _(pe):
                pe.wait_ge(w_ready, 1)
                for u, (kind, b, w, g) in enumerate(units):
                    if u >= 4:
                        pe.wait_ge(bank_free, u - 3)
                    for kc in range(2):
                        kk = KC + kc
                        if kind == "qk":
                            ins = nc.tensor.matmul(k.ps[:, u % 4, 0:S], wqk[0:kk, kc, w, 4 * g:4 * g + 4, :].rearrange("p h d -> p (h d)"),
                                                   k.xt[0:kk, kc, b * S:(b + 1) * S], start=(kc == 0), stop=(kc == 1))
                        else:
                            ins = nc.tensor.matmul(k.ps[0:R, u % 4, 0:D], k.xt[0:kk, kc, b * R:(b + 1) * R], wv[0:kk, kc, :],
                                                   start=(kc == 0), stop=(kc == 1))
                    ins.then_inc(unit_ready, 1)

            @block.vector
            def _(dve):
                V = nc.vector
                step = Steps(dve, dve_done)
                dve.wait_ge(loaded, 96)
                dve.wait_ge(filled, 3)
                step(V.reciprocal(inv[:, :], sc[:, :]))

                def fake_quant(x, s, parts):
                    step(V.tensor_scalar(x, x, inv[0:parts, s:s + 1], ROUND, ALU.mult, ALU.add))
                    step(V.tensor_scalar(x, x, ROUND + QMAX, ROUND + QMIN, ALU.min, ALU.max))

                fake_quant(raw[:, :, :], W_S, KC)
                fake_quant(praw[:, :, :], WP_S, KC)
                for kc in range(2):
                    step(V.tensor_scalar(wqk[0:KC, kc, :, :, 0:HW], raw[:, kc, 0:2 * D].rearrange("p (w h d) -> p w h d", w=2, d=HW),
                                         ROUND, sc[0:KC, W_S:W_S + 1], ALU.subtract, ALU.mult))
                step(V.tensor_scalar(wv[0:KC, :, :], raw[:, :, 2 * D:3 * D], ROUND, sc[0:KC, W_S:W_S + 1], ALU.subtract, ALU.mult))
                step(V.tensor_scalar(wp[0:KC, :, :], praw[:, :, :], ROUND, sc[0:KC, WP_S:WP_S + 1], ALU.subtract, ALU.mult))
                V.tensor_copy(wqk[KC:KC + 1, 1, :, :, 0:HW], bias_raw[KC:KC + 1, 0:2 * D].rearrange("p (w h d) -> p w h d", w=2, d=HW)
                              ).then_inc(w_ready, 1)
                step(V.tensor_tensor(logit, sc[:, A1:A1 + 1], sc[:, A1:A1 + 1], ALU.mult))
                step(V.tensor_scalar(logit, logit, inv[:, ATT:ATT + 1], HW ** -0.5, ALU.mult, ALU.mult))
                step(V.tensor_scalar(negx0, inv[:, ATT:ATT + 1], -0.6931, None, ALU.mult))
                floor(V, step, negx0)
                step(V.tensor_scalar(lowest, negx0, 30.0, None, ALU.mult))
                step(V.reciprocal(invx0, negx0))
                step(V.tensor_scalar(negx0, negx0, -1.0, None, ALU.mult))
                step(V.tensor_scalar(off, invx0, -0.5, -0.5, ALU.mult, ALU.add))
                step(V.tensor_scalar(b_int, inv[:, ATT:ATT + 1], 0.96963238 / 0.35815147, None, ALU.mult))
                floor(V, step, b_int)
                step(V.tensor_tensor(c_int, inv[:, ATT:ATT + 1], inv[:, ATT:ATT + 1], ALU.mult))
                step(V.tensor_scalar(c_int, c_int, 1.0 / 0.35815147, None, ALU.mult))
                floor(V, step, c_int)
                step(V.tensor_scalar(ctx_s, sc[:, A1:A1 + 1], inv[:, A2:A2 + 1], 0.5, ALU.mult, ALU.mult))
                for u, (kind, b, w, g) in enumerate(units):
                    dve.wait_ge(unit_ready, u + 1)
                    rows, cols = (128, S) if kind == "qk" else (R, D)
                    t = tmp[0:rows, u % 2, 0:cols]
                    V.tensor_scalar(t, k.ps[0:rows, u % 4, 0:cols], inv[0:rows, A1:A1 + 1], ROUND, ALU.mult, ALU.add).then_inc(bank_free, 1)
                    dve.wait_ge(bank_free, u + 1)
                    step(V.tensor_scalar(t, t, ROUND + QMAX, ROUND + QMIN, ALU.min, ALU.max))
                    out = qk_t[:, w, b, g, :] if kind == "qk" else v_q[:, b, :]
                    step.start(V.tensor_scalar(out, t, ROUND, None, ALU.subtract))
                step.wait()

        t1 = [k.sb(f"qa_t1_{n}", [R, HG, S], F32, c) for n in range(2)]
        nn = [k.sb(f"qa_n_{n}", [R, HG, S], F32, c) for n in range(2)]
        qq = [k.sb(f"qa_q_{n}", [R, HG, S], F32, c) for n in range(2)]
        pw = k.sb("qa_pw", [R, HG, S], I32, c)
        rr = k.sb("qa_r", [R, HG, S], F32, c)
        zz = k.sb("qa_z", [R, HG, S], F32, c)
        mx = k.sb("qa_mx", [R, HG], F32, c)
        sm = k.sb("qa_sm", [R, HG], F32, c)
        hp = k.sb("qa_hp", [R, HG, S], I32, c)
        pp = k.sb("qa_p", [R, HG, S], BF16, c)
        pt = k.sb("qa_pt", [R, HG, TPB, RP], BF16, c)
        pt_ps = k.ps[0:R, 6, :].bitcast(BF16)[:, 0:HG * TPB * RP].rearrange("p (h m n) -> p h m n", h=HG, m=TPB)

        def batch(first_tile, b):
            units = [(u, nt, g) for u, (nt, g) in enumerate((nt, g) for nt in range(TPB) for g in range(NHG))]
            with stage(nc, "picked", "scores", "scaled", "shifted", "divided", "dve_done", "p_ready", "turned", "pt_ready", "pv_done", "ctx_out",
                       "hp_done") as (block, picked, scores, scaled, shifted, divided, dve_done, p_ready, turned, pt_ready, pv_done, ctx_out, hp_done):
                @block.gpsimd
                def _(pool):
                    nc.gpsimd.tensor_copy(qk_b[:, 0, :, :], qk_t[:, 0, bass.ds(b, 1), :, :].rearrange("p o g s -> p (o g) s")).then_inc(picked, 1)
                    nc.gpsimd.tensor_copy(qk_b[:, 1, :, :], qk_t[:, 1, bass.ds(b, 1), :, :].rearrange("p o g s -> p (o g) s")).then_inc(picked, 1)
                    nc.gpsimd.tensor_copy(v_b[:, :, :], v_q[:, bass.ds(first_tile, TPB), :]).then_inc(picked, 1)

                @block.tensor
                def _(pe):
                    def score(u, nt, g):
                        if u >= 2:
                            pe.wait_ge(scaled, u - 1)
                        for i in range(HG):
                            rows, grp = head_rows(HG * g + i)
                            ins = nc.tensor.matmul(k.ps[0:R, (u % 2) * HG + i, 0:S], qk_b[rows, 0, grp, nt * R:(nt + 1) * R],
                                                   qk_b[rows, 1, grp, :], start=True, stop=True)
                        ins.then_inc(scores, 1)

                    def turn(u):
                        pe.wait_ge(p_ready, u + 1)
                        if u:
                            pe.wait_ge(pt_ready, u)
                        for i in range(HG):
                            for m in range(TPB):
                                ins = nc.tensor.transpose(pt_ps[:, i, m, 0:R], pp[:, i, m * R:(m + 1) * R], id16[0:R, 0:R])
                        ins.then_inc(turned, 1)

                    def weigh(u, nt, g):
                        pe.wait_ge(pt_ready, u + 1)
                        if g == 0 and nt:
                            pe.wait_ge(ctx_out, nt)
                        for i in range(HG):
                            h = HG * g + i
                            for m in range(TPB):
                                ins = nc.tensor.matmul(k.ps[0:R, 7, h * HW:(h + 1) * HW], pt[:, i, m, 0:R], v_b[:, m, h * HW:(h + 1) * HW],
                                                       start=(m == 0), stop=(m == TPB - 1))
                        ins.then_inc(pv_done, 1)

                    pe.wait_ge(picked, 3)
                    score(*units[0])
                    for u, nt, g in units:
                        if u + 1 < len(units):
                            score(*units[u + 1])
                        turn(u)
                        weigh(u, nt, g)

                @block.scalar
                def _(act):
                    def scale_logits(u):
                        act.wait_ge(scores, u + 1)
                        if u >= 2:
                            act.wait_ge(shifted, u - 1)
                        nc.scalar.activation(t1[u % 2][:, :, :], k.ps[0:R, (u % 2) * HG:(u % 2 + 1) * HG, 0:S], ACT.Identity,
                                             scale=logit[0:R, :], bias=rnd[0:R, :]).then_inc(scaled, 1)

                    scale_logits(0)
                    for u, nt, g in units:
                        act.wait_ge(shifted, u + 1)
                        nc.scalar.activation(qq[u % 2][:, :, :], nn[u % 2][:, :, :], ACT.Identity, scale=invx0[0:R, :], bias=off[0:R, :]
                                             ).then_inc(divided, 1)
                        if u + 1 < len(units):
                            scale_logits(u + 1)
                        act.wait_ge(turned, u + 1)
                        if u:
                            act.wait_ge(pv_done, u)
                        nc.scalar.copy(pt[:, :, :, 0:R], pt_ps[:, :, :, 0:R]).then_inc(pt_ready, 1)

                def context(dve, V, step, nt):
                    dve.wait_ge(pv_done, NHG * (nt + 1))
                    t = tmp[0:R, 0, 0:D]
                    V.tensor_scalar(t, k.ps[0:R, 7, 0:D], ctx_s[0:R, :], ROUND, ALU.mult, ALU.add).then_inc(ctx_out, 1)
                    dve.wait_ge(ctx_out, nt + 1)
                    step(V.tensor_scalar(t, t, ROUND + QMAX, ROUND + QMIN, ALU.min, ALU.max))
                    step(V.tensor_scalar(k.xn[:, bass.ds(first_tile + nt, 1), :].rearrange("p o d -> p (o d)"), t, ROUND, sc[0:R, A2:A2 + 1],
                                         ALU.subtract, ALU.mult))

                @block.vector
                def _(dve):
                    V = nc.vector
                    step = Steps(dve, dve_done)

                    def shift(u):
                        t, n_ = t1[u % 2], nn[u % 2]
                        dve.wait_ge(scaled, u + 1)
                        step(V.tensor_scalar(t[:, :, :], t[:, :, :], ROUND + QMAX, ROUND + QMIN, ALU.min, ALU.max))
                        step(V.tensor_reduce(mx[:, :], t[:, :, :], AX.X, ALU.max))
                        for i in range(HG):
                            ins = V.tensor_scalar(n_[:, i, :], t[:, i, :], mx[:, i:i + 1], lowest[0:R, :], ALU.subtract, ALU.max)
                            if i < HG - 1:
                                step.start(ins)
                        ins.then_inc(shifted, 1)

                    shift(0)
                    for u, nt, g in units:
                        n_, q = nn[u % 2], qq[u % 2]
                        if u + 1 < len(units):
                            shift(u + 1)
                        dve.wait_ge(divided, u + 1)
                        step(V.tensor_scalar(q[:, :, :], q[:, :, :], ROUND, ROUND, ALU.add, ALU.subtract))
                        step.start(V.tensor_scalar(pw[:, :, :], q[:, :, :], -2.0 ** 23, 127.0 * 2.0 ** 23, ALU.mult, ALU.add))
                        step(V.scalar_tensor_tensor(rr[:, :, :], q[:, :, :], negx0[0:R, :], n_[:, :, :], ALU.mult, ALU.add))
                        step(V.scalar_tensor_tensor(zz[:, :, :], rr[:, :, :], b_int[0:R, :], rr[:, :, :], ALU.add, ALU.mult))
                        step(V.tensor_scalar(zz[:, :, :], zz[:, :, :], c_int[0:R, :], 1e-6, ALU.add, ALU.max))
                        for i in range(HG):
                            step.start(V.scalar_tensor_tensor(rr[:, i, :], zz[:, i, :], 1.0, pw[:, i, :].bitcast(F32), ALU.mult, ALU.mult,
                                                              accum_out=sm[:, i:i + 1]))
                        step.wait()
                        step(V.reciprocal(zz[:, :, :], rr[:, :, :]))
                        for i in range(HG):
                            step.start(V.tensor_scalar(rr[:, i, :], zz[:, i, :], sm[:, i:i + 1], ROUND, ALU.mult, ALU.add))
                        step.wait()
                        step(V.tensor_scalar(zz[:, :, :], rr[:, :, :], ROUND, 4.0 / 3.0, ALU.subtract, ALU.mult))
                        step(V.tensor_scalar(hp[:, :, :], zz[:, :, :].bitcast(I32), 0x7F800000, 0x7F800000, ALU.bitwise_and, ALU.bitwise_xor))
                        if u:
                            dve.wait_ge(turned, u)
                        V.scalar_tensor_tensor(pp[:, :, :], zz[:, :, :], 65536.0, hp[:, :, :].bitcast(F32), ALU.is_lt, ALU.mult
                                               ).then_inc(p_ready, 1)
                        dve.wait_ge(p_ready, u + 1)
                        if g == 0 and nt:
                            context(dve, V, step, nt - 1)
                    context(dve, V, step, TPB - 1)

        with nc.Fori(0, B) as b:
            batch(b * TPB, b)
        to_columns(nc, k, k.xn, k.xt)
        project(nc, k, wp, dst=k.xn)
        with stage(nc, "dve_done") as (block, dve_done):
            @block.vector
            def _(dve):
                V = nc.vector
                step = Steps(dve, dve_done)
                step(V.tensor_scalar(k.xn[:, :, :], k.xn[:, :, :], inv[0:R, A3:A3 + 1], ROUND, ALU.mult, ALU.add))
                step(V.tensor_scalar(k.xn[:, :, :], k.xn[:, :, :], ROUND + QMAX, ROUND + QMIN, ALU.min, ALU.max))
                step(V.tensor_scalar(k.xn[:, :, :], k.xn[:, :, :], ROUND, sc[0:R, A3:A3 + 1], ALU.subtract, ALU.mult))
                step(V.tensor_tensor(k.h[:, :, :], k.h[:, :, :], k.xn[:, :, :], ALU.add))


def ternary(V, step, x, inv, parts):
    step(V.tensor_scalar(x, x, inv, 1.0, ALU.mult, ALU.min))
    step(V.tensor_scalar(x, x, -1.0, ROUND, ALU.max, ALU.add))


def ternary_attention(nc, k, a):
    normalise(nc, k, k.h, k.xn, 1e-5)
    to_columns(nc, k, k.xn, k.xt)
    EPS = 1e-5
    with ExitStack() as c:
        w = k.sb("ta_w", [KC, 2, 3 * D], F32, c)
        qkv = k.sb("ta_qkv", [R, NT, 3, NHEAD, HW], F32, c)
        l1 = k.sb("ta_l1", [R, NT, 3 * NHEAD], F32, c)
        part = k.sb("ta_part", [128, NT * 3], F32, c)
        sc = k.sb("ta_sc", [128, 4], F32, c)
        inv = k.sb("ta_inv", [128, 4], F32, c)
        pad = k.sb("ta_pad", [R, NT, 2, NHEAD, 32], BF16, c)
        qk_t = k.sb("ta_qkt", [128, 2, B, 3, S], BF16, c)
        qk_b = k.sb("ta_qkb", [128, 2, 3, S], BF16, c)
        v_q = k.sb("ta_v", [R, NT, D], BF16, c)
        v_b = k.sb("ta_vb", [R, TPB, D], BF16, c)
        id16 = k.sb("ta_id", [128, 128], BF16, c)
        with stage(nc, "loaded", "filled", "dve_done", "part_ready", "summed", "w_ready", "tile_ready", "copied", "padded", "turned") as \
                (block, loaded, filled, dve_done, part_ready, summed, w_ready, tile_ready, copied, padded, turned):
            def turned_bank(which, b):
                return k.ps[:, 2 * which + b, :].bitcast(BF16)[:, 0:9 * RP].rearrange("p (g t n) -> p g t n", g=3, t=TPB)

            @block.sync
            def _(sp):
                sp.dma_start(w[:, :, :], a["L3_attn_w_qkv"].rearrange("(c p) n -> p c n", p=KC)).then_inc(loaded, 16)

            @block.gpsimd
            def _(pool):
                nc.gpsimd.memset(pad[:, :, :, :, :], 0.0).then_inc(filled, 1)
                nc.gpsimd.tensor_copy(id16[:, :], k.ident[:, :]).then_inc(filled, 1)

            @block.tensor
            def _(pe):
                pe.wait_ge(part_ready, 1)
                nc.tensor.matmul(k.ps[:, 6, 0:1], k.ones[0:KC, :], part[0:KC, 0:1], start=True, stop=True).then_inc(summed, 1)
                pe.wait_ge(w_ready, 1)
                for t in range(NT):
                    for bank, lo, hi in ((t % 3, 0, 2 * D), (3 + t % 3, 2 * D, 3 * D)):
                        if t >= 3:
                            pe.wait_ge(copied, 2 * (t - 3) + 1 + (lo > 0))
                        for kc in range(2):
                            ins = nc.tensor.matmul(k.ps[0:R, bank, 0:hi - lo], k.xt[0:KC, kc, t * R:(t + 1) * R], w[:, kc, lo:hi],
                                                   start=(kc == 0), stop=(kc == 1))
                        ins.then_inc(tile_ready, 1)
                pe.wait_ge(part_ready, 2)
                nc.tensor.matmul(k.ps[:, 7, 0:3 * NT], k.ones[0:R, :], part[0:R, :], start=True, stop=True).then_inc(summed, 1)
                pe.wait_ge(padded, 3)
                pe.wait_ge(filled, 2)
                for which in range(2):
                    for b in range(B):
                        to = turned_bank(which, b)
                        for g in range(3):
                            for t in range(TPB):
                                ins = nc.tensor.transpose(to[:, g, t, 0:R], pad[:, b * TPB + t, which, 4 * g:4 * g + 4, :].rearrange("p h d -> p (h d)"),
                                                          id16[0:R, 0:R])
                        ins.then_inc(turned, 1)

            @block.scalar
            def _(act):
                for t in range(NT):
                    act.wait_ge(tile_ready, 2 * t + 1)
                    nc.scalar.copy(qkv[:, t, 0:2, :, :].rearrange("p w h d -> p (w h d)"), k.ps[0:R, t % 3, 0:2 * D]).then_inc(copied, 1)
                    act.wait_ge(tile_ready, 2 * t + 2)
                    nc.scalar.copy(qkv[:, t, 2, :, :].rearrange("p h d -> p (h d)"), k.ps[0:R, 3 + t % 3, 0:D]).then_inc(copied, 1)
                for n in (1, 3):
                    act.wait_ge(turned, n + 1)
                    nc.scalar.copy(qk_t[:, n // 2, n % 2, :, :].rearrange("p g (t n) -> p g t n", t=TPB), turned_bank(n // 2, n % 2)[:, :, :, 0:R]
                                   ).then_inc(copied, 1)

            @block.vector
            def _(dve):
                V = nc.vector
                step = Steps(dve, dve_done)
                dve.wait_ge(loaded, 16)
                V.tensor_reduce(part[0:KC, 0:1], w[:, :, :], AX.XY, ALU.add, apply_absolute_value=True).then_inc(part_ready, 1)
                dve.wait_ge(summed, 1)
                step(V.tensor_scalar(sc[:, 3:4], k.ps[:, 6, 0:1], 1.0 / (3 * D * D), EPS, ALU.mult, ALU.add))
                step(V.reciprocal(inv[:, 3:4], sc[:, 3:4]))
                ternary(V, step, w[:, :, :], inv[0:KC, 3:4], KC)
                V.tensor_scalar(w[:, :, :], w[:, :, :], ROUND, sc[0:KC, 3:4], ALU.subtract, ALU.mult).then_inc(w_ready, 1)
                dve.wait_ge(copied, 2 * NT)
                heads = qkv[:, :, :, :, :].rearrange("p t w h d -> p (t w h) d")
                l1_ = l1[:, :, :].rearrange("p t n -> p (t n)")
                step(V.tensor_reduce(l1_, heads, AX.X, ALU.add, apply_absolute_value=True))
                step(V.tensor_scalar(l1_, l1_, EPS, None, ALU.add))
                step(V.reciprocal(l1_, l1_))
                step(V.tensor_tensor(heads, heads, l1_.unsqueeze(2).broadcast_to([R, NT * 3 * NHEAD, HW]), ALU.mult))
                V.tensor_reduce(part[0:R, :], qkv[:, :, :, :, :].rearrange("p t w h d -> p (t w) (h d)"), AX.X, ALU.add,
                                apply_absolute_value=True).then_inc(part_ready, 1)
                dve.wait_ge(summed, 2)
                step(V.tensor_reduce(sc[:, 0:3], k.ps[:, 7, 0:3 * NT].rearrange("p (t w) -> p w t", w=3), AX.X, ALU.add))
                step(V.tensor_scalar(sc[:, 0:3], sc[:, 0:3], 1.0 / (B * S * D), EPS, ALU.mult, ALU.add))
                step(V.reciprocal(inv[:, 0:3], sc[:, 0:3]))
                dve.wait_ge(filled, 1)
                for i in range(3):
                    x = qkv[:, :, i, :, :].rearrange("p t h d -> p t (h d)")
                    ternary(V, step, x, inv[0:R, i:i + 1], R)
                    out = pad[:, :, i, :, 0:HW] if i < 2 else v_q[:, :, :].rearrange("p t (h d) -> p t h d", d=HW)
                    V.tensor_scalar(out, qkv[:, :, i, :, :], ROUND, None, ALU.subtract).then_inc(padded, 1)
                for n in (0, 2):
                    dve.wait_ge(turned, n + 1)
                    step.start(V.tensor_copy(qk_t[:, n // 2, n % 2, :, :].rearrange("p g (t n) -> p g t n", t=TPB),
                                             turned_bank(n // 2, n % 2)[:, :, :, 0:R]))
                step.wait()

        acc = k.sb("ta_acc", [R, B, 12, HG], F32, c)
        acc_b = k.sb("ta_acc_b", [R, 12, HG], F32, c)
        junk = k.sb("ta_junk", [R, HG, S], F32, c)
        rows_sum = k.sb("ta_rows", [R, 1], F32, c)
        cc = k.sb("ta_cc", [128, 4], F32, c)
        rnd = k.sb("ta_round", [128, 1], F32, c)
        t1 = [k.sb(f"ta_t1_{n}", [R, HG, S], F32, c) for n in range(2)]
        at = [k.sb(f"ta_at_{n}", [R, TPB, HG, S], BF16, c) for n in range(2)]
        c_qk, qk_s, alpha, out_s = (cc[:, n:n + 1] for n in range(4))
        units = [(u, u // TPB, u % TPB) for u in range(NHG * TPB)]

        def pick(pool, first_tile, b, picked):
            nc.gpsimd.tensor_copy(qk_b[:, 0, :, :], qk_t[:, 0, bass.ds(b, 1), :, :].rearrange("p o g s -> p (o g) s")).then_inc(picked, 1)
            nc.gpsimd.tensor_copy(qk_b[:, 1, :, :], qk_t[:, 1, bass.ds(b, 1), :, :].rearrange("p o g s -> p (o g) s")).then_inc(picked, 1)
            nc.gpsimd.tensor_copy(v_b[:, :, :], v_q[:, bass.ds(first_tile, TPB), :]).then_inc(picked, 1)

        def score(pe, scores, u, g, mt):
            for i in range(HG):
                rows, grp = head_rows(HG * g + i)
                ins = nc.tensor.matmul(k.ps[0:R, (u % 2) * HG + i, 0:S], qk_b[rows, 1, grp, mt * R:(mt + 1) * R], qk_b[rows, 0, grp, :],
                                       start=True, stop=True)
            ins.then_inc(scores, 1)

        def sizes(first_tile, b):
            with stage(nc, "picked", "scores", "act_summed", "dve_summed", "zeroed", "moved") as \
                    (block, picked, scores, act_summed, dve_summed, zeroed, moved):
                @block.gpsimd
                def _(pool):
                    pick(pool, first_tile, b, picked)
                    nc.gpsimd.memset(acc_b[:, :, :], 0.0).then_inc(zeroed, 1)
                    pool.wait_ge(act_summed, len(units) // 2)
                    pool.wait_ge(dve_summed, len(units) // 2)
                    nc.gpsimd.tensor_copy(acc[:, bass.ds(b, 1), :, :].rearrange("p o u h -> p (o u) h"), acc_b[:, :, :]).then_inc(moved, 1)
                    pool.wait_ge(moved, 1)

                @block.tensor
                def _(pe):
                    pe.wait_ge(picked, 3)
                    for u, g, mt in units:
                        if u >= 2:
                            pe.wait_ge(dve_summed if u % 2 else act_summed, u // 2)
                        score(pe, scores, u, g, mt)

                @block.scalar
                def _(act):
                    act.wait_ge(zeroed, 1)
                    for u, g, mt in units[0::2]:
                        act.wait_ge(scores, u + 1)
                        if u:
                            act.wait_ge(act_summed, u // 2)
                        nc.scalar.activation(junk[:, :, :], k.ps[0:R, 0:HG, 0:S], ACT.Abs, accum_out=acc_b[:, u, 0:1]).then_inc(act_summed, 1)

                @block.vector
                def _(dve):
                    dve.wait_ge(zeroed, 1)
                    for u, g, mt in units[1::2]:
                        dve.wait_ge(scores, u + 1)
                        nc.vector.tensor_reduce(acc_b[:, u, :], k.ps[0:R, HG:2 * HG, 0:S], AX.X, ALU.add, apply_absolute_value=True
                                                ).then_inc(dve_summed, 1)

        def weigh(first_tile, b):
            with stage(nc, "picked", "scores", "scaled", "dve_done", "rounded", "ctx_ready", "ctx_added") as \
                    (block, picked, scores, scaled, dve_done, rounded, ctx_ready, ctx_added):
                @block.gpsimd
                def _(pool):
                    pick(pool, first_tile, b, picked)

                @block.tensor
                def _(pe):
                    def context(g):
                        pe.wait_ge(rounded, TPB * (g + 1))
                        if g >= 2:
                            pe.wait_ge(ctx_added, g - 1)
                        for nt in range(TPB):
                            for i in range(HG):
                                col = (nt * HG + i) * HW
                                h = HG * g + i
                                for mt in range(TPB):
                                    ins = nc.tensor.matmul(k.ps[0:R, 6 + g % 2, col:col + HW], at[g % 2][:, mt, i, nt * R:(nt + 1) * R],
                                                           v_b[:, mt, h * HW:(h + 1) * HW], start=(mt == 0), stop=(mt == TPB - 1))
                        ins.then_inc(ctx_ready, 1)

                    pe.wait_ge(picked, 3)
                    for u, g, mt in units:
                        if u >= 2:
                            pe.wait_ge(scaled, u - 1)
                        score(pe, scores, u, g, mt)
                        if mt == TPB - 1 and g:
                            context(g - 1)
                    context(NHG - 1)

                @block.scalar
                def _(act):
                    for u, g, mt in units:
                        act.wait_ge(scores, u + 1)
                        if u >= 2:
                            act.wait_ge(rounded, u - 1)
                        nc.scalar.activation(t1[u % 2][:, :, :], k.ps[0:R, (u % 2) * HG:(u % 2 + 1) * HG, 0:S], ACT.Identity,
                                             scale=alpha[0:R, :], bias=rnd[0:R, :]).then_inc(scaled, 1)

                @block.vector
                def _(dve):
                    V = nc.vector
                    step = Steps(dve, dve_done)

                    def add(g):
                        dve.wait_ge(ctx_ready, g + 1)
                        out = k.h[:, bass.ds(first_tile, TPB), g * HG * HW:(g + 1) * HG * HW]
                        V.scalar_tensor_tensor(out, k.ps[0:R, 6 + g % 2, 0:TPB * HG * HW].rearrange("p (t n) -> p t n", t=TPB), out_s[0:R, :],
                                               out, ALU.mult, ALU.add).then_inc(ctx_added, 1)

                    for u, g, mt in units:
                        dve.wait_ge(scaled, u + 1)
                        step(V.tensor_scalar(t1[u % 2][:, :, :], t1[u % 2][:, :, :], ROUND + 1.0, ROUND - 1.0, ALU.min, ALU.max))
                        if g >= 2 and mt == 0:
                            dve.wait_ge(ctx_ready, g - 1)
                        V.tensor_scalar(at[g % 2][:, mt, :, :], t1[u % 2][:, :, :], ROUND, None, ALU.subtract).then_inc(rounded, 1)
                        if g and mt == 1:
                            add(g - 1)
                    add(NHG - 1)

        with nc.Fori(0, B) as b:
            sizes(b * TPB, b)
        with stage(nc, "filled", "row_ready", "summed", "dve_done") as (block, filled, row_ready, summed, dve_done):
            @block.gpsimd
            def _(pool):
                nc.gpsimd.memset(rnd[:, :], ROUND).then_inc(filled, 1)
                pool.wait_ge(filled, 1)

            @block.tensor
            def _(pe):
                pe.wait_ge(row_ready, 1)
                nc.tensor.matmul(k.ps[:, 0, 0:1], k.ones[0:R, :], rows_sum[:, :], start=True, stop=True).then_inc(summed, 1)

            @block.vector
            def _(dve):
                V = nc.vector
                step = Steps(dve, dve_done)
                V.tensor_reduce(rows_sum[:, :], acc[:, :, :, :].rearrange("p b u h -> p (b u h)"), AX.X, ALU.add).then_inc(row_ready, 1)
                step(V.tensor_tensor(c_qk, sc[:, 0:1], sc[:, 1:2], ALU.mult))
                step(V.tensor_scalar(c_qk, c_qk, HW ** -0.5, None, ALU.mult))
                dve.wait_ge(summed, 1)
                step(V.tensor_scalar(qk_s, k.ps[:, 0, 0:1], 1.0 / (B * NHEAD * S * S), c_qk, ALU.mult, ALU.mult))
                step(V.tensor_scalar(qk_s, qk_s, EPS, None, ALU.add))
                step(V.reciprocal(alpha, qk_s))
                step(V.tensor_tensor(alpha, alpha, c_qk, ALU.mult))
                step(V.tensor_tensor(out_s, qk_s, sc[:, 2:3], ALU.mult))
        with nc.Fori(0, B) as b:
            weigh(b * TPB, b)


def norm_experts(nc, k, a, ffn, gain, shift):
    hc = ffn.hc
    with ExitStack() as c:
        up = [k.sb(f"ne_up{n}", [R, ffn.hid], F32, c) for n in range(3)]
        hn = [k.sb(f"ne_hn{n}", [R, ffn.hid], F32, c) for n in range(2)]
        hT = [k.sb(f"ne_hT{n}", [128, hc, R], F32, c) for n in range(2)]
        st = [k.sb(f"ne_st{n}", [R, 6], F32, c) for n in range(4)]
        mv = [k.sb(f"ne_mv{n}", [R, 2], F32, c) for n in range(4)]
        rs = [k.sb(f"ne_rs{n}", [R, 1], F32, c) for n in range(4)]
        sc = [k.sb(f"ne_sc{n}", [128, 2, hc], F32, c) for n in range(2)]
        U = GROUP * NT

        def group(first, last):
            with stage(nc, "up_ready", "gelu_done", "stats_done", "var_ready", "var_eps", "rstd_ready", "normed", "turned", "scaled", "y_ready",
                       "y_added", "sc_ready") as (block, up_ready, gelu_done, stats_done, var_ready, var_eps, rstd_ready, normed, turned, scaled,
                                                  y_ready, y_added, sc_ready):
                @block.sync
                def _(sp):
                    if not last:
                        for n in range(GROUP):
                            sp.wait_ge(y_added, NT * (n + 1))
                            sp.sem_clear(k.w_in[n])
                            load_expert(sp, k, a, ffn, n, first + (GROUP + n))

                @block.tensor
                def _(pe):
                    mm = nc.tensor.matmul
                    for s in range(U + 3):
                        if s < U:
                            n, t = s // NT, s % NT
                            if t == 0:
                                pe.wait_ge(k.w_in[n], 16 * ffn.loads)
                            if s >= 3:
                                pe.wait_ge(gelu_done, s - 2)
                            mm(k.ps[0:R, s % 3, 0:ffn.hid], k.xt[0:KC, 0, t * R:(t + 1) * R], k.w1[n][0:KC, 0, 0:ffn.hid], start=True, stop=False)
                            mm(k.ps[0:R, s % 3, 0:ffn.hid], k.xt[0:KC + 1, 1, t * R:(t + 1) * R], k.w1[n][0:KC + 1, 1, 0:ffn.hid],
                               start=False, stop=True).then_inc(up_ready, 1)
                        u = s - 2
                        if 0 <= u < U:
                            pe.wait_ge(normed, u + 1)
                            if u >= 2:
                                pe.wait_ge(scaled, hc * (u - 1))
                            for j in range(hc):
                                ins = nc.tensor.transpose(k.ps[:, 3 + u % 2, j * 128:j * 128 + R], hn[u % 2][:, j * 128:(j + 1) * 128], k.ident[0:R, 0:R])
                            ins.then_inc(turned, 1)
                        u = s - 3
                        if u >= 0:
                            pe.wait_ge(scaled, hc * (u + 1))
                            if u >= 3:
                                pe.wait_ge(y_added, u - 2)
                            for j in range(hc):
                                ins = mm(k.ps[0:R, 5 + u % 3, 0:D], hT[u % 2][:, j, :], k.w2[u // NT][:, j, :], start=(j == 0), stop=(j == hc - 1))
                            ins.then_inc(y_ready, 1)

                @block.scalar
                def _(act):
                    for s in range(U + 2):
                        if s < U:
                            act.wait_ge(up_ready, s + 1)
                            if s >= 3:
                                act.wait_ge(normed, s - 2)
                            nc.scalar.activation(up[s % 3][:, :], k.ps[0:R, s % 3, 0:ffn.hid], ACT.Gelu).then_inc(gelu_done, 1)
                        u = s - 2
                        if u >= 0:
                            n = u // NT
                            act.wait_ge(turned, u + 1)
                            act.wait_ge(sc_ready, 2 * (n + 1))
                            if u >= 2:
                                act.wait_ge(y_ready, u - 1)
                            for j in range(hc):
                                nc.scalar.activation(hT[u % 2][:, j, :], k.ps[:, 3 + u % 2, j * 128:j * 128 + R], ACT.Identity,
                                                     scale=sc[n % 2][:, 0, j:j + 1], bias=sc[n % 2][:, 1, j:j + 1]).then_inc(scaled, 1)

                @block.gpsimd
                def _(pool):
                    def take(n):
                        if n >= 2:
                            pool.wait_ge(scaled, hc * NT * (n - 1))
                        for i, x in enumerate((gain, shift)):
                            nc.gpsimd.tensor_copy(sc[n % 2][:, i, :], x[:, bass.ds(first + n, 1), :].rearrange("p o j -> p (o j)")).then_inc(sc_ready, 1)

                    for s in range(U):
                        if s == 0:
                            take(0)
                            take(1)
                        elif s % NT == 3 and s // NT in (1, 2):
                            take(s // NT + 1)
                        pool.wait_ge(var_ready, s + 1)
                        nc.gpsimd.tensor_scalar(rs[s % 4][:, :], mv[s % 4][:, 1:2], 1e-5, None, ALU.add).then_inc(var_eps, 1)
                        pool.wait_ge(var_eps, s + 1)
                        nc.gpsimd.tensor_tensor(rs[s % 4][:, :], rs[s % 4][:, :], k.neg_half[0:R, 0:1], ALU.pow).then_inc(rstd_ready, 1)

                @block.vector
                def _(dve):
                    V = nc.vector
                    for s in range(U + 4):
                        if s < U:
                            dve.wait_ge(gelu_done, s + 1)
                            V.bn_stats(st[s % 4][:, :], up[s % 3][:, :]).then_inc(stats_done, 1)
                        u = s - 1
                        if 0 <= u < U:
                            dve.wait_ge(rstd_ready, u + 1)
                            if u >= 2:
                                dve.wait_ge(turned, u - 1)
                            V.tensor_scalar(hn[u % 2][:, :], up[u % 3][:, :], mv[u % 4][:, 0:1], rs[u % 4][:, :], ALU.subtract, ALU.mult
                                            ).then_inc(normed, 1)
                        if s < U:
                            dve.wait_ge(stats_done, s + 1)
                            V.bn_aggr(mv[s % 4][:, :], st[s % 4][:, :]).then_inc(var_ready, 1)
                        u = s - 4
                        if u >= 0:
                            n, t = u // NT, u % NT
                            dve.wait_ge(y_ready, u + 1)
                            if t == 0 and n:
                                dve.wait_ge(y_added, NT * n)
                            V.scalar_tensor_tensor(k.h[:, t, :], k.ps[0:R, 5 + u % 3, 0:D], k.gate[:, t, bass.ds(first + n, 1)], k.h[:, t, :],
                                                   ALU.mult, ALU.add).then_inc(y_added, 1)

        with nc.Fori(0, ffn.n // GROUP - 1) as g:
            group(g * GROUP, False)
        group(ffn.n - GROUP, True)


def gelu_norm_layer(nc, k, a):
    ffn = FFN[3]
    normalise(nc, k, k.h, k.xn, 1e-5)
    to_columns(nc, k, k.xn, k.xt)
    with ExitStack() as c:
        b2 = k.sb("gn_b2", [16, D], F32, c)
        gain = k.sb("gn_gain", [128, ffn.n, ffn.hc], F32, c)
        shift = k.sb("gn_shift", [128, ffn.n, ffn.hc], F32, c)
        with stage(nc, "loaded") as (block, loaded):
            @block.sync
            def _(sp):
                sp.dma_start(b2[:, :], a["L3_ffn_fc2_b"]).then_inc(loaded, 16)
                sp.dma_start(gain[:, :, :], a["L3_ffn_ln_w"]).then_inc(loaded, 16)
                sp.dma_start(shift[:, :, :], a["L3_ffn_ln_b"]).then_inc(loaded, 16)
                sp.wait_ge(loaded, 48)
        router(nc, k, a, 3, ffn.n, "L3_ffn_gate_w", "L3_ffn_gate_b", 3)
        norm_experts(nc, k, a, ffn, gain, shift)
        gated_bias(nc, k, ffn.n, b2)


def program(nc, a, out):
    with ExitStack() as ctx:
        k = Chip(nc, ctx)
        weight_buffers(k)
        first_experts(nc, k, a)
        constants(nc, k)
        embed(nc, k, a)
        ttt_attention(nc, k, a)
        swiglu_layer(nc, k, a)
        channel_attention(nc, k, a)
        gelu_layer(nc, k, a)
        quantised_attention(nc, k, a)
        silu_layer(nc, k, a)
        ternary_attention(nc, k, a)
        gelu_norm_layer(nc, k, a)
        with stage(nc, "stored") as (block, stored):
            @block.sync
            def _(sp):
                sp.dma_start(out.rearrange("b (t p) d -> p (b t) d", p=R), k.h[:, :, :]).then_inc(stored, 16)
                sp.wait_ge(stored, 16)


def layout(inputs):
    out = {n: np.asarray(x) for n, x in inputs.items()}
    x = out.pop("x")
    for n, (p, _) in enumerate(LEVELS):
        e = x.shape[-1] // p
        out[f"pix{n}"] = x.reshape(B, 3, e, p, e, p).transpose(2, 4, 0, 3, 5, 1).reshape(e * e, -1)
        out[f"L0_tok_W{n}"] = out[f"L0_tok_W{n}"].T
        if n:
            out[f"inter{n}"] = interpolation(LEVELS[n][1], IMG_TOK)
    for n in ("x_txt", "mask_BS_i1_0"):
        out[n] = out[n].T
    out["L0_tok_bf"] = out["L0_tok_bf"].reshape(2, KC).T
    out["L0_tok_Wf"] = out["L0_tok_Wf"].T
    out["L0_txt_residual_weight"] = out["L0_txt_residual_weight"].reshape(1)
    out["ttt_w_row"] = np.concatenate([out.pop("L0_attn_" + n).reshape(D, NH0, -1) for n in ("Wk", "Wv", "Wq", "lr_w")], axis=2)
    out["L0_attn_b_down"] = out["L0_attn_b_down"].reshape(2, KC).T
    out.update(ttt_constants())
    out["L0_ffn_gate_w"] = out["L0_ffn_gate_w"].T
    w, v = out["L0_ffn_mlp1_w"], out["L0_ffn_mlp1_b"]
    out["L0_ffn_mlp1_w"] = np.concatenate([w[:, 0::2], w[:, 1::2]], axis=1).transpose(0, 2, 1)
    out["L0_ffn_mlp1_b"] = np.concatenate([v[:, 0::2], v[:, 1::2]], axis=1)
    out["L0_ffn_mlp2_w"] = out["L0_ffn_mlp2_w"].transpose(0, 2, 1)
    for n in ("L2_attn_qkv_w", "L2_attn_proj_w", "L3_attn_w_qkv"):
        out[n] = out[n].T
    out["qa_scales"] = np.stack([out.pop("L2_attn_" + n + "_scale") for n in ("w_qkv", "a1", "attn", "a2", "w_proj", "a3")])
    for n in ("L3_ffn_ln_w", "L3_ffn_ln_b"):
        out[n] = out[n].reshape(16, 3, 128).transpose(2, 0, 1)
    return {n: np.ascontiguousarray(v) for n, v in out.items()}


def kernel(**inputs):
    import concourse.bacc as bacc
    from concourse.bass_utils import run_bass_kernel_spmd

    nc = bacc.Bacc("TRN2", target_bir_lowering=False, num_devices=1)
    arrays, a = {}, {}
    for name, x in layout(inputs).items():
        arrays[f"in_{name}_dram"] = x
        a[name] = nc.dram_tensor(f"in_{name}_dram", x.shape, mybir.dt.from_np(x.dtype), kind="ExternalInput").ap()
    out = nc.dram_tensor("out_dram", (B, S, D), F32, kind="ExternalOutput").ap()
    program(nc, a, out)
    r = run_bass_kernel_spmd(nc, [arrays], core_ids=[0])
    return r.results[0]["out_dram"]
```

```python
from contextlib import ExitStack, contextmanager

import numpy as np

import concourse.bass as bass
from concourse import mybir

F32 = mybir.dt.float32
BF16 = mybir.dt.bfloat16
I32 = mybir.dt.int32
U32 = mybir.dt.uint32
ALU = mybir.AluOpType
ACT = mybir.ActivationFunctionType
AX = mybir.AxisListType

B = 2
IMG_TOK, TXT_TOK = 256, 77
S = IMG_TOK + TXT_TOK
D = 192
R = 111
NT = B * S // R
TPB = S // R
KC = 96
ROUND = 1.5 * 2.0 ** 23


class Steps:

    def __init__(self, eng, sem):
        self.eng, self.sem, self.n = eng, sem, 0

    def __call__(self, ins):
        self.n += 1
        ins.then_inc(self.sem, 1)
        self.eng.wait_ge(self.sem, self.n)

    def start(self, ins):
        self.n += 1
        ins.then_inc(self.sem, 1)

    def wait(self):
        self.eng.wait_ge(self.sem, self.n)


@contextmanager
def stage(nc, *names):
    with ExitStack() as c:
        sems = [c.enter_context(nc.semaphore(n)) for n in names]
        with nc.Block(no_gpsimd_drain=True) as block:
            yield (block, *sems)
        nums = sorted(s.num for s in sems)
        first = nums[0]
        for n, after in zip(nums, nums[1:] + [None]):
            if after != n + 1:
                nc.gpsimd.sem_clear(range(first, n + 1))
                first = after
        nc.all_engine_barrier(sem_only=True)


def bcast(ap, parts):
    return bass.AP(tensor=ap.tensor, offset=ap.offset, ap=[[0, parts]] + [list(x) for x in ap.ap])


class Chip:

    def __init__(self, nc, ctx):
        self.nc, self.ctx = nc, ctx
        self.h = self.sb("h", [R, NT, D])
        self.xn = self.sb("xn", [R, NT, D])
        self.xt = self.sb("xt", [KC + 1, 2, B * S])
        self.ident = self.sb("ident", [128, 128])
        self.ones = self.sb("ones", [128, 128])
        self.stats = self.sb("stats", [R, NT, 6])
        self.mv = self.sb("mv", [R, NT, 2])
        self.rstd = self.sb("rstd", [R, NT, 1])
        self.neg_half = self.sb("neg_half", [128, 8])
        self.ps = ctx.enter_context(nc.psum_tensor("ps", [128, 8, 512], F32))

    def sb(self, name, shape, dt=F32, ctx=None):
        return (ctx or self.ctx).enter_context(self.nc.sbuf_tensor(name, shape, dt))


def constants(nc, k):
    with stage(nc, "filled", "selected") as (block, filled, selected):
        @block.gpsimd
        def _(pool):
            nc.gpsimd.memset(k.ident[:, :], 0.0).then_inc(filled, 1)
            nc.gpsimd.memset(k.ones[:, :], 1.0).then_inc(filled, 1)
            nc.gpsimd.memset(k.neg_half[:, :], -0.5).then_inc(filled, 1)
            nc.gpsimd.memset(k.xt[:, :, :], 1.0).then_inc(filled, 1)
            pool.wait_ge(filled, 4)
            nc.gpsimd.affine_select(out=k.ident[:, :], in_=k.ident[:, :], compare_op=ALU.not_equal, fill=1.0,
                                    base=0, pattern=[[-1, 128]], channel_multiplier=1).then_inc(selected, 1)
            pool.wait_ge(selected, 1)


def normalise(nc, k, src, dst, eps, gain=None, shift=None):
    with stage(nc, "dve_done", "aggregated", "rstd_eps", "rstd_ready") as (block, dve_done, aggregated, rstd_eps, rstd_ready):
        @block.vector
        def _(dve):
            step = Steps(dve, dve_done)
            for t in range(NT):
                step.start(nc.vector.bn_stats(k.stats[:, t, :], src[:, t, :]))
            step.wait()
            for t in range(NT):
                nc.vector.bn_aggr(k.mv[:, t, :], k.stats[:, t, :]).then_inc(aggregated, 1)
            dve.wait_ge(aggregated, NT)
            dve.wait_ge(rstd_ready, 1)
            for t in range(NT):
                step.start(nc.vector.tensor_scalar(dst[:, t, :], src[:, t, :], k.mv[:, t, 0:1], k.rstd[:, t, 0:1],
                                                   ALU.subtract, ALU.mult))
            step.wait()
            if gain is not None:
                step(nc.vector.tensor_tensor(dst[:, :, :], dst[:, :, :], gain.unsqueeze(1).broadcast_to([R, NT, D]), ALU.mult))
                step(nc.vector.tensor_tensor(dst[:, :, :], dst[:, :, :], shift.unsqueeze(1).broadcast_to([R, NT, D]), ALU.add))

        @block.gpsimd
        def _(pool):
            pool.wait_ge(aggregated, NT)
            nc.gpsimd.tensor_scalar(k.rstd[:, :, :], k.mv[:, :, 1:2], eps, None, ALU.add).then_inc(rstd_eps, 1)
            pool.wait_ge(rstd_eps, 1)
            nc.gpsimd.tensor_tensor(k.rstd[:, :, 0], k.rstd[:, :, 0], k.neg_half[0:R, 0:NT], ALU.pow).then_inc(rstd_ready, 1)


def to_columns(nc, k, src, dst):
    with stage(nc, "bank_ready", "act_copied", "dve_copied") as (block, bank_ready, act_copied, dve_copied):
        banks = [(b, c) for b in range(B) for c in range(2)]

        @block.tensor
        def _(pe):
            for n, (b, c) in enumerate(banks):
                for j in range(TPB):
                    ins = nc.tensor.transpose(k.ps[0:KC, n, j * R:(j + 1) * R], src[:, b * TPB + j, c * KC:(c + 1) * KC],
                                              k.ident[0:R, 0:R])
                ins.then_inc(bank_ready, 1)

        @block.scalar
        def _(act):
            for n in (0, 2):
                b, c = banks[n]
                act.wait_ge(bank_ready, n + 1)
                nc.scalar.copy(dst[0:KC, c, b * S:(b + 1) * S], k.ps[0:KC, n, 0:S]).then_inc(act_copied, 1)
            act.wait_ge(act_copied, 2)

        @block.vector
        def _(dve):
            for n in (1, 3):
                b, c = banks[n]
                dve.wait_ge(bank_ready, n + 1)
                nc.vector.tensor_copy(dst[0:KC, c, b * S:(b + 1) * S], k.ps[0:KC, n, 0:S]).then_inc(dve_copied, 1)
            dve.wait_ge(dve_copied, 2)


def to_rows(nc, k, src, dst):
    with stage(nc, "tile_ready", "dve_copied") as (block, tile_ready, dve_copied):
        @block.tensor
        def _(pe):
            for t in range(NT):
                for c in range(2):
                    ins = nc.tensor.transpose(k.ps[0:R, t, c * KC:(c + 1) * KC], src[0:KC, c, t * R:(t + 1) * R],
                                              k.ident[0:KC, 0:KC])
                ins.then_inc(tile_ready, 1)

        @block.vector
        def _(dve):
            for t in range(NT):
                dve.wait_ge(tile_ready, t + 1)
                nc.vector.tensor_copy(dst[:, t, :], k.ps[0:R, t, 0:D]).then_inc(dve_copied, 1)
            dve.wait_ge(dve_copied, NT)


def interpolation(n_in, n_out):
    pos = np.clip((np.arange(n_out, dtype=np.float32) + 0.5) * (n_in / n_out) - 0.5, 0.0, n_in - 1).astype(np.float32)
    i0 = np.floor(pos).astype(np.int32)
    w = (pos - i0).astype(np.float32)
    m = np.zeros((n_in, n_out), np.float32)
    m[i0, np.arange(n_out)] += np.float32(1.0) - w
    m[np.minimum(i0 + 1, n_in - 1), np.arange(n_out)] += w
    return m
PATCHES = 16
LEVELS = [(1, 256), (2, 64), (4, 16)]
EMB = 64


def embed(nc, k, a):
    with ExitStack() as c:
        idx = [k.sb(f"idx{n}", [min(tok, 128), max(tok // 128, 1), PATCHES], I32, c) for n, (_, tok) in enumerate(LEVELS)]
        width = [B * p * p * 3 for p, _ in LEVELS]
        got = [k.sb(f"got{n}", [min(tok, 128), max(tok // 128, 1), PATCHES, w], F32, c)
               for n, ((_, tok), w) in enumerate(zip(LEVELS, width))]
        feat = [k.sb(f"feat{n}", [min(tok, 128), max(tok // 128, 1), B, PATCHES * w // B], F32, c)
                for n, ((_, tok), w) in enumerate(zip(LEVELS, width))]
        din = [PATCHES * w // B for w in width]
        kw = [min(d, KC) for d in din]
        nk = [d // w for d, w in zip(din, kw)]
        wt = [k.sb(f"tokw{n}", [kw[n], nk[n], EMB], F32, c) for n in range(3)]
        bias0 = k.sb("tok_bias0", [EMB, 1], F32, c)
        bias = [None] + [k.sb(f"tok_bias{n}", [1, EMB], F32, c) for n in (1, 2)]
        wf = k.sb("tok_wf", [EMB, 3, D], F32, c)
        bf = k.sb("tok_bf", [KC, 2], F32, c)
        inter = [None] + [k.sb(f"inter{n}", [LEVELS[n][1], IMG_TOK], F32, c) for n in (1, 2)]
        ft = [k.sb("ft0", [48, B, 256], F32, c), k.sb("ft1", [KC, B, 2, 64], F32, c), k.sb("ft2", [KC, B, 8, 16], F32, c)]
        lev = [None, k.sb("lev1", [64, B, EMB], F32, c), k.sb("lev2", [16, B, EMB], F32, c)]
        yt = k.sb("yt", [EMB, 3, B * IMG_TOK], F32, c)
        ids = k.sb("ids", [TXT_TOK, B], I32, c)
        typ = k.sb("typ", [TXT_TOK, B], I32, c)
        we = k.sb("we", [TXT_TOK, B, D], F32, c)
        te = k.sb("te", [TXT_TOK, B, D], F32, c)
        pe_ = k.sb("pos", [TXT_TOK, D], F32, c)
        wpad = k.sb("wpad", [TXT_TOK, B, D + 2], F32, c)
        ppad = k.sb("ppad", [TXT_TOK, B, D + 2], F32, c)
        cw = k.sb("conv_w", [TXT_TOK, 8], F32, c)
        gamma = k.sb("txt_gamma", [TXT_TOK, D], F32, c)
        beta = k.sb("txt_beta", [TXT_TOK, D], F32, c)
        conv = k.sb("conv", [TXT_TOK, B, D], F32, c)
        emb = k.sb("emb", [TXT_TOK, B, D], F32, c)
        one_minus = k.sb("one_minus", [TXT_TOK, 1], F32, c)
        st = k.sb("txt_stats", [TXT_TOK, B, 6], F32, c)
        mv = k.sb("txt_mv", [TXT_TOK, B, 2], F32, c)
        rs = k.sb("txt_rstd", [TXT_TOK, B], F32, c)
        N_SMALL = 21

        gathered = [k.ctx.enter_context(nc.semaphore(f"gathered{n}")) for n in range(3)]
        txt_gathered = k.ctx.enter_context(nc.semaphore("txt_gathered"))
        with stage(nc, "idx_in", "small_in", "feat_done", "feat_t", "ft_done", "mm_done",
                   "evac", "dve_done", "var_ready", "rstd_ready", "ready", "pool_done") as \
                (block, idx_in, small_in, feat_done, feat_t, ft_done, mm_done,
                 evac, dve_done, var_ready, rstd_ready, ready, pool_done):
            @block.sync
            def _(sp):
                for n, (_, tok) in enumerate(LEVELS):
                    sp.dma_start(idx[n][:, :, :], a[f"L0_tok_idx{n}"].rearrange("(t p g) -> p t g", g=PATCHES, p=min(tok, 128))
                                 ).then_inc(idx_in, 16)
                sp.dma_start(ids[:, :], a["x_txt"]).then_inc(idx_in, 16)
                sp.dma_start(typ[:, :], a["mask_BS_i1_0"]).then_inc(idx_in, 16)
                for n in range(3):
                    sp.dma_start(wt[n][:, :, :], a[f"L0_tok_W{n}"].rearrange("(c p) e -> p c e", p=kw[n])).then_inc(small_in, 16)
                sp.dma_start(bias0[:, :], a["L0_tok_b0"].unsqueeze(1)).then_inc(small_in, 16)
                for n in (1, 2):
                    sp.dma_start(bias[n][:, :], a[f"L0_tok_b{n}"].unsqueeze(0)).then_inc(small_in, 16)
                    sp.dma_start(inter[n][:, :], a[f"inter{n}"]).then_inc(small_in, 16)
                sp.dma_start(wf[:, :, :], a["L0_tok_Wf"].rearrange("(l p) e -> p l e", p=EMB)).then_inc(small_in, 16)
                sp.dma_start(bf[:, :], a["L0_tok_bf"]).then_inc(small_in, 16)

            @block.scalar
            def _(act):
                act.dma_start(pe_[:, :], a["L0_txt_pos_emb"][0:TXT_TOK, :]).then_inc(small_in, 16)
                act.dma_start(cw[:, 0:6], bcast(a["L0_txt_conv_w"].rearrange("a b -> (a b)"), TXT_TOK)).then_inc(small_in, 16)
                act.dma_start(cw[:, 6:7], bcast(a["L0_txt_conv_b"], TXT_TOK)).then_inc(small_in, 16)
                act.dma_start(cw[:, 7:8], bcast(a["L0_txt_residual_weight"], TXT_TOK)).then_inc(small_in, 16)
                act.dma_start(gamma[:, :], bcast(a["L0_txt_ln_gamma"], TXT_TOK)).then_inc(small_in, 16)
                act.dma_start(beta[:, :], bcast(a["L0_txt_ln_beta"], TXT_TOK)).then_inc(small_in, 16)
                act.wait_ge(small_in, 16 * 16)

            @block.gpsimd
            def _(pool):
                pool.wait_ge(idx_in, 16 * 5)
                for b in range(B):
                    for dst, table, at in ((we, "L0_txt_word_emb", ids), (te, "L0_txt_type_emb", typ)):
                        pool.indirect_dma_start(dst[:, b, :], None, a[table], bass.IndirectOffsetOnAxis(ap=at[:, b:b + 1], axis=0)
                                                ).then_inc(txt_gathered, 16)
                for n, (_, tok) in enumerate(LEVELS):
                    for t in range(max(tok // 128, 1)):
                        for g in range(PATCHES):
                            pool.indirect_dma_start(got[n][:, t, g, :], None, a[f"pix{n}"],
                                                    bass.IndirectOffsetOnAxis(ap=idx[n][:, t, g:g + 1], axis=0)
                                                    ).then_inc(gathered[n], 16)
                pool.wait_ge(var_ready, 1)
                nc.gpsimd.tensor_tensor(rs[:, :], rs[:, :], k.neg_half[0:TXT_TOK, 0:B], ALU.pow).then_inc(rstd_ready, 1)


            @block.vector
            def _(dve):
                step = Steps(dve, dve_done)
                step.start(nc.vector.memset(wpad[:, :, :], 0.0))
                step(nc.vector.memset(ppad[:, :, :], 0.0))
                dve.wait_ge(small_in, 16 * 16)
                dve.wait_ge(txt_gathered, 16 * 4)
                for b in range(B):
                    step.start(nc.vector.tensor_copy(wpad[:, b, 1:D + 1], we[:, b, :]))
                    step.start(nc.vector.tensor_copy(ppad[:, b, 1:D + 1], pe_[:, :]))
                step(nc.vector.tensor_scalar(one_minus[:, :], cw[:, 7:8], -1.0, 1.0, ALU.mult, ALU.add))
                step(nc.vector.tensor_scalar(conv[:, :, :], wpad[:, :, 0:D], cw[:, 0:1], cw[:, 6:7], ALU.mult, ALU.add))
                for pad, first, taps in ((wpad, 0, (1, 2)), (ppad, 3, (0, 1, 2))):
                    for tap in taps:
                        step(nc.vector.scalar_tensor_tensor(conv[:, :, :], pad[:, :, tap:tap + D], cw[:, first + tap:first + tap + 1],
                                                            conv[:, :, :], ALU.mult, ALU.add))
                step(nc.vector.tensor_tensor(emb[:, :, :], wpad[:, :, 1:D + 1], ppad[:, :, 1:D + 1], ALU.add))
                step(nc.vector.scalar_tensor_tensor(emb[:, :, :], emb[:, :, :], one_minus[:, 0:1], te[:, :, :], ALU.mult, ALU.add))
                step(nc.vector.scalar_tensor_tensor(emb[:, :, :], conv[:, :, :], cw[:, 7:8], emb[:, :, :], ALU.mult, ALU.add))
                for b in range(B):
                    step(nc.vector.bn_stats(st[:, b, :], emb[:, b, :]))
                    step(nc.vector.bn_aggr(mv[:, b, :], st[:, b, :]))
                nc.vector.tensor_scalar(rs[:, :], mv[:, :, 1], 1e-12, None, ALU.add).then_inc(var_ready, 1)
                dve.wait_ge(rstd_ready, 1)
                for b in range(B):
                    step(nc.vector.tensor_scalar(emb[:, b, :], emb[:, b, :], mv[:, b, 0:1], rs[:, b:b + 1], ALU.subtract, ALU.mult))
                    step(nc.vector.tensor_tensor(emb[:, b, :], emb[:, b, :], gamma[:, :], ALU.mult))
                    nc.vector.tensor_tensor(emb[:, b, :], emb[:, b, :], beta[:, :], ALU.add).then_inc(feat_done, 1)
                for n, (_, tok) in enumerate(LEVELS):
                    dve.wait_ge(gathered[n], 16 * PATCHES * max(tok // 128, 1))
                    f = width[n] // B
                    for t in range(max(tok // 128, 1)):
                        for b in range(B):
                            nc.vector.tensor_copy(feat[n][:, t, b, :].rearrange("p (g f) -> p g f", f=f),
                                                  got[n][:, t, :, b * f:(b + 1) * f]).then_inc(feat_done, 1)
                dve.wait_ge(feat_t, 1)
                step.start(nc.vector.tensor_copy(k.xt[0:KC, 0, :].rearrange("p (b s) -> p b s", b=B)[:, :, IMG_TOK:S],
                                                 k.ps[0:KC, 0, 0:B * TXT_TOK].rearrange("p (b s) -> p b s", b=B)))
                step.start(nc.vector.tensor_copy(k.xt[0:KC, 1, :].rearrange("p (b s) -> p b s", b=B)[:, :, IMG_TOK:S],
                                                 k.ps[0:KC, 1, 0:B * TXT_TOK].rearrange("p (b s) -> p b s", b=B)))
                dve.wait_ge(feat_t, 2)
                nc.vector.tensor_copy(ft[0][:, :, :], k.ps[0:48, 2, :].rearrange("p (b s) -> p b s", b=B)).then_inc(ft_done, 1)
                dve.wait_ge(feat_t, 3)
                nc.vector.tensor_copy(ft[1][:, :, :, :], k.ps[0:KC, 3, 0:256].rearrange("p (b c s) -> p b c s", b=B, c=2)).then_inc(ft_done, 1)
                dve.wait_ge(feat_t, 4)
                nc.vector.tensor_copy(ft[2][:, :, :, :], k.ps[0:KC, 4, 0:256].rearrange("p (b c s) -> p b c s", b=B, c=8)).then_inc(ft_done, 1)
                dve.wait_ge(mm_done, 1)
                nc.vector.tensor_scalar(yt[:, 0, :], k.ps[0:EMB, 5, :], bias0[:, 0:1], None, ALU.add).then_inc(evac, 1)
                dve.wait_ge(mm_done, 2)
                nc.vector.tensor_copy(lev[1][:, :, :], k.ps[0:64, 6, 0:B * EMB].rearrange("p (b e) -> p b e", b=B)).then_inc(evac, 1)
                dve.wait_ge(mm_done, 3)
                nc.vector.tensor_copy(lev[2][:, :, :], k.ps[0:16, 7, 0:B * EMB].rearrange("p (b e) -> p b e", b=B)).then_inc(evac, 1)
                for n in (1, 2):
                    dve.wait_ge(mm_done, 3 + n)
                    nc.vector.tensor_copy(yt[:, n, :], k.ps[0:EMB, n + 1, :]).then_inc(evac, 1)
                for ch in range(2):
                    dve.wait_ge(mm_done, 6 + ch)
                    step.start(nc.vector.tensor_scalar(k.xt[0:KC, ch, :].rearrange("p (b s) -> p b s", b=B)[:, :, 0:IMG_TOK],
                                                       k.ps[0:KC, ch, :].rearrange("p (b s) -> p b s", b=B), bf[:, ch:ch + 1], None, ALU.add))
                step.wait()

            @block.tensor
            def _(pe):
                mm, tr = nc.tensor.matmul, nc.tensor.transpose
                pe.wait_ge(feat_done, 2)
                for ch in range(2):
                    for b in range(B):
                        ins = tr(k.ps[0:KC, ch, b * TXT_TOK:(b + 1) * TXT_TOK], emb[:, b, ch * KC:(ch + 1) * KC], k.ident[0:TXT_TOK, 0:TXT_TOK])
                ins.then_inc(feat_t, 1)
                pe.wait_ge(feat_done, 2 + 4)
                for b in range(B):
                    for t in range(2):
                        ins = tr(k.ps[0:48, 2, b * 256 + t * 128:b * 256 + (t + 1) * 128], feat[0][:, t, b, :], k.ident[:, :])
                ins.then_inc(feat_t, 1)
                pe.wait_ge(feat_done, 2 + 6)
                for b in range(B):
                    for ch in range(2):
                        ins = tr(k.ps[0:KC, 3, (b * 2 + ch) * 64:(b * 2 + ch + 1) * 64], feat[1][:, 0, b, ch * KC:(ch + 1) * KC], k.ident[0:64, 0:64])
                ins.then_inc(feat_t, 1)
                pe.wait_ge(feat_done, 2 + 8)
                for b in range(B):
                    for ch in range(8):
                        ins = tr(k.ps[0:KC, 4, (b * 8 + ch) * 16:(b * 8 + ch + 1) * 16], feat[2][:, 0, b, ch * KC:(ch + 1) * KC], k.ident[0:16, 0:16])
                ins.then_inc(feat_t, 1)
                pe.wait_ge(small_in, 16 * 16)
                pe.wait_ge(ft_done, 1)
                mm(k.ps[0:EMB, 5, :], wt[0][:, 0, :], ft[0][:, :, :].rearrange("p b s -> p (b s)"), start=True, stop=True).then_inc(mm_done, 1)
                for n in (1, 2):
                    pe.wait_ge(ft_done, n + 1)
                    tok = LEVELS[n][1]
                    for b in range(B):
                        for ch in range(nk[n]):
                            mm(k.ps[0:tok, 5 + n, b * EMB:(b + 1) * EMB], ft[n][:, b, ch, :], wt[n][:, ch, :], start=(ch == 0), stop=False)
                        ins = mm(k.ps[0:tok, 5 + n, b * EMB:(b + 1) * EMB], k.ones[0:1, 0:tok], bias[n][:, :], start=False, stop=True)
                    ins.then_inc(mm_done, 1)
                for n in (1, 2):
                    pe.wait_ge(evac, 1 + n)
                    for b in range(B):
                        ins = mm(k.ps[0:EMB, n + 1, b * IMG_TOK:(b + 1) * IMG_TOK], lev[n][:, b, :], inter[n][:, :], start=True, stop=True)
                    ins.then_inc(mm_done, 1)
                pe.wait_ge(evac, 5)
                pe.wait_ge(dve_done, 21)
                for ch in range(2):
                    for n in range(3):
                        ins = mm(k.ps[0:KC, ch, :], wf[:, n, ch * KC:(ch + 1) * KC], yt[:, n, :], start=(n == 0), stop=(n == 2))
                    ins.then_inc(mm_done, 1)
    to_rows(nc, k, k.xt, k.h)


def project(nc, k, w, dst=None, add_to=None):
    kk = w.shape[0]
    with stage(nc, "tile_ready", "dve_done") as (block, tile_ready, dve_done):
        @block.tensor
        def _(pe):
            for t in range(NT):
                nc.tensor.matmul(k.ps[0:R, t, 0:D], k.xt[0:KC, 0, t * R:(t + 1) * R], w[0:KC, 0, :], start=True, stop=False)
                nc.tensor.matmul(k.ps[0:R, t, 0:D], k.xt[0:kk, 1, t * R:(t + 1) * R], w[0:kk, 1, :], start=False, stop=True
                                 ).then_inc(tile_ready, 1)

        @block.vector
        def _(dve):
            for t in range(NT):
                dve.wait_ge(tile_ready, t + 1)
                if dst is not None:
                    nc.vector.tensor_copy(dst[:, t, :], k.ps[0:R, t, 0:D]).then_inc(dve_done, 1)
                else:
                    nc.vector.tensor_tensor(add_to[:, t, :], k.ps[0:R, t, 0:D], add_to[:, t, :], ALU.add).then_inc(dve_done, 1)
            dve.wait_ge(dve_done, NT)


NH0, HD = 3, 64
NJ = B * NH0
C = 21
PASS = 4
NCH = PASS * -(-S // (PASS * C))
SP = (NCH + 1) * C
RJ = NJ * C
TTT_EPS = 1e-6


def ttt_constants():
    j, t = np.divmod(np.arange(RJ), C)
    same = j[:, None] == j[None, :]
    centre = np.zeros((HD + 1, HD + 2), np.float32)
    centre[0:HD, 0:HD] = np.eye(HD, dtype=np.float32) - np.float32(1.0 / HD)
    centre[HD, HD + 1] = 1.0
    return {"ttt_before": -(same & (t[:, None] < t[None, :])).astype(np.float32),
            "ttt_upto": -(same & (t[:, None] <= t[None, :])).astype(np.float32),
            "ttt_same": -same.astype(np.float32),
            "ttt_member": -(j[:, None] == np.arange(NJ)[None, :]).astype(np.float32),
            "ttt_centre": centre}


def ttt_attention(nc, k, a):
    with ExitStack() as c:
        rowsum = k.sb("ttt_rowsum", [HD + 1, NJ], F32, c)
        w_out = k.sb("w_out", [KC, 2, D], F32, c)
        w_up = k.sb("w_up", [KC + 1, 2, D], F32, c)
        post = k.sb("post", [R, 4, D], F32, c)
        g_row = k.sb("g_row", [RJ, HD], F32, c)
        g2_row = k.sb("g2_row", [RJ, HD], F32, c)
        b_row = k.sb("b_row", [RJ, HD], F32, c)
        g_col = k.sb("g_col", [HD, NH0], F32, c)
        b_col = k.sb("b_col", [HD, NH0], F32, c)
        before = k.sb("before", [RJ, RJ], F32, c)
        upto = k.sb("upto", [RJ, RJ], F32, c)
        same = k.sb("same", [RJ, RJ], F32, c)
        member = k.sb("member", [RJ, NJ], F32, c)
        centre = k.sb("centre", [HD + 1, HD + 2], F32, c)
        cols = k.sb("ttt_cols", [HD + 1, 3, NJ, SP], F32, c)
        state = k.sb("state", [HD + 1, NJ, HD], F32, c)
        ktm = k.sb("ktm", [HD + 1, 2, NJ, RJ], F32, c)
        kt = [k.sb(f"kt{p}", [HD + 1, 3, NJ, C], F32, c) for p in range(2)]
        rows = [k.sb(f"rows{p}", [RJ, 3 * (HD + 1) + 1], F32, c) for p in range(2)]
        k_1 = [x[:, 0:HD + 1] for x in rows]
        q_row = [x[:, HD + 1:2 * HD + 1] for x in rows]
        target = [x[:, 2 * (HD + 1):3 * (HD + 1)] for x in rows]
        eta = [x[:, 3 * (HD + 1):] for x in rows]
        inner = [k.sb(f"inner{p}", [RJ, RJ], F32, c) for p in range(2)]
        inner_q = [k.sb(f"inner_q{p}", [RJ, RJ], F32, c) for p in range(2)]
        inner_x = k.sb("inner_x", [RJ, RJ], F32, c)
        lhs = k.sb("ttt_lhs", [RJ, RJ], F32, c)
        v = k.sb("ttt_v", [RJ, 1], F32, c)
        std = k.sb("ttt_std", [RJ, 1], F32, c)
        r2 = k.sb("ttt_r2", [RJ, 1], F32, c)
        zsum, a1, a2, w = (k.sb("ttt_" + n, [RJ, 1], F32, c) for n in ("zsum", "a1", "a2", "w"))
        pz = k.sb("ttt_pz", [RJ, HD + 1], F32, c)
        q_ = k.sb("ttt_q", [RJ, HD + 1], F32, c)
        zr = k.sb("ttt_zr", [RJ, HD + 1], F32, c)
        gh = k.sb("ttt_gh", [RJ, HD + 1], F32, c)
        junk_a = k.sb("ttt_junk_a", [RJ, HD + 1], F32, c)
        junk = [k.sb(f"ttt_junk{n}", [RJ, HD], F32, c) for n in range(3)]
        gd = k.sb("ttt_gd", [RJ, HD], F32, c)
        ge = k.sb("ttt_ge", [RJ, HD], F32, c)
        eg = k.sb("eg", [RJ, NJ, HD], F32, c)
        z0 = [k.sb(f"z0_{p}", [RJ, HD], F32, c) for p in range(2)]
        zs = k.sb("ttt_z", [RJ, HD + 2], F32, c)
        y = k.sb("ttt_y", [RJ, HD], F32, c)
        outr = k.sb("outr", [RJ, HD], F32, c)
        st6 = k.sb("ttt_st6", [RJ, 6], F32, c)
        mv = k.sb("ttt_mv", [RJ, 2], F32, c)
        rq = k.sb("ttt_rq", [RJ, 1], F32, c)
        out_d = nc.dram_tensor("ttt_rows", [B, C + SP, D], F32).ap()
        z_bank = k.ps[0:RJ, 0, 0:HD + 1]
        z, z_mean = zs[:, 1:HD + 1], zs[:, HD + 1:]
        rows_b, gram_b, zq_b, state_b = (k.ps[:, 4 + n, :] for n in range(4))
        base = state_b[0:RJ, NJ * HD:NJ * HD + HD]

        def flat(x):
            return x.rearrange("p j t -> p (j t)")

        def own(which):
            x = ktm[:, which, :, :]
            return bass.AP(tensor=x.tensor, offset=x.offset, ap=[list(x.ap[0]), [RJ + C, NJ], [1, C]])

        normalise(nc, k, k.h, k.xn, 1e-5)
        to_columns(nc, k, k.xn, k.xt)
        with ExitStack() as c1:
            w_down = k.sb("w_down", [KC, 2, D], F32, c1)
            b_down = k.sb("b_down", [KC, 2], F32, c1)
            hid = k.sb("hid", [KC + 1, 2, B, S], F32, c1)
            w_row = k.sb("w_row", [KC + 1, 2, NH0, 3 * HD + 1], F32, c1)
            N_LOADS = 6 + 4 + 4 * NJ + 2 + 5 + 1
            with stage(nc, "loaded", "filled", "bank_ready", "act_done", "dve_done") as (block, loaded, filled, bank_ready, act_done, dve_done):
                @block.sync
                def _(sp):
                    sp.dma_start(w_down[:, :, :], a["L0_attn_W_down"].rearrange("(c p) n -> p c n", p=KC)).then_inc(loaded, 16)
                    sp.dma_start(b_down[:, :], a["L0_attn_b_down"]).then_inc(loaded, 16)
                    sp.dma_start(w_row[0:KC, :, :, :], a["ttt_w_row"].rearrange("(c p) h n -> p c h n", p=KC)).then_inc(loaded, 16)
                    sp.dma_start(w_out[:, :, :], a["L0_attn_Wo"].rearrange("(c p) n -> p c n", p=KC)).then_inc(loaded, 16)
                    sp.dma_start(w_up[0:KC, :, :], a["L0_attn_W_up"].rearrange("(c p) n -> p c n", p=KC)).then_inc(loaded, 16)
                    sp.dma_start(w_up[KC:KC + 1, 1, :], a["L0_attn_b_up"].unsqueeze(0)).then_inc(loaded, 16)
                    for n, name in enumerate(("post_g", "post_b", "norm_g", "norm_b")):
                        sp.dma_start(post[:, n, :], bcast(a["L0_attn_" + name], R)).then_inc(loaded, 16)
                    for j in range(NJ):
                        sp.dma_start(g_row[j * C:(j + 1) * C, :], bcast(a["L0_attn_ttt_g"][j % NH0], C)).then_inc(loaded, 16)
                        sp.dma_start(b_row[j * C:(j + 1) * C, :], bcast(a["L0_attn_ttt_b"][j % NH0], C)).then_inc(loaded, 16)
                        sp.dma_start(state[0:HD, j, :], a["L0_attn_W1"][j % NH0]).then_inc(loaded, 16)
                        sp.dma_start(state[HD:HD + 1, j, :], a["L0_attn_b1"][j % NH0]).then_inc(loaded, 16)
                    sp.dma_start(g_col[:, :], a["ttt_g_col"]).then_inc(loaded, 16)
                    sp.dma_start(b_col[:, :], a["ttt_b_col"]).then_inc(loaded, 16)
                    for dst, name in ((before, "before"), (upto, "upto"), (same, "same"), (member, "member"), (centre, "centre")):
                        sp.dma_start(dst[:, :], a["ttt_" + name]).then_inc(loaded, 16)
                    sp.wait_ge(filled, 1)
                    sp.dma_start(w_row[KC:KC + 1, 1, :, 3 * HD:3 * HD + 1], a["L0_attn_lr_b"].unsqueeze(0).unsqueeze(2),
                                 allow_slow_non_contiguous=True).then_inc(loaded, 16)
                    sp.wait_ge(loaded, 16 * N_LOADS)

                @block.gpsimd
                def _(pool):
                    step = Steps(pool, filled)
                    G = nc.gpsimd
                    step(G.memset(w_row[KC:KC + 1, :, :, :], 0.0))
                    step(G.memset(hid[KC:KC + 1, :, :, :], 1.0))
                    step.start(G.memset(ktm[:, :, :, :], 0.0))
                    step.start(G.memset(cols[:, 0:2, :, :], 1.0))
                    step.start(G.memset(cols[:, 2, :, :], 0.0))
                    step.start(G.memset(gd[:, :], 0.0))
                    step.start(G.memset(ge[:, :], 0.0))
                    step.start(G.memset(rows[1][:, :], 0.0))
                    step.start(G.memset(inner_q[1][:, :], 0.0))
                    step.wait()

                @block.tensor
                def _(pe):
                    pe.wait_ge(loaded, 16 * N_LOADS)
                    for b in range(B):
                        for m in range(2):
                            for kc in range(2):
                                ins = nc.tensor.matmul(k.ps[0:KC, 2 * b + m, 0:S], w_down[:, kc, m * KC:(m + 1) * KC],
                                                       k.xt[0:KC, kc, b * S:(b + 1) * S], start=(kc == 0), stop=(kc == 1))
                            ins.then_inc(bank_ready, 1)

                @block.scalar
                def _(act):
                    for n in range(2 * B):
                        act.wait_ge(bank_ready, n + 1)
                        nc.scalar.activation(hid[0:KC, n % 2, n // 2, 0:S], k.ps[0:KC, n, 0:S], ACT.Silu,
                                             bias=b_down[:, n % 2:n % 2 + 1]).then_inc(act_done, 1)
                    act.wait_ge(act_done, 2 * B)

                @block.vector
                def _(dve):
                    V = nc.vector
                    step = Steps(dve, dve_done)
                    dve.wait_ge(loaded, 16 * N_LOADS)
                    step.start(V.tensor_tensor(g2_row[:, :], g_row[:, :], g_row[:, :], ALU.mult))
                    step(V.tensor_reduce(rowsum[:, :], state[:, :, :], AX.X, ALU.add))
                    step(V.tensor_scalar(rowsum[:, :], rowsum[:, :], 1.0 / HD, None, ALU.mult))
                    step(V.tensor_tensor(state[:, :, :], state[:, :, :], rowsum[:, :].unsqueeze(2).broadcast_to([HD + 1, NJ, HD]), ALU.subtract))

            with stage(nc, "kq_ready", "vl_ready", "k_copied", "q_copied", "eta_out", "t_done", "dve_done") as                     (block, kq_ready, vl_ready, k_copied, q_copied, eta_out, t_done, dve_done):
                @block.tensor
                def _(pe):
                    for j in range(NJ):
                        b, h = j // NH0, j % NH0
                        for bank, lo, hi, ready, free in ((j % 2, 0, 2 * HD, kq_ready, q_copied), (2 + j % 2, 2 * HD, 3 * HD + 1, vl_ready, t_done)):
                            if j >= 2:
                                pe.wait_ge(free, j - 1)
                            for kc in range(2):
                                kk = KC + kc
                                ins = nc.tensor.matmul(k.ps[0:hi - lo, bank, 0:S], w_row[0:kk, kc, h, lo:hi], hid[0:kk, kc, b, :],
                                                       start=(kc == 0), stop=(kc == 1))
                            ins.then_inc(ready, 1)

                @block.scalar
                def _(act):
                    for j in range(NJ):
                        act.wait_ge(kq_ready, j + 1)
                        nc.scalar.copy(cols[0:HD, 0, j, 0:S], k.ps[0:HD, j % 2, 0:S]).then_inc(k_copied, 1)
                        nc.scalar.copy(cols[0:HD, 1, j, 0:S], k.ps[HD:2 * HD, j % 2, 0:S]).then_inc(q_copied, 1)
                        act.wait_ge(vl_ready, j + 1)
                        nc.scalar.activation(cols[HD:HD + 1, 2, j, 0:S], k.ps[HD:HD + 1, 2 + j % 2, 0:S], ACT.Sigmoid).then_inc(eta_out, 1)
                    act.wait_ge(q_copied, NJ)

                @block.vector
                def _(dve):
                    V = nc.vector
                    step = Steps(dve, dve_done)
                    for j in range(NJ):
                        x = cols[0:HD, 2, j, 0:S]
                        dve.wait_ge(k_copied, j + 1)
                        dve.wait_ge(eta_out, j + 1)
                        step(V.scalar_tensor_tensor(x, k.ps[0:HD, 2 + j % 2, 0:S], -1.0, cols[0:HD, 0, j, 0:S], ALU.mult, ALU.add))
                        V.tensor_scalar(x, x, b_col[:, j % NH0:j % NH0 + 1], g_col[:, j % NH0:j % NH0 + 1], ALU.add, ALU.mult).then_inc(t_done, 1)
                    dve.wait_ge(t_done, NJ)
                    step(V.tensor_scalar(cols[HD:HD + 1, 2, :, 0:S], cols[HD:HD + 1, 2, :, 0:S], 1.0 / HD, None, ALU.mult))

        def grams(p, mm, gram_ready):
            mm(gram_b[0:RJ, 0:2 * RJ], flat(kt[p][:, 0, :, :]), kt[p][:, 0:2, :, :].rearrange("p w j t -> p (w j t)"), start=True, stop=True
               ).then_inc(gram_ready, 1)

        def to_row_order(p, mm, rows_ready):
            for n, right in enumerate((k.ident[0:HD + 1, 0:HD + 1], k.ident[0:HD + 1, 0:HD + 1], centre[:, :])):
                at = n * (HD + 1)
                ins = mm(rows_b[0:RJ, at:at + HD + 1 + (n == 2)], flat(kt[p][:, n, :, :]), right, start=True, stop=True)
            ins.then_inc(rows_ready, 1)

        def masked_products(dst, which, mm, done, j):
            mm(dst, ktm[:, which, j, :], state[:, j, :], start=(j == 0), stop=(which == 0 and j == NJ - 1)).then_inc(done, 1)

        def mask(V, dst, src, p, m):
            return V.scalar_tensor_tensor(dst[:, :], src, eta[p], m[:, :], ALU.mult, ALU.mult)

        with stage(nc, "picked", "gram_ready", "rows_ready", "rows_out", "base_mm", "zq_set", "dve_done") as                 (block, picked, gram_ready, rows_ready, rows_out, base_mm, zq_set, dve_done):
            @block.gpsimd
            def _(pool):
                for n in range(3):
                    nc.gpsimd.tensor_copy(kt[0][:, n, :, :], cols[:, n, :, 0:C]).then_inc(picked, 1)
                pool.wait_ge(picked, 3)
                nc.gpsimd.tensor_copy(own(0), kt[0][:, 0, :, :]).then_inc(picked, 1)
                pool.wait_ge(picked, 4)

            @block.tensor
            def _(pe):
                mm = nc.tensor.matmul
                pe.wait_ge(picked, 4)
                grams(0, mm, gram_ready)
                to_row_order(0, mm, rows_ready)
                for j in range(NJ):
                    masked_products(base, 0, mm, base_mm, j)
                mm(zq_b[0:RJ, 0:HD], inner_q[1][:, :], gd[:, :], start=True, stop=False).then_inc(zq_set, 1)
                pe.wait_ge(zq_set, 1)

            @block.scalar
            def _(act):
                act.wait_ge(rows_ready, 1)
                nc.scalar.copy(rows[0][:, :], rows_b[0:RJ, 0:3 * (HD + 1) + 1]).then_inc(rows_out, 1)
                act.wait_ge(rows_out, 1)

            @block.vector
            def _(dve):
                V = nc.vector
                step = Steps(dve, dve_done)
                step.start(V.memset(zs[:, 0:1], (HD * TTT_EPS) ** 0.5))
                dve.wait_ge(base_mm, NJ)
                step.start(V.tensor_copy(z0[0][:, :], base))
                step.start(V.tensor_scalar(z, base, 1.0, 0.0, ALU.mult, ALU.add, accum_out=zsum[:, :]))
                dve.wait_ge(rows_out, 1)
                dve.wait_ge(gram_ready, 1)
                step.start(mask(V, inner[0], gram_b[0:RJ, 0:RJ], 0, before))
                step.start(mask(V, inner_q[0], gram_b[0:RJ, RJ:2 * RJ], 0, upto))
                step.wait()

        def store_rows(sp, first_row, stored):
            for b in range(B):
                dst = out_d[b, bass.ds(first_row, C), :].rearrange("t (h e) -> h t e", h=NH0)
                for h in range(NH0):
                    j = b * NH0 + h
                    sp.dma_start(dst[h], outr[j * C:(j + 1) * C, :]).then_inc(stored, 16)

        def chunks(first_token):
            with stage(nc, "mm_ready", "z_ready", "v_ready", "std_ready", "r2_ready", "pz_ready", "mean_ready", "lhs_ready", "zr_ready", "dve_done", "g_ready",
                       "gd_ready", "ge_ready", "picked", "spread", "zq_ready", "zq_var", "zq_rstd", "out_ready", "stored", "state_mm", "state_ready",
                       "k_masked", "q_masked", "gram_ready", "rows_ready", "rows_out", "inner_ready", "base_mm", "base_out", "zq_base", "warmed") as \
                    (block, mm_ready, z_ready, v_ready, std_ready, r2_ready, pz_ready, mean_ready, lhs_ready, zr_ready, dve_done, g_ready,
                     gd_ready, ge_ready, picked, spread, zq_ready, zq_var, zq_rstd, out_ready, stored, state_mm, state_ready,
                     k_masked, q_masked, gram_ready, rows_ready, rows_out, inner_ready, base_mm, base_out, zq_base, warmed):
                sweeps = [(c * C + i, c, i) for c in range(PASS) for i in range(C)]

                @block.sync
                def _(sp):
                    for c in range(PASS):
                        sp.wait_ge(out_ready, c + 1)
                        store_rows(sp, first_token + c * C, stored)
                    sp.wait_ge(stored, PASS * 16 * NJ)

                @block.gpsimd
                def _(pool):
                    G = nc.gpsimd
                    for m, c, i in sweeps:
                        p, n = c % 2, 1 - c % 2
                        if m:
                            pool.wait_ge(z_ready, m)
                        G.tensor_tensor(pz[:, 0:HD], z, g2_row[:, :], ALU.mult).then_inc(pz_ready, 1)
                        if i < 3:
                            if i == 0 and c:
                                pool.wait_ge(ge_ready, c)
                                pool.wait_ge(state_mm, 2 * c)
                            js = slice(2 * i, 2 * i + 2)
                            G.tensor_tensor(eg[:, js, :], ge[:, :].unsqueeze(1).broadcast_to([RJ, 2, HD]),
                                            member[:, js].unsqueeze(2).broadcast_to([RJ, 2, HD]), ALU.mult).then_inc(spread, 1)
                        elif i < 6:
                            if i == 3 and c:
                                pool.wait_ge(q_masked, c)
                                pool.wait_ge(rows_ready, c)
                                pool.wait_ge(gram_ready, 2 * c)
                            which = i - 3
                            G.tensor_copy(kt[n][:, which, :, :], cols[:, which, :, bass.ds(first_token + (c + 1) * C, C)]).then_inc(picked, 1)
                        elif i == 7:
                            pool.wait_ge(zq_var, c + 1)
                            G.tensor_tensor(rq[:, :], mv[:, 1:2], k.neg_half[0:RJ, 0:1], ALU.pow).then_inc(zq_rstd, 1)

                @block.tensor
                def _(pe):
                    mm = nc.tensor.matmul
                    for m, c, i in sweeps:
                        p, n = c % 2, 1 - c % 2
                        if i == 0:
                            if c:
                                pe.wait_ge(gd_ready, c)
                            mm(zq_b[0:RJ, 0:HD], inner_q[n][:, :], gd[:, :], start=False, stop=True).then_inc(zq_ready, 1)
                        elif i in (4, 5):
                            half = i - 4
                            pe.wait_ge(spread, 3 * (c + 1))
                            mm(state_b[0:HD + 1, half * 3 * HD:(half + 1) * 3 * HD], k_1[n],
                               eg[:, 3 * half:3 * half + 3, :].rearrange("p j e -> p (j e)"), start=True, stop=True).then_inc(state_mm, 1)
                        elif i == 6:
                            pe.wait_ge(picked, 3 * (c + 1))
                            if c:
                                pe.wait_ge(inner_ready, 3 * c)
                            grams(n, mm, gram_ready)
                        elif i == 7:
                            mm(gram_b[0:RJ, 2 * RJ:3 * RJ], flat(kt[p][:, 0, :, :]), flat(kt[n][:, 0, :, :]), start=True, stop=True
                               ).then_inc(gram_ready, 1)
                        elif i == 8:
                            if c:
                                pe.wait_ge(rows_out, c)
                            to_row_order(n, mm, rows_ready)
                        if 7 <= i < 7 + NJ:
                            if i == 7:
                                pe.wait_ge(state_ready, 2 * (c + 1))
                                pe.wait_ge(k_masked, c + 1)
                                if c:
                                    pe.wait_ge(base_out, c)
                            masked_products(base, 0, mm, base_mm, i - 7)
                        elif 13 <= i < 13 + NJ:
                            if i == 13:
                                pe.wait_ge(out_ready, c + 1)
                                pe.wait_ge(q_masked, c + 1)
                            masked_products(zq_b[0:RJ, 0:HD], 1, mm, zq_base, i - 13)
                        pe.wait_ge(lhs_ready, m + 1)
                        pe.wait_ge(g_ready, m + 1)
                        mm(z_bank, lhs[:, :], gh[:, :], start=True, stop=True).then_inc(mm_ready, 1)
                    pe.wait_ge(zq_base, PASS * NJ)

                @block.scalar
                def _(act):
                    nc.scalar.activation(std[:, :], k.ones[0:RJ, 0:1], ACT.Sqrt).then_inc(warmed, 1)
                    act.wait_ge(warmed, 1)
                    for m, c, i in sweeps:
                        p, n = c % 2, 1 - c % 2
                        if m:
                            act.wait_ge(z_ready, m)
                        nc.scalar.activation(junk_a[:, :], zs[:, 0:HD + 1], ACT.Square, scale=HD ** -0.5, accum_out=v[:, :]).then_inc(v_ready, 1)
                        nc.scalar.activation(z_mean, zsum[:, :], ACT.Copy, scale=-1.0 / HD).then_inc(mean_ready, 1)
                        act.wait_ge(v_ready, m + 1)
                        nc.scalar.activation(std[:, :], v[:, :], ACT.Sqrt).then_inc(std_ready, 1)
                        act.wait_ge(mean_ready, m + 1)
                        act.wait_ge(r2_ready, m + 1)
                        nc.scalar.activation(zr[:, :], zs[:, 1:HD + 2], ACT.Copy, scale=r2[:, :]).then_inc(zr_ready, 1)
                        if i == C - 1:
                            act.wait_ge(inner_ready, 3 * (c + 1))
                        nc.scalar.activation(lhs[:, :], (inner_x if i == C - 1 else inner[p])[:, :], ACT.Copy, scale=r2[:, :]).then_inc(lhs_ready, 1)
                        if i == 11:
                            act.wait_ge(rows_ready, c + 1)
                            act.wait_ge(out_ready, c + 1)
                            act.wait_ge(state_mm, 2 * (c + 1))
                            nc.scalar.copy(rows[n][:, :], rows_b[0:RJ, 0:3 * (HD + 1) + 1]).then_inc(rows_out, 1)
                        elif i == 3:
                            if c:
                                act.wait_ge(zq_base, NJ * c)
                            nc.scalar.copy(own(1), kt[p][:, 1, :, :]).then_inc(q_masked, 1)
                        elif i == 6:
                            act.wait_ge(picked, 3 * (c + 1))
                            if c:
                                act.wait_ge(base_mm, NJ * c)
                            nc.scalar.copy(own(0), kt[n][:, 0, :, :]).then_inc(k_masked, 1)

                @block.vector
                def _(dve):
                    V = nc.vector
                    step = Steps(dve, dve_done)
                    for m, c, i in sweeps:
                        p, n = c % 2, 1 - c % 2
                        step.start(V.tensor_tensor_reduce(junk[0][:, :], z, g2_row[:, :], -1.0 / HD, 0.0, ALU.mult, ALU.add, pz[:, HD:HD + 1]))
                        step.start(V.tensor_tensor_reduce(junk[1][:, :], z, target[p][:, 0:HD], -1.0 / HD, 0.0, ALU.mult, ALU.add, a1[:, :]))
                        dve.wait_ge(v_ready, m + 1)
                        V.reciprocal(r2[:, :], v[:, :]).then_inc(r2_ready, 1)
                        dve.wait_ge(pz_ready, m + 1)
                        step.start(V.tensor_tensor_reduce(junk[2][:, :], z, pz[:, 0:HD], -1.0 / HD, 0.0, ALU.mult, ALU.add, a2[:, :]))
                        a2_done = step.n
                        dve.wait_ge(std_ready, m + 1)
                        dve.wait_ge(dve_done, a2_done - 1)
                        step.start(V.scalar_tensor_tensor(q_[:, :], target[p], std[:, :], pz[:, :], ALU.mult, ALU.add))
                        dve.wait_ge(dve_done, a2_done)
                        step(V.scalar_tensor_tensor(w[:, :], a1[:, :], std[:, :], a2[:, :], ALU.mult, ALU.add))
                        dve.wait_ge(zr_ready, m + 1)
                        V.scalar_tensor_tensor(gh[:, :], zr[:, :], w[:, :], q_[:, :], ALU.mult, ALU.add).then_inc(g_ready, 1)
                        if i == 0:
                            step(V.tensor_copy(z0[p][:, :], z))
                        elif i == 1:
                            dve.wait_ge(zq_ready, c + 1)
                            step(V.bn_stats(st6[:, :], zq_b[0:RJ, 0:HD]))
                        elif i == 2:
                            step(V.bn_aggr(mv[:, :], st6[:, :]))
                        elif i == 3:
                            V.tensor_scalar(mv[:, 1:2], mv[:, 1:2], TTT_EPS, None, ALU.add).then_inc(zq_var, 1)
                        elif i in (5, 6):
                            half = i - 5
                            dve.wait_ge(state_mm, 2 * (c + 1))
                            if c and half == 0:
                                dve.wait_ge(zq_base, NJ * c)
                                dve.wait_ge(base_mm, NJ * c)
                            part = state[:, 3 * half:3 * half + 3, :]
                            V.tensor_tensor(part, part, state_b[0:HD + 1, half * 3 * HD:(half + 1) * 3 * HD].rearrange("p (j e) -> p j e", j=3),
                                            ALU.add).then_inc(state_ready, 1)
                        elif i == 7:
                            dve.wait_ge(zq_rstd, c + 1)
                            step(V.tensor_scalar(y[:, :], zq_b[0:RJ, 0:HD], mv[:, 0:1], rq[:, 0:1], ALU.subtract, ALU.mult))
                        elif i == 8:
                            step(V.tensor_tensor(y[:, :], y[:, :], g_row[:, :], ALU.mult))
                        elif i == 9:
                            step(V.tensor_tensor(y[:, :], y[:, :], b_row[:, :], ALU.add))
                        elif i == 10:
                            if c:
                                dve.wait_ge(stored, 16 * NJ * c)
                            V.tensor_tensor(outr[:, :], y[:, :], q_row[n], ALU.add).then_inc(out_ready, 1)
                        elif i in (12, 13, 14):
                            dve.wait_ge(rows_out, c + 1)
                            dve.wait_ge(gram_ready, 2 * (c + 1))
                            if i == 12:
                                mask(V, inner[n], gram_b[0:RJ, 0:RJ], n, before).then_inc(inner_ready, 1)
                            elif i == 13:
                                mask(V, inner_q[n], gram_b[0:RJ, RJ:2 * RJ], n, upto).then_inc(inner_ready, 1)
                            else:
                                if c:
                                    dve.wait_ge(lhs_ready, C * c)
                                mask(V, inner_x, gram_b[0:RJ, 2 * RJ:3 * RJ], p, same).then_inc(inner_ready, 1)
                        elif i == 15:
                            dve.wait_ge(base_mm, NJ * (c + 1))
                            V.tensor_copy(z0[n][:, :], base).then_inc(base_out, 1)
                        elif i == C - 1:
                            dve.wait_ge(zq_ready, c + 1)
                            dve.wait_ge(spread, 3 * (c + 1))
                            dve.wait_ge(g_ready, m + 1)
                            V.tensor_scalar(gd[:, :], gh[:, 0:HD], gh[:, HD:HD + 1], r2[:, :], ALU.add, ALU.mult).then_inc(gd_ready, 1)
                            dve.wait_ge(gd_ready, c + 1)
                            V.tensor_scalar(ge[:, :], gd[:, :], eta[p], None, ALU.mult).then_inc(ge_ready, 1)
                            dve.wait_ge(base_out, c + 1)
                        dve.wait_ge(mm_ready, m + 1)
                        V.scalar_tensor_tensor(z, z_bank[:, 0:HD], z_bank[:, HD:HD + 1], z0[n if i == C - 1 else p][:, :], ALU.add, ALU.add, accum_out=zsum[:, :]
                                               ).then_inc(z_ready, 1)
                        dve.wait_ge(z_ready, m + 1)
                    dve.wait_ge(ge_ready, PASS)

        with nc.Fori(0, NCH // PASS) as i:
            chunks(i * (PASS * C))

        with stage(nc, "zq_ready", "zq_var", "zq_rstd", "dve_done", "out_ready", "stored", "back") as \
                (block, zq_ready, zq_var, zq_rstd, dve_done, out_ready, stored, back):
            @block.tensor
            def _(pe):
                nc.tensor.matmul(zq_b[0:RJ, 0:HD], inner_q[1][:, :], gd[:, :], start=False, stop=True).then_inc(zq_ready, 1)

            @block.gpsimd
            def _(pool):
                pool.wait_ge(zq_var, 1)
                nc.gpsimd.tensor_tensor(rq[:, :], mv[:, 1:2], k.neg_half[0:RJ, 0:1], ALU.pow).then_inc(zq_rstd, 1)

            @block.vector
            def _(dve):
                V = nc.vector
                step = Steps(dve, dve_done)
                dve.wait_ge(zq_ready, 1)
                step(V.bn_stats(st6[:, :], zq_b[0:RJ, 0:HD]))
                step(V.bn_aggr(mv[:, :], st6[:, :]))
                V.tensor_scalar(mv[:, 1:2], mv[:, 1:2], TTT_EPS, None, ALU.add).then_inc(zq_var, 1)
                dve.wait_ge(zq_rstd, 1)
                step(V.tensor_scalar(y[:, :], zq_b[0:RJ, 0:HD], mv[:, 0:1], rq[:, 0:1], ALU.subtract, ALU.mult))
                step(V.tensor_tensor(y[:, :], y[:, :], g_row[:, :], ALU.mult))
                step(V.tensor_tensor(y[:, :], y[:, :], b_row[:, :], ALU.add))
                V.tensor_tensor(outr[:, :], y[:, :], q_row[1], ALU.add).then_inc(out_ready, 1)

            @block.sync
            def _(sp):
                sp.wait_ge(out_ready, 1)
                store_rows(sp, NCH * C, stored)
                sp.wait_ge(stored, 16 * NJ)
                for b in range(B):
                    sp.dma_start(k.xn[:, b * TPB:(b + 1) * TPB, :], out_d[b, C:C + S, :].rearrange("(j p) d -> p j d", p=R)).then_inc(back, 16)
                sp.wait_ge(back, 16 * B)
        normalise(nc, k, k.xn, k.xn, 1e-6, post[:, 0, :], post[:, 1, :])
        to_columns(nc, k, k.xn, k.xt)
        project(nc, k, w_out, dst=k.xn)
        normalise(nc, k, k.xn, k.xn, 1e-6, post[:, 2, :], post[:, 3, :])
        to_columns(nc, k, k.xn, k.xt)
        project(nc, k, w_up, add_to=k.h)


GROUP = 4


class Experts:

    def __init__(self, name, n, f1, hid, w1, b1, w2):
        self.name, self.n, self.f1, self.hid, self.w1, self.b1, self.w2 = name, n, f1, hid, w1, b1, w2
        self.hc = hid // 128
        self.loads = 2 + (b1 is not None)


FFN = [Experts("swiglu", 16, 768, 384, "L0_ffn_mlp1_w", "L0_ffn_mlp1_b", "L0_ffn_mlp2_w"),
       Experts("gelu", 4, 768, 768, "L1_ffn_W1", "L1_ffn_b1", "L1_ffn_W2"),
       Experts("silu", 8, 1024, 512, "L2_ffn_W1", None, "L2_ffn_W2"),
       Experts("gelu_norm", 16, 384, 384, "L3_ffn_fc1_w", "L3_ffn_fc1_b", "L3_ffn_fc2_w")]


def weight_buffers(k):
    k.w1 = [k.sb(f"w1_{n}", [KC + 1, 2, 1024]) for n in range(GROUP)]
    k.w2 = [k.sb(f"w2_{n}", [128, 6, D]) for n in range(GROUP)]
    k.gate = k.sb("gate", [R, NT, 16])
    k.w_in = [k.ctx.enter_context(k.nc.semaphore(f"w_in{n}")) for n in range(GROUP)]


def load_expert(eng, k, a, ffn, n, e):
    eng.dma_start(k.w1[n][0:KC, :, 0:ffn.f1], a[ffn.w1][bass.ds(e, 1)].rearrange("o (c p) f -> p (o c) f", p=KC)).then_inc(k.w_in[n], 16)
    if ffn.b1 is not None:
        eng.dma_start(k.w1[n][KC:KC + 1, 1, 0:ffn.f1], a[ffn.b1][bass.ds(e, 1), :]).then_inc(k.w_in[n], 16)
    eng.dma_start(k.w2[n][:, 0:ffn.hc, :], a[ffn.w2][bass.ds(e, 1)].rearrange("o (c p) d -> p (o c) d", p=128)).then_inc(k.w_in[n], 16)


def first_experts(nc, k, a):
    with nc.Block(no_gpsimd_drain=True) as block:
        @block.sync
        def _(sp):
            for n in range(GROUP):
                load_expert(sp, k, a, FFN[0], n, n)


def router(nc, k, a, kind, n_exp, w_name, b_name, top):
    P = f"L{kind}_"
    PAD, TAKEN, NEVER = -1.0e38, -3.0e38, 3.0e38
    with ExitStack() as c:
        gw = k.sb(P + "gw", [KC + 1, 2, n_exp], F32, c)
        lg = k.sb(P + "lg", [R, NT, 16], F32, c)
        top8 = k.sb(P + "top8", [R, NT, 8], F32, c)
        best = k.sb(P + "best", [R, NT, 8], F32, c)
        mr = k.sb(P + "mr", [R, NT, 16], F32, c)
        mask = k.sb(P + "mask", [R, NT, 16], F32, c)
        mask0 = k.sb(P + "mask0", [R, NT, 16], F32, c)
        ex = k.sb(P + "ex", [R, NT, 16], F32, c)
        tot = k.sb(P + "tot", [R, NT], F32, c)
        wk = k.sb(P + "wk", [R, NT, 2], F32, c)
        pos = k.sb(P + "pos", [R, NT, 2, 8], F32, c)
        both = k.sb(P + "both", [R, NT, 2, 8], F32, c)
        tri = k.sb(P + "tri", [R, R], F32, c)
        capacity = int(1.2 * B * S / 8)
        with stage(nc, P + "gw_in", P + "logits", P + "dve_done", P + "act_in", P + "act_out", P + "onehot", P + "counted", P + "tri_ready") as \
                (block, gw_in, logits, dve_done, act_in, act_out, onehot, counted, tri_ready):
            n_loads = 2 if b_name else 1

            @block.sync
            def _(sp):
                sp.dma_start(gw[0:KC, :, :], a[w_name].rearrange("(c p) e -> p c e", p=KC)).then_inc(gw_in, 16)
                if b_name:
                    sp.dma_start(gw[KC:KC + 1, 1, :], a[b_name].unsqueeze(0)).then_inc(gw_in, 16)

            @block.gpsimd
            def _(pool):
                if kind == 2:
                    nc.gpsimd.memset(tri[:, :], 1.0).then_inc(tri_ready, 1)
                    pool.wait_ge(tri_ready, 1)
                    nc.gpsimd.affine_select(out=tri[:, :], in_=tri[:, :], compare_op=ALU.is_ge, fill=0.0, base=0,
                                            pattern=[[1, R]], channel_multiplier=-1).then_inc(tri_ready, 1)

            @block.tensor
            def _(pe):
                pe.wait_ge(gw_in, 16 * n_loads)
                kk = KC + (b_name is not None)
                for t in range(NT):
                    own = k.ps[0:R, 0, t * n_exp:(t + 1) * n_exp]
                    nc.tensor.matmul(own, k.xt[0:KC, 0, t * R:(t + 1) * R], gw[0:KC, 0, :], start=True, stop=False)
                    ins = nc.tensor.matmul(own, k.xt[0:kk, 1, t * R:(t + 1) * R], gw[0:kk, 1, :], start=False, stop=True)
                ins.then_inc(logits, 1)
                if kind == 2:
                    pe.wait_ge(tri_ready, 2)
                    pe.wait_ge(onehot, 1)
                    for t in range(NT):
                        for s in range(t + 1):
                            ins = nc.tensor.matmul(k.ps[0:R, 1, t * 16:(t + 1) * 16], tri[:, :] if s == t else k.ones[0:R, 0:R],
                                                   both[:, s, :, :].rearrange("p k e -> p (k e)"), start=(s == 0), stop=(s == t))
                    ins.then_inc(counted, 1)

            @block.scalar
            def _(act):
                if kind == 0 or kind == 3:
                    act.wait_ge(act_in, 1)
                    nc.scalar.activation(ex[:, :, :], lg[:, :, :], ACT.Exp).then_inc(act_out, 1)
                if kind == 2:
                    act.wait_ge(act_in, 1)
                    nc.scalar.activation(wk[:, :, 1], wk[:, :, 0], ACT.Exp).then_inc(act_out, 1)

            @block.vector
            def _(dve):
                V = nc.vector
                step = Steps(dve, dve_done)

                def choose(values, n, out):
                    for t in range(NT):
                        step.start(V.max(top8[:, t, :], values[:, t, :]))
                    step.wait()
                    step(V.tensor_copy(best[:, :, :], top8[:, :, :]))
                    step(V.memset(best[:, :, n:8], NEVER))
                    for t in range(NT):
                        step(V.match_replace(mr[:, t, :], best[:, t, :], values[:, t, :], TAKEN))
                    step(V.tensor_scalar(out[:, :, :], mr[:, :, :], 2.0 * PAD, None, ALU.is_lt))

                step(V.memset(lg[:, :, :], PAD))
                dve.wait_ge(logits, 1)
                step(V.tensor_copy(lg[:, :, 0:n_exp], k.ps[0:R, 0, 0:NT * n_exp].rearrange("p (t e) -> p t e", t=NT)))
                if kind == 0:
                    choose(lg, top, mask)
                    V.tensor_tensor(lg[:, :, :], lg[:, :, :], top8[:, :, 0:1].broadcast_to([R, NT, 16]), ALU.subtract).then_inc(act_in, 1)
                    dve.wait_ge(act_out, 1)
                    step(V.tensor_tensor(ex[:, :, :], ex[:, :, :], mask[:, :, :], ALU.mult))
                    step(V.tensor_reduce(tot[:, :], ex[:, :, :], AX.X, ALU.add))
                    step(V.reciprocal(tot[:, :], tot[:, :]))
                    step(V.tensor_tensor(k.gate[:, :, :], ex[:, :, :], tot[:, :].unsqueeze(2).broadcast_to([R, NT, 16]), ALU.mult))
                elif kind == 1:
                    choose(lg, top, k.gate)
                elif kind == 2:
                    choose(lg, 2, mask)
                    choose(lg, 1, mask0)
                    step.start(V.tensor_copy(both[:, :, 0, :], mask0[:, :, 0:8]))
                    V.tensor_tensor(both[:, :, 1, :], mask[:, :, 0:8], mask0[:, :, 0:8], ALU.subtract).then_inc(onehot, 1)
                    V.tensor_tensor(wk[:, :, 0], top8[:, :, 1], top8[:, :, 0], ALU.subtract).then_inc(act_in, 1)
                    dve.wait_ge(act_out, 1)
                    step(V.tensor_scalar(tot[:, :], wk[:, :, 1], 1.0, None, ALU.add))
                    step(V.reciprocal(wk[:, :, 0], tot[:, :]))
                    step(V.tensor_tensor(wk[:, :, 1], wk[:, :, 1], wk[:, :, 0], ALU.mult))
                    dve.wait_ge(counted, 1)
                    step(V.tensor_scalar(pos[:, :, :, :], k.ps[0:R, 1, 0:NT * 16].rearrange("p (t k e) -> p t k e", t=NT, k=2),
                                         float(capacity), None, ALU.is_le))
                    dve.wait_ge(onehot, 1)
                    step(V.tensor_tensor(pos[:, :, :, :], pos[:, :, :, :], both[:, :, :, :], ALU.mult))
                    step(V.tensor_tensor(pos[:, :, :, :], pos[:, :, :, :], wk[:, :, :].unsqueeze(3).broadcast_to([R, NT, 2, 8]), ALU.mult))
                    step(V.tensor_tensor(k.gate[:, :, 0:8], pos[:, :, 0, :], pos[:, :, 1, :], ALU.add))
                else:
                    step(V.memset(lg[:, :, 0:1], -1.0e9))
                    step(V.tensor_reduce(tot[:, :], lg[:, :, :], AX.X, ALU.max))
                    V.tensor_tensor(lg[:, :, :], lg[:, :, :], tot[:, :].unsqueeze(2).broadcast_to([R, NT, 16]), ALU.subtract).then_inc(act_in, 1)
                    dve.wait_ge(act_out, 1)
                    step(V.tensor_reduce(tot[:, :], ex[:, :, :], AX.X, ALU.add))
                    step(V.reciprocal(tot[:, :], tot[:, :]))
                    step(V.tensor_tensor(ex[:, :, :], ex[:, :, :], tot[:, :].unsqueeze(2).broadcast_to([R, NT, 16]), ALU.mult))
                    choose(ex, top, mask)
                    step(V.tensor_tensor(k.gate[:, :, :], ex[:, :, :], mask[:, :, :], ALU.mult))
                    step(V.tensor_scalar(k.gate[:, :, 0:1], k.gate[:, :, 0:1], 1.0, None, ALU.add))


def run_experts(nc, k, a, ffn, following):
    with ExitStack() as c:
        hT = [k.sb(f"{ffn.name}_hT{n}", [128, ffn.hc, B * S], F32, c) for n in range(2)]
        ga = [k.sb(f"{ffn.name}_ga{n}", [128, S], F32, c) for n in range(2)]
        li = [k.sb(f"{ffn.name}_li{n}", [128, S], F32, c) for n in range(2)]
        sg = [k.sb(f"{ffn.name}_sg{n}", [128, S], F32, c) for n in range(2)]
        paired = ffn.name != "gelu"
        per = ffn.hc * B
        ring = 2 if paired else 4

        def group(first, last):
            with stage(nc, "unit_ready", "bank_free", "clipped", "gate_act", "dve_done", "unit_done", "y_ready", "y_added") as \
                    (block, unit_ready, bank_free, clipped, gate_act, dve_done, unit_done, y_ready, y_added):
                def units(n):
                    return [(n * per + m, m // B, m % B) for m in range(per)]

                def bank(u, which):
                    return k.ps[:, (u % ring) * (2 if paired else 1) + which, 0:S]

                @block.sync
                def _(sp):
                    for n in range(GROUP):
                        if last and following is None:
                            break
                        sp.wait_ge(y_added, NT * (n + 1))
                        sp.sem_clear(k.w_in[n])
                        if last:
                            load_expert(sp, k, a, following, n, n)
                        else:
                            load_expert(sp, k, a, ffn, n, first + (GROUP + n))

                @block.tensor
                def _(pe):
                    mm = nc.tensor.matmul

                    def up(n):
                        pe.wait_ge(k.w_in[n], 16 * ffn.loads)
                        kk = KC + (ffn.b1 is not None)
                        for u, j, b in units(n):
                            if u >= ring:
                                pe.wait_ge(bank_free if ffn.name == "swiglu" else unit_done, u - ring + 1)
                            for which in range(2 if paired else 1):
                                f = (j + which * ffn.hc) * 128
                                mm(bank(u, which), k.w1[n][0:KC, 0, f:f + 128], k.xt[0:KC, 0, b * S:(b + 1) * S], start=True, stop=False)
                                ins = mm(bank(u, which), k.w1[n][0:kk, 1, f:f + 128], k.xt[0:kk, 1, b * S:(b + 1) * S], start=False, stop=True)
                            ins.then_inc(unit_ready, 1)

                    def down(n):
                        pe.wait_ge(unit_done, per * (n + 1))
                        for t in range(NT):
                            m = NT * n + t
                            if m >= 3:
                                pe.wait_ge(y_added, m - 2)
                            for j in range(ffn.hc):
                                ins = mm(k.ps[0:R, 4 + m % 3, 0:D], hT[n % 2][:, j, t * R:(t + 1) * R], k.w2[n][:, j, :],
                                         start=(j == 0), stop=(j == ffn.hc - 1))
                            ins.then_inc(y_ready, 1)

                    up(0)
                    for n in range(GROUP):
                        if n + 1 < GROUP:
                            up(n + 1)
                        down(n)

                @block.scalar
                def _(act):
                    for n in range(GROUP):
                        for u, j, b in units(n):
                            if ffn.name == "swiglu":
                                act.wait_ge(clipped, u + 1)
                                nc.scalar.activation(sg[u % 2][:, :], ga[u % 2][:, :], ACT.Sigmoid, scale=1.702).then_inc(gate_act, 1)
                            elif ffn.name == "silu":
                                act.wait_ge(unit_ready, u + 1)
                                if u >= 2:
                                    act.wait_ge(unit_done, u - 1)
                                nc.scalar.activation(sg[u % 2][:, :], bank(u, 1), ACT.Silu).then_inc(gate_act, 1)
                            else:
                                act.wait_ge(unit_ready, u + 1)
                                nc.scalar.activation(hT[n % 2][:, j, b * S:(b + 1) * S], bank(u, 0), ACT.Gelu).then_inc(unit_done, 1)

                @block.vector
                def _(dve):
                    V = nc.vector
                    step = Steps(dve, dve_done)

                    def add(n):
                        for t in range(NT):
                            dve.wait_ge(y_ready, NT * n + t + 1)
                            ins = V.scalar_tensor_tensor(k.h[:, t, :], k.ps[0:R, 4 + (NT * n + t) % 3, 0:D], k.gate[:, t, bass.ds(first + n, 1)],
                                                         k.h[:, t, :], ALU.mult, ALU.add)
                            ins.then_inc(y_added, 1)
                        dve.wait_ge(y_added, NT * (n + 1))

                    for n in range(GROUP):
                        for u, j, b in units(n):
                            out = hT[n % 2][:, j, b * S:(b + 1) * S]
                            if ffn.name == "swiglu":
                                dve.wait_ge(unit_ready, u + 1)
                                V.tensor_scalar(ga[u % 2][:, :], bank(u, 0), 7.0, None, ALU.min).then_inc(clipped, 1)
                                V.tensor_scalar(li[u % 2][:, :], bank(u, 1), 7.0, -7.0, ALU.min, ALU.max).then_inc(bank_free, 1)
                                dve.wait_ge(bank_free, u + 1)
                                step(V.scalar_tensor_tensor(li[u % 2][:, :], li[u % 2][:, :], 1.0, ga[u % 2][:, :], ALU.add, ALU.mult))
                                dve.wait_ge(gate_act, u + 1)
                                V.tensor_tensor(out, li[u % 2][:, :], sg[u % 2][:, :], ALU.mult).then_inc(unit_done, 1)
                            elif ffn.name == "silu":
                                dve.wait_ge(gate_act, u + 1)
                                V.tensor_tensor(out, bank(u, 0), sg[u % 2][:, :], ALU.mult).then_inc(unit_done, 1)
                        if n:
                            add(n - 1)
                    add(GROUP - 1)

        if ffn.n > GROUP:
            with nc.Fori(0, ffn.n // GROUP - 1) as g:
                group(g * GROUP, False)
        group(ffn.n - GROUP, True)


def gated_bias(nc, k, n_exp, b2):
    with ExitStack() as c:
        gt = k.sb(f"gate_t{n_exp}_{nc.next_id()}", [16, B * S], F32, c)
        with stage(nc, "turned", "copied", "tile_ready", "dve_done") as (block, turned, copied, tile_ready, dve_done):
            @block.tensor
            def _(pe):
                for t in range(NT):
                    ins = nc.tensor.transpose(k.ps[0:n_exp, t // 3, (t % 3) * R:(t % 3 + 1) * R], k.gate[:, t, 0:n_exp], k.ident[0:R, 0:R])
                    if t % 3 == 2:
                        ins.then_inc(turned, 1)
                for t in range(NT):
                    pe.wait_ge(copied, t // 3 + 1)
                    nc.tensor.matmul(k.ps[0:R, 2 + t, 0:D], gt[0:n_exp, t * R:(t + 1) * R], b2[0:n_exp, :], start=True, stop=True
                                     ).then_inc(tile_ready, 1)

            @block.vector
            def _(dve):
                for b in range(B):
                    dve.wait_ge(turned, b + 1)
                    nc.vector.tensor_copy(gt[0:n_exp, b * S:(b + 1) * S], k.ps[0:n_exp, b, 0:S]).then_inc(copied, 1)
                for t in range(NT):
                    dve.wait_ge(tile_ready, t + 1)
                    nc.vector.tensor_tensor(k.h[:, t, :], k.ps[0:R, 2 + t, 0:D], k.h[:, t, :], ALU.add).then_inc(dve_done, 1)
                dve.wait_ge(dve_done, NT)


def swiglu_layer(nc, k, a):
    normalise(nc, k, k.h, k.xn, 1e-5)
    with ExitStack() as c:
        scale = k.sb("rms_scale", [R, D], F32, c)
        t_ = k.sb("rms_t", [R, NT, D], F32, c)
        junk = k.sb("rms_junk", [R, NT, D], F32, c)
        ms = k.sb("rms_ms", [R, NT], F32, c)
        b2 = k.sb("swiglu_b2", [16, D], F32, c)
        with stage(nc, "loaded", "ms_ready", "rms_ready", "dve_done") as (block, loaded, ms_ready, rms_ready, dve_done):
            @block.sync
            def _(sp):
                sp.dma_start(scale[:, :], bcast(a["L0_ffn_norm_scale"], R)).then_inc(loaded, 16)
                sp.dma_start(b2[:, :], a["L0_ffn_mlp2_b"]).then_inc(loaded, 16)
                sp.wait_ge(loaded, 32)

            @block.gpsimd
            def _(pool):
                pool.wait_ge(ms_ready, NT)
                nc.gpsimd.tensor_tensor(k.rstd[:, :, 0], ms[:, :], k.neg_half[0:R, 0:NT], ALU.pow).then_inc(rms_ready, 1)

            @block.vector
            def _(dve):
                step = Steps(dve, dve_done)
                for t in range(NT):
                    nc.vector.tensor_tensor_reduce(junk[:, t, :], k.xn[:, t, :], k.xn[:, t, :], 1.0 / D, 1e-5, ALU.mult, ALU.add,
                                                   ms[:, t:t + 1]).then_inc(ms_ready, 1)
                step.start(nc.vector.tensor_tensor(k.h[:, :, :], k.h[:, :, :], k.xn[:, :, :], ALU.add))
                dve.wait_ge(rms_ready, 1)
                dve.wait_ge(loaded, 32)
                for t in range(NT):
                    step.start(nc.vector.scalar_tensor_tensor(t_[:, t, :], k.xn[:, t, :], k.rstd[:, t, 0:1], scale[:, :], ALU.mult, ALU.mult))
                step.wait()
        to_columns(nc, k, t_, k.xt)
        router(nc, k, a, 0, 16, "L0_ffn_gate_w", "L0_ffn_gate_b", 4)
        run_experts(nc, k, a, FFN[0], FFN[1])
        gated_bias(nc, k, 16, b2)


def gelu_layer(nc, k, a):
    normalise(nc, k, k.h, k.xn, 1e-5)
    to_columns(nc, k, k.xn, k.xt)
    with ExitStack() as c:
        b2 = k.sb("gelu_b2", [4, D], F32, c)
        with stage(nc, "loaded") as (block, loaded):
            @block.sync
            def _(sp):
                sp.dma_start(b2[:, :], a["L1_ffn_b2"]).then_inc(loaded, 16)
                sp.wait_ge(loaded, 16)
        router(nc, k, a, 1, 4, "L1_ffn_Wg", "L1_ffn_bg", 1)
        run_experts(nc, k, a, FFN[1], FFN[2])
        gated_bias(nc, k, 4, b2)


def silu_layer(nc, k, a):
    normalise(nc, k, k.h, k.xn, 1e-5)
    to_columns(nc, k, k.xn, k.xt)
    router(nc, k, a, 2, 8, "L2_ffn_Wg", None, 2)
    run_experts(nc, k, a, FFN[2], FFN[3])


def channel_attention(nc, k, a):
    normalise(nc, k, k.h, k.xn, 1e-5)
    to_columns(nc, k, k.xn, k.xt)
    with ExitStack() as c:
        w = k.sb("ca_w", [KC, 2, 3 * D], F32, c)
        wp = k.sb("ca_wp", [KC + 1, 2, D], F32, c)
        qkv = [k.sb("ca_" + n, [KC, 4, S], F32, c) for n in "qkv"]
        junk = k.sb("ca_junk", [KC, S], F32, c)
        tmp = k.sb("ca_tmp", [KC, 4, S], F32, c)
        sums = k.sb("ca_sums", [KC, 2, 4], F32, c)
        ssq = k.sb("ca_ssq", [KC, 2, 4], F32, c)
        coef = k.sb("ca_coef", [KC, 4], F32, c)
        prod = k.sb("ca_prod", [KC, 4], F32, c)
        with stage(nc, "loaded", "unit_ready", "act_done", "dve_done", "rnorm", "copied") as \
                (block, loaded, unit_ready, act_done, dve_done, rnorm, copied):
            parts = [(cb, i) for cb in range(4) for i in range(3)]

            @block.sync
            def _(sp):
                sp.dma_start(w[:, :, :], a["L1_attn_w_qkv"].rearrange("(c p) n -> p c n", p=KC)).then_inc(loaded, 16)
                sp.dma_start(wp[0:KC, :, :], a["L1_attn_w_proj"].rearrange("(c p) n -> p c n", p=KC)).then_inc(loaded, 16)
                sp.dma_start(wp[KC:KC + 1, 1, :], a["L1_attn_b_proj"].unsqueeze(0)).then_inc(loaded, 16)

            @block.tensor
            def _(pe):
                pe.wait_ge(loaded, 48)
                for cb in range(4):
                    m, b = cb // 2, cb % 2
                    for i in range(3):
                        bank = (cb % 2) * 3 + i
                        if cb >= 2:
                            if i < 2:
                                pe.wait_ge(act_done, 4 * (cb - 2) + 2 * i + 2)
                            else:
                                pe.wait_ge(copied, cb - 1)
                        for kc in range(2):
                            ins = nc.tensor.matmul(k.ps[0:KC, bank, 0:S], w[:, kc, i * D + m * KC:i * D + (m + 1) * KC],
                                                   k.xt[0:KC, kc, b * S:(b + 1) * S], start=(kc == 0), stop=(kc == 1))
                        ins.then_inc(unit_ready, 1)

            @block.scalar
            def _(act):
                for cb in range(4):
                    for i in range(2):
                        bank = k.ps[0:KC, (cb % 2) * 3 + i, 0:S]
                        act.wait_ge(unit_ready, 3 * cb + i + 1)
                        nc.scalar.activation(qkv[i][:, cb, :], bank, ACT.Copy, accum_out=sums[:, i, cb:cb + 1]).then_inc(act_done, 1)
                        n = 4 * cb + 2 * i
                        if n:
                            act.wait_ge(act_done, n)
                        nc.scalar.activation(junk[:, :], bank, ACT.Square, accum_out=ssq[:, i, cb:cb + 1]).then_inc(act_done, 1)

            @block.gpsimd
            def _(pool):
                pool.wait_ge(act_done, 16)
                nc.gpsimd.tensor_tensor(ssq[:, :, :].rearrange("p i c -> p (i c)"), ssq[:, :, :].rearrange("p i c -> p (i c)"),
                                        k.neg_half[0:KC, 0:8], ALU.pow).then_inc(rnorm, 1)

            @block.vector
            def _(dve):
                V = nc.vector
                step = Steps(dve, dve_done)
                for cb in range(4):
                    dve.wait_ge(unit_ready, 3 * cb + 3)
                    V.tensor_copy(qkv[2][:, cb, :], k.ps[0:KC, (cb % 2) * 3 + 2, 0:S]).then_inc(copied, 1)
                dve.wait_ge(copied, 4)
                dve.wait_ge(rnorm, 1)
                step(V.tensor_tensor(sums[:, :, :], sums[:, :, :], ssq[:, :, :], ALU.mult))
                step(V.tensor_tensor(prod[:, :], sums[:, 0, :], sums[:, 1, :], ALU.mult))
                step(V.tensor_scalar(prod[:, :], prod[:, :], float(S), None, ALU.add))
                step(V.reciprocal(prod[:, :], prod[:, :]))
                step(V.tensor_tensor(coef[:, :], prod[:, :], ssq[:, 0, :], ALU.mult))
                for cb in range(4):
                    step.start(V.scalar_tensor_tensor(tmp[:, cb, :], qkv[1][:, cb, :], ssq[:, 1, cb:cb + 1], qkv[0][:, cb, :], ALU.mult, ALU.mult))
                step.wait()
                for cb in range(4):
                    step.start(V.scalar_tensor_tensor(tmp[:, cb, :], qkv[1][:, cb, :], ssq[:, 1, cb:cb + 1], tmp[:, cb, :], ALU.mult, ALU.mult))
                step.wait()
                for cb in range(4):
                    step.start(V.scalar_tensor_tensor(k.xt[0:KC, cb // 2, (cb % 2) * S:(cb % 2 + 1) * S], qkv[2][:, cb, :],
                                                      coef[:, cb:cb + 1], tmp[:, cb, :], ALU.mult, ALU.mult))
                step.wait()
        project(nc, k, wp, add_to=k.h)


NHEAD, HW = 12, 16
HG = 3
NHG = NHEAD // HG
RP = R + 1
QMIN, QMAX = -128.0, 127.0
SHIFT = 112


def head_rows(h):
    return slice(32 * (h % 4), 32 * (h % 4) + HW), h // 4


def quantised_attention(nc, k, a):
    normalise(nc, k, k.h, k.xn, 1e-5)
    to_columns(nc, k, k.xn, k.xt)
    with ExitStack() as c:
        raw = k.sb("qa_raw", [KC, 2, 3 * D], F32, c)
        bias_raw = k.sb("qa_bias", [KC + 1, 3 * D], F32, c)
        praw = k.sb("qa_praw", [KC, 2, D], F32, c)
        wqk = k.sb("qa_wqk", [KC + 1, 2, 2, NHEAD, 32], F32, c)
        wv = k.sb("qa_wv", [KC + 1, 2, D], F32, c)
        wp = k.sb("qa_wp", [KC + 1, 2, D], F32, c)
        qk_t = k.sb("qa_qkt", [128, 2, B, 3, S], BF16, c)
        qk_b = k.sb("qa_qkb", [128, 2, 3, S], BF16, c)
        v_q = k.sb("qa_v", [R, NT, D], BF16, c)
        v_b = k.sb("qa_vb", [R, TPB, D], BF16, c)
        id16 = k.sb("qa_id", [128, 128], BF16, c)
        sc = k.sb("qa_scales", [128, 6], F32, c)
        inv = k.sb("qa_inv", [128, 6], F32, c)
        cc = k.sb("qa_cc", [128, 16], F32, c)
        rnd = k.sb("qa_round", [128, 1], F32, c)
        tmp = k.sb("qa_tmp", [128, 2, 3 * D], F32, c)
        W_S, A1, ATT, A2, WP_S, A3 = range(6)
        logit, negx0, invx0, off, half_b, c_rest, lowest, ctx_s = (cc[:, n:n + 1] for n in range(8))

        def floor(V, step, x):
            y = tmp[:, 0, 0:1]
            step(V.tensor_scalar(y, x, ROUND, ROUND, ALU.add, ALU.subtract))
            step(V.tensor_tensor(tmp[:, 0, 1:2], y, x, ALU.is_gt))
            step(V.tensor_tensor(x, y, tmp[:, 0, 1:2], ALU.subtract))

        with stage(nc, "loaded", "filled", "dve_done", "unit_ready", "act_done", "bank_free", "w_ready", "consts") as \
                (block, loaded, filled, dve_done, unit_ready, act_done, bank_free, w_ready, consts):
            @block.sync
            def _(sp):
                sp.dma_start(sc[:, :], bcast(a["qa_scales"], 128)).then_inc(loaded, 16)
                sp.dma_start(raw[:, :, :], a["L2_attn_qkv_w"].rearrange("(c p) n -> p c n", p=KC)).then_inc(loaded, 16)
                sp.dma_start(praw[:, :, :], a["L2_attn_proj_w"].rearrange("(c p) n -> p c n", p=KC)).then_inc(loaded, 16)
                sp.dma_start(bias_raw[KC:KC + 1, :], a["L2_attn_qkv_b"].unsqueeze(0)).then_inc(loaded, 16)
                sp.dma_start(wp[KC:KC + 1, 1, :], a["L2_attn_proj_b"].unsqueeze(0)).then_inc(loaded, 16)
                sp.dma_start(wv[KC:KC + 1, 1, :], a["L2_attn_qkv_b"][2 * D:3 * D].unsqueeze(0)).then_inc(loaded, 16)

            @block.gpsimd
            def _(pool):
                step = Steps(pool, filled)
                step(nc.gpsimd.memset(wqk[:, :, :, :, :], 0.0))
                step(nc.gpsimd.memset(rnd[:, :], ROUND))
                step(nc.gpsimd.tensor_copy(id16[:, :], k.ident[:, :]))

            units = [("qk", b, w, g) for b in range(B) for w in range(2) for g in range(3)] + [("v", t, 0, 0) for t in range(NT)]

            @block.tensor
            def _(pe):
                pe.wait_ge(w_ready, 1)
                for u, (kind, b, w, g) in enumerate(units):
                    if u >= 4:
                        pe.wait_ge(bank_free, u - 3)
                    for kc in range(2):
                        kk = KC + kc
                        if kind == "qk":
                            ins = nc.tensor.matmul(k.ps[:, u % 4, 0:S], wqk[0:kk, kc, w, 4 * g:4 * g + 4, :].rearrange("p h d -> p (h d)"),
                                                   k.xt[0:kk, kc, b * S:(b + 1) * S], start=(kc == 0), stop=(kc == 1))
                        else:
                            ins = nc.tensor.matmul(k.ps[0:R, u % 4, 0:D], k.xt[0:kk, kc, b * R:(b + 1) * R], wv[0:kk, kc, :],
                                                   start=(kc == 0), stop=(kc == 1))
                    ins.then_inc(unit_ready, 1)

            @block.vector
            def _(dve):
                V = nc.vector
                step = Steps(dve, dve_done)
                dve.wait_ge(loaded, 96)
                dve.wait_ge(filled, 3)
                step(V.reciprocal(inv[:, :], sc[:, :]))

                def fake_quant(x, s, parts):
                    step(V.tensor_scalar(x, x, inv[0:parts, s:s + 1], ROUND, ALU.mult, ALU.add))
                    step(V.tensor_scalar(x, x, ROUND + QMAX, ROUND + QMIN, ALU.min, ALU.max))

                fake_quant(raw[:, :, :], W_S, KC)
                fake_quant(praw[:, :, :], WP_S, KC)
                for kc in range(2):
                    step(V.tensor_scalar(wqk[0:KC, kc, :, :, 0:HW], raw[:, kc, 0:2 * D].rearrange("p (w h d) -> p w h d", w=2, d=HW),
                                         ROUND, sc[0:KC, W_S:W_S + 1], ALU.subtract, ALU.mult))
                step(V.tensor_scalar(wv[0:KC, :, :], raw[:, :, 2 * D:3 * D], ROUND, sc[0:KC, W_S:W_S + 1], ALU.subtract, ALU.mult))
                step(V.tensor_scalar(wp[0:KC, :, :], praw[:, :, :], ROUND, sc[0:KC, WP_S:WP_S + 1], ALU.subtract, ALU.mult))
                V.tensor_copy(wqk[KC:KC + 1, 1, :, :, 0:HW], bias_raw[KC:KC + 1, 0:2 * D].rearrange("p (w h d) -> p w h d", w=2, d=HW)
                              ).then_inc(w_ready, 1)
                step(V.tensor_tensor(logit, sc[:, A1:A1 + 1], sc[:, A1:A1 + 1], ALU.mult))
                step(V.tensor_scalar(logit, logit, inv[:, ATT:ATT + 1], HW ** -0.5, ALU.mult, ALU.mult))
                step(V.tensor_scalar(negx0, inv[:, ATT:ATT + 1], -0.6931, None, ALU.mult))
                floor(V, step, negx0)
                step(V.tensor_scalar(lowest, negx0, 30.0, None, ALU.mult))
                step(V.reciprocal(invx0, negx0))
                step(V.tensor_scalar(negx0, negx0, -1.0, None, ALU.mult))
                step(V.tensor_scalar(off, invx0, -0.5, -0.5, ALU.mult, ALU.add))
                step(V.tensor_scalar(half_b, inv[:, ATT:ATT + 1], 0.96963238 / 0.35815147, None, ALU.mult))
                floor(V, step, half_b)
                step(V.tensor_scalar(half_b, half_b, 0.5, None, ALU.mult))
                step(V.tensor_tensor(c_rest, inv[:, ATT:ATT + 1], inv[:, ATT:ATT + 1], ALU.mult))
                step(V.tensor_scalar(c_rest, c_rest, 1.0 / 0.35815147, None, ALU.mult))
                floor(V, step, c_rest)
                step(V.tensor_tensor(tmp[:, 0, 0:1], half_b, half_b, ALU.mult))
                step(V.tensor_tensor(c_rest, c_rest, tmp[:, 0, 0:1], ALU.subtract))
                step(V.tensor_tensor(ctx_s, sc[:, A1:A1 + 1], inv[:, A2:A2 + 1], ALU.mult))
                step(V.tensor_scalar(ctx_s, ctx_s, 2.0 ** (SHIFT - 1), None, ALU.mult))
                for u, (kind, b, w, g) in enumerate(units):
                    dve.wait_ge(unit_ready, u + 1)
                    rows, cols = (128, S) if kind == "qk" else (R, D)
                    t = tmp[0:rows, u % 2, 0:cols]
                    V.tensor_scalar(t, k.ps[0:rows, u % 4, 0:cols], inv[0:rows, A1:A1 + 1], ROUND, ALU.mult, ALU.add).then_inc(bank_free, 1)
                    dve.wait_ge(bank_free, u + 1)
                    step(V.tensor_scalar(t, t, ROUND + QMAX, ROUND + QMIN, ALU.min, ALU.max))
                    out = qk_t[:, w, b, g, :] if kind == "qk" else v_q[:, b, :]
                    step.start(V.tensor_scalar(out, t, ROUND, None, ALU.subtract))
                step.wait()

        t1 = [k.sb(f"qa_t1_{n}", [R, HG, S], F32, c) for n in range(2)]
        nn = [k.sb(f"qa_n_{n}", [R, HG, S], F32, c) for n in range(2)]
        qq = [k.sb(f"qa_q_{n}", [R, HG, S], F32, c) for n in range(2)]
        ee = [k.sb(f"qa_e_{n}", [R, HG, S], F32, c) for n in range(2)]
        hp = [k.sb(f"qa_hp_{n}", [R, HG, S], I32, c) for n in range(2)]
        pw = [k.sb(f"qa_pw_{n}", [R, HG, S], I32, c) for n in range(2)]
        rr = k.sb("qa_r", [R, HG, S], F32, c)
        ln_e = k.sb("qa_ln_e", [R, HG, S], F32, c)
        rho = k.sb("qa_rho", [R, HG, S], F32, c)
        dd = k.sb("qa_d", [R, HG, S], F32, c)
        ff = k.sb("qa_f", [R, HG, S], F32, c)
        mx = k.sb("qa_mx", [R, HG], F32, c)
        sm = [k.sb(f"qa_sm_{n}", [R, HG], F32, c) for n in range(2)]
        inv_sm = [k.sb(f"qa_inv_sm_{n}", [R, HG], F32, c) for n in range(2)]
        ln_sm = k.sb("qa_ln_sm", [R, HG], F32, c)
        pt = k.sb("qa_pt", [R, HG, TPB, RP], BF16, c)
        pt_ps = k.ps[0:R, 6, :].bitcast(BF16)[:, 0:HG * TPB * RP].rearrange("p (h m n) -> p h m n", h=HG, m=TPB)
        pp = [x[:, :, :].bitcast(BF16).rearrange("p h (m two) -> p h m two", two=2)[:, :, :, 1] for x in hp]

        def batch(first_tile, b):
            units = [(u, nt, g) for u, (nt, g) in enumerate((nt, g) for nt in range(TPB) for g in range(NHG))]
            U = len(units)
            with stage(nc, "picked", "scores", "scaled", "shifted", "divided", "dve_done", "r_ready", "squared", "e_ready", "ln_ready", "rho_ready",
                       "moved", "q_ready", "pw_ready", "rho_exact", "n_moved", "n_ready", "n_scaled", "p_ready", "turned", "pt_ready", "pv_done", "ctx_out") as \
                    (block, picked, scores, scaled, shifted, divided, dve_done, r_ready, squared, e_ready, ln_ready, rho_ready,
                     moved, q_ready, pw_ready, rho_exact, n_moved, n_ready, n_scaled, p_ready, turned, pt_ready, pv_done, ctx_out):
                @block.gpsimd
                def _(pool):
                    G = nc.gpsimd

                    def move(out, x, offset):
                        return G.tensor_scalar(out[:, :, :], x[:, :, :], 1.0, offset, ALU.mult, ALU.add)

                    def quotients(u):
                        q = qq[u % 2]
                        pool.wait_ge(divided, u + 1)
                        move(q, q, ROUND).then_inc(moved, 1)
                        pool.wait_ge(moved, u + 1)
                        move(q, q, -ROUND).then_inc(q_ready, 1)
                        pool.wait_ge(q_ready, u + 1)
                        if u >= 2:
                            pool.wait_ge(e_ready, HG * (u - 1))
                        G.tensor_scalar(pw[u % 2][:, :, :], q[:, :, :], -2.0 ** 23, 127.0 * 2.0 ** 23, ALU.mult, ALU.add).then_inc(pw_ready, 1)

                    quotients(0)
                    for v in range(U + 1):
                        if v + 1 < U:
                            quotients(v + 1)
                        if v:
                            pool.wait_ge(rho_exact, v)
                            move(dd, dd, ROUND).then_inc(n_moved, 1)
                            pool.wait_ge(n_moved, v)
                            move(dd, dd, -ROUND).then_inc(n_ready, 1)
                            pool.wait_ge(n_ready, v)
                            G.tensor_scalar(ff[:, :, :], dd[:, :, :], -4.0 / 3.0 * 2.0 ** SHIFT, 0.0, ALU.mult, ALU.add).then_inc(n_scaled, 1)

                @block.tensor
                def _(pe):
                    def score(u, nt, g):
                        if u >= 2:
                            pe.wait_ge(scaled, u - 1)
                        for i in range(HG):
                            rows, grp = head_rows(HG * g + i)
                            ins = nc.tensor.matmul(k.ps[0:R, (u % 2) * HG + i, 0:S], qk_b[rows, 0, grp, nt * R:(nt + 1) * R],
                                                   qk_b[rows, 1, grp, :], start=True, stop=True)
                        ins.then_inc(scores, 1)

                    def turn(u):
                        pe.wait_ge(p_ready, u + 1)
                        if u:
                            pe.wait_ge(pt_ready, u)
                        for i in range(HG):
                            for m in range(TPB):
                                ins = nc.tensor.transpose(pt_ps[:, i, m, 0:R], pp[u % 2][:, i, m * R:(m + 1) * R], id16[0:R, 0:R])
                        ins.then_inc(turned, 1)

                    def weigh(u, nt, g):
                        pe.wait_ge(pt_ready, u + 1)
                        if g == 0 and nt:
                            pe.wait_ge(ctx_out, nt)
                        for i in range(HG):
                            h = HG * g + i
                            for m in range(TPB):
                                ins = nc.tensor.matmul(k.ps[0:R, 7, h * HW:(h + 1) * HW], pt[:, i, m, 0:R], v_b[:, m, h * HW:(h + 1) * HW],
                                                       start=(m == 0), stop=(m == TPB - 1))
                        ins.then_inc(pv_done, 1)

                    pe.wait_ge(picked, 3)
                    score(*units[0])
                    score(*units[1])
                    for v in range(U + 2):
                        if v + 2 < U:
                            score(*units[v + 2])
                        if v >= 2:
                            turn(v - 2)
                            weigh(*units[v - 2])

                @block.scalar
                def _(act):
                    A = nc.scalar.activation

                    def scale_logits(u):
                        act.wait_ge(scores, u + 1)
                        if u >= 2:
                            act.wait_ge(shifted, u - 1)
                        A(t1[u % 2][:, :, :], k.ps[0:R, (u % 2) * HG:(u % 2 + 1) * HG, 0:S], ACT.Identity,
                          scale=logit[0:R, :], bias=rnd[0:R, :]).then_inc(scaled, 1)

                    def divide(u):
                        act.wait_ge(shifted, u + 1)
                        A(qq[u % 2][:, :, :], nn[u % 2][:, :, :], ACT.Identity, scale=invx0[0:R, :], bias=off[0:R, :]).then_inc(divided, 1)

                    scale_logits(0)
                    scale_logits(1)
                    divide(0)
                    for v in range(U + 2):
                        if v + 1 < U:
                            divide(v + 1)
                        if v + 2 < U:
                            scale_logits(v + 2)
                        if v < U:
                            act.wait_ge(r_ready, v + 1)
                            A(rr[:, :, :], rr[:, :, :], ACT.Square, bias=half_b[0:R, :]).then_inc(squared, 1)
                            act.wait_ge(e_ready, HG * (v + 1))
                            A(ln_e[:, :, :], ee[v % 2][:, :, :], ACT.Ln).then_inc(ln_ready, 1)
                            A(ln_sm[:, :], sm[v % 2][:, :], ACT.Ln).then_inc(ln_ready, 1)
                            act.wait_ge(ln_ready, 2 * (v + 1))
                            for i in range(HG):
                                A(rho[:, i, :], ln_e[:, i, :], ACT.Exp, scale=-1.0, bias=ln_sm[:, i:i + 1]).then_inc(rho_ready, 1)
                        if v >= 2:
                            act.wait_ge(turned, v - 1)
                            if v > 2:
                                act.wait_ge(pv_done, v - 2)
                            nc.scalar.copy(pt[:, :, :, 0:R], pt_ps[:, :, :, 0:R]).then_inc(pt_ready, 1)

                def context(dve, V, step, nt):
                    dve.wait_ge(pv_done, NHG * (nt + 1))
                    t = tmp[0:R, 0, 0:D]
                    V.tensor_scalar(t, k.ps[0:R, 7, 0:D], ctx_s[0:R, :], ROUND, ALU.mult, ALU.add).then_inc(ctx_out, 1)
                    dve.wait_ge(ctx_out, nt + 1)
                    step(V.tensor_scalar(t, t, ROUND + QMAX, ROUND + QMIN, ALU.min, ALU.max))
                    step(V.tensor_scalar(k.xn[:, bass.ds(first_tile + nt, 1), :].rearrange("p o d -> p (o d)"), t, ROUND, sc[0:R, A2:A2 + 1],
                                         ALU.subtract, ALU.mult))

                @block.vector
                def _(dve):
                    V = nc.vector
                    step = Steps(dve, dve_done)

                    def shift(u):
                        t, n_ = t1[u % 2], nn[u % 2]
                        dve.wait_ge(scaled, u + 1)
                        step(V.tensor_scalar(t[:, :, :], t[:, :, :], ROUND + QMAX, ROUND + QMIN, ALU.min, ALU.max))
                        step(V.tensor_reduce(mx[:, :], t[:, :, :], AX.X, ALU.max))
                        for i in range(HG):
                            ins = V.tensor_scalar(n_[:, i, :], t[:, i, :], mx[:, i:i + 1], lowest[0:R, :], ALU.subtract, ALU.max)
                            if i < HG - 1:
                                step.start(ins)
                        ins.then_inc(shifted, 1)

                    def remainder(u):
                        dve.wait_ge(q_ready, u + 1)
                        V.scalar_tensor_tensor(rr[:, :, :], qq[u % 2][:, :, :], negx0[0:R, :], nn[u % 2][:, :, :], ALU.mult, ALU.add
                                               ).then_inc(r_ready, 1)

                    def exponentials(u):
                        dve.wait_ge(squared, u + 1)
                        dve.wait_ge(pw_ready, u + 1)
                        for i in range(HG):
                            ins = V.scalar_tensor_tensor(ee[u % 2][:, i, :], rr[:, i, :], c_rest[0:R, :], pw[u % 2][:, i, :].bitcast(F32), ALU.add, ALU.mult,
                                                         accum_out=sm[u % 2][:, i:i + 1])
                            ins.then_inc(e_ready, 1)
                        dve.wait_ge(e_ready, HG * (u + 1))
                        step.start(V.reciprocal(inv_sm[u % 2][:, :], sm[u % 2][:, :]))

                    def counts(u):
                        dve.wait_ge(rho_ready, HG * (u + 1))
                        step.wait()
                        for i in range(HG):
                            step.start(V.scalar_tensor_tensor(dd[:, i, :], ee[u % 2][:, i, :], inv_sm[u % 2][:, i:i + 1], rho[:, i, :], ALU.mult, ALU.mult))
                        step.wait()
                        V.scalar_tensor_tensor(dd[:, :, :], dd[:, :, :], 2.0, rho[:, :, :], ALU.subtract, ALU.mult).then_inc(rho_exact, 1)

                    def weights(u):
                        dve.wait_ge(n_scaled, u + 1)
                        if u >= 2:
                            dve.wait_ge(turned, u - 1)
                        V.tensor_scalar(hp[u % 2][:, :, :], ff[:, :, :].bitcast(I32), 0x7F800000, 0x7F800000, ALU.bitwise_and, ALU.bitwise_xor
                                        ).then_inc(p_ready, 1)

                    for w in range(2):
                        V.tensor_copy(qk_b[:, w, :, :], qk_t[:, w, bass.ds(b, 1), :, :].rearrange("p o g s -> p (o g) s")).then_inc(picked, 1)
                    V.tensor_copy(v_b[:, :, :], v_q[:, bass.ds(first_tile, TPB), :]).then_inc(picked, 1)
                    shift(0)
                    for v in range(U + 2):
                        if v + 1 < U:
                            shift(v + 1)
                        if v >= 2:
                            weights(v - 2)
                        if v < U:
                            remainder(v)
                        if 1 <= v <= U:
                            counts(v - 1)
                        if v < U:
                            exponentials(v)
                        if v >= 3 and units[v - 3][2] == NHG - 1:
                            context(dve, V, step, units[v - 3][1])
                    context(dve, V, step, TPB - 1)

        with nc.Fori(0, B) as b:
            batch(b * TPB, b)
        to_columns(nc, k, k.xn, k.xt)
        project(nc, k, wp, dst=k.xn)
        with stage(nc, "dve_done") as (block, dve_done):
            @block.vector
            def _(dve):
                V = nc.vector
                step = Steps(dve, dve_done)
                step(V.tensor_scalar(k.xn[:, :, :], k.xn[:, :, :], inv[0:R, A3:A3 + 1], ROUND, ALU.mult, ALU.add))
                step(V.tensor_scalar(k.xn[:, :, :], k.xn[:, :, :], ROUND + QMAX, ROUND + QMIN, ALU.min, ALU.max))
                step(V.tensor_scalar(k.xn[:, :, :], k.xn[:, :, :], ROUND, sc[0:R, A3:A3 + 1], ALU.subtract, ALU.mult))
                step(V.tensor_tensor(k.h[:, :, :], k.h[:, :, :], k.xn[:, :, :], ALU.add))


def ternary(V, step, x, inv, parts):
    step(V.tensor_scalar(x, x, inv, 1.0, ALU.mult, ALU.min))
    step(V.tensor_scalar(x, x, -1.0, ROUND, ALU.max, ALU.add))


def ternary_attention(nc, k, a):
    normalise(nc, k, k.h, k.xn, 1e-5)
    to_columns(nc, k, k.xn, k.xt)
    EPS = 1e-5
    with ExitStack() as c:
        w = k.sb("ta_w", [KC, 2, 3 * D], F32, c)
        qkv = k.sb("ta_qkv", [R, NT, 3, NHEAD, HW], F32, c)
        l1 = k.sb("ta_l1", [R, NT, 3 * NHEAD], F32, c)
        part = k.sb("ta_part", [128, NT * 3], F32, c)
        sc = k.sb("ta_sc", [128, 4], F32, c)
        inv = k.sb("ta_inv", [128, 4], F32, c)
        pad = k.sb("ta_pad", [R, NT, 2, NHEAD, 32], BF16, c)
        qk_t = k.sb("ta_qkt", [128, 2, B, 3, S], BF16, c)
        qk_b = k.sb("ta_qkb", [128, 2, 3, S], BF16, c)
        v_q = k.sb("ta_v", [R, NT, D], BF16, c)
        v_b = k.sb("ta_vb", [R, TPB, D], BF16, c)
        id16 = k.sb("ta_id", [128, 128], BF16, c)
        with stage(nc, "loaded", "filled", "dve_done", "part_ready", "summed", "w_ready", "tile_ready", "copied", "padded", "turned") as \
                (block, loaded, filled, dve_done, part_ready, summed, w_ready, tile_ready, copied, padded, turned):
            def turned_bank(which, b):
                return k.ps[:, 2 * which + b, :].bitcast(BF16)[:, 0:9 * RP].rearrange("p (g t n) -> p g t n", g=3, t=TPB)

            @block.sync
            def _(sp):
                sp.dma_start(w[:, :, :], a["L3_attn_w_qkv"].rearrange("(c p) n -> p c n", p=KC)).then_inc(loaded, 16)

            @block.gpsimd
            def _(pool):
                nc.gpsimd.memset(pad[:, :, :, :, :], 0.0).then_inc(filled, 1)
                nc.gpsimd.tensor_copy(id16[:, :], k.ident[:, :]).then_inc(filled, 1)

            @block.tensor
            def _(pe):
                pe.wait_ge(part_ready, 1)
                nc.tensor.matmul(k.ps[:, 6, 0:1], k.ones[0:KC, :], part[0:KC, 0:1], start=True, stop=True).then_inc(summed, 1)
                pe.wait_ge(w_ready, 1)
                for t in range(NT):
                    for bank, lo, hi in ((t % 3, 0, 2 * D), (3 + t % 3, 2 * D, 3 * D)):
                        if t >= 3:
                            pe.wait_ge(copied, 2 * (t - 3) + 1 + (lo > 0))
                        for kc in range(2):
                            ins = nc.tensor.matmul(k.ps[0:R, bank, 0:hi - lo], k.xt[0:KC, kc, t * R:(t + 1) * R], w[:, kc, lo:hi],
                                                   start=(kc == 0), stop=(kc == 1))
                        ins.then_inc(tile_ready, 1)
                pe.wait_ge(part_ready, 2)
                nc.tensor.matmul(k.ps[:, 7, 0:3 * NT], k.ones[0:R, :], part[0:R, :], start=True, stop=True).then_inc(summed, 1)
                pe.wait_ge(padded, 3)
                pe.wait_ge(filled, 2)
                for which in range(2):
                    for b in range(B):
                        to = turned_bank(which, b)
                        for g in range(3):
                            for t in range(TPB):
                                ins = nc.tensor.transpose(to[:, g, t, 0:R], pad[:, b * TPB + t, which, 4 * g:4 * g + 4, :].rearrange("p h d -> p (h d)"),
                                                          id16[0:R, 0:R])
                        ins.then_inc(turned, 1)

            @block.scalar
            def _(act):
                for t in range(NT):
                    act.wait_ge(tile_ready, 2 * t + 1)
                    nc.scalar.copy(qkv[:, t, 0:2, :, :].rearrange("p w h d -> p (w h d)"), k.ps[0:R, t % 3, 0:2 * D]).then_inc(copied, 1)
                    act.wait_ge(tile_ready, 2 * t + 2)
                    nc.scalar.copy(qkv[:, t, 2, :, :].rearrange("p h d -> p (h d)"), k.ps[0:R, 3 + t % 3, 0:D]).then_inc(copied, 1)
                for n in (1, 3):
                    act.wait_ge(turned, n + 1)
                    nc.scalar.copy(qk_t[:, n // 2, n % 2, :, :].rearrange("p g (t n) -> p g t n", t=TPB), turned_bank(n // 2, n % 2)[:, :, :, 0:R]
                                   ).then_inc(copied, 1)

            @block.vector
            def _(dve):
                V = nc.vector
                step = Steps(dve, dve_done)
                dve.wait_ge(loaded, 16)
                V.tensor_reduce(part[0:KC, 0:1], w[:, :, :], AX.XY, ALU.add, apply_absolute_value=True).then_inc(part_ready, 1)
                dve.wait_ge(summed, 1)
                step(V.tensor_scalar(sc[:, 3:4], k.ps[:, 6, 0:1], 1.0 / (3 * D * D), EPS, ALU.mult, ALU.add))
                step(V.reciprocal(inv[:, 3:4], sc[:, 3:4]))
                ternary(V, step, w[:, :, :], inv[0:KC, 3:4], KC)
                V.tensor_scalar(w[:, :, :], w[:, :, :], ROUND, sc[0:KC, 3:4], ALU.subtract, ALU.mult).then_inc(w_ready, 1)
                dve.wait_ge(copied, 2 * NT)
                heads = qkv[:, :, :, :, :].rearrange("p t w h d -> p (t w h) d")
                l1_ = l1[:, :, :].rearrange("p t n -> p (t n)")
                step(V.tensor_reduce(l1_, heads, AX.X, ALU.add, apply_absolute_value=True))
                step(V.tensor_scalar(l1_, l1_, EPS, None, ALU.add))
                step(V.reciprocal(l1_, l1_))
                step(V.tensor_tensor(heads, heads, l1_.unsqueeze(2).broadcast_to([R, NT * 3 * NHEAD, HW]), ALU.mult))
                V.tensor_reduce(part[0:R, :], qkv[:, :, :, :, :].rearrange("p t w h d -> p (t w) (h d)"), AX.X, ALU.add,
                                apply_absolute_value=True).then_inc(part_ready, 1)
                dve.wait_ge(summed, 2)
                step(V.tensor_reduce(sc[:, 0:3], k.ps[:, 7, 0:3 * NT].rearrange("p (t w) -> p w t", w=3), AX.X, ALU.add))
                step(V.tensor_scalar(sc[:, 0:3], sc[:, 0:3], 1.0 / (B * S * D), EPS, ALU.mult, ALU.add))
                step(V.reciprocal(inv[:, 0:3], sc[:, 0:3]))
                dve.wait_ge(filled, 1)
                for i in range(3):
                    x = qkv[:, :, i, :, :].rearrange("p t h d -> p t (h d)")
                    ternary(V, step, x, inv[0:R, i:i + 1], R)
                    out = pad[:, :, i, :, 0:HW] if i < 2 else v_q[:, :, :].rearrange("p t (h d) -> p t h d", d=HW)
                    V.tensor_scalar(out, qkv[:, :, i, :, :], ROUND, None, ALU.subtract).then_inc(padded, 1)
                for n in (0, 2):
                    dve.wait_ge(turned, n + 1)
                    step.start(V.tensor_copy(qk_t[:, n // 2, n % 2, :, :].rearrange("p g (t n) -> p g t n", t=TPB),
                                             turned_bank(n // 2, n % 2)[:, :, :, 0:R]))
                step.wait()

        acc = k.sb("ta_acc", [R, B, 12, HG], F32, c)
        acc_b = k.sb("ta_acc_b", [R, 12, HG], F32, c)
        junk = k.sb("ta_junk", [R, HG, S], F32, c)
        rows_sum = k.sb("ta_rows", [R, 1], F32, c)
        cc = k.sb("ta_cc", [128, 4], F32, c)
        rnd = k.sb("ta_round", [128, 1], F32, c)
        t1 = [k.sb(f"ta_t1_{n}", [R, HG, S], F32, c) for n in range(2)]
        at = [k.sb(f"ta_at_{n}", [R, TPB, HG, S], BF16, c) for n in range(2)]
        c_qk, qk_s, alpha, out_s = (cc[:, n:n + 1] for n in range(4))
        units = [(u, u // TPB, u % TPB) for u in range(NHG * TPB)]

        def pick(first_tile, b, picked):
            nc.vector.tensor_copy(qk_b[:, 0, :, :], qk_t[:, 0, bass.ds(b, 1), :, :].rearrange("p o g s -> p (o g) s")).then_inc(picked, 1)
            nc.vector.tensor_copy(qk_b[:, 1, :, :], qk_t[:, 1, bass.ds(b, 1), :, :].rearrange("p o g s -> p (o g) s")).then_inc(picked, 1)
            nc.vector.tensor_copy(v_b[:, :, :], v_q[:, bass.ds(first_tile, TPB), :]).then_inc(picked, 1)

        def score(pe, scores, u, g, mt):
            for i in range(HG):
                rows, grp = head_rows(HG * g + i)
                ins = nc.tensor.matmul(k.ps[0:R, (u % 2) * HG + i, 0:S], qk_b[rows, 1, grp, mt * R:(mt + 1) * R], qk_b[rows, 0, grp, :],
                                       start=True, stop=True)
            ins.then_inc(scores, 1)

        def sizes(first_tile, b):
            with stage(nc, "picked", "scores", "act_summed", "dve_summed", "zeroed", "moved") as \
                    (block, picked, scores, act_summed, dve_summed, zeroed, moved):
                @block.gpsimd
                def _(pool):
                    nc.gpsimd.memset(acc_b[:, :, :], 0.0).then_inc(zeroed, 1)
                    pool.wait_ge(act_summed, len(units) // 2)
                    pool.wait_ge(dve_summed, len(units) // 2)
                    nc.gpsimd.tensor_copy(acc[:, bass.ds(b, 1), :, :].rearrange("p o u h -> p (o u) h"), acc_b[:, :, :]).then_inc(moved, 1)
                    pool.wait_ge(moved, 1)

                @block.tensor
                def _(pe):
                    pe.wait_ge(picked, 3)
                    for u, g, mt in units:
                        if u >= 2:
                            pe.wait_ge(dve_summed if u % 2 else act_summed, u // 2)
                        score(pe, scores, u, g, mt)

                @block.scalar
                def _(act):
                    act.wait_ge(zeroed, 1)
                    for u, g, mt in units[0::2]:
                        act.wait_ge(scores, u + 1)
                        if u:
                            act.wait_ge(act_summed, u // 2)
                        nc.scalar.activation(junk[:, :, :], k.ps[0:R, 0:HG, 0:S], ACT.Abs, accum_out=acc_b[:, u, 0:1]).then_inc(act_summed, 1)

                @block.vector
                def _(dve):
                    pick(first_tile, b, picked)
                    dve.wait_ge(zeroed, 1)
                    for u, g, mt in units[1::2]:
                        dve.wait_ge(scores, u + 1)
                        nc.vector.tensor_reduce(acc_b[:, u, :], k.ps[0:R, HG:2 * HG, 0:S], AX.X, ALU.add, apply_absolute_value=True
                                                ).then_inc(dve_summed, 1)

        def weigh(first_tile, b):
            with stage(nc, "picked", "scores", "scaled", "dve_done", "rounded", "ctx_ready", "ctx_added") as \
                    (block, picked, scores, scaled, dve_done, rounded, ctx_ready, ctx_added):
                @block.tensor
                def _(pe):
                    def context(g):
                        pe.wait_ge(rounded, TPB * (g + 1))
                        if g >= 2:
                            pe.wait_ge(ctx_added, g - 1)
                        for nt in range(TPB):
                            for i in range(HG):
                                col = (nt * HG + i) * HW
                                h = HG * g + i
                                for mt in range(TPB):
                                    ins = nc.tensor.matmul(k.ps[0:R, 6 + g % 2, col:col + HW], at[g % 2][:, mt, i, nt * R:(nt + 1) * R],
                                                           v_b[:, mt, h * HW:(h + 1) * HW], start=(mt == 0), stop=(mt == TPB - 1))
                        ins.then_inc(ctx_ready, 1)

                    pe.wait_ge(picked, 3)
                    for u, g, mt in units:
                        if u >= 2:
                            pe.wait_ge(scaled, u - 1)
                        score(pe, scores, u, g, mt)
                        if mt == TPB - 1 and g:
                            context(g - 1)
                    context(NHG - 1)

                @block.scalar
                def _(act):
                    for u, g, mt in units:
                        act.wait_ge(scores, u + 1)
                        if u >= 2:
                            act.wait_ge(rounded, u - 1)
                        nc.scalar.activation(t1[u % 2][:, :, :], k.ps[0:R, (u % 2) * HG:(u % 2 + 1) * HG, 0:S], ACT.Identity,
                                             scale=alpha[0:R, :], bias=rnd[0:R, :]).then_inc(scaled, 1)

                @block.vector
                def _(dve):
                    V = nc.vector
                    step = Steps(dve, dve_done)

                    def add(g):
                        dve.wait_ge(ctx_ready, g + 1)
                        out = k.h[:, bass.ds(first_tile, TPB), g * HG * HW:(g + 1) * HG * HW]
                        V.scalar_tensor_tensor(out, k.ps[0:R, 6 + g % 2, 0:TPB * HG * HW].rearrange("p (t n) -> p t n", t=TPB), out_s[0:R, :],
                                               out, ALU.mult, ALU.add).then_inc(ctx_added, 1)

                    pick(first_tile, b, picked)
                    for u, g, mt in units:
                        dve.wait_ge(scaled, u + 1)
                        step(V.tensor_scalar(t1[u % 2][:, :, :], t1[u % 2][:, :, :], ROUND + 1.0, ROUND - 1.0, ALU.min, ALU.max))
                        if g >= 2 and mt == 0:
                            dve.wait_ge(ctx_ready, g - 1)
                        V.tensor_scalar(at[g % 2][:, mt, :, :], t1[u % 2][:, :, :], ROUND, None, ALU.subtract).then_inc(rounded, 1)
                        if g and mt == 1:
                            add(g - 1)
                    add(NHG - 1)

        with nc.Fori(0, B) as b:
            sizes(b * TPB, b)
        with stage(nc, "filled", "row_ready", "summed", "dve_done") as (block, filled, row_ready, summed, dve_done):
            @block.gpsimd
            def _(pool):
                nc.gpsimd.memset(rnd[:, :], ROUND).then_inc(filled, 1)
                pool.wait_ge(filled, 1)

            @block.tensor
            def _(pe):
                pe.wait_ge(row_ready, 1)
                nc.tensor.matmul(k.ps[:, 0, 0:1], k.ones[0:R, :], rows_sum[:, :], start=True, stop=True).then_inc(summed, 1)

            @block.vector
            def _(dve):
                V = nc.vector
                step = Steps(dve, dve_done)
                V.tensor_reduce(rows_sum[:, :], acc[:, :, :, :].rearrange("p b u h -> p (b u h)"), AX.X, ALU.add).then_inc(row_ready, 1)
                step(V.tensor_tensor(c_qk, sc[:, 0:1], sc[:, 1:2], ALU.mult))
                step(V.tensor_scalar(c_qk, c_qk, HW ** -0.5, None, ALU.mult))
                dve.wait_ge(summed, 1)
                step(V.tensor_scalar(qk_s, k.ps[:, 0, 0:1], 1.0 / (B * NHEAD * S * S), c_qk, ALU.mult, ALU.mult))
                step(V.tensor_scalar(qk_s, qk_s, EPS, None, ALU.add))
                step(V.reciprocal(alpha, qk_s))
                step(V.tensor_tensor(alpha, alpha, c_qk, ALU.mult))
                step(V.tensor_tensor(out_s, qk_s, sc[:, 2:3], ALU.mult))
        with nc.Fori(0, B) as b:
            weigh(b * TPB, b)


def norm_experts(nc, k, a, ffn, gain, shift):
    hc = ffn.hc
    with ExitStack() as c:
        up = [k.sb(f"ne_up{n}", [R, ffn.hid], F32, c) for n in range(3)]
        hn = [k.sb(f"ne_hn{n}", [R, ffn.hid], F32, c) for n in range(2)]
        hT = [k.sb(f"ne_hT{n}", [128, hc, R], F32, c) for n in range(2)]
        st = [k.sb(f"ne_st{n}", [R, 6], F32, c) for n in range(4)]
        mv = [k.sb(f"ne_mv{n}", [R, 2], F32, c) for n in range(4)]
        rs = [k.sb(f"ne_rs{n}", [R, 1], F32, c) for n in range(4)]
        sc = [k.sb(f"ne_sc{n}", [128, 2, hc], F32, c) for n in range(2)]
        U = GROUP * NT

        def group(first, last):
            with stage(nc, "up_ready", "gelu_done", "stats_done", "var_ready", "var_eps", "rstd_ready", "normed", "turned", "scaled", "y_ready",
                       "y_added", "sc_ready") as (block, up_ready, gelu_done, stats_done, var_ready, var_eps, rstd_ready, normed, turned, scaled,
                                                  y_ready, y_added, sc_ready):
                @block.sync
                def _(sp):
                    if not last:
                        for n in range(GROUP):
                            sp.wait_ge(y_added, NT * (n + 1))
                            sp.sem_clear(k.w_in[n])
                            load_expert(sp, k, a, ffn, n, first + (GROUP + n))

                @block.tensor
                def _(pe):
                    mm = nc.tensor.matmul
                    for s in range(U + 3):
                        if s < U:
                            n, t = s // NT, s % NT
                            if t == 0:
                                pe.wait_ge(k.w_in[n], 16 * ffn.loads)
                            if s >= 3:
                                pe.wait_ge(gelu_done, s - 2)
                            mm(k.ps[0:R, s % 3, 0:ffn.hid], k.xt[0:KC, 0, t * R:(t + 1) * R], k.w1[n][0:KC, 0, 0:ffn.hid], start=True, stop=False)
                            mm(k.ps[0:R, s % 3, 0:ffn.hid], k.xt[0:KC + 1, 1, t * R:(t + 1) * R], k.w1[n][0:KC + 1, 1, 0:ffn.hid],
                               start=False, stop=True).then_inc(up_ready, 1)
                        u = s - 2
                        if 0 <= u < U:
                            pe.wait_ge(normed, u + 1)
                            if u >= 2:
                                pe.wait_ge(scaled, hc * (u - 1))
                            for j in range(hc):
                                ins = nc.tensor.transpose(k.ps[:, 3 + u % 2, j * 128:j * 128 + R], hn[u % 2][:, j * 128:(j + 1) * 128], k.ident[0:R, 0:R])
                            ins.then_inc(turned, 1)
                        u = s - 3
                        if u >= 0:
                            pe.wait_ge(scaled, hc * (u + 1))
                            if u >= 3:
                                pe.wait_ge(y_added, u - 2)
                            for j in range(hc):
                                ins = mm(k.ps[0:R, 5 + u % 3, 0:D], hT[u % 2][:, j, :], k.w2[u // NT][:, j, :], start=(j == 0), stop=(j == hc - 1))
                            ins.then_inc(y_ready, 1)

                @block.scalar
                def _(act):
                    for s in range(U + 2):
                        if s < U:
                            act.wait_ge(up_ready, s + 1)
                            if s >= 3:
                                act.wait_ge(normed, s - 2)
                            nc.scalar.activation(up[s % 3][:, :], k.ps[0:R, s % 3, 0:ffn.hid], ACT.Gelu).then_inc(gelu_done, 1)
                        u = s - 2
                        if u >= 0:
                            n = u // NT
                            act.wait_ge(turned, u + 1)
                            act.wait_ge(sc_ready, 2 * (n + 1))
                            if u >= 2:
                                act.wait_ge(y_ready, u - 1)
                            for j in range(hc):
                                nc.scalar.activation(hT[u % 2][:, j, :], k.ps[:, 3 + u % 2, j * 128:j * 128 + R], ACT.Identity,
                                                     scale=sc[n % 2][:, 0, j:j + 1], bias=sc[n % 2][:, 1, j:j + 1]).then_inc(scaled, 1)

                @block.gpsimd
                def _(pool):
                    def take(n):
                        if n >= 2:
                            pool.wait_ge(scaled, hc * NT * (n - 1))
                        for i, x in enumerate((gain, shift)):
                            nc.gpsimd.tensor_copy(sc[n % 2][:, i, :], x[:, bass.ds(first + n, 1), :].rearrange("p o j -> p (o j)")).then_inc(sc_ready, 1)

                    for s in range(U):
                        if s == 0:
                            take(0)
                            take(1)
                        elif s % NT == 3 and s // NT in (1, 2):
                            take(s // NT + 1)
                        pool.wait_ge(var_ready, s + 1)
                        nc.gpsimd.tensor_scalar(rs[s % 4][:, :], mv[s % 4][:, 1:2], 1e-5, None, ALU.add).then_inc(var_eps, 1)
                        pool.wait_ge(var_eps, s + 1)
                        nc.gpsimd.tensor_tensor(rs[s % 4][:, :], rs[s % 4][:, :], k.neg_half[0:R, 0:1], ALU.pow).then_inc(rstd_ready, 1)

                @block.vector
                def _(dve):
                    V = nc.vector
                    for s in range(U + 4):
                        if s < U:
                            dve.wait_ge(gelu_done, s + 1)
                            V.bn_stats(st[s % 4][:, :], up[s % 3][:, :]).then_inc(stats_done, 1)
                        u = s - 1
                        if 0 <= u < U:
                            dve.wait_ge(rstd_ready, u + 1)
                            if u >= 2:
                                dve.wait_ge(turned, u - 1)
                            V.tensor_scalar(hn[u % 2][:, :], up[u % 3][:, :], mv[u % 4][:, 0:1], rs[u % 4][:, :], ALU.subtract, ALU.mult
                                            ).then_inc(normed, 1)
                        if s < U:
                            dve.wait_ge(stats_done, s + 1)
                            V.bn_aggr(mv[s % 4][:, :], st[s % 4][:, :]).then_inc(var_ready, 1)
                        u = s - 4
                        if u >= 0:
                            n, t = u // NT, u % NT
                            dve.wait_ge(y_ready, u + 1)
                            if t == 0 and n:
                                dve.wait_ge(y_added, NT * n)
                            V.scalar_tensor_tensor(k.h[:, t, :], k.ps[0:R, 5 + u % 3, 0:D], k.gate[:, t, bass.ds(first + n, 1)], k.h[:, t, :],
                                                   ALU.mult, ALU.add).then_inc(y_added, 1)

        with nc.Fori(0, ffn.n // GROUP - 1) as g:
            group(g * GROUP, False)
        group(ffn.n - GROUP, True)


def gelu_norm_layer(nc, k, a):
    ffn = FFN[3]
    normalise(nc, k, k.h, k.xn, 1e-5)
    to_columns(nc, k, k.xn, k.xt)
    with ExitStack() as c:
        b2 = k.sb("gn_b2", [16, D], F32, c)
        gain = k.sb("gn_gain", [128, ffn.n, ffn.hc], F32, c)
        shift = k.sb("gn_shift", [128, ffn.n, ffn.hc], F32, c)
        with stage(nc, "loaded") as (block, loaded):
            @block.sync
            def _(sp):
                sp.dma_start(b2[:, :], a["L3_ffn_fc2_b"]).then_inc(loaded, 16)
                sp.dma_start(gain[:, :, :], a["L3_ffn_ln_w"]).then_inc(loaded, 16)
                sp.dma_start(shift[:, :, :], a["L3_ffn_ln_b"]).then_inc(loaded, 16)
                sp.wait_ge(loaded, 48)
        router(nc, k, a, 3, ffn.n, "L3_ffn_gate_w", "L3_ffn_gate_b", 3)
        norm_experts(nc, k, a, ffn, gain, shift)
        gated_bias(nc, k, ffn.n, b2)


def program(nc, a, out):
    with ExitStack() as ctx:
        k = Chip(nc, ctx)
        weight_buffers(k)
        first_experts(nc, k, a)
        constants(nc, k)
        embed(nc, k, a)
        ttt_attention(nc, k, a)
        swiglu_layer(nc, k, a)
        channel_attention(nc, k, a)
        gelu_layer(nc, k, a)
        quantised_attention(nc, k, a)
        silu_layer(nc, k, a)
        ternary_attention(nc, k, a)
        gelu_norm_layer(nc, k, a)
        with stage(nc, "stored") as (block, stored):
            @block.sync
            def _(sp):
                sp.dma_start(out.rearrange("b (t p) d -> p (b t) d", p=R), k.h[:, :, :]).then_inc(stored, 16)
                sp.wait_ge(stored, 16)


def layout(inputs):
    out = {n: np.asarray(x) for n, x in inputs.items()}
    x = out.pop("x")
    for n, (p, _) in enumerate(LEVELS):
        e = x.shape[-1] // p
        out[f"pix{n}"] = x.reshape(B, 3, e, p, e, p).transpose(2, 4, 0, 3, 5, 1).reshape(e * e, -1)
        out[f"L0_tok_W{n}"] = out[f"L0_tok_W{n}"].T
        if n:
            out[f"inter{n}"] = interpolation(LEVELS[n][1], IMG_TOK)
    for n in ("x_txt", "mask_BS_i1_0"):
        out[n] = out[n].T
    out["L0_tok_bf"] = out["L0_tok_bf"].reshape(2, KC).T
    out["L0_tok_Wf"] = out["L0_tok_Wf"].T
    out["L0_txt_residual_weight"] = out["L0_txt_residual_weight"].reshape(1)
    out["ttt_w_row"] = np.concatenate([out.pop("L0_attn_" + n).reshape(D, NH0, -1) for n in ("Wk", "Wq", "Wv", "lr_w")], axis=2)
    for n in "gb":
        out[f"ttt_{n}_col"] = out[f"L0_attn_ttt_{n}"].T
    out["L0_attn_b_down"] = out["L0_attn_b_down"].reshape(2, KC).T
    out.update(ttt_constants())
    out["L0_ffn_gate_w"] = out["L0_ffn_gate_w"].T
    w, v = out["L0_ffn_mlp1_w"], out["L0_ffn_mlp1_b"]
    out["L0_ffn_mlp1_w"] = np.concatenate([w[:, 0::2], w[:, 1::2]], axis=1).transpose(0, 2, 1)
    out["L0_ffn_mlp1_b"] = np.concatenate([v[:, 0::2], v[:, 1::2]], axis=1)
    out["L0_ffn_mlp2_w"] = out["L0_ffn_mlp2_w"].transpose(0, 2, 1)
    for n in ("L2_attn_qkv_w", "L2_attn_proj_w", "L3_attn_w_qkv"):
        out[n] = out[n].T
    out["qa_scales"] = np.stack([out.pop("L2_attn_" + n + "_scale") for n in ("w_qkv", "a1", "attn", "a2", "w_proj", "a3")])
    for n in ("L3_ffn_ln_w", "L3_ffn_ln_b"):
        out[n] = out[n].reshape(16, 3, 128).transpose(2, 0, 1)
    return {n: np.ascontiguousarray(v) for n, v in out.items()}


def kernel(**inputs):
    import concourse.bacc as bacc
    from concourse.bass_utils import run_bass_kernel_spmd

    nc = bacc.Bacc("TRN2", target_bir_lowering=False, num_devices=1)
    arrays, a = {}, {}
    for name, x in layout(inputs).items():
        arrays[f"in_{name}_dram"] = x
        a[name] = nc.dram_tensor(f"in_{name}_dram", x.shape, mybir.dt.from_np(x.dtype), kind="ExternalInput").ap()
    out = nc.dram_tensor("out_dram", (B, S, D), F32, kind="ExternalOutput").ap()
    program(nc, a, out)
    r = run_bass_kernel_spmd(nc, [arrays], core_ids=[0])
    return r.results[0]["out_dram"]
```

```python
from contextlib import ExitStack, contextmanager

import numpy as np

import concourse.bass as bass
from concourse import mybir

F32 = mybir.dt.float32
BF16 = mybir.dt.bfloat16
I32 = mybir.dt.int32
U32 = mybir.dt.uint32
ALU = mybir.AluOpType
ACT = mybir.ActivationFunctionType
AX = mybir.AxisListType

B = 2
IMG_TOK, TXT_TOK = 256, 77
S = IMG_TOK + TXT_TOK
D = 192
R = 111
NT = B * S // R
TPB = S // R
KC = 96
ROUND = 1.5 * 2.0 ** 23


class Steps:

    def __init__(self, eng, sem):
        self.eng, self.sem, self.n = eng, sem, 0

    def __call__(self, ins):
        self.n += 1
        ins.then_inc(self.sem, 1)
        self.eng.wait_ge(self.sem, self.n)

    def start(self, ins):
        self.n += 1
        ins.then_inc(self.sem, 1)

    def wait(self):
        self.eng.wait_ge(self.sem, self.n)


@contextmanager
def stage(nc, *names):
    with ExitStack() as c:
        sems = [c.enter_context(nc.semaphore(n)) for n in names]
        with nc.Block(no_gpsimd_drain=True) as block:
            yield (block, *sems)
        nums = sorted(s.num for s in sems)
        first = nums[0]
        for n, after in zip(nums, nums[1:] + [None]):
            if after != n + 1:
                nc.gpsimd.sem_clear(range(first, n + 1))
                first = after
        nc.all_engine_barrier(sem_only=True)


def bcast(ap, parts):
    return bass.AP(tensor=ap.tensor, offset=ap.offset, ap=[[0, parts]] + [list(x) for x in ap.ap])


class Chip:

    def __init__(self, nc, ctx):
        self.nc, self.ctx = nc, ctx
        self.h = self.sb("h", [R, NT, D])
        self.xn = self.sb("xn", [R, NT, D])
        self.xt = self.sb("xt", [KC + 1, 2, B * S])
        self.ident = self.sb("ident", [128, 128])
        self.ones = self.sb("ones", [128, 128])
        self.stats = self.sb("stats", [R, NT, 6])
        self.mv = self.sb("mv", [R, NT, 2])
        self.rstd = self.sb("rstd", [R, NT, 1])
        self.neg_half = self.sb("neg_half", [128, 8])
        self.ps = ctx.enter_context(nc.psum_tensor("ps", [128, 8, 512], F32))

    def sb(self, name, shape, dt=F32, ctx=None):
        return (ctx or self.ctx).enter_context(self.nc.sbuf_tensor(name, shape, dt))


def constants(nc, k):
    with stage(nc, "filled", "selected") as (block, filled, selected):
        @block.gpsimd
        def _(pool):
            nc.gpsimd.memset(k.ident[:, :], 0.0).then_inc(filled, 1)
            nc.gpsimd.memset(k.ones[:, :], 1.0).then_inc(filled, 1)
            nc.gpsimd.memset(k.neg_half[:, :], -0.5).then_inc(filled, 1)
            nc.gpsimd.memset(k.xt[:, :, :], 1.0).then_inc(filled, 1)
            pool.wait_ge(filled, 4)
            nc.gpsimd.affine_select(out=k.ident[:, :], in_=k.ident[:, :], compare_op=ALU.not_equal, fill=1.0,
                                    base=0, pattern=[[-1, 128]], channel_multiplier=1).then_inc(selected, 1)
            pool.wait_ge(selected, 1)


def normalise(nc, k, src, dst, eps, gain=None, shift=None):
    with stage(nc, "dve_done", "aggregated", "rstd_eps", "rstd_ready") as (block, dve_done, aggregated, rstd_eps, rstd_ready):
        @block.vector
        def _(dve):
            step = Steps(dve, dve_done)
            for t in range(NT):
                step.start(nc.vector.bn_stats(k.stats[:, t, :], src[:, t, :]))
            step.wait()
            for t in range(NT):
                nc.vector.bn_aggr(k.mv[:, t, :], k.stats[:, t, :]).then_inc(aggregated, 1)
            dve.wait_ge(aggregated, NT)
            dve.wait_ge(rstd_ready, 1)
            for t in range(NT):
                step.start(nc.vector.tensor_scalar(dst[:, t, :], src[:, t, :], k.mv[:, t, 0:1], k.rstd[:, t, 0:1],
                                                   ALU.subtract, ALU.mult))
            step.wait()
            if gain is not None:
                step(nc.vector.tensor_tensor(dst[:, :, :], dst[:, :, :], gain.unsqueeze(1).broadcast_to([R, NT, D]), ALU.mult))
                step(nc.vector.tensor_tensor(dst[:, :, :], dst[:, :, :], shift.unsqueeze(1).broadcast_to([R, NT, D]), ALU.add))

        @block.gpsimd
        def _(pool):
            pool.wait_ge(aggregated, NT)
            nc.gpsimd.tensor_scalar(k.rstd[:, :, :], k.mv[:, :, 1:2], eps, None, ALU.add).then_inc(rstd_eps, 1)
            pool.wait_ge(rstd_eps, 1)
            nc.gpsimd.tensor_tensor(k.rstd[:, :, 0], k.rstd[:, :, 0], k.neg_half[0:R, 0:NT], ALU.pow).then_inc(rstd_ready, 1)


def to_columns(nc, k, src, dst):
    with stage(nc, "bank_ready", "act_copied", "dve_copied") as (block, bank_ready, act_copied, dve_copied):
        banks = [(b, c) for b in range(B) for c in range(2)]

        @block.tensor
        def _(pe):
            for n, (b, c) in enumerate(banks):
                for j in range(TPB):
                    ins = nc.tensor.transpose(k.ps[0:KC, n, j * R:(j + 1) * R], src[:, b * TPB + j, c * KC:(c + 1) * KC],
                                              k.ident[0:R, 0:R])
                ins.then_inc(bank_ready, 1)

        @block.scalar
        def _(act):
            for n in (0, 2):
                b, c = banks[n]
                act.wait_ge(bank_ready, n + 1)
                nc.scalar.copy(dst[0:KC, c, b * S:(b + 1) * S], k.ps[0:KC, n, 0:S]).then_inc(act_copied, 1)
            act.wait_ge(act_copied, 2)

        @block.vector
        def _(dve):
            for n in (1, 3):
                b, c = banks[n]
                dve.wait_ge(bank_ready, n + 1)
                nc.vector.tensor_copy(dst[0:KC, c, b * S:(b + 1) * S], k.ps[0:KC, n, 0:S]).then_inc(dve_copied, 1)
            dve.wait_ge(dve_copied, 2)


def to_rows(nc, k, src, dst):
    with stage(nc, "tile_ready", "dve_copied") as (block, tile_ready, dve_copied):
        @block.tensor
        def _(pe):
            for t in range(NT):
                for c in range(2):
                    ins = nc.tensor.transpose(k.ps[0:R, t, c * KC:(c + 1) * KC], src[0:KC, c, t * R:(t + 1) * R],
                                              k.ident[0:KC, 0:KC])
                ins.then_inc(tile_ready, 1)

        @block.vector
        def _(dve):
            for t in range(NT):
                dve.wait_ge(tile_ready, t + 1)
                nc.vector.tensor_copy(dst[:, t, :], k.ps[0:R, t, 0:D]).then_inc(dve_copied, 1)
            dve.wait_ge(dve_copied, NT)


def normalise_columns(nc, k, src, dst, cols, eps, gain=None, shift=None):
    with stage(nc, "dve_done", "aggregated", "rstd_eps", "rstd_ready", "row_ready", "bank_ready", "act_copied", "dve_copied") as \
            (block, dve_done, aggregated, rstd_eps, rstd_ready, row_ready, bank_ready, act_copied, dve_copied):
        @block.vector
        def _(dve):
            V = nc.vector
            step = Steps(dve, dve_done)
            for t in range(NT):
                step.start(V.bn_stats(k.stats[:, t, :], src[:, t, :]))
            step.wait()
            for t in range(NT):
                V.bn_aggr(k.mv[:, t, :], k.stats[:, t, :]).then_inc(aggregated, 1)
            dve.wait_ge(rstd_ready, 1)
            for t in range(NT):
                ins = V.tensor_scalar(dst[:, t, :], src[:, t, :], k.mv[:, t, 0:1], k.rstd[:, t, 0:1], ALU.subtract, ALU.mult)
                if gain is not None:
                    step(ins)
                    step(V.tensor_tensor(dst[:, t, :], dst[:, t, :], gain, ALU.mult))
                    ins = V.tensor_tensor(dst[:, t, :], dst[:, t, :], shift, ALU.add)
                ins.then_inc(row_ready, 1)
            dve.wait_ge(bank_ready, 4)
            V.tensor_copy(cols[0:KC, 1, S:2 * S], k.ps[0:KC, 3, 0:S]).then_inc(dve_copied, 1)
            dve.wait_ge(dve_copied, 1)

        @block.gpsimd
        def _(pool):
            pool.wait_ge(aggregated, NT)
            nc.gpsimd.tensor_scalar(k.rstd[:, :, :], k.mv[:, :, 1:2], 1.0, eps, ALU.mult, ALU.add).then_inc(rstd_eps, 1)
            pool.wait_ge(rstd_eps, 1)
            nc.gpsimd.tensor_tensor(k.rstd[:, :, 0], k.rstd[:, :, 0], k.neg_half[0:R, 0:NT], ALU.pow).then_inc(rstd_ready, 1)

        @block.tensor
        def _(pe):
            for t in range(NT):
                pe.wait_ge(row_ready, t + 1)
                for c in range(2):
                    ins = nc.tensor.transpose(k.ps[0:KC, t // TPB * 2 + c, t % TPB * R:(t % TPB + 1) * R], dst[:, t, c * KC:(c + 1) * KC],
                                              k.ident[0:R, 0:R])
                    if t % TPB == TPB - 1:
                        ins.then_inc(bank_ready, 1)

        @block.scalar
        def _(act):
            for n in range(3):
                act.wait_ge(bank_ready, n + 1)
                nc.scalar.copy(cols[0:KC, n % 2, n // 2 * S:(n // 2 + 1) * S], k.ps[0:KC, n, 0:S]).then_inc(act_copied, 1)
            act.wait_ge(act_copied, 3)


def interpolation(n_in, n_out):
    pos = np.clip((np.arange(n_out, dtype=np.float32) + 0.5) * (n_in / n_out) - 0.5, 0.0, n_in - 1).astype(np.float32)
    i0 = np.floor(pos).astype(np.int32)
    w = (pos - i0).astype(np.float32)
    m = np.zeros((n_in, n_out), np.float32)
    m[i0, np.arange(n_out)] += np.float32(1.0) - w
    m[np.minimum(i0 + 1, n_in - 1), np.arange(n_out)] += w
    return m
PATCHES = 16
LEVELS = [(1, 256), (2, 64), (4, 16)]
EMB = 64


def embed(nc, k, a):
    with ExitStack() as c:
        idx = [k.sb(f"idx{n}", [min(tok, 128), max(tok // 128, 1), PATCHES], I32, c) for n, (_, tok) in enumerate(LEVELS)]
        width = [B * p * p * 3 for p, _ in LEVELS]
        got = [k.sb(f"got{n}", [min(tok, 128), max(tok // 128, 1), PATCHES, w], F32, c)
               for n, ((_, tok), w) in enumerate(zip(LEVELS, width))]
        feat = [k.sb(f"feat{n}", [min(tok, 128), max(tok // 128, 1), B, PATCHES * w // B], F32, c)
                for n, ((_, tok), w) in enumerate(zip(LEVELS, width))]
        din = [PATCHES * w // B for w in width]
        kw = [min(d, KC) for d in din]
        nk = [d // w for d, w in zip(din, kw)]
        wt = [k.sb(f"tokw{n}", [kw[n], nk[n], EMB], F32, c) for n in range(3)]
        bias0 = k.sb("tok_bias0", [EMB, 1], F32, c)
        bias = [None] + [k.sb(f"tok_bias{n}", [1, EMB], F32, c) for n in (1, 2)]
        wf = k.sb("tok_wf", [EMB, 3, D], F32, c)
        bf = k.sb("tok_bf", [KC, 2], F32, c)
        inter = [None] + [k.sb(f"inter{n}", [LEVELS[n][1], IMG_TOK], F32, c) for n in (1, 2)]
        ft = [k.sb("ft0", [48, B, 256], F32, c), k.sb("ft1", [KC, B, 2, 64], F32, c), k.sb("ft2", [KC, B, 8, 16], F32, c)]
        lev = [None, k.sb("lev1", [64, B, EMB], F32, c), k.sb("lev2", [16, B, EMB], F32, c)]
        yt = k.sb("yt", [EMB, 3, B * IMG_TOK], F32, c)
        ids = k.sb("ids", [TXT_TOK, B], I32, c)
        typ = k.sb("typ", [TXT_TOK, B], I32, c)
        we = k.sb("we", [TXT_TOK, B, D], F32, c)
        te = k.sb("te", [TXT_TOK, B, D], F32, c)
        pe_ = k.sb("pos", [TXT_TOK, D], F32, c)
        wpad = k.sb("wpad", [TXT_TOK, B, D + 2], F32, c)
        ppad = k.sb("ppad", [TXT_TOK, B, D + 2], F32, c)
        cw = k.sb("conv_w", [TXT_TOK, 8], F32, c)
        gamma = k.sb("txt_gamma", [TXT_TOK, D], F32, c)
        beta = k.sb("txt_beta", [TXT_TOK, D], F32, c)
        conv = k.sb("conv", [TXT_TOK, B, D], F32, c)
        emb = k.sb("emb", [TXT_TOK, B, D], F32, c)
        one_minus = k.sb("one_minus", [TXT_TOK, 1], F32, c)
        st = k.sb("txt_stats", [TXT_TOK, B, 6], F32, c)
        mv = k.sb("txt_mv", [TXT_TOK, B, 2], F32, c)
        rs = k.sb("txt_rstd", [TXT_TOK, B], F32, c)
        N_SMALL = 21

        gathered = [k.ctx.enter_context(nc.semaphore(f"gathered{n}")) for n in range(3)]
        txt_gathered = k.ctx.enter_context(nc.semaphore("txt_gathered"))
        with stage(nc, "idx_in", "small_in", "feat_done", "feat_t", "ft_done", "mm_done",
                   "evac", "dve_done", "var_ready", "rstd_ready", "ready", "pool_done") as \
                (block, idx_in, small_in, feat_done, feat_t, ft_done, mm_done,
                 evac, dve_done, var_ready, rstd_ready, ready, pool_done):
            @block.sync
            def _(sp):
                for n, (_, tok) in enumerate(LEVELS):
                    sp.dma_start(idx[n][:, :, :], a[f"L0_tok_idx{n}"].rearrange("(t p g) -> p t g", g=PATCHES, p=min(tok, 128))
                                 ).then_inc(idx_in, 16)
                sp.dma_start(ids[:, :], a["x_txt"]).then_inc(idx_in, 16)
                sp.dma_start(typ[:, :], a["mask_BS_i1_0"]).then_inc(idx_in, 16)
                for n in range(3):
                    sp.dma_start(wt[n][:, :, :], a[f"L0_tok_W{n}"].rearrange("(c p) e -> p c e", p=kw[n])).then_inc(small_in, 16)
                sp.dma_start(bias0[:, :], a["L0_tok_b0"].unsqueeze(1)).then_inc(small_in, 16)
                for n in (1, 2):
                    sp.dma_start(bias[n][:, :], a[f"L0_tok_b{n}"].unsqueeze(0)).then_inc(small_in, 16)
                    sp.dma_start(inter[n][:, :], a[f"inter{n}"]).then_inc(small_in, 16)
                sp.dma_start(wf[:, :, :], a["L0_tok_Wf"].rearrange("(l p) e -> p l e", p=EMB)).then_inc(small_in, 16)
                sp.dma_start(bf[:, :], a["L0_tok_bf"]).then_inc(small_in, 16)
                ttt_loads(sp, k, a)
                first_experts(sp, k, a)
                later_loads(sp, k, a)

            @block.scalar
            def _(act):
                act.dma_start(pe_[:, :], a["L0_txt_pos_emb"][0:TXT_TOK, :]).then_inc(small_in, 16)
                act.dma_start(cw[:, 0:6], bcast(a["L0_txt_conv_w"].rearrange("a b -> (a b)"), TXT_TOK)).then_inc(small_in, 16)
                act.dma_start(cw[:, 6:7], bcast(a["L0_txt_conv_b"], TXT_TOK)).then_inc(small_in, 16)
                act.dma_start(cw[:, 7:8], bcast(a["L0_txt_residual_weight"], TXT_TOK)).then_inc(small_in, 16)
                act.dma_start(gamma[:, :], bcast(a["L0_txt_ln_gamma"], TXT_TOK)).then_inc(small_in, 16)
                act.dma_start(beta[:, :], bcast(a["L0_txt_ln_beta"], TXT_TOK)).then_inc(small_in, 16)
                act.wait_ge(small_in, 16 * 16)

            @block.gpsimd
            def _(pool):
                pool.wait_ge(idx_in, 16 * 5)
                for b in range(B):
                    for dst, table, at in ((we, "L0_txt_word_emb", ids), (te, "L0_txt_type_emb", typ)):
                        pool.indirect_dma_start(dst[:, b, :], None, a[table], bass.IndirectOffsetOnAxis(ap=at[:, b:b + 1], axis=0)
                                                ).then_inc(txt_gathered, 16)
                for n, (_, tok) in enumerate(LEVELS):
                    for t in range(max(tok // 128, 1)):
                        for g in range(PATCHES):
                            pool.indirect_dma_start(got[n][:, t, g, :], None, a[f"pix{n}"],
                                                    bass.IndirectOffsetOnAxis(ap=idx[n][:, t, g:g + 1], axis=0)
                                                    ).then_inc(gathered[n], 16)
                pool.wait_ge(var_ready, 1)
                nc.gpsimd.tensor_tensor(rs[:, :], rs[:, :], k.neg_half[0:TXT_TOK, 0:B], ALU.pow).then_inc(rstd_ready, 1)


            @block.vector
            def _(dve):
                step = Steps(dve, dve_done)
                step.start(nc.vector.memset(wpad[:, :, :], 0.0))
                step(nc.vector.memset(ppad[:, :, :], 0.0))
                dve.wait_ge(small_in, 16 * 16)
                dve.wait_ge(txt_gathered, 16 * 4)
                for b in range(B):
                    step.start(nc.vector.tensor_copy(wpad[:, b, 1:D + 1], we[:, b, :]))
                    step.start(nc.vector.tensor_copy(ppad[:, b, 1:D + 1], pe_[:, :]))
                step(nc.vector.tensor_scalar(one_minus[:, :], cw[:, 7:8], -1.0, 1.0, ALU.mult, ALU.add))
                step(nc.vector.tensor_scalar(conv[:, :, :], wpad[:, :, 0:D], cw[:, 0:1], cw[:, 6:7], ALU.mult, ALU.add))
                for pad, first, taps in ((wpad, 0, (1, 2)), (ppad, 3, (0, 1, 2))):
                    for tap in taps:
                        step(nc.vector.scalar_tensor_tensor(conv[:, :, :], pad[:, :, tap:tap + D], cw[:, first + tap:first + tap + 1],
                                                            conv[:, :, :], ALU.mult, ALU.add))
                step(nc.vector.tensor_tensor(emb[:, :, :], wpad[:, :, 1:D + 1], ppad[:, :, 1:D + 1], ALU.add))
                step(nc.vector.scalar_tensor_tensor(emb[:, :, :], emb[:, :, :], one_minus[:, 0:1], te[:, :, :], ALU.mult, ALU.add))
                step(nc.vector.scalar_tensor_tensor(emb[:, :, :], conv[:, :, :], cw[:, 7:8], emb[:, :, :], ALU.mult, ALU.add))
                for b in range(B):
                    step(nc.vector.bn_stats(st[:, b, :], emb[:, b, :]))
                    step(nc.vector.bn_aggr(mv[:, b, :], st[:, b, :]))
                nc.vector.tensor_scalar(rs[:, :], mv[:, :, 1], 1e-12, None, ALU.add).then_inc(var_ready, 1)
                dve.wait_ge(rstd_ready, 1)
                for b in range(B):
                    step(nc.vector.tensor_scalar(emb[:, b, :], emb[:, b, :], mv[:, b, 0:1], rs[:, b:b + 1], ALU.subtract, ALU.mult))
                    step(nc.vector.tensor_tensor(emb[:, b, :], emb[:, b, :], gamma[:, :], ALU.mult))
                    nc.vector.tensor_tensor(emb[:, b, :], emb[:, b, :], beta[:, :], ALU.add).then_inc(feat_done, 1)
                for n, (_, tok) in enumerate(LEVELS):
                    dve.wait_ge(gathered[n], 16 * PATCHES * max(tok // 128, 1))
                    f = width[n] // B
                    for t in range(max(tok // 128, 1)):
                        for b in range(B):
                            nc.vector.tensor_copy(feat[n][:, t, b, :].rearrange("p (g f) -> p g f", f=f),
                                                  got[n][:, t, :, b * f:(b + 1) * f]).then_inc(feat_done, 1)
                dve.wait_ge(feat_t, 1)
                step.start(nc.vector.tensor_copy(k.xt[0:KC, 0, :].rearrange("p (b s) -> p b s", b=B)[:, :, IMG_TOK:S],
                                                 k.ps[0:KC, 0, 0:B * TXT_TOK].rearrange("p (b s) -> p b s", b=B)))
                step.start(nc.vector.tensor_copy(k.xt[0:KC, 1, :].rearrange("p (b s) -> p b s", b=B)[:, :, IMG_TOK:S],
                                                 k.ps[0:KC, 1, 0:B * TXT_TOK].rearrange("p (b s) -> p b s", b=B)))
                dve.wait_ge(feat_t, 2)
                nc.vector.tensor_copy(ft[0][:, :, :], k.ps[0:48, 2, :].rearrange("p (b s) -> p b s", b=B)).then_inc(ft_done, 1)
                dve.wait_ge(feat_t, 3)
                nc.vector.tensor_copy(ft[1][:, :, :, :], k.ps[0:KC, 3, 0:256].rearrange("p (b c s) -> p b c s", b=B, c=2)).then_inc(ft_done, 1)
                dve.wait_ge(feat_t, 4)
                nc.vector.tensor_copy(ft[2][:, :, :, :], k.ps[0:KC, 4, 0:256].rearrange("p (b c s) -> p b c s", b=B, c=8)).then_inc(ft_done, 1)
                dve.wait_ge(mm_done, 1)
                nc.vector.tensor_scalar(yt[:, 0, :], k.ps[0:EMB, 5, :], bias0[:, 0:1], None, ALU.add).then_inc(evac, 1)
                dve.wait_ge(mm_done, 2)
                nc.vector.tensor_copy(lev[1][:, :, :], k.ps[0:64, 6, 0:B * EMB].rearrange("p (b e) -> p b e", b=B)).then_inc(evac, 1)
                dve.wait_ge(mm_done, 3)
                nc.vector.tensor_copy(lev[2][:, :, :], k.ps[0:16, 7, 0:B * EMB].rearrange("p (b e) -> p b e", b=B)).then_inc(evac, 1)
                for n in (1, 2):
                    dve.wait_ge(mm_done, 3 + n)
                    nc.vector.tensor_copy(yt[:, n, :], k.ps[0:EMB, n + 1, :]).then_inc(evac, 1)
                for ch in range(2):
                    dve.wait_ge(mm_done, 6 + ch)
                    step.start(nc.vector.tensor_scalar(k.xt[0:KC, ch, :].rearrange("p (b s) -> p b s", b=B)[:, :, 0:IMG_TOK],
                                                       k.ps[0:KC, ch, :].rearrange("p (b s) -> p b s", b=B), bf[:, ch:ch + 1], None, ALU.add))
                step.wait()

            @block.tensor
            def _(pe):
                mm, tr = nc.tensor.matmul, nc.tensor.transpose
                pe.wait_ge(feat_done, 2)
                for ch in range(2):
                    for b in range(B):
                        ins = tr(k.ps[0:KC, ch, b * TXT_TOK:(b + 1) * TXT_TOK], emb[:, b, ch * KC:(ch + 1) * KC], k.ident[0:TXT_TOK, 0:TXT_TOK])
                ins.then_inc(feat_t, 1)
                pe.wait_ge(feat_done, 2 + 4)
                for b in range(B):
                    for t in range(2):
                        ins = tr(k.ps[0:48, 2, b * 256 + t * 128:b * 256 + (t + 1) * 128], feat[0][:, t, b, :], k.ident[:, :])
                ins.then_inc(feat_t, 1)
                pe.wait_ge(feat_done, 2 + 6)
                for b in range(B):
                    for ch in range(2):
                        ins = tr(k.ps[0:KC, 3, (b * 2 + ch) * 64:(b * 2 + ch + 1) * 64], feat[1][:, 0, b, ch * KC:(ch + 1) * KC], k.ident[0:64, 0:64])
                ins.then_inc(feat_t, 1)
                pe.wait_ge(feat_done, 2 + 8)
                for b in range(B):
                    for ch in range(8):
                        ins = tr(k.ps[0:KC, 4, (b * 8 + ch) * 16:(b * 8 + ch + 1) * 16], feat[2][:, 0, b, ch * KC:(ch + 1) * KC], k.ident[0:16, 0:16])
                ins.then_inc(feat_t, 1)
                pe.wait_ge(small_in, 16 * 16)
                pe.wait_ge(ft_done, 1)
                mm(k.ps[0:EMB, 5, :], wt[0][:, 0, :], ft[0][:, :, :].rearrange("p b s -> p (b s)"), start=True, stop=True).then_inc(mm_done, 1)
                for n in (1, 2):
                    pe.wait_ge(ft_done, n + 1)
                    tok = LEVELS[n][1]
                    for b in range(B):
                        for ch in range(nk[n]):
                            mm(k.ps[0:tok, 5 + n, b * EMB:(b + 1) * EMB], ft[n][:, b, ch, :], wt[n][:, ch, :], start=(ch == 0), stop=False)
                        ins = mm(k.ps[0:tok, 5 + n, b * EMB:(b + 1) * EMB], k.ones[0:1, 0:tok], bias[n][:, :], start=False, stop=True)
                    ins.then_inc(mm_done, 1)
                for n in (1, 2):
                    pe.wait_ge(evac, 1 + n)
                    for b in range(B):
                        ins = mm(k.ps[0:EMB, n + 1, b * IMG_TOK:(b + 1) * IMG_TOK], lev[n][:, b, :], inter[n][:, :], start=True, stop=True)
                    ins.then_inc(mm_done, 1)
                pe.wait_ge(evac, 5)
                pe.wait_ge(dve_done, 21)
                for ch in range(2):
                    for n in range(3):
                        ins = mm(k.ps[0:KC, ch, :], wf[:, n, ch * KC:(ch + 1) * KC], yt[:, n, :], start=(n == 0), stop=(n == 2))
                    ins.then_inc(mm_done, 1)
    to_rows(nc, k, k.xt, k.h)


def project(nc, k, w, dst=None, add_to=None):
    kk = w.shape[0]
    with stage(nc, "tile_ready", "dve_done") as (block, tile_ready, dve_done):
        @block.tensor
        def _(pe):
            for t in range(NT):
                nc.tensor.matmul(k.ps[0:R, t, 0:D], k.xt[0:KC, 0, t * R:(t + 1) * R], w[0:KC, 0, :], start=True, stop=False)
                nc.tensor.matmul(k.ps[0:R, t, 0:D], k.xt[0:kk, 1, t * R:(t + 1) * R], w[0:kk, 1, :], start=False, stop=True
                                 ).then_inc(tile_ready, 1)

        @block.vector
        def _(dve):
            for t in range(NT):
                dve.wait_ge(tile_ready, t + 1)
                if dst is not None:
                    nc.vector.tensor_copy(dst[:, t, :], k.ps[0:R, t, 0:D]).then_inc(dve_done, 1)
                else:
                    nc.vector.tensor_tensor(add_to[:, t, :], k.ps[0:R, t, 0:D], add_to[:, t, :], ALU.add).then_inc(dve_done, 1)
            dve.wait_ge(dve_done, NT)


NH0, HD = 3, 64
NJ = B * NH0
C = 21
PASS = 4
NCH = PASS * -(-S // (PASS * C))
SP = (NCH + 1) * C
RJ = NJ * C
TTT_EPS = 1e-6


def ttt_constants():
    j, t = np.divmod(np.arange(RJ), C)
    same = j[:, None] == j[None, :]
    centre = np.zeros((HD + 1, HD + 2), np.float32)
    centre[0:HD, 0:HD] = np.eye(HD, dtype=np.float32) - np.float32(1.0 / HD)
    centre[HD, HD + 1] = 1.0
    masks = (same & (t[:, None] < t[None, :]), same & (t[:, None] <= t[None, :]), same, j[:, None] == np.arange(NJ)[None, :])
    return {"ttt_masks": -np.concatenate(masks, axis=1).astype(np.float32), "ttt_centre": centre}


def ttt_inputs(nc, k, c):
    k.w_down = k.sb("w_down", [KC, 2, D], F32, c)
    k.b_down = k.sb("b_down", [KC, 2], F32, c)
    k.w_row = k.sb("w_row", [KC + 1, 2, NH0, 3 * HD + 1], F32, c)
    k.w_out = k.sb("w_out", [KC, 2, D], F32, c)
    k.w_up = k.sb("w_up", [KC + 1, 2, D], F32, c)
    k.post = k.sb("post", [R, 4 * D], F32, c)
    k.gb_row = k.sb("gb_row", [RJ, 2 * HD], F32, c)
    k.gb_col = k.sb("gb_col", [HD, 2 * NH0], F32, c)
    k.state = k.sb("state", [HD + 1, NJ, HD], F32, c)
    k.masks = k.sb("masks", [RJ, 3 * RJ + NJ], F32, c)
    k.centre = k.sb("centre", [HD + 1, HD + 2], F32, c)
    k.ttt_in = k.ctx.enter_context(nc.semaphore("ttt_in"))


TTT_LOADS = 12


def ttt_loads(sp, k, a):
    sp.dma_start(k.w_down[:, :, :], a["L0_attn_W_down"].rearrange("(c p) n -> p c n", p=KC)).then_inc(k.ttt_in, 16)
    sp.dma_start(k.b_down[:, :], a["L0_attn_b_down"]).then_inc(k.ttt_in, 16)
    sp.dma_start(k.w_row[:, :, :, :], a["ttt_w_row"]).then_inc(k.ttt_in, 16)
    sp.dma_start(k.w_out[:, :, :], a["L0_attn_Wo"].rearrange("(c p) n -> p c n", p=KC)).then_inc(k.ttt_in, 16)
    sp.dma_start(k.w_up[0:KC, :, :], a["L0_attn_W_up"].rearrange("(c p) n -> p c n", p=KC)).then_inc(k.ttt_in, 16)
    sp.dma_start(k.w_up[KC:KC + 1, 1, :], a["L0_attn_b_up"].unsqueeze(0)).then_inc(k.ttt_in, 16)
    sp.dma_start(k.post[:, :], bcast(a["ttt_post"], R)).then_inc(k.ttt_in, 16)
    sp.dma_start(k.gb_row[:, :], a["ttt_gb_row"]).then_inc(k.ttt_in, 16)
    sp.dma_start(k.gb_col[:, :], a["ttt_gb_col"]).then_inc(k.ttt_in, 16)
    sp.dma_start(k.state[:, :, :], a["ttt_state"]).then_inc(k.ttt_in, 16)
    sp.dma_start(k.masks[:, :], a["ttt_masks"]).then_inc(k.ttt_in, 16)
    sp.dma_start(k.centre[:, :], a["ttt_centre"]).then_inc(k.ttt_in, 16)


def later_inputs(nc, k):
    k.gate_w = [k.sb(f"gate_w{n}", [KC + 1, 2, e]) for n, e in enumerate((16, 4, 8, 16))]
    k.b2 = [k.sb("swiglu_b2", [16, D]), k.sb("gelu_b2", [4, D]), None, k.sb("gn_b2", [16, D])]
    k.rms_scale = k.sb("rms_scale", [R, D])
    k.token_number = k.sb("token_number", [R, NT])
    k.ca_w = k.sb("ca_w", [KC, 2, 3 * D])
    k.ca_wp = k.sb("ca_wp", [KC + 1, 2, D])
    k.qa_scales = k.sb("qa_scales", [128, 6])
    k.qa_raw = k.sb("qa_raw", [KC, 2, 3 * D])
    k.qa_praw = k.sb("qa_praw", [KC, 2, D])
    k.qa_bias = k.sb("qa_bias", [KC + 1, 4 * D])
    k.ta_w = k.sb("ta_w", [KC, 2, 3 * D])
    k.gn_gain = k.sb("gn_gain", [128, 16, 3])
    k.gn_shift = k.sb("gn_shift", [128, 16, 3])
    k.later_in = k.ctx.enter_context(nc.semaphore("later_in"))


LATER_LOADS = 22


def later_loads(sp, k, a):
    for n, name in enumerate(("L0_ffn_gate_", "L1_ffn_", "L2_ffn_", "L3_ffn_gate_")):
        weight, bias = ("w", "b") if n in (0, 3) else ("Wg", "bg")
        sp.dma_start(k.gate_w[n][0:KC, :, :], a[name + weight].rearrange("(c p) e -> p c e", p=KC)).then_inc(k.later_in, 16)
        if n != 2:
            sp.dma_start(k.gate_w[n][KC:KC + 1, 1, :], a[name + bias].unsqueeze(0)).then_inc(k.later_in, 16)
    for n, name in ((0, "L0_ffn_mlp2_b"), (1, "L1_ffn_b2"), (3, "L3_ffn_fc2_b")):
        sp.dma_start(k.b2[n][:, :], a[name]).then_inc(k.later_in, 16)
    sp.dma_start(k.rms_scale[:, :], bcast(a["L0_ffn_norm_scale"], R)).then_inc(k.later_in, 16)
    sp.dma_start(k.token_number[:, :], a["token_number"]).then_inc(k.later_in, 16)
    for tile, name in ((k.ca_w, "L1_attn_w_qkv"), (k.qa_raw, "L2_attn_qkv_w"), (k.qa_praw, "L2_attn_proj_w"), (k.ta_w, "L3_attn_w_qkv")):
        sp.dma_start(tile[:, :, :], a[name].rearrange("(c p) n -> p c n", p=KC)).then_inc(k.later_in, 16)
    sp.dma_start(k.ca_wp[0:KC, :, :], a["L1_attn_w_proj"].rearrange("(c p) n -> p c n", p=KC)).then_inc(k.later_in, 16)
    sp.dma_start(k.ca_wp[KC:KC + 1, 1, :], a["L1_attn_b_proj"].unsqueeze(0)).then_inc(k.later_in, 16)
    sp.dma_start(k.qa_scales[:, :], bcast(a["qa_scales"], 128)).then_inc(k.later_in, 16)
    sp.dma_start(k.qa_bias[KC:KC + 1, :], a["qa_bias"].unsqueeze(0)).then_inc(k.later_in, 16)
    sp.dma_start(k.gn_gain[:, :, :], a["L3_ffn_ln_w"]).then_inc(k.later_in, 16)
    sp.dma_start(k.gn_shift[:, :, :], a["L3_ffn_ln_b"]).then_inc(k.later_in, 16)


def ttt_attention(nc, k, a):
    with ExitStack() as c:
        w_down, b_down, w_row, w_out, w_up, state, centre = k.w_down, k.b_down, k.w_row, k.w_out, k.w_up, k.state, k.centre
        post_g, post_b, norm_g, norm_b = (k.post[:, n * D:(n + 1) * D] for n in range(4))
        g_row, b_row = k.gb_row[:, 0:HD], k.gb_row[:, HD:]
        g_col, b_col = k.gb_col[:, 0:NH0], k.gb_col[:, NH0:]
        before, upto, same = (k.masks[:, n * RJ:(n + 1) * RJ] for n in range(3))
        member = k.masks[:, 3 * RJ:]
        rowsum = k.sb("ttt_rowsum", [HD + 1, NJ], F32, c)
        g2_row = k.sb("g2_row", [RJ, HD], F32, c)
        cols = k.sb("ttt_cols", [HD + 1, 3, NJ, SP], F32, c)
        ktm = k.sb("ktm", [HD + 1, 2, NJ, RJ], F32, c)
        kt = [k.sb(f"kt{p}", [HD + 1, 3, NJ, C], F32, c) for p in range(2)]
        rows = [k.sb(f"rows{p}", [RJ, 3 * (HD + 1) + 1], F32, c) for p in range(2)]
        k_1 = [x[:, 0:HD + 1] for x in rows]
        q_row = [x[:, HD + 1:2 * HD + 1] for x in rows]
        target = [x[:, 2 * (HD + 1):3 * (HD + 1)] for x in rows]
        eta = [x[:, 3 * (HD + 1):] for x in rows]
        inner = [k.sb(f"inner{p}", [RJ, RJ], F32, c) for p in range(2)]
        inner_q = [k.sb(f"inner_q{p}", [RJ, RJ], F32, c) for p in range(2)]
        inner_x = k.sb("inner_x", [RJ, RJ], F32, c)
        lhs = k.sb("ttt_lhs", [RJ, RJ], F32, c)
        v = k.sb("ttt_v", [RJ, 1], F32, c)
        std = k.sb("ttt_std", [RJ, 1], F32, c)
        r2 = k.sb("ttt_r2", [RJ, 1], F32, c)
        zsum, a1, a2, w = (k.sb("ttt_" + n, [RJ, 1], F32, c) for n in ("zsum", "a1", "a2", "w"))
        pz = k.sb("ttt_pz", [RJ, HD + 1], F32, c)
        q_ = k.sb("ttt_q", [RJ, HD + 1], F32, c)
        zr = k.sb("ttt_zr", [RJ, HD + 1], F32, c)
        gh = k.sb("ttt_gh", [RJ, HD + 1], F32, c)
        junk_a = k.sb("ttt_junk_a", [RJ, HD + 1], F32, c)
        junk = [k.sb(f"ttt_junk{n}", [RJ, HD], F32, c) for n in range(3)]
        gd = k.sb("ttt_gd", [RJ, HD], F32, c)
        ge = k.sb("ttt_ge", [RJ, HD], F32, c)
        eg = k.sb("eg", [RJ, NJ, HD], F32, c)
        z0 = [k.sb(f"z0_{p}", [RJ, HD], F32, c) for p in range(2)]
        zs = k.sb("ttt_z", [RJ, HD + 2], F32, c)
        y = k.sb("ttt_y", [RJ, HD], F32, c)
        outr = k.sb("outr", [RJ, HD], F32, c)
        st6 = k.sb("ttt_st6", [RJ, 6], F32, c)
        mv = k.sb("ttt_mv", [RJ, 2], F32, c)
        rq = k.sb("ttt_rq", [RJ, 1], F32, c)
        out_d = nc.dram_tensor("ttt_rows", [B, C + SP, D], F32).ap()
        z_bank = k.ps[0:RJ, 0, 0:HD + 1]
        z, z_mean = zs[:, 1:HD + 1], zs[:, HD + 1:]
        rows_b, gram_b, zq_b, state_b = (k.ps[:, 4 + n, :] for n in range(4))
        base = state_b[0:RJ, NJ * HD:NJ * HD + HD]

        def flat(x):
            return x.rearrange("p j t -> p (j t)")

        def own(which):
            x = ktm[:, which, :, :]
            return bass.AP(tensor=x.tensor, offset=x.offset, ap=[list(x.ap[0]), [RJ + C, NJ], [1, C]])

        normalise_columns(nc, k, k.h, k.xn, k.xt, 1e-5)
        with ExitStack() as c1:
            hid = k.sb("hid", [KC + 1, 2, B, S], F32, c1)
            with stage(nc, "filled", "bank_ready", "act_done", "dve_done") as (block, filled, bank_ready, act_done, dve_done):
                @block.gpsimd
                def _(pool):
                    step = Steps(pool, filled)
                    G = nc.gpsimd
                    step(G.memset(k.zeros[:, :], 0.0))
                    step(G.memset(hid[KC:KC + 1, :, :, :], 1.0))
                    step.start(G.memset(ktm[:, :, :, :], 0.0))
                    step.start(G.memset(cols[:, 0:2, :, :], 1.0))
                    step.start(G.memset(cols[:, 2, :, :], 0.0))
                    step.start(G.memset(gd[:, :], 0.0))
                    step.start(G.memset(ge[:, :], 0.0))
                    step.start(G.memset(rows[1][:, :], 0.0))
                    step.start(G.memset(inner_q[1][:, :], 0.0))
                    step.wait()

                @block.tensor
                def _(pe):
                    pe.wait_ge(k.ttt_in, 16 * TTT_LOADS)
                    for b in range(B):
                        for m in range(2):
                            for kc in range(2):
                                ins = nc.tensor.matmul(k.ps[0:KC, 2 * b + m, 0:S], w_down[:, kc, m * KC:(m + 1) * KC],
                                                       k.xt[0:KC, kc, b * S:(b + 1) * S], start=(kc == 0), stop=(kc == 1))
                            ins.then_inc(bank_ready, 1)

                @block.scalar
                def _(act):
                    for n in range(2 * B):
                        act.wait_ge(bank_ready, n + 1)
                        nc.scalar.activation(hid[0:KC, n % 2, n // 2, 0:S], k.ps[0:KC, n, 0:S], ACT.Silu,
                                             bias=b_down[:, n % 2:n % 2 + 1]).then_inc(act_done, 1)
                    act.wait_ge(act_done, 2 * B)

                @block.vector
                def _(dve):
                    V = nc.vector
                    step = Steps(dve, dve_done)
                    dve.wait_ge(k.ttt_in, 16 * TTT_LOADS)
                    step.start(V.tensor_tensor(g2_row[:, :], g_row[:, :], g_row[:, :], ALU.mult))
                    step(V.tensor_reduce(rowsum[:, :], state[:, :, :], AX.X, ALU.add))
                    step(V.tensor_scalar(rowsum[:, :], rowsum[:, :], 1.0 / HD, None, ALU.mult))
                    step(V.tensor_tensor(state[:, :, :], state[:, :, :], rowsum[:, :].unsqueeze(2).broadcast_to([HD + 1, NJ, HD]), ALU.subtract))

            with stage(nc, "kq_ready", "vl_ready", "k_copied", "q_copied", "eta_out", "t_done", "dve_done") as \
                    (block, kq_ready, vl_ready, k_copied, q_copied, eta_out, t_done, dve_done):
                @block.sync
                def _(sp):
                    zero_rows(sp, k)
                    sp.wait_ge(k.later_in, 16 * LATER_LOADS)

                @block.tensor
                def _(pe):
                    for j in range(NJ):
                        b, h = j // NH0, j % NH0
                        for bank, lo, hi, ready, free in ((j % 2, 0, 2 * HD, kq_ready, q_copied), (2 + j % 2, 2 * HD, 3 * HD + 1, vl_ready, t_done)):
                            if j >= 2:
                                pe.wait_ge(free, j - 1)
                            for kc in range(2):
                                kk = KC + kc
                                ins = nc.tensor.matmul(k.ps[0:hi - lo, bank, 0:S], w_row[0:kk, kc, h, lo:hi], hid[0:kk, kc, b, :],
                                                       start=(kc == 0), stop=(kc == 1))
                            ins.then_inc(ready, 1)

                @block.scalar
                def _(act):
                    for j in range(NJ):
                        act.wait_ge(kq_ready, j + 1)
                        nc.scalar.copy(cols[0:HD, 0, j, 0:S], k.ps[0:HD, j % 2, 0:S]).then_inc(k_copied, 1)
                        nc.scalar.copy(cols[0:HD, 1, j, 0:S], k.ps[HD:2 * HD, j % 2, 0:S]).then_inc(q_copied, 1)
                        act.wait_ge(vl_ready, j + 1)
                        nc.scalar.activation(cols[HD:HD + 1, 2, j, 0:S], k.ps[HD:HD + 1, 2 + j % 2, 0:S], ACT.Sigmoid).then_inc(eta_out, 1)
                    act.wait_ge(q_copied, NJ)

                @block.vector
                def _(dve):
                    V = nc.vector
                    step = Steps(dve, dve_done)
                    for j in range(NJ):
                        x = cols[0:HD, 2, j, 0:S]
                        dve.wait_ge(k_copied, j + 1)
                        dve.wait_ge(eta_out, j + 1)
                        step(V.scalar_tensor_tensor(x, k.ps[0:HD, 2 + j % 2, 0:S], -1.0, cols[0:HD, 0, j, 0:S], ALU.mult, ALU.add))
                        V.tensor_scalar(x, x, b_col[:, j % NH0:j % NH0 + 1], g_col[:, j % NH0:j % NH0 + 1], ALU.add, ALU.mult).then_inc(t_done, 1)
                    dve.wait_ge(t_done, NJ)
                    step(V.tensor_scalar(cols[HD:HD + 1, 2, :, 0:S], cols[HD:HD + 1, 2, :, 0:S], 1.0 / HD, None, ALU.mult))

        def grams(p, mm, gram_ready):
            mm(gram_b[0:RJ, 0:2 * RJ], flat(kt[p][:, 0, :, :]), kt[p][:, 0:2, :, :].rearrange("p w j t -> p (w j t)"), start=True, stop=True
               ).then_inc(gram_ready, 1)

        def to_row_order(p, mm, rows_ready):
            for n, right in enumerate((k.ident[0:HD + 1, 0:HD + 1], k.ident[0:HD + 1, 0:HD + 1], centre[:, :])):
                at = n * (HD + 1)
                ins = mm(rows_b[0:RJ, at:at + HD + 1 + (n == 2)], flat(kt[p][:, n, :, :]), right, start=True, stop=True)
            ins.then_inc(rows_ready, 1)

        def masked_products(dst, which, mm, done, j):
            mm(dst, ktm[:, which, j, :], state[:, j, :], start=(j == 0), stop=(which == 0 and j == NJ - 1)).then_inc(done, 1)

        def mask(V, dst, src, p, m):
            return V.scalar_tensor_tensor(dst[:, :], src, eta[p], m[:, :], ALU.mult, ALU.mult)

        with stage(nc, "picked", "gram_ready", "rows_ready", "rows_out", "base_mm", "zq_set", "dve_done") as \
                    (block, picked, gram_ready, rows_ready, rows_out, base_mm, zq_set, dve_done):
            @block.gpsimd
            def _(pool):
                for n in range(3):
                    nc.gpsimd.tensor_copy(kt[0][:, n, :, :], cols[:, n, :, 0:C]).then_inc(picked, 1)
                pool.wait_ge(picked, 3)
                nc.gpsimd.tensor_copy(own(0), kt[0][:, 0, :, :]).then_inc(picked, 1)
                pool.wait_ge(picked, 4)

            @block.tensor
            def _(pe):
                mm = nc.tensor.matmul
                pe.wait_ge(picked, 4)
                grams(0, mm, gram_ready)
                to_row_order(0, mm, rows_ready)
                for j in range(NJ):
                    masked_products(base, 0, mm, base_mm, j)
                mm(zq_b[0:RJ, 0:HD], inner_q[1][:, :], gd[:, :], start=True, stop=False).then_inc(zq_set, 1)
                pe.wait_ge(zq_set, 1)

            @block.scalar
            def _(act):
                act.wait_ge(rows_ready, 1)
                nc.scalar.copy(rows[0][:, :], rows_b[0:RJ, 0:3 * (HD + 1) + 1]).then_inc(rows_out, 1)
                act.wait_ge(rows_out, 1)

            @block.vector
            def _(dve):
                V = nc.vector
                step = Steps(dve, dve_done)
                step.start(V.memset(zs[:, 0:1], (HD * TTT_EPS) ** 0.5))
                dve.wait_ge(base_mm, NJ)
                step.start(V.tensor_copy(z0[0][:, :], base))
                step.start(V.tensor_scalar(z, base, 1.0, 0.0, ALU.mult, ALU.add, accum_out=zsum[:, :]))
                dve.wait_ge(rows_out, 1)
                dve.wait_ge(gram_ready, 1)
                step.start(mask(V, inner[0], gram_b[0:RJ, 0:RJ], 0, before))
                step.start(mask(V, inner_q[0], gram_b[0:RJ, RJ:2 * RJ], 0, upto))
                step.wait()

        def store_rows(sp, first_row, stored):
            for b in range(B):
                dst = out_d[b, bass.ds(first_row, C), :].rearrange("t (h e) -> h t e", h=NH0)
                for h in range(NH0):
                    j = b * NH0 + h
                    sp.dma_start(dst[h], outr[j * C:(j + 1) * C, :]).then_inc(stored, 16)

        def chunks(first_token):
            with stage(nc, "mm_ready", "z_ready", "v_ready", "std_ready", "r2_ready", "pz_ready", "mean_ready", "lhs_ready", "zr_ready", "dve_done", "g_ready",
                       "gd_ready", "ge_ready", "picked", "spread", "zq_ready", "zq_var", "zq_rstd", "out_ready", "stored", "state_mm", "state_ready",
                       "k_masked", "q_masked", "gram_ready", "rows_ready", "rows_out", "inner_ready", "base_mm", "base_out", "zq_base", "warmed") as \
                    (block, mm_ready, z_ready, v_ready, std_ready, r2_ready, pz_ready, mean_ready, lhs_ready, zr_ready, dve_done, g_ready,
                     gd_ready, ge_ready, picked, spread, zq_ready, zq_var, zq_rstd, out_ready, stored, state_mm, state_ready,
                     k_masked, q_masked, gram_ready, rows_ready, rows_out, inner_ready, base_mm, base_out, zq_base, warmed):
                sweeps = [(c * C + i, c, i) for c in range(PASS) for i in range(C)]

                @block.sync
                def _(sp):
                    for c in range(PASS):
                        sp.wait_ge(out_ready, c + 1)
                        store_rows(sp, first_token + c * C, stored)
                    sp.wait_ge(stored, PASS * 16 * NJ)

                @block.gpsimd
                def _(pool):
                    G = nc.gpsimd
                    for m, c, i in sweeps:
                        p, n = c % 2, 1 - c % 2
                        if m:
                            pool.wait_ge(z_ready, m)
                        G.tensor_tensor(pz[:, 0:HD], z, g2_row[:, :], ALU.mult).then_inc(pz_ready, 1)
                        if i < 3:
                            if i == 0 and c:
                                pool.wait_ge(ge_ready, c)
                                pool.wait_ge(state_mm, 2 * c)
                            js = slice(2 * i, 2 * i + 2)
                            G.tensor_tensor(eg[:, js, :], ge[:, :].unsqueeze(1).broadcast_to([RJ, 2, HD]),
                                            member[:, js].unsqueeze(2).broadcast_to([RJ, 2, HD]), ALU.mult).then_inc(spread, 1)
                        elif i < 6:
                            if i == 3 and c:
                                pool.wait_ge(q_masked, c)
                                pool.wait_ge(rows_ready, c)
                                pool.wait_ge(gram_ready, 2 * c)
                            which = i - 3
                            G.tensor_copy(kt[n][:, which, :, :], cols[:, which, :, bass.ds(first_token + (c + 1) * C, C)]).then_inc(picked, 1)
                        elif i == 7:
                            pool.wait_ge(zq_var, c + 1)
                            G.tensor_tensor(rq[:, :], mv[:, 1:2], k.neg_half[0:RJ, 0:1], ALU.pow).then_inc(zq_rstd, 1)

                @block.tensor
                def _(pe):
                    mm = nc.tensor.matmul
                    for m, c, i in sweeps:
                        p, n = c % 2, 1 - c % 2
                        if i == 0:
                            if c:
                                pe.wait_ge(gd_ready, c)
                            mm(zq_b[0:RJ, 0:HD], inner_q[n][:, :], gd[:, :], start=False, stop=True).then_inc(zq_ready, 1)
                        elif i in (4, 5):
                            half = i - 4
                            pe.wait_ge(spread, 3 * (c + 1))
                            mm(state_b[0:HD + 1, half * 3 * HD:(half + 1) * 3 * HD], k_1[n],
                               eg[:, 3 * half:3 * half + 3, :].rearrange("p j e -> p (j e)"), start=True, stop=True).then_inc(state_mm, 1)
                        elif i == 6:
                            pe.wait_ge(picked, 3 * (c + 1))
                            if c:
                                pe.wait_ge(inner_ready, 3 * c)
                            grams(n, mm, gram_ready)
                        elif i == 7:
                            mm(gram_b[0:RJ, 2 * RJ:3 * RJ], flat(kt[p][:, 0, :, :]), flat(kt[n][:, 0, :, :]), start=True, stop=True
                               ).then_inc(gram_ready, 1)
                        elif i == 8:
                            if c:
                                pe.wait_ge(rows_out, c)
                            to_row_order(n, mm, rows_ready)
                        if 7 <= i < 7 + NJ:
                            if i == 7:
                                pe.wait_ge(state_ready, 2 * (c + 1))
                                pe.wait_ge(k_masked, c + 1)
                                if c:
                                    pe.wait_ge(base_out, c)
                            masked_products(base, 0, mm, base_mm, i - 7)
                        elif 13 <= i < 13 + NJ:
                            if i == 13:
                                pe.wait_ge(out_ready, c + 1)
                                pe.wait_ge(q_masked, c + 1)
                            masked_products(zq_b[0:RJ, 0:HD], 1, mm, zq_base, i - 13)
                        pe.wait_ge(lhs_ready, m + 1)
                        pe.wait_ge(g_ready, m + 1)
                        mm(z_bank, lhs[:, :], gh[:, :], start=True, stop=True).then_inc(mm_ready, 1)
                    pe.wait_ge(zq_base, PASS * NJ)

                @block.scalar
                def _(act):
                    nc.scalar.activation(std[:, :], k.ones[0:RJ, 0:1], ACT.Sqrt).then_inc(warmed, 1)
                    act.wait_ge(warmed, 1)
                    for m, c, i in sweeps:
                        p, n = c % 2, 1 - c % 2
                        if m:
                            act.wait_ge(z_ready, m)
                        nc.scalar.activation(junk_a[:, :], zs[:, 0:HD + 1], ACT.Square, scale=HD ** -0.5, accum_out=v[:, :]).then_inc(v_ready, 1)
                        nc.scalar.activation(z_mean, zsum[:, :], ACT.Copy, scale=-1.0 / HD).then_inc(mean_ready, 1)
                        act.wait_ge(v_ready, m + 1)
                        nc.scalar.activation(std[:, :], v[:, :], ACT.Sqrt).then_inc(std_ready, 1)
                        act.wait_ge(mean_ready, m + 1)
                        act.wait_ge(r2_ready, m + 1)
                        nc.scalar.activation(zr[:, :], zs[:, 1:HD + 2], ACT.Copy, scale=r2[:, :]).then_inc(zr_ready, 1)
                        if i == C - 1:
                            act.wait_ge(inner_ready, 3 * (c + 1))
                        nc.scalar.activation(lhs[:, :], (inner_x if i == C - 1 else inner[p])[:, :], ACT.Copy, scale=r2[:, :]).then_inc(lhs_ready, 1)
                        if i == 11:
                            act.wait_ge(rows_ready, c + 1)
                            act.wait_ge(out_ready, c + 1)
                            act.wait_ge(state_mm, 2 * (c + 1))
                            nc.scalar.copy(rows[n][:, :], rows_b[0:RJ, 0:3 * (HD + 1) + 1]).then_inc(rows_out, 1)
                        elif i == 3:
                            if c:
                                act.wait_ge(zq_base, NJ * c)
                            nc.scalar.copy(own(1), kt[p][:, 1, :, :]).then_inc(q_masked, 1)
                        elif i == 6:
                            act.wait_ge(picked, 3 * (c + 1))
                            if c:
                                act.wait_ge(base_mm, NJ * c)
                            nc.scalar.copy(own(0), kt[n][:, 0, :, :]).then_inc(k_masked, 1)

                @block.vector
                def _(dve):
                    V = nc.vector
                    step = Steps(dve, dve_done)
                    for m, c, i in sweeps:
                        p, n = c % 2, 1 - c % 2
                        step.start(V.tensor_tensor_reduce(junk[0][:, :], z, g2_row[:, :], -1.0 / HD, 0.0, ALU.mult, ALU.add, pz[:, HD:HD + 1]))
                        step.start(V.tensor_tensor_reduce(junk[1][:, :], z, target[p][:, 0:HD], -1.0 / HD, 0.0, ALU.mult, ALU.add, a1[:, :]))
                        dve.wait_ge(v_ready, m + 1)
                        V.reciprocal(r2[:, :], v[:, :]).then_inc(r2_ready, 1)
                        dve.wait_ge(pz_ready, m + 1)
                        step.start(V.tensor_tensor_reduce(junk[2][:, :], z, pz[:, 0:HD], -1.0 / HD, 0.0, ALU.mult, ALU.add, a2[:, :]))
                        a2_done = step.n
                        dve.wait_ge(std_ready, m + 1)
                        dve.wait_ge(dve_done, a2_done - 1)
                        step.start(V.scalar_tensor_tensor(q_[:, :], target[p], std[:, :], pz[:, :], ALU.mult, ALU.add))
                        dve.wait_ge(dve_done, a2_done)
                        step(V.scalar_tensor_tensor(w[:, :], a1[:, :], std[:, :], a2[:, :], ALU.mult, ALU.add))
                        dve.wait_ge(zr_ready, m + 1)
                        V.scalar_tensor_tensor(gh[:, :], zr[:, :], w[:, :], q_[:, :], ALU.mult, ALU.add).then_inc(g_ready, 1)
                        if i == 0:
                            step(V.tensor_copy(z0[p][:, :], z))
                        elif i == 1:
                            dve.wait_ge(zq_ready, c + 1)
                            step(V.bn_stats(st6[:, :], zq_b[0:RJ, 0:HD]))
                        elif i == 2:
                            step(V.bn_aggr(mv[:, :], st6[:, :]))
                        elif i == 3:
                            V.tensor_scalar(mv[:, 1:2], mv[:, 1:2], TTT_EPS, None, ALU.add).then_inc(zq_var, 1)
                        elif i in (5, 6):
                            half = i - 5
                            dve.wait_ge(state_mm, 2 * (c + 1))
                            if c and half == 0:
                                dve.wait_ge(zq_base, NJ * c)
                                dve.wait_ge(base_mm, NJ * c)
                            part = state[:, 3 * half:3 * half + 3, :]
                            V.tensor_tensor(part, part, state_b[0:HD + 1, half * 3 * HD:(half + 1) * 3 * HD].rearrange("p (j e) -> p j e", j=3),
                                            ALU.add).then_inc(state_ready, 1)
                        elif i == 7:
                            dve.wait_ge(zq_rstd, c + 1)
                            step(V.tensor_scalar(y[:, :], zq_b[0:RJ, 0:HD], mv[:, 0:1], rq[:, 0:1], ALU.subtract, ALU.mult))
                        elif i == 8:
                            step(V.tensor_tensor(y[:, :], y[:, :], g_row[:, :], ALU.mult))
                        elif i == 9:
                            step(V.tensor_tensor(y[:, :], y[:, :], b_row[:, :], ALU.add))
                        elif i == 10:
                            if c:
                                dve.wait_ge(stored, 16 * NJ * c)
                            V.tensor_tensor(outr[:, :], y[:, :], q_row[n], ALU.add).then_inc(out_ready, 1)
                        elif i in (12, 13, 14):
                            dve.wait_ge(rows_out, c + 1)
                            dve.wait_ge(gram_ready, 2 * (c + 1))
                            if i == 12:
                                mask(V, inner[n], gram_b[0:RJ, 0:RJ], n, before).then_inc(inner_ready, 1)
                            elif i == 13:
                                mask(V, inner_q[n], gram_b[0:RJ, RJ:2 * RJ], n, upto).then_inc(inner_ready, 1)
                            else:
                                if c:
                                    dve.wait_ge(lhs_ready, C * c)
                                mask(V, inner_x, gram_b[0:RJ, 2 * RJ:3 * RJ], p, same).then_inc(inner_ready, 1)
                        elif i == 15:
                            dve.wait_ge(base_mm, NJ * (c + 1))
                            V.tensor_copy(z0[n][:, :], base).then_inc(base_out, 1)
                        elif i == C - 1:
                            dve.wait_ge(zq_ready, c + 1)
                            dve.wait_ge(spread, 3 * (c + 1))
                            dve.wait_ge(g_ready, m + 1)
                            V.tensor_scalar(gd[:, :], gh[:, 0:HD], gh[:, HD:HD + 1], r2[:, :], ALU.add, ALU.mult).then_inc(gd_ready, 1)
                            dve.wait_ge(gd_ready, c + 1)
                            V.tensor_scalar(ge[:, :], gd[:, :], eta[p], None, ALU.mult).then_inc(ge_ready, 1)
                            dve.wait_ge(base_out, c + 1)
                        dve.wait_ge(mm_ready, m + 1)
                        V.scalar_tensor_tensor(z, z_bank[:, 0:HD], z_bank[:, HD:HD + 1], z0[n if i == C - 1 else p][:, :], ALU.add, ALU.add, accum_out=zsum[:, :]
                                               ).then_inc(z_ready, 1)
                        dve.wait_ge(z_ready, m + 1)
                    dve.wait_ge(ge_ready, PASS)

        with nc.Fori(0, NCH // PASS) as i:
            chunks(i * (PASS * C))

        with stage(nc, "zq_ready", "zq_var", "zq_rstd", "dve_done", "out_ready", "stored", "back") as \
                (block, zq_ready, zq_var, zq_rstd, dve_done, out_ready, stored, back):
            @block.tensor
            def _(pe):
                nc.tensor.matmul(zq_b[0:RJ, 0:HD], inner_q[1][:, :], gd[:, :], start=False, stop=True).then_inc(zq_ready, 1)

            @block.gpsimd
            def _(pool):
                pool.wait_ge(zq_var, 1)
                nc.gpsimd.tensor_tensor(rq[:, :], mv[:, 1:2], k.neg_half[0:RJ, 0:1], ALU.pow).then_inc(zq_rstd, 1)

            @block.vector
            def _(dve):
                V = nc.vector
                step = Steps(dve, dve_done)
                dve.wait_ge(zq_ready, 1)
                step(V.bn_stats(st6[:, :], zq_b[0:RJ, 0:HD]))
                step(V.bn_aggr(mv[:, :], st6[:, :]))
                V.tensor_scalar(mv[:, 1:2], mv[:, 1:2], TTT_EPS, None, ALU.add).then_inc(zq_var, 1)
                dve.wait_ge(zq_rstd, 1)
                step(V.tensor_scalar(y[:, :], zq_b[0:RJ, 0:HD], mv[:, 0:1], rq[:, 0:1], ALU.subtract, ALU.mult))
                step(V.tensor_tensor(y[:, :], y[:, :], g_row[:, :], ALU.mult))
                step(V.tensor_tensor(y[:, :], y[:, :], b_row[:, :], ALU.add))
                V.tensor_tensor(outr[:, :], y[:, :], q_row[1], ALU.add).then_inc(out_ready, 1)

            @block.sync
            def _(sp):
                sp.wait_ge(out_ready, 1)
                store_rows(sp, NCH * C, stored)
                sp.wait_ge(stored, 16 * NJ)
                for b in range(B):
                    sp.dma_start(k.xn[:, b * TPB:(b + 1) * TPB, :], out_d[b, C:C + S, :].rearrange("(j p) d -> p j d", p=R)).then_inc(back, 16)
                sp.wait_ge(back, 16 * B)
        normalise_columns(nc, k, k.xn, k.xn, k.xt, 1e-6, post_g, post_b)
        project(nc, k, w_out, dst=k.xn)
        normalise_columns(nc, k, k.xn, k.xn, k.xt, 1e-6, norm_g, norm_b)
        project(nc, k, w_up, add_to=k.h)


GROUP = 4


class Experts:

    def __init__(self, name, n, f1, hid, w1, b1, w2):
        self.name, self.n, self.f1, self.hid, self.w1, self.b1, self.w2 = name, n, f1, hid, w1, b1, w2
        self.hc = hid // 128
        self.loads = 2 + (b1 is not None)


FFN = [Experts("swiglu", 16, 768, 384, "L0_ffn_mlp1_w", "L0_ffn_mlp1_b", "L0_ffn_mlp2_w"),
       Experts("gelu", 4, 768, 768, "L1_ffn_W1", "L1_ffn_b1", "L1_ffn_W2"),
       Experts("silu", 8, 1024, 512, "L2_ffn_W1", None, "L2_ffn_W2"),
       Experts("gelu_norm", 16, 384, 384, "L3_ffn_fc1_w", "L3_ffn_fc1_b", "L3_ffn_fc2_w")]


def weight_buffers(k):
    k.w1 = [k.sb(f"w1_{n}", [KC + 1, 2, 1024]) for n in range(GROUP)]
    k.w2 = [k.sb(f"w2_{n}", [128, 6, D]) for n in range(GROUP)]
    k.gate = k.sb("gate", [R, NT, 16])
    k.w_in = [k.ctx.enter_context(k.nc.semaphore(f"w_in{n}")) for n in range(GROUP)]


def load_expert(eng, k, a, ffn, n, e):
    eng.dma_start(k.w1[n][0:KC, :, 0:ffn.f1], a[ffn.w1][bass.ds(e, 1)].rearrange("o (c p) f -> p (o c) f", p=KC)).then_inc(k.w_in[n], 16)
    if ffn.b1 is not None:
        eng.dma_start(k.w1[n][KC:KC + 1, 1, 0:ffn.f1], a[ffn.b1][bass.ds(e, 1), :]).then_inc(k.w_in[n], 16)
    eng.dma_start(k.w2[n][:, 0:ffn.hc, :], a[ffn.w2][bass.ds(e, 1)].rearrange("o (c p) d -> p (o c) d", p=128)).then_inc(k.w_in[n], 16)


def first_experts(sp, k, a):
    for n in range(GROUP):
        load_expert(sp, k, a, FFN[0], n, n)


CAP = int(1.2 * B * S / 8)
SLOTS = 8 * CAP + B * S


def router(nc, k, kind, n_exp, top):
    P = f"L{kind}_"
    PAD, TAKEN, NEVER = -1.0e38, -3.0e38, 3.0e38
    with ExitStack() as c:
        gw = k.gate_w[kind]
        lg = k.sb(P + "lg", [R, NT, 16], F32, c)
        top8 = k.sb(P + "top8", [R, NT, 8], F32, c)
        best = k.sb(P + "best", [R, NT, 8], F32, c)
        mr = k.sb(P + "mr", [R, NT, 16], F32, c)
        mask = k.sb(P + "mask", [R, NT, 16], F32, c)
        mask0 = k.sb(P + "mask0", [R, NT, 16], F32, c)
        ex = k.sb(P + "ex", [R, NT, 16], F32, c)
        tot = k.sb(P + "tot", [R, NT], F32, c)
        wk = k.sb(P + "wk", [R, NT, 2], F32, c)
        pos = k.sb(P + "pos", [R, NT, 2, 8], F32, c)
        both = k.sb(P + "both", [R, NT, 2, 8], F32, c)
        tri = k.sb(P + "tri", [R, R], F32, c)
        base = k.sb(P + "base", [R, 8], F32, c)
        over = k.sb(P + "over", [R, NT, 2], F32, c)
        with stage(nc, P + "logits", P + "dve_done", P + "act_in", P + "act_out", P + "onehot", P + "counted", P + "tri_ready") as \
                (block, logits, dve_done, act_in, act_out, onehot, counted, tri_ready):
            @block.gpsimd
            def _(pool):
                if kind == 2:
                    nc.gpsimd.memset(tri[:, :], 1.0).then_inc(tri_ready, 1)
                    pool.wait_ge(tri_ready, 1)
                    nc.gpsimd.affine_select(out=tri[:, :], in_=tri[:, :], compare_op=ALU.is_ge, fill=0.0, base=0,
                                            pattern=[[1, R]], channel_multiplier=-1).then_inc(tri_ready, 1)
                    for e in range(8):
                        nc.gpsimd.memset(base[:, e:e + 1], float((e - 8) * CAP - 1)).then_inc(tri_ready, 1)

            @block.tensor
            def _(pe):
                kk = KC + (kind != 2)
                for t in range(NT):
                    own = k.ps[0:R, 0, t * n_exp:(t + 1) * n_exp]
                    nc.tensor.matmul(own, k.xt[0:KC, 0, t * R:(t + 1) * R], gw[0:KC, 0, :], start=True, stop=False)
                    ins = nc.tensor.matmul(own, k.xt[0:kk, 1, t * R:(t + 1) * R], gw[0:kk, 1, :], start=False, stop=True)
                ins.then_inc(logits, 1)
                if kind == 2:
                    pe.wait_ge(tri_ready, 2)
                    pe.wait_ge(onehot, 1)
                    for t in range(NT):
                        for s in range(t + 1):
                            ins = nc.tensor.matmul(k.ps[0:R, 1, t * 16:(t + 1) * 16], tri[:, :] if s == t else k.ones[0:R, 0:R],
                                                   both[:, s, :, :].rearrange("p k e -> p (k e)"), start=(s == 0), stop=(s == t))
                    ins.then_inc(counted, 1)

            @block.scalar
            def _(act):
                if kind == 0 or kind == 3:
                    act.wait_ge(act_in, 1)
                    nc.scalar.activation(ex[:, :, :], lg[:, :, :], ACT.Exp).then_inc(act_out, 1)
                if kind == 2:
                    act.wait_ge(act_in, 1)
                    nc.scalar.activation(wk[:, :, 1], wk[:, :, 0], ACT.Exp).then_inc(act_out, 1)

            @block.vector
            def _(dve):
                V = nc.vector
                step = Steps(dve, dve_done)

                def choose(values, n, out):
                    for t in range(NT):
                        step.start(V.max(top8[:, t, :], values[:, t, :]))
                    step.wait()
                    step(V.tensor_copy(best[:, :, :], top8[:, :, :]))
                    step(V.memset(best[:, :, n:8], NEVER))
                    for t in range(NT):
                        step(V.match_replace(mr[:, t, :], best[:, t, :], values[:, t, :], TAKEN))
                    step(V.tensor_scalar(out[:, :, :], mr[:, :, :], 2.0 * PAD, None, ALU.is_lt))

                step(V.memset(lg[:, :, :], PAD))
                dve.wait_ge(logits, 1)
                step(V.tensor_copy(lg[:, :, 0:n_exp], k.ps[0:R, 0, 0:NT * n_exp].rearrange("p (t e) -> p t e", t=NT)))
                if kind == 0:
                    choose(lg, top, mask)
                    V.tensor_tensor(lg[:, :, :], lg[:, :, :], top8[:, :, 0:1].broadcast_to([R, NT, 16]), ALU.subtract).then_inc(act_in, 1)
                    dve.wait_ge(act_out, 1)
                    step(V.tensor_tensor(ex[:, :, :], ex[:, :, :], mask[:, :, :], ALU.mult))
                    step(V.tensor_reduce(tot[:, :], ex[:, :, :], AX.X, ALU.add))
                    step(V.reciprocal(tot[:, :], tot[:, :]))
                    step(V.tensor_tensor(k.gate[:, :, :], ex[:, :, :], tot[:, :].unsqueeze(2).broadcast_to([R, NT, 16]), ALU.mult))
                elif kind == 1:
                    choose(lg, top, k.gate)
                elif kind == 2:
                    choose(lg, 2, mask)
                    choose(lg, 1, mask0)
                    step.start(V.tensor_copy(both[:, :, 0, :], mask0[:, :, 0:8]))
                    V.tensor_tensor(both[:, :, 1, :], mask[:, :, 0:8], mask0[:, :, 0:8], ALU.subtract).then_inc(onehot, 1)
                    V.tensor_tensor(wk[:, :, 0], top8[:, :, 1], top8[:, :, 0], ALU.subtract).then_inc(act_in, 1)
                    dve.wait_ge(act_out, 1)
                    step(V.tensor_scalar(tot[:, :], wk[:, :, 1], 1.0, None, ALU.add))
                    step(V.reciprocal(wk[:, :, 0], tot[:, :]))
                    step(V.tensor_tensor(wk[:, :, 1], wk[:, :, 1], wk[:, :, 0], ALU.mult))
                    dve.wait_ge(counted, 1)
                    counts = k.ps[0:R, 1, 0:NT * 16].rearrange("p (t e) -> p t e", t=2 * NT)
                    flat = lambda x: x[:, :, :, :].rearrange("p t k e -> p (t k) e")
                    slots = lambda x: x[:, :, :].rearrange("p t k -> p (t k)")
                    step(V.tensor_scalar(flat(pos), counts, float(CAP), None, ALU.is_le))
                    dve.wait_ge(onehot, 1)
                    step(V.tensor_tensor(flat(both), flat(pos), flat(both), ALU.mult))
                    step(V.tensor_reduce(slots(k.choice_w), flat(both), AX.X, ALU.add))
                    for n in range(2):
                        step(V.tensor_scalar(over[:, :, n], k.choice_w[:, :, n], 1.0, -1.0, ALU.subtract, ALU.mult))
                        step(V.tensor_tensor(over[:, :, n], over[:, :, n], k.token_number[:, :], ALU.mult))
                    step(V.tensor_tensor(slots(k.choice_w), slots(k.choice_w), slots(wk), ALU.mult))
                    dve.wait_ge(tri_ready, 2 + 8)
                    step(V.tensor_tensor(flat(pos), counts, base[:, :].unsqueeze(1).broadcast_to([R, 2 * NT, 8]), ALU.add))
                    step(V.tensor_tensor(flat(pos), flat(pos), flat(both), ALU.mult))
                    step(V.tensor_reduce(slots(wk), flat(pos), AX.X, ALU.add))
                    step(V.tensor_tensor(slots(wk), slots(wk), slots(over), ALU.add))
                    for n in range(2):
                        step(V.tensor_scalar(k.slot[:, :, n], wk[:, :, n], float(8 * CAP + n * SLOTS), None, ALU.add))
                else:
                    step(V.memset(lg[:, :, 0:1], -1.0e9))
                    step(V.tensor_reduce(tot[:, :], lg[:, :, :], AX.X, ALU.max))
                    V.tensor_tensor(lg[:, :, :], lg[:, :, :], tot[:, :].unsqueeze(2).broadcast_to([R, NT, 16]), ALU.subtract).then_inc(act_in, 1)
                    dve.wait_ge(act_out, 1)
                    step(V.tensor_reduce(tot[:, :], ex[:, :, :], AX.X, ALU.add))
                    step(V.reciprocal(tot[:, :], tot[:, :]))
                    step(V.tensor_tensor(ex[:, :, :], ex[:, :, :], tot[:, :].unsqueeze(2).broadcast_to([R, NT, 16]), ALU.mult))
                    choose(ex, top, mask)
                    step(V.tensor_tensor(k.gate[:, :, :], ex[:, :, :], mask[:, :, :], ALU.mult))
                    step(V.tensor_scalar(k.gate[:, :, 0:1], k.gate[:, :, 0:1], 1.0, None, ALU.add))


def run_experts(nc, k, a, ffn, following):
    with ExitStack() as c:
        hT = [k.sb(f"{ffn.name}_hT{n}", [128, ffn.hc, B * S], F32, c) for n in range(2)]
        ga = [k.sb(f"{ffn.name}_ga{n}", [128, S], F32, c) for n in range(2)]
        li = [k.sb(f"{ffn.name}_li{n}", [128, S], F32, c) for n in range(2)]
        sg = [k.sb(f"{ffn.name}_sg{n}", [128, S], F32, c) for n in range(2)]
        paired = ffn.name != "gelu"
        per = ffn.hc * B
        ring = 2 if paired else 4

        def group(first, last):
            with stage(nc, "unit_ready", "bank_free", "clipped", "gate_act", "dve_done", "unit_done", "y_ready", "y_added") as \
                    (block, unit_ready, bank_free, clipped, gate_act, dve_done, unit_done, y_ready, y_added):
                def units(n):
                    return [(n * per + m, m // B, m % B) for m in range(per)]

                def bank(u, which):
                    return k.ps[:, (u % ring) * (2 if paired else 1) + which, 0:S]

                @block.sync
                def _(sp):
                    for n in range(GROUP):
                        if last and following is None:
                            break
                        sp.wait_ge(y_added, NT * (n + 1))
                        sp.sem_clear(k.w_in[n])
                        if last:
                            load_expert(sp, k, a, following, n, n)
                        else:
                            load_expert(sp, k, a, ffn, n, first + (GROUP + n))

                @block.tensor
                def _(pe):
                    mm = nc.tensor.matmul

                    def up(n):
                        pe.wait_ge(k.w_in[n], 16 * ffn.loads)
                        kk = KC + (ffn.b1 is not None)
                        for u, j, b in units(n):
                            if u >= ring:
                                pe.wait_ge(bank_free if ffn.name == "swiglu" else unit_done, u - ring + 1)
                            for which in range(2 if paired else 1):
                                f = (j + which * ffn.hc) * 128
                                mm(bank(u, which), k.w1[n][0:KC, 0, f:f + 128], k.xt[0:KC, 0, b * S:(b + 1) * S], start=True, stop=False)
                                ins = mm(bank(u, which), k.w1[n][0:kk, 1, f:f + 128], k.xt[0:kk, 1, b * S:(b + 1) * S], start=False, stop=True)
                            ins.then_inc(unit_ready, 1)

                    def down(n):
                        pe.wait_ge(unit_done, per * (n + 1))
                        for t in range(NT):
                            m = NT * n + t
                            if m >= 3:
                                pe.wait_ge(y_added, m - 2)
                            for j in range(ffn.hc):
                                ins = mm(k.ps[0:R, 4 + m % 3, 0:D], hT[n % 2][:, j, t * R:(t + 1) * R], k.w2[n][:, j, :],
                                         start=(j == 0), stop=(j == ffn.hc - 1))
                            ins.then_inc(y_ready, 1)

                    up(0)
                    for n in range(GROUP):
                        if n + 1 < GROUP:
                            up(n + 1)
                        down(n)

                @block.scalar
                def _(act):
                    for n in range(GROUP):
                        for u, j, b in units(n):
                            if ffn.name == "swiglu":
                                act.wait_ge(clipped, u + 1)
                                nc.scalar.activation(sg[u % 2][:, :], ga[u % 2][:, :], ACT.Sigmoid, scale=1.702).then_inc(gate_act, 1)
                            elif ffn.name == "silu":
                                act.wait_ge(unit_ready, u + 1)
                                if u >= 2:
                                    act.wait_ge(unit_done, u - 1)
                                nc.scalar.activation(sg[u % 2][:, :], bank(u, 1), ACT.Silu).then_inc(gate_act, 1)
                            else:
                                act.wait_ge(unit_ready, u + 1)
                                nc.scalar.activation(hT[n % 2][:, j, b * S:(b + 1) * S], bank(u, 0), ACT.Gelu).then_inc(unit_done, 1)

                @block.vector
                def _(dve):
                    V = nc.vector
                    step = Steps(dve, dve_done)

                    def add(n):
                        for t in range(NT):
                            dve.wait_ge(y_ready, NT * n + t + 1)
                            ins = V.scalar_tensor_tensor(k.h[:, t, :], k.ps[0:R, 4 + (NT * n + t) % 3, 0:D], k.gate[:, t, bass.ds(first + n, 1)],
                                                         k.h[:, t, :], ALU.mult, ALU.add)
                            ins.then_inc(y_added, 1)
                        dve.wait_ge(y_added, NT * (n + 1))

                    for n in range(GROUP):
                        for u, j, b in units(n):
                            out = hT[n % 2][:, j, b * S:(b + 1) * S]
                            if ffn.name == "swiglu":
                                dve.wait_ge(unit_ready, u + 1)
                                V.tensor_scalar(ga[u % 2][:, :], bank(u, 0), 7.0, None, ALU.min).then_inc(clipped, 1)
                                V.tensor_scalar(li[u % 2][:, :], bank(u, 1), 7.0, -7.0, ALU.min, ALU.max).then_inc(bank_free, 1)
                                dve.wait_ge(bank_free, u + 1)
                                step(V.scalar_tensor_tensor(li[u % 2][:, :], li[u % 2][:, :], 1.0, ga[u % 2][:, :], ALU.add, ALU.mult))
                                dve.wait_ge(gate_act, u + 1)
                                V.tensor_tensor(out, li[u % 2][:, :], sg[u % 2][:, :], ALU.mult).then_inc(unit_done, 1)
                            elif ffn.name == "silu":
                                dve.wait_ge(gate_act, u + 1)
                                V.tensor_tensor(out, bank(u, 0), sg[u % 2][:, :], ALU.mult).then_inc(unit_done, 1)
                        if n:
                            add(n - 1)
                    add(GROUP - 1)

        if ffn.n > GROUP:
            with nc.Fori(0, ffn.n // GROUP - 1) as g:
                group(g * GROUP, False)
        group(ffn.n - GROUP, True)


def gated_bias(nc, k, n_exp, b2):
    with ExitStack() as c:
        gt = k.sb(f"gate_t{n_exp}_{nc.next_id()}", [16, B * S], F32, c)
        with stage(nc, "turned", "copied", "tile_ready", "dve_done") as (block, turned, copied, tile_ready, dve_done):
            @block.tensor
            def _(pe):
                for t in range(NT):
                    ins = nc.tensor.transpose(k.ps[0:n_exp, t // 3, (t % 3) * R:(t % 3 + 1) * R], k.gate[:, t, 0:n_exp], k.ident[0:R, 0:R])
                    if t % 3 == 2:
                        ins.then_inc(turned, 1)
                for t in range(NT):
                    pe.wait_ge(copied, t // 3 + 1)
                    nc.tensor.matmul(k.ps[0:R, 2 + t, 0:D], gt[0:n_exp, t * R:(t + 1) * R], b2[0:n_exp, :], start=True, stop=True
                                     ).then_inc(tile_ready, 1)

            @block.vector
            def _(dve):
                for b in range(B):
                    dve.wait_ge(turned, b + 1)
                    nc.vector.tensor_copy(gt[0:n_exp, b * S:(b + 1) * S], k.ps[0:n_exp, b, 0:S]).then_inc(copied, 1)
                for t in range(NT):
                    dve.wait_ge(tile_ready, t + 1)
                    nc.vector.tensor_tensor(k.h[:, t, :], k.ps[0:R, 2 + t, 0:D], k.h[:, t, :], ALU.add).then_inc(dve_done, 1)
                dve.wait_ge(dve_done, NT)


def swiglu_layer(nc, k, a):
    normalise(nc, k, k.h, k.xn, 1e-5)
    with ExitStack() as c:
        t_ = k.sb("rms_t", [R, NT, D], F32, c)
        junk = k.sb("rms_junk", [R, NT, D], F32, c)
        ms = k.sb("rms_ms", [R, NT], F32, c)
        with stage(nc, "ms_ready", "rms_ready", "dve_done") as (block, ms_ready, rms_ready, dve_done):
            @block.gpsimd
            def _(pool):
                pool.wait_ge(ms_ready, NT)
                nc.gpsimd.tensor_tensor(k.rstd[:, :, 0], ms[:, :], k.neg_half[0:R, 0:NT], ALU.pow).then_inc(rms_ready, 1)

            @block.vector
            def _(dve):
                step = Steps(dve, dve_done)
                for t in range(NT):
                    nc.vector.tensor_tensor_reduce(junk[:, t, :], k.xn[:, t, :], k.xn[:, t, :], 1.0 / D, 1e-5, ALU.mult, ALU.add,
                                                   ms[:, t:t + 1]).then_inc(ms_ready, 1)
                step.start(nc.vector.tensor_tensor(k.h[:, :, :], k.h[:, :, :], k.xn[:, :, :], ALU.add))
                dve.wait_ge(rms_ready, 1)
                for t in range(NT):
                    step.start(nc.vector.scalar_tensor_tensor(t_[:, t, :], k.xn[:, t, :], k.rstd[:, t, 0:1], k.rms_scale[:, :], ALU.mult, ALU.mult))
                step.wait()
        to_columns(nc, k, t_, k.xt)
        router(nc, k, 0, 16, 4)
        run_experts(nc, k, a, FFN[0], FFN[1])
        gated_bias(nc, k, 16, k.b2[0])


def gelu_layer(nc, k, a):
    normalise_columns(nc, k, k.h, k.xn, k.xt, 1e-5)
    router(nc, k, 1, 4, 1)
    run_experts(nc, k, a, FFN[1], FFN[2])
    gated_bias(nc, k, 4, k.b2[1])


def slot_buffers(nc, k):
    k.x_rows = nc.dram_tensor("silu_x", [2 * SLOTS, D], F32).ap()
    k.y_rows = nc.dram_tensor("silu_y", [2 * SLOTS, D], F32).ap()
    k.slot = k.sb("slot", [R, NT, 2], I32)
    k.choice_w = k.sb("choice_w", [R, NT, 2])
    k.zeroed = k.ctx.enter_context(nc.semaphore("rows_zeroed"))
    k.x_sent = k.ctx.enter_context(nc.semaphore("x_sent"))
    k.y_back = k.ctx.enter_context(nc.semaphore("y_back"))
    k.zeros = k.sb("zeros", [128, D])


def zero_rows(sp, k):
    for n in range(2):
        sp.dma_start(k.x_rows[n * SLOTS:n * SLOTS + 8 * CAP, :].rearrange("(e s) d -> s e d", e=8),
                     k.zeros[0:CAP, :].unsqueeze(1).broadcast_to([CAP, 8, D])).then_inc(k.zeroed, 16)
        sp.dma_start(k.y_rows[n * SLOTS + 8 * CAP:(n + 1) * SLOTS, :].rearrange("(t s) d -> s t d", t=NT),
                     k.zeros[0:R, :].unsqueeze(1).broadcast_to([R, NT, D])).then_inc(k.zeroed, 16)


def silu_layer(nc, k, a):
    ffn, E = FFN[2], 8
    normalise_columns(nc, k, k.h, k.xn, k.xt, 1e-5)
    router(nc, k, 2, E, 2)
    with ExitStack() as c:
        rows = k.sb("silu_rows", [CAP, E, 2, D], F32, c)
        cols = k.sb("silu_cols", [KC, 2, E, 2 * CAP], F32, c)
        hT = [k.sb(f"silu_hT{n}", [128, ffn.hc, 2 * CAP], F32, c) for n in range(2)]
        sg = [k.sb(f"silu_sg{n}", [128, 2 * CAP], F32, c) for n in range(2)]
        y = [k.sb(f"silu_out{n}", [CAP, 2, D], F32, c) for n in range(2)]
        back = k.sb("silu_back", [R, NT, 2, D], F32, c)

        def of_expert(x, e):
            return x.rearrange("(n s) d -> s n d", n=2)[e * CAP:(e + 1) * CAP, :, :]

        with stage(nc, "rows_in", "turned", "cols_ready", "unit_ready", "gate_act", "unit_done", "y_ready", "y_copied", "y_sent0", "y_sent1", "added") as \
                (block, rows_in, turned, cols_ready, unit_ready, gate_act, unit_done, y_ready, y_copied, y_sent0, y_sent1, added):
            y_sent = (y_sent0, y_sent1)
            units = [(u, u // ffn.hc, u % ffn.hc) for u in range(E * ffn.hc)]

            @block.gpsimd
            def _(pool):
                pool.wait_ge(k.zeroed, 16 * 4)
                for t in range(NT):
                    for n in range(2):
                        pool.indirect_dma_start(k.x_rows, bass.IndirectOffsetOnAxis(ap=k.slot[:, t, n:n + 1], axis=0), k.xn[:, t, :], None
                                                ).then_inc(k.x_sent, 16)
                for n in range(2):
                    pool.wait_ge(y_sent[n], 16 * E // 2)
                for t in range(NT):
                    for n in range(2):
                        pool.indirect_dma_start(back[:, t, n, :], None, k.y_rows, bass.IndirectOffsetOnAxis(ap=k.slot[:, t, n:n + 1], axis=0)
                                                ).then_inc(k.y_back, 16)
                pool.wait_ge(k.y_back, 16 * 2 * NT)

            @block.sync
            def _(sp):
                sp.wait_ge(k.x_sent, 16 * 2 * NT)
                for e in range(E):
                    sp.dma_start(rows[:, e, :, :], of_expert(k.x_rows, e)).then_inc(rows_in, 16)
                for e in range(E):
                    n = e % GROUP
                    sp.wait_ge(y_copied, e + 1)
                    if e + GROUP < E:
                        load_expert(sp, k, a, ffn, n, e + GROUP)
                    else:
                        sp.sem_clear(k.w_in[n])
                        load_expert(sp, k, a, FFN[3], n, n)
                    sp.dma_start(of_expert(k.y_rows, e), y[e % 2][:, :, :]).then_inc(y_sent[e % 2], 16)

            @block.tensor
            def _(pe):
                mm = nc.tensor.matmul

                def turn(e):
                    pe.wait_ge(rows_in, 16 * E)
                    if e >= 2:
                        pe.wait_ge(cols_ready, e - 1)
                    for kc in range(2):
                        for n in range(2):
                            ins = nc.tensor.transpose(k.ps[0:KC, 6 + e % 2, (kc * 2 + n) * CAP:(kc * 2 + n + 1) * CAP], rows[:, e, n, kc * KC:(kc + 1) * KC],
                                                      k.ident[0:CAP, 0:CAP])
                    ins.then_inc(turned, 1)

                def up(e):
                    pe.wait_ge(cols_ready, e + 1)
                    pe.wait_ge(k.w_in[e % GROUP], 16 * ffn.loads * (e // GROUP + 1))
                    for u, _, j in units[e * ffn.hc:(e + 1) * ffn.hc]:
                        if u >= 4:
                            pe.wait_ge(unit_done, u - 3)
                        for which in range(2):
                            f = (j + which * ffn.hc) * 128
                            for kc in range(2):
                                ins = mm(k.ps[:, u % 4, which * 2 * CAP:(which + 1) * 2 * CAP], k.w1[e % GROUP][0:KC, kc, f:f + 128],
                                         cols[:, kc, e, :], start=(kc == 0), stop=(kc == 1))
                        ins.then_inc(unit_ready, 1)

                def down(e):
                    pe.wait_ge(unit_done, ffn.hc * (e + 1))
                    if e >= 2:
                        pe.wait_ge(y_copied, e - 1)
                    for n in range(2):
                        for j in range(ffn.hc):
                            ins = mm(k.ps[0:CAP, 4 + e % 2, n * D:(n + 1) * D], hT[e % 2][:, j, n * CAP:(n + 1) * CAP], k.w2[e % GROUP][:, j, :],
                                     start=(j == 0), stop=(j == ffn.hc - 1))
                    ins.then_inc(y_ready, 1)

                turn(0)
                turn(1)
                up(0)
                for e in range(E):
                    if e + 2 < E:
                        turn(e + 2)
                    if e + 1 < E:
                        up(e + 1)
                    down(e)

            @block.scalar
            def _(act):
                def copy_columns(e):
                    act.wait_ge(turned, e + 1)
                    nc.scalar.copy(cols[:, :, e, :], k.ps[0:KC, 6 + e % 2, 0:4 * CAP].rearrange("p (c s) -> p c s", c=2)).then_inc(cols_ready, 1)

                copy_columns(0)
                copy_columns(1)
                for u, e, j in units:
                    act.wait_ge(unit_ready, u + 1)
                    if u >= 2:
                        act.wait_ge(unit_done, u - 1)
                    nc.scalar.activation(sg[u % 2][:, :], k.ps[:, u % 4, 2 * CAP:4 * CAP], ACT.Silu).then_inc(gate_act, 1)
                    if j == 0 and e + 2 < E:
                        copy_columns(e + 2)

            @block.vector
            def _(dve):
                V = nc.vector

                def leave(e):
                    dve.wait_ge(y_ready, e + 1)
                    if e >= 2:
                        dve.wait_ge(y_sent[e % 2], 16 * (e // 2))
                    V.tensor_copy(y[e % 2][:, :, :], k.ps[0:CAP, 4 + e % 2, 0:2 * D].rearrange("p (n d) -> p n d", n=2)).then_inc(y_copied, 1)

                for u, e, j in units:
                    dve.wait_ge(gate_act, u + 1)
                    if e >= 2 and j == 0:
                        dve.wait_ge(y_ready, e - 1)
                    V.tensor_tensor(hT[e % 2][:, j, :], k.ps[:, u % 4, 0:2 * CAP], sg[u % 2][:, :], ALU.mult).then_inc(unit_done, 1)
                    if j == ffn.hc - 1 and e:
                        leave(e - 1)
                leave(E - 1)
                dve.wait_ge(k.y_back, 16 * 2 * NT)
                for n in range(2):
                    for t in range(NT):
                        V.scalar_tensor_tensor(k.h[:, t, :], back[:, t, n, :], k.choice_w[:, t, n:n + 1], k.h[:, t, :], ALU.mult, ALU.add
                                               ).then_inc(added, 1)
                    dve.wait_ge(added, NT * (n + 1))


def channel_attention(nc, k, a):
    normalise_columns(nc, k, k.h, k.xn, k.xt, 1e-5)
    with ExitStack() as c:
        w, wp = k.ca_w, k.ca_wp
        qkv = [k.sb("ca_" + n, [KC, 4, S], F32, c) for n in "qkv"]
        junk = k.sb("ca_junk", [KC, S], F32, c)
        tmp = k.sb("ca_tmp", [KC, 4, S], F32, c)
        sums = k.sb("ca_sums", [KC, 2, 4], F32, c)
        ssq = k.sb("ca_ssq", [KC, 2, 4], F32, c)
        coef = k.sb("ca_coef", [KC, 4], F32, c)
        prod = k.sb("ca_prod", [KC, 4], F32, c)
        with stage(nc, "unit_ready", "act_done", "dve_done", "rnorm", "copied") as \
                (block, unit_ready, act_done, dve_done, rnorm, copied):
            parts = [(cb, i) for cb in range(4) for i in range(3)]

            @block.tensor
            def _(pe):
                for cb in range(4):
                    m, b = cb // 2, cb % 2
                    for i in range(3):
                        bank = (cb % 2) * 3 + i
                        if cb >= 2:
                            if i < 2:
                                pe.wait_ge(act_done, 4 * (cb - 2) + 2 * i + 2)
                            else:
                                pe.wait_ge(copied, cb - 1)
                        for kc in range(2):
                            ins = nc.tensor.matmul(k.ps[0:KC, bank, 0:S], w[:, kc, i * D + m * KC:i * D + (m + 1) * KC],
                                                   k.xt[0:KC, kc, b * S:(b + 1) * S], start=(kc == 0), stop=(kc == 1))
                        ins.then_inc(unit_ready, 1)

            @block.scalar
            def _(act):
                for cb in range(4):
                    for i in range(2):
                        bank = k.ps[0:KC, (cb % 2) * 3 + i, 0:S]
                        act.wait_ge(unit_ready, 3 * cb + i + 1)
                        nc.scalar.activation(qkv[i][:, cb, :], bank, ACT.Copy, accum_out=sums[:, i, cb:cb + 1]).then_inc(act_done, 1)
                        n = 4 * cb + 2 * i
                        if n:
                            act.wait_ge(act_done, n)
                        nc.scalar.activation(junk[:, :], bank, ACT.Square, accum_out=ssq[:, i, cb:cb + 1]).then_inc(act_done, 1)

            @block.gpsimd
            def _(pool):
                pool.wait_ge(act_done, 16)
                nc.gpsimd.tensor_tensor(ssq[:, :, :].rearrange("p i c -> p (i c)"), ssq[:, :, :].rearrange("p i c -> p (i c)"),
                                        k.neg_half[0:KC, 0:8], ALU.pow).then_inc(rnorm, 1)

            @block.vector
            def _(dve):
                V = nc.vector
                step = Steps(dve, dve_done)
                for cb in range(4):
                    dve.wait_ge(unit_ready, 3 * cb + 3)
                    V.tensor_copy(qkv[2][:, cb, :], k.ps[0:KC, (cb % 2) * 3 + 2, 0:S]).then_inc(copied, 1)
                dve.wait_ge(copied, 4)
                dve.wait_ge(rnorm, 1)
                step(V.tensor_tensor(sums[:, :, :], sums[:, :, :], ssq[:, :, :], ALU.mult))
                step(V.tensor_tensor(prod[:, :], sums[:, 0, :], sums[:, 1, :], ALU.mult))
                step(V.tensor_scalar(prod[:, :], prod[:, :], float(S), None, ALU.add))
                step(V.reciprocal(prod[:, :], prod[:, :]))
                step(V.tensor_tensor(coef[:, :], prod[:, :], ssq[:, 0, :], ALU.mult))
                for cb in range(4):
                    step.start(V.scalar_tensor_tensor(tmp[:, cb, :], qkv[1][:, cb, :], ssq[:, 1, cb:cb + 1], qkv[0][:, cb, :], ALU.mult, ALU.mult))
                step.wait()
                for cb in range(4):
                    step.start(V.scalar_tensor_tensor(tmp[:, cb, :], qkv[1][:, cb, :], ssq[:, 1, cb:cb + 1], tmp[:, cb, :], ALU.mult, ALU.mult))
                step.wait()
                for cb in range(4):
                    step.start(V.scalar_tensor_tensor(k.xt[0:KC, cb // 2, (cb % 2) * S:(cb % 2 + 1) * S], qkv[2][:, cb, :],
                                                      coef[:, cb:cb + 1], tmp[:, cb, :], ALU.mult, ALU.mult))
                step.wait()
        project(nc, k, wp, add_to=k.h)


NHEAD, HW = 12, 16
HG = 3
NHG = NHEAD // HG
RP = R + 1
QMIN, QMAX = -128.0, 127.0
SHIFT = 112


def head_rows(h):
    return slice(32 * (h % 4), 32 * (h % 4) + HW), h // 4


def quantised_attention(nc, k, a):
    normalise_columns(nc, k, k.h, k.xn, k.xt, 1e-5)
    with ExitStack() as c:
        raw, praw, sc = k.qa_raw, k.qa_praw, k.qa_scales
        wqk = k.sb("qa_wqk", [KC + 1, 2, 2, NHEAD, 32], F32, c)
        wv = k.sb("qa_wv", [KC + 1, 2, D], F32, c)
        wp = k.sb("qa_wp", [KC + 1, 2, D], F32, c)
        qk_t = k.sb("qa_qkt", [128, 2, B, 3, S], BF16, c)
        qk_b = k.sb("qa_qkb", [128, 2, 3, S], BF16, c)
        v_q = k.sb("qa_v", [R, NT, D], BF16, c)
        v_b = k.sb("qa_vb", [R, TPB, D], BF16, c)
        id16 = k.sb("qa_id", [128, 128], BF16, c)
        inv = k.sb("qa_inv", [128, 6], F32, c)
        cc = k.sb("qa_cc", [128, 16], F32, c)
        rnd = k.sb("qa_round", [128, 1], F32, c)
        tmp = k.sb("qa_tmp", [128, 2, 3 * D], F32, c)
        W_S, A1, ATT, A2, WP_S, A3 = range(6)
        logit, negx0, invx0, off, half_b, c_rest, lowest, ctx_s = (cc[:, n:n + 1] for n in range(8))

        def floor(V, step, x):
            y = tmp[:, 0, 0:1]
            step(V.tensor_scalar(y, x, ROUND, ROUND, ALU.add, ALU.subtract))
            step(V.tensor_tensor(tmp[:, 0, 1:2], y, x, ALU.is_gt))
            step(V.tensor_tensor(x, y, tmp[:, 0, 1:2], ALU.subtract))

        with stage(nc, "filled", "dve_done", "unit_ready", "act_done", "bank_free", "w_ready", "consts") as \
                (block, filled, dve_done, unit_ready, act_done, bank_free, w_ready, consts):
            @block.gpsimd
            def _(pool):
                step = Steps(pool, filled)
                step(nc.gpsimd.memset(wqk[:, :, :, :, :], 0.0))
                step(nc.gpsimd.memset(rnd[:, :], ROUND))
                step(nc.gpsimd.tensor_copy(id16[:, :], k.ident[:, :]))

            units = [("qk", b, w, g) for b in range(B) for w in range(2) for g in range(3)] + [("v", t, 0, 0) for t in range(NT)]

            @block.tensor
            def _(pe):
                pe.wait_ge(w_ready, 1)
                for u, (kind, b, w, g) in enumerate(units):
                    if u >= 4:
                        pe.wait_ge(bank_free, u - 3)
                    for kc in range(2):
                        kk = KC + kc
                        if kind == "qk":
                            ins = nc.tensor.matmul(k.ps[:, u % 4, 0:S], wqk[0:kk, kc, w, 4 * g:4 * g + 4, :].rearrange("p h d -> p (h d)"),
                                                   k.xt[0:kk, kc, b * S:(b + 1) * S], start=(kc == 0), stop=(kc == 1))
                        else:
                            ins = nc.tensor.matmul(k.ps[0:R, u % 4, 0:D], k.xt[0:kk, kc, b * R:(b + 1) * R], wv[0:kk, kc, :],
                                                   start=(kc == 0), stop=(kc == 1))
                    ins.then_inc(unit_ready, 1)

            @block.vector
            def _(dve):
                V = nc.vector
                step = Steps(dve, dve_done)
                dve.wait_ge(filled, 3)
                step(V.reciprocal(inv[:, :], sc[:, :]))

                def fake_quant(x, s, parts):
                    step(V.tensor_scalar(x, x, inv[0:parts, s:s + 1], ROUND, ALU.mult, ALU.add))
                    step(V.tensor_scalar(x, x, ROUND + QMAX, ROUND + QMIN, ALU.min, ALU.max))

                fake_quant(raw[:, :, :], W_S, KC)
                fake_quant(praw[:, :, :], WP_S, KC)
                for kc in range(2):
                    step(V.tensor_scalar(wqk[0:KC, kc, :, :, 0:HW], raw[:, kc, 0:2 * D].rearrange("p (w h d) -> p w h d", w=2, d=HW),
                                         ROUND, sc[0:KC, W_S:W_S + 1], ALU.subtract, ALU.mult))
                step(V.tensor_scalar(wv[0:KC, :, :], raw[:, :, 2 * D:3 * D], ROUND, sc[0:KC, W_S:W_S + 1], ALU.subtract, ALU.mult))
                step(V.tensor_scalar(wp[0:KC, :, :], praw[:, :, :], ROUND, sc[0:KC, WP_S:WP_S + 1], ALU.subtract, ALU.mult))
                step(V.tensor_copy(wv[KC:KC + 1, 1, :], k.qa_bias[KC:KC + 1, 2 * D:3 * D]))
                step(V.tensor_copy(wp[KC:KC + 1, 1, :], k.qa_bias[KC:KC + 1, 3 * D:4 * D]))
                V.tensor_copy(wqk[KC:KC + 1, 1, :, :, 0:HW], k.qa_bias[KC:KC + 1, 0:2 * D].rearrange("p (w h d) -> p w h d", w=2, d=HW)
                              ).then_inc(w_ready, 1)
                step(V.tensor_tensor(logit, sc[:, A1:A1 + 1], sc[:, A1:A1 + 1], ALU.mult))
                step(V.tensor_scalar(logit, logit, inv[:, ATT:ATT + 1], HW ** -0.5, ALU.mult, ALU.mult))
                step(V.tensor_scalar(negx0, inv[:, ATT:ATT + 1], -0.6931, None, ALU.mult))
                floor(V, step, negx0)
                step(V.tensor_scalar(lowest, negx0, 30.0, None, ALU.mult))
                step(V.reciprocal(invx0, negx0))
                step(V.tensor_scalar(negx0, negx0, -1.0, None, ALU.mult))
                step(V.tensor_scalar(off, invx0, -0.5, -0.5, ALU.mult, ALU.add))
                step(V.tensor_scalar(half_b, inv[:, ATT:ATT + 1], 0.96963238 / 0.35815147, None, ALU.mult))
                floor(V, step, half_b)
                step(V.tensor_scalar(half_b, half_b, 0.5, None, ALU.mult))
                step(V.tensor_tensor(c_rest, inv[:, ATT:ATT + 1], inv[:, ATT:ATT + 1], ALU.mult))
                step(V.tensor_scalar(c_rest, c_rest, 1.0 / 0.35815147, None, ALU.mult))
                floor(V, step, c_rest)
                step(V.tensor_tensor(tmp[:, 0, 0:1], half_b, half_b, ALU.mult))
                step(V.tensor_tensor(c_rest, c_rest, tmp[:, 0, 0:1], ALU.subtract))
                step(V.tensor_tensor(ctx_s, sc[:, A1:A1 + 1], inv[:, A2:A2 + 1], ALU.mult))
                step(V.tensor_scalar(ctx_s, ctx_s, 2.0 ** (SHIFT - 1), None, ALU.mult))
                for u, (kind, b, w, g) in enumerate(units):
                    dve.wait_ge(unit_ready, u + 1)
                    rows, cols = (128, S) if kind == "qk" else (R, D)
                    t = tmp[0:rows, u % 2, 0:cols]
                    V.tensor_scalar(t, k.ps[0:rows, u % 4, 0:cols], inv[0:rows, A1:A1 + 1], ROUND, ALU.mult, ALU.add).then_inc(bank_free, 1)
                    dve.wait_ge(bank_free, u + 1)
                    step(V.tensor_scalar(t, t, ROUND + QMAX, ROUND + QMIN, ALU.min, ALU.max))
                    out = qk_t[:, w, b, g, :] if kind == "qk" else v_q[:, b, :]
                    step.start(V.tensor_scalar(out, t, ROUND, None, ALU.subtract))
                step.wait()

        t1 = [k.sb(f"qa_t1_{n}", [R, HG, S], F32, c) for n in range(2)]
        nn = [k.sb(f"qa_n_{n}", [R, HG, S], F32, c) for n in range(2)]
        qq = [k.sb(f"qa_q_{n}", [R, HG, S], F32, c) for n in range(2)]
        ee = [k.sb(f"qa_e_{n}", [R, HG, S], F32, c) for n in range(2)]
        hp = [k.sb(f"qa_hp_{n}", [R, HG, S], I32, c) for n in range(2)]
        pw = [k.sb(f"qa_pw_{n}", [R, HG, S], I32, c) for n in range(2)]
        rr = k.sb("qa_r", [R, HG, S], F32, c)
        ln_e = k.sb("qa_ln_e", [R, HG, S], F32, c)
        rho = k.sb("qa_rho", [R, HG, S], F32, c)
        dd = k.sb("qa_d", [R, HG, S], F32, c)
        ff = k.sb("qa_f", [R, HG, S], F32, c)
        mx = k.sb("qa_mx", [R, HG], F32, c)
        sm = [k.sb(f"qa_sm_{n}", [R, HG], F32, c) for n in range(2)]
        inv_sm = [k.sb(f"qa_inv_sm_{n}", [R, HG], F32, c) for n in range(2)]
        ln_sm = k.sb("qa_ln_sm", [R, HG], F32, c)
        pt = k.sb("qa_pt", [R, HG, TPB, RP], BF16, c)
        pt_ps = k.ps[0:R, 6, :].bitcast(BF16)[:, 0:HG * TPB * RP].rearrange("p (h m n) -> p h m n", h=HG, m=TPB)
        pp = [x[:, :, :].bitcast(BF16).rearrange("p h (m two) -> p h m two", two=2)[:, :, :, 1] for x in hp]

        def batch(first_tile, b):
            units = [(u, nt, g) for u, (nt, g) in enumerate((nt, g) for nt in range(TPB) for g in range(NHG))]
            U = len(units)
            with stage(nc, "picked", "scores", "scaled", "shifted", "divided", "dve_done", "r_ready", "squared", "e_ready", "ln_ready", "rho_ready",
                       "moved", "q_ready", "pw_ready", "rho_exact", "n_moved", "n_ready", "n_scaled", "p_ready", "turned", "pt_ready", "pv_done", "ctx_out") as \
                    (block, picked, scores, scaled, shifted, divided, dve_done, r_ready, squared, e_ready, ln_ready, rho_ready,
                     moved, q_ready, pw_ready, rho_exact, n_moved, n_ready, n_scaled, p_ready, turned, pt_ready, pv_done, ctx_out):
                @block.gpsimd
                def _(pool):
                    G = nc.gpsimd

                    def move(out, x, offset):
                        return G.tensor_scalar(out[:, :, :], x[:, :, :], 1.0, offset, ALU.mult, ALU.add)

                    def quotients(u):
                        q = qq[u % 2]
                        pool.wait_ge(divided, u + 1)
                        move(q, q, ROUND).then_inc(moved, 1)
                        pool.wait_ge(moved, u + 1)
                        move(q, q, -ROUND).then_inc(q_ready, 1)
                        pool.wait_ge(q_ready, u + 1)
                        if u >= 2:
                            pool.wait_ge(e_ready, HG * (u - 1))
                        G.tensor_scalar(pw[u % 2][:, :, :], q[:, :, :], -2.0 ** 23, 127.0 * 2.0 ** 23, ALU.mult, ALU.add).then_inc(pw_ready, 1)

                    quotients(0)
                    for v in range(U + 1):
                        if v + 1 < U:
                            quotients(v + 1)
                        if v:
                            pool.wait_ge(rho_exact, v)
                            move(dd, dd, ROUND).then_inc(n_moved, 1)
                            pool.wait_ge(n_moved, v)
                            move(dd, dd, -ROUND).then_inc(n_ready, 1)
                            pool.wait_ge(n_ready, v)
                            G.tensor_scalar(ff[:, :, :], dd[:, :, :], -4.0 / 3.0 * 2.0 ** SHIFT, 0.0, ALU.mult, ALU.add).then_inc(n_scaled, 1)

                @block.tensor
                def _(pe):
                    def score(u, nt, g):
                        if u >= 2:
                            pe.wait_ge(scaled, u - 1)
                        for i in range(HG):
                            rows, grp = head_rows(HG * g + i)
                            ins = nc.tensor.matmul(k.ps[0:R, (u % 2) * HG + i, 0:S], qk_b[rows, 0, grp, nt * R:(nt + 1) * R],
                                                   qk_b[rows, 1, grp, :], start=True, stop=True)
                        ins.then_inc(scores, 1)

                    def turn(u):
                        pe.wait_ge(p_ready, u + 1)
                        if u:
                            pe.wait_ge(pt_ready, u)
                        for i in range(HG):
                            for m in range(TPB):
                                ins = nc.tensor.transpose(pt_ps[:, i, m, 0:R], pp[u % 2][:, i, m * R:(m + 1) * R], id16[0:R, 0:R])
                        ins.then_inc(turned, 1)

                    def weigh(u, nt, g):
                        pe.wait_ge(pt_ready, u + 1)
                        if g == 0 and nt:
                            pe.wait_ge(ctx_out, nt)
                        for i in range(HG):
                            h = HG * g + i
                            for m in range(TPB):
                                ins = nc.tensor.matmul(k.ps[0:R, 7, h * HW:(h + 1) * HW], pt[:, i, m, 0:R], v_b[:, m, h * HW:(h + 1) * HW],
                                                       start=(m == 0), stop=(m == TPB - 1))
                        ins.then_inc(pv_done, 1)

                    pe.wait_ge(picked, 3)
                    score(*units[0])
                    score(*units[1])
                    for v in range(U + 2):
                        if v + 2 < U:
                            score(*units[v + 2])
                        if v >= 2:
                            turn(v - 2)
                            weigh(*units[v - 2])

                @block.scalar
                def _(act):
                    A = nc.scalar.activation

                    def scale_logits(u):
                        act.wait_ge(scores, u + 1)
                        if u >= 2:
                            act.wait_ge(shifted, u - 1)
                        A(t1[u % 2][:, :, :], k.ps[0:R, (u % 2) * HG:(u % 2 + 1) * HG, 0:S], ACT.Identity,
                          scale=logit[0:R, :], bias=rnd[0:R, :]).then_inc(scaled, 1)

                    def divide(u):
                        act.wait_ge(shifted, u + 1)
                        A(qq[u % 2][:, :, :], nn[u % 2][:, :, :], ACT.Identity, scale=invx0[0:R, :], bias=off[0:R, :]).then_inc(divided, 1)

                    scale_logits(0)
                    scale_logits(1)
                    divide(0)
                    for v in range(U + 2):
                        if v + 1 < U:
                            divide(v + 1)
                        if v + 2 < U:
                            scale_logits(v + 2)
                        if v < U:
                            act.wait_ge(r_ready, v + 1)
                            A(rr[:, :, :], rr[:, :, :], ACT.Square, bias=half_b[0:R, :]).then_inc(squared, 1)
                            act.wait_ge(e_ready, HG * (v + 1))
                            A(ln_e[:, :, :], ee[v % 2][:, :, :], ACT.Ln).then_inc(ln_ready, 1)
                            A(ln_sm[:, :], sm[v % 2][:, :], ACT.Ln).then_inc(ln_ready, 1)
                            act.wait_ge(ln_ready, 2 * (v + 1))
                            for i in range(HG):
                                A(rho[:, i, :], ln_e[:, i, :], ACT.Exp, scale=-1.0, bias=ln_sm[:, i:i + 1]).then_inc(rho_ready, 1)
                        if v >= 2:
                            act.wait_ge(turned, v - 1)
                            if v > 2:
                                act.wait_ge(pv_done, v - 2)
                            nc.scalar.copy(pt[:, :, :, 0:R], pt_ps[:, :, :, 0:R]).then_inc(pt_ready, 1)

                def context(dve, V, step, nt):
                    dve.wait_ge(pv_done, NHG * (nt + 1))
                    t = tmp[0:R, 0, 0:D]
                    V.tensor_scalar(t, k.ps[0:R, 7, 0:D], ctx_s[0:R, :], ROUND, ALU.mult, ALU.add).then_inc(ctx_out, 1)
                    dve.wait_ge(ctx_out, nt + 1)
                    step(V.tensor_scalar(t, t, ROUND + QMAX, ROUND + QMIN, ALU.min, ALU.max))
                    step(V.tensor_scalar(k.xn[:, bass.ds(first_tile + nt, 1), :].rearrange("p o d -> p (o d)"), t, ROUND, sc[0:R, A2:A2 + 1],
                                         ALU.subtract, ALU.mult))

                @block.vector
                def _(dve):
                    V = nc.vector
                    step = Steps(dve, dve_done)

                    def shift(u):
                        t, n_ = t1[u % 2], nn[u % 2]
                        dve.wait_ge(scaled, u + 1)
                        step(V.tensor_scalar(t[:, :, :], t[:, :, :], ROUND + QMAX, ROUND + QMIN, ALU.min, ALU.max))
                        step(V.tensor_reduce(mx[:, :], t[:, :, :], AX.X, ALU.max))
                        for i in range(HG):
                            ins = V.tensor_scalar(n_[:, i, :], t[:, i, :], mx[:, i:i + 1], lowest[0:R, :], ALU.subtract, ALU.max)
                            if i < HG - 1:
                                step.start(ins)
                        ins.then_inc(shifted, 1)

                    def remainder(u):
                        dve.wait_ge(q_ready, u + 1)
                        V.scalar_tensor_tensor(rr[:, :, :], qq[u % 2][:, :, :], negx0[0:R, :], nn[u % 2][:, :, :], ALU.mult, ALU.add
                                               ).then_inc(r_ready, 1)

                    def exponentials(u):
                        dve.wait_ge(squared, u + 1)
                        dve.wait_ge(pw_ready, u + 1)
                        for i in range(HG):
                            ins = V.scalar_tensor_tensor(ee[u % 2][:, i, :], rr[:, i, :], c_rest[0:R, :], pw[u % 2][:, i, :].bitcast(F32), ALU.add, ALU.mult,
                                                         accum_out=sm[u % 2][:, i:i + 1])
                            ins.then_inc(e_ready, 1)
                        dve.wait_ge(e_ready, HG * (u + 1))
                        step.start(V.reciprocal(inv_sm[u % 2][:, :], sm[u % 2][:, :]))

                    def counts(u):
                        dve.wait_ge(rho_ready, HG * (u + 1))
                        step.wait()
                        for i in range(HG):
                            step.start(V.scalar_tensor_tensor(dd[:, i, :], ee[u % 2][:, i, :], inv_sm[u % 2][:, i:i + 1], rho[:, i, :], ALU.mult, ALU.mult))
                        step.wait()
                        V.scalar_tensor_tensor(dd[:, :, :], dd[:, :, :], 2.0, rho[:, :, :], ALU.subtract, ALU.mult).then_inc(rho_exact, 1)

                    def weights(u):
                        dve.wait_ge(n_scaled, u + 1)
                        if u >= 2:
                            dve.wait_ge(turned, u - 1)
                        V.tensor_scalar(hp[u % 2][:, :, :], ff[:, :, :].bitcast(I32), 0x7F800000, 0x7F800000, ALU.bitwise_and, ALU.bitwise_xor
                                        ).then_inc(p_ready, 1)

                    for w in range(2):
                        V.tensor_copy(qk_b[:, w, :, :], qk_t[:, w, bass.ds(b, 1), :, :].rearrange("p o g s -> p (o g) s")).then_inc(picked, 1)
                    V.tensor_copy(v_b[:, :, :], v_q[:, bass.ds(first_tile, TPB), :]).then_inc(picked, 1)
                    shift(0)
                    for v in range(U + 2):
                        if v + 1 < U:
                            shift(v + 1)
                        if v >= 2:
                            weights(v - 2)
                        if v < U:
                            remainder(v)
                        if 1 <= v <= U:
                            counts(v - 1)
                        if v < U:
                            exponentials(v)
                        if v >= 3 and units[v - 3][2] == NHG - 1:
                            context(dve, V, step, units[v - 3][1])
                    context(dve, V, step, TPB - 1)

        with nc.Fori(0, B) as b:
            batch(b * TPB, b)
        to_columns(nc, k, k.xn, k.xt)
        project(nc, k, wp, dst=k.xn)
        with stage(nc, "dve_done") as (block, dve_done):
            @block.vector
            def _(dve):
                V = nc.vector
                step = Steps(dve, dve_done)
                step(V.tensor_scalar(k.xn[:, :, :], k.xn[:, :, :], inv[0:R, A3:A3 + 1], ROUND, ALU.mult, ALU.add))
                step(V.tensor_scalar(k.xn[:, :, :], k.xn[:, :, :], ROUND + QMAX, ROUND + QMIN, ALU.min, ALU.max))
                step(V.tensor_scalar(k.xn[:, :, :], k.xn[:, :, :], ROUND, sc[0:R, A3:A3 + 1], ALU.subtract, ALU.mult))
                step(V.tensor_tensor(k.h[:, :, :], k.h[:, :, :], k.xn[:, :, :], ALU.add))


def ternary(V, step, x, inv, parts):
    step(V.tensor_scalar(x, x, inv, 1.0, ALU.mult, ALU.min))
    step(V.tensor_scalar(x, x, -1.0, ROUND, ALU.max, ALU.add))


def ternary_attention(nc, k, a):
    normalise_columns(nc, k, k.h, k.xn, k.xt, 1e-5)
    EPS = 1e-5
    with ExitStack() as c:
        w = k.ta_w
        qkv = k.sb("ta_qkv", [R, NT, 3, NHEAD, HW], F32, c)
        l1 = k.sb("ta_l1", [R, NT, 3 * NHEAD], F32, c)
        part = k.sb("ta_part", [128, NT * 3], F32, c)
        sc = k.sb("ta_sc", [128, 4], F32, c)
        inv = k.sb("ta_inv", [128, 4], F32, c)
        pad = k.sb("ta_pad", [R, NT, 2, NHEAD, 32], BF16, c)
        qk_t = k.sb("ta_qkt", [128, 2, B, 3, S], BF16, c)
        qk_b = k.sb("ta_qkb", [128, 2, 3, S], BF16, c)
        v_q = k.sb("ta_v", [R, NT, D], BF16, c)
        v_b = k.sb("ta_vb", [R, TPB, D], BF16, c)
        id16 = k.sb("ta_id", [128, 128], BF16, c)
        with stage(nc, "filled", "dve_done", "part_ready", "summed", "w_ready", "tile_ready", "copied", "padded", "turned") as \
                (block, filled, dve_done, part_ready, summed, w_ready, tile_ready, copied, padded, turned):
            def turned_bank(which, b):
                return k.ps[:, 2 * which + b, :].bitcast(BF16)[:, 0:9 * RP].rearrange("p (g t n) -> p g t n", g=3, t=TPB)

            @block.gpsimd
            def _(pool):
                nc.gpsimd.memset(pad[:, :, :, :, :], 0.0).then_inc(filled, 1)
                nc.gpsimd.tensor_copy(id16[:, :], k.ident[:, :]).then_inc(filled, 1)

            @block.tensor
            def _(pe):
                pe.wait_ge(part_ready, 1)
                nc.tensor.matmul(k.ps[:, 6, 0:1], k.ones[0:KC, :], part[0:KC, 0:1], start=True, stop=True).then_inc(summed, 1)
                pe.wait_ge(w_ready, 1)
                for t in range(NT):
                    for bank, lo, hi in ((t % 3, 0, 2 * D), (3 + t % 3, 2 * D, 3 * D)):
                        if t >= 3:
                            pe.wait_ge(copied, 2 * (t - 3) + 1 + (lo > 0))
                        for kc in range(2):
                            ins = nc.tensor.matmul(k.ps[0:R, bank, 0:hi - lo], k.xt[0:KC, kc, t * R:(t + 1) * R], w[:, kc, lo:hi],
                                                   start=(kc == 0), stop=(kc == 1))
                        ins.then_inc(tile_ready, 1)
                pe.wait_ge(part_ready, 2)
                nc.tensor.matmul(k.ps[:, 7, 0:3 * NT], k.ones[0:R, :], part[0:R, :], start=True, stop=True).then_inc(summed, 1)
                pe.wait_ge(padded, 3)
                pe.wait_ge(filled, 2)
                for which in range(2):
                    for b in range(B):
                        to = turned_bank(which, b)
                        for g in range(3):
                            for t in range(TPB):
                                ins = nc.tensor.transpose(to[:, g, t, 0:R], pad[:, b * TPB + t, which, 4 * g:4 * g + 4, :].rearrange("p h d -> p (h d)"),
                                                          id16[0:R, 0:R])
                        ins.then_inc(turned, 1)

            @block.scalar
            def _(act):
                for t in range(NT):
                    act.wait_ge(tile_ready, 2 * t + 1)
                    nc.scalar.copy(qkv[:, t, 0:2, :, :].rearrange("p w h d -> p (w h d)"), k.ps[0:R, t % 3, 0:2 * D]).then_inc(copied, 1)
                    act.wait_ge(tile_ready, 2 * t + 2)
                    nc.scalar.copy(qkv[:, t, 2, :, :].rearrange("p h d -> p (h d)"), k.ps[0:R, 3 + t % 3, 0:D]).then_inc(copied, 1)
                for n in (1, 3):
                    act.wait_ge(turned, n + 1)
                    nc.scalar.copy(qk_t[:, n // 2, n % 2, :, :].rearrange("p g (t n) -> p g t n", t=TPB), turned_bank(n // 2, n % 2)[:, :, :, 0:R]
                                   ).then_inc(copied, 1)

            @block.vector
            def _(dve):
                V = nc.vector
                step = Steps(dve, dve_done)
                V.tensor_reduce(part[0:KC, 0:1], w[:, :, :], AX.XY, ALU.add, apply_absolute_value=True).then_inc(part_ready, 1)
                dve.wait_ge(summed, 1)
                step(V.tensor_scalar(sc[:, 3:4], k.ps[:, 6, 0:1], 1.0 / (3 * D * D), EPS, ALU.mult, ALU.add))
                step(V.reciprocal(inv[:, 3:4], sc[:, 3:4]))
                ternary(V, step, w[:, :, :], inv[0:KC, 3:4], KC)
                V.tensor_scalar(w[:, :, :], w[:, :, :], ROUND, sc[0:KC, 3:4], ALU.subtract, ALU.mult).then_inc(w_ready, 1)
                dve.wait_ge(copied, 2 * NT)
                heads = qkv[:, :, :, :, :].rearrange("p t w h d -> p (t w h) d")
                l1_ = l1[:, :, :].rearrange("p t n -> p (t n)")
                step(V.tensor_reduce(l1_, heads, AX.X, ALU.add, apply_absolute_value=True))
                step(V.tensor_scalar(l1_, l1_, EPS, None, ALU.add))
                step(V.reciprocal(l1_, l1_))
                step(V.tensor_tensor(heads, heads, l1_.unsqueeze(2).broadcast_to([R, NT * 3 * NHEAD, HW]), ALU.mult))
                V.tensor_reduce(part[0:R, :], qkv[:, :, :, :, :].rearrange("p t w h d -> p (t w) (h d)"), AX.X, ALU.add,
                                apply_absolute_value=True).then_inc(part_ready, 1)
                dve.wait_ge(summed, 2)
                step(V.tensor_reduce(sc[:, 0:3], k.ps[:, 7, 0:3 * NT].rearrange("p (t w) -> p w t", w=3), AX.X, ALU.add))
                step(V.tensor_scalar(sc[:, 0:3], sc[:, 0:3], 1.0 / (B * S * D), EPS, ALU.mult, ALU.add))
                step(V.reciprocal(inv[:, 0:3], sc[:, 0:3]))
                dve.wait_ge(filled, 1)
                for i in range(3):
                    x = qkv[:, :, i, :, :].rearrange("p t h d -> p t (h d)")
                    ternary(V, step, x, inv[0:R, i:i + 1], R)
                    out = pad[:, :, i, :, 0:HW] if i < 2 else v_q[:, :, :].rearrange("p t (h d) -> p t h d", d=HW)
                    V.tensor_scalar(out, qkv[:, :, i, :, :], ROUND, None, ALU.subtract).then_inc(padded, 1)
                for n in (0, 2):
                    dve.wait_ge(turned, n + 1)
                    step.start(V.tensor_copy(qk_t[:, n // 2, n % 2, :, :].rearrange("p g (t n) -> p g t n", t=TPB),
                                             turned_bank(n // 2, n % 2)[:, :, :, 0:R]))
                step.wait()

        acc = k.sb("ta_acc", [R, B, 12, HG], F32, c)
        acc_b = k.sb("ta_acc_b", [R, 12, HG], F32, c)
        junk = k.sb("ta_junk", [R, HG, S], F32, c)
        rows_sum = k.sb("ta_rows", [R, 1], F32, c)
        cc = k.sb("ta_cc", [128, 4], F32, c)
        rnd = k.sb("ta_round", [128, 1], F32, c)
        t1 = [k.sb(f"ta_t1_{n}", [R, HG, S], F32, c) for n in range(2)]
        at = [k.sb(f"ta_at_{n}", [R, TPB, HG, S], BF16, c) for n in range(2)]
        c_qk, qk_s, alpha, out_s = (cc[:, n:n + 1] for n in range(4))
        units = [(u, u // TPB, u % TPB) for u in range(NHG * TPB)]

        def pick(first_tile, b, picked):
            nc.vector.tensor_copy(qk_b[:, 0, :, :], qk_t[:, 0, bass.ds(b, 1), :, :].rearrange("p o g s -> p (o g) s")).then_inc(picked, 1)
            nc.vector.tensor_copy(qk_b[:, 1, :, :], qk_t[:, 1, bass.ds(b, 1), :, :].rearrange("p o g s -> p (o g) s")).then_inc(picked, 1)
            nc.vector.tensor_copy(v_b[:, :, :], v_q[:, bass.ds(first_tile, TPB), :]).then_inc(picked, 1)

        def score(pe, scores, u, g, mt):
            for i in range(HG):
                rows, grp = head_rows(HG * g + i)
                ins = nc.tensor.matmul(k.ps[0:R, (u % 2) * HG + i, 0:S], qk_b[rows, 1, grp, mt * R:(mt + 1) * R], qk_b[rows, 0, grp, :],
                                       start=True, stop=True)
            ins.then_inc(scores, 1)

        def sizes(first_tile, b):
            with stage(nc, "picked", "scores", "act_summed", "dve_summed", "zeroed", "moved") as \
                    (block, picked, scores, act_summed, dve_summed, zeroed, moved):
                @block.gpsimd
                def _(pool):
                    nc.gpsimd.memset(acc_b[:, :, :], 0.0).then_inc(zeroed, 1)
                    pool.wait_ge(act_summed, len(units) // 2)
                    pool.wait_ge(dve_summed, len(units) // 2)
                    nc.gpsimd.tensor_copy(acc[:, bass.ds(b, 1), :, :].rearrange("p o u h -> p (o u) h"), acc_b[:, :, :]).then_inc(moved, 1)
                    pool.wait_ge(moved, 1)

                @block.tensor
                def _(pe):
                    pe.wait_ge(picked, 3)
                    for u, g, mt in units:
                        if u >= 2:
                            pe.wait_ge(dve_summed if u % 2 else act_summed, u // 2)
                        score(pe, scores, u, g, mt)

                @block.scalar
                def _(act):
                    act.wait_ge(zeroed, 1)
                    for u, g, mt in units[0::2]:
                        act.wait_ge(scores, u + 1)
                        if u:
                            act.wait_ge(act_summed, u // 2)
                        nc.scalar.activation(junk[:, :, :], k.ps[0:R, 0:HG, 0:S], ACT.Abs, accum_out=acc_b[:, u, 0:1]).then_inc(act_summed, 1)

                @block.vector
                def _(dve):
                    pick(first_tile, b, picked)
                    dve.wait_ge(zeroed, 1)
                    for u, g, mt in units[1::2]:
                        dve.wait_ge(scores, u + 1)
                        nc.vector.tensor_reduce(acc_b[:, u, :], k.ps[0:R, HG:2 * HG, 0:S], AX.X, ALU.add, apply_absolute_value=True
                                                ).then_inc(dve_summed, 1)

        def weigh(first_tile, b):
            with stage(nc, "picked", "scores", "scaled", "dve_done", "rounded", "ctx_ready", "ctx_added") as \
                    (block, picked, scores, scaled, dve_done, rounded, ctx_ready, ctx_added):
                @block.tensor
                def _(pe):
                    def context(g):
                        pe.wait_ge(rounded, TPB * (g + 1))
                        if g >= 2:
                            pe.wait_ge(ctx_added, g - 1)
                        for nt in range(TPB):
                            for i in range(HG):
                                col = (nt * HG + i) * HW
                                h = HG * g + i
                                for mt in range(TPB):
                                    ins = nc.tensor.matmul(k.ps[0:R, 6 + g % 2, col:col + HW], at[g % 2][:, mt, i, nt * R:(nt + 1) * R],
                                                           v_b[:, mt, h * HW:(h + 1) * HW], start=(mt == 0), stop=(mt == TPB - 1))
                        ins.then_inc(ctx_ready, 1)

                    pe.wait_ge(picked, 3)
                    for u, g, mt in units:
                        if u >= 2:
                            pe.wait_ge(scaled, u - 1)
                        score(pe, scores, u, g, mt)
                        if mt == TPB - 1 and g:
                            context(g - 1)
                    context(NHG - 1)

                @block.scalar
                def _(act):
                    for u, g, mt in units:
                        act.wait_ge(scores, u + 1)
                        if u >= 2:
                            act.wait_ge(rounded, u - 1)
                        nc.scalar.activation(t1[u % 2][:, :, :], k.ps[0:R, (u % 2) * HG:(u % 2 + 1) * HG, 0:S], ACT.Identity,
                                             scale=alpha[0:R, :], bias=rnd[0:R, :]).then_inc(scaled, 1)

                @block.vector
                def _(dve):
                    V = nc.vector
                    step = Steps(dve, dve_done)

                    def add(g):
                        dve.wait_ge(ctx_ready, g + 1)
                        out = k.h[:, bass.ds(first_tile, TPB), g * HG * HW:(g + 1) * HG * HW]
                        V.scalar_tensor_tensor(out, k.ps[0:R, 6 + g % 2, 0:TPB * HG * HW].rearrange("p (t n) -> p t n", t=TPB), out_s[0:R, :],
                                               out, ALU.mult, ALU.add).then_inc(ctx_added, 1)

                    pick(first_tile, b, picked)
                    for u, g, mt in units:
                        dve.wait_ge(scaled, u + 1)
                        step(V.tensor_scalar(t1[u % 2][:, :, :], t1[u % 2][:, :, :], ROUND + 1.0, ROUND - 1.0, ALU.min, ALU.max))
                        if g >= 2 and mt == 0:
                            dve.wait_ge(ctx_ready, g - 1)
                        V.tensor_scalar(at[g % 2][:, mt, :, :], t1[u % 2][:, :, :], ROUND, None, ALU.subtract).then_inc(rounded, 1)
                        if g and mt == 1:
                            add(g - 1)
                    add(NHG - 1)

        with nc.Fori(0, B) as b:
            sizes(b * TPB, b)
        with stage(nc, "filled", "row_ready", "summed", "dve_done") as (block, filled, row_ready, summed, dve_done):
            @block.gpsimd
            def _(pool):
                nc.gpsimd.memset(rnd[:, :], ROUND).then_inc(filled, 1)
                pool.wait_ge(filled, 1)

            @block.tensor
            def _(pe):
                pe.wait_ge(row_ready, 1)
                nc.tensor.matmul(k.ps[:, 0, 0:1], k.ones[0:R, :], rows_sum[:, :], start=True, stop=True).then_inc(summed, 1)

            @block.vector
            def _(dve):
                V = nc.vector
                step = Steps(dve, dve_done)
                V.tensor_reduce(rows_sum[:, :], acc[:, :, :, :].rearrange("p b u h -> p (b u h)"), AX.X, ALU.add).then_inc(row_ready, 1)
                step(V.tensor_tensor(c_qk, sc[:, 0:1], sc[:, 1:2], ALU.mult))
                step(V.tensor_scalar(c_qk, c_qk, HW ** -0.5, None, ALU.mult))
                dve.wait_ge(summed, 1)
                step(V.tensor_scalar(qk_s, k.ps[:, 0, 0:1], 1.0 / (B * NHEAD * S * S), c_qk, ALU.mult, ALU.mult))
                step(V.tensor_scalar(qk_s, qk_s, EPS, None, ALU.add))
                step(V.reciprocal(alpha, qk_s))
                step(V.tensor_tensor(alpha, alpha, c_qk, ALU.mult))
                step(V.tensor_tensor(out_s, qk_s, sc[:, 2:3], ALU.mult))
        with nc.Fori(0, B) as b:
            weigh(b * TPB, b)


def norm_experts(nc, k, a, ffn, gain, shift):
    hc = ffn.hc
    with ExitStack() as c:
        up = [k.sb(f"ne_up{n}", [R, ffn.hid], F32, c) for n in range(3)]
        hn = [k.sb(f"ne_hn{n}", [R, ffn.hid], F32, c) for n in range(2)]
        hT = [k.sb(f"ne_hT{n}", [128, hc, R], F32, c) for n in range(2)]
        st = [k.sb(f"ne_st{n}", [R, 6], F32, c) for n in range(4)]
        mv = [k.sb(f"ne_mv{n}", [R, 2], F32, c) for n in range(4)]
        rs = [k.sb(f"ne_rs{n}", [R, 1], F32, c) for n in range(4)]
        sc = [k.sb(f"ne_sc{n}", [128, 2, hc], F32, c) for n in range(2)]
        U = GROUP * NT

        def group(first, last):
            with stage(nc, "up_ready", "gelu_done", "stats_done", "var_ready", "var_eps", "rstd_ready", "normed", "turned", "scaled", "y_ready",
                       "y_added", "sc_ready") as (block, up_ready, gelu_done, stats_done, var_ready, var_eps, rstd_ready, normed, turned, scaled,
                                                  y_ready, y_added, sc_ready):
                @block.sync
                def _(sp):
                    if not last:
                        for n in range(GROUP):
                            sp.wait_ge(y_added, NT * (n + 1))
                            sp.sem_clear(k.w_in[n])
                            load_expert(sp, k, a, ffn, n, first + (GROUP + n))

                @block.tensor
                def _(pe):
                    mm = nc.tensor.matmul
                    for s in range(U + 3):
                        if s < U:
                            n, t = s // NT, s % NT
                            if t == 0:
                                pe.wait_ge(k.w_in[n], 16 * ffn.loads)
                            if s >= 3:
                                pe.wait_ge(gelu_done, s - 2)
                            mm(k.ps[0:R, s % 3, 0:ffn.hid], k.xt[0:KC, 0, t * R:(t + 1) * R], k.w1[n][0:KC, 0, 0:ffn.hid], start=True, stop=False)
                            mm(k.ps[0:R, s % 3, 0:ffn.hid], k.xt[0:KC + 1, 1, t * R:(t + 1) * R], k.w1[n][0:KC + 1, 1, 0:ffn.hid],
                               start=False, stop=True).then_inc(up_ready, 1)
                        u = s - 2
                        if 0 <= u < U:
                            pe.wait_ge(normed, u + 1)
                            if u >= 2:
                                pe.wait_ge(scaled, hc * (u - 1))
                            for j in range(hc):
                                ins = nc.tensor.transpose(k.ps[:, 3 + u % 2, j * 128:j * 128 + R], hn[u % 2][:, j * 128:(j + 1) * 128], k.ident[0:R, 0:R])
                            ins.then_inc(turned, 1)
                        u = s - 3
                        if u >= 0:
                            pe.wait_ge(scaled, hc * (u + 1))
                            if u >= 3:
                                pe.wait_ge(y_added, u - 2)
                            for j in range(hc):
                                ins = mm(k.ps[0:R, 5 + u % 3, 0:D], hT[u % 2][:, j, :], k.w2[u // NT][:, j, :], start=(j == 0), stop=(j == hc - 1))
                            ins.then_inc(y_ready, 1)

                @block.scalar
                def _(act):
                    for s in range(U + 2):
                        if s < U:
                            act.wait_ge(up_ready, s + 1)
                            if s >= 3:
                                act.wait_ge(normed, s - 2)
                            nc.scalar.activation(up[s % 3][:, :], k.ps[0:R, s % 3, 0:ffn.hid], ACT.Gelu).then_inc(gelu_done, 1)
                        u = s - 2
                        if u >= 0:
                            n = u // NT
                            act.wait_ge(turned, u + 1)
                            act.wait_ge(sc_ready, 2 * (n + 1))
                            if u >= 2:
                                act.wait_ge(y_ready, u - 1)
                            for j in range(hc):
                                nc.scalar.activation(hT[u % 2][:, j, :], k.ps[:, 3 + u % 2, j * 128:j * 128 + R], ACT.Identity,
                                                     scale=sc[n % 2][:, 0, j:j + 1], bias=sc[n % 2][:, 1, j:j + 1]).then_inc(scaled, 1)

                @block.gpsimd
                def _(pool):
                    def take(n):
                        if n >= 2:
                            pool.wait_ge(scaled, hc * NT * (n - 1))
                        for i, x in enumerate((gain, shift)):
                            nc.gpsimd.tensor_copy(sc[n % 2][:, i, :], x[:, bass.ds(first + n, 1), :].rearrange("p o j -> p (o j)")).then_inc(sc_ready, 1)

                    for s in range(U):
                        if s == 0:
                            take(0)
                            take(1)
                        elif s % NT == 3 and s // NT in (1, 2):
                            take(s // NT + 1)
                        pool.wait_ge(var_ready, s + 1)
                        nc.gpsimd.tensor_scalar(rs[s % 4][:, :], mv[s % 4][:, 1:2], 1e-5, None, ALU.add).then_inc(var_eps, 1)
                        pool.wait_ge(var_eps, s + 1)
                        nc.gpsimd.tensor_tensor(rs[s % 4][:, :], rs[s % 4][:, :], k.neg_half[0:R, 0:1], ALU.pow).then_inc(rstd_ready, 1)

                @block.vector
                def _(dve):
                    V = nc.vector
                    for s in range(U + 4):
                        if s < U:
                            dve.wait_ge(gelu_done, s + 1)
                            V.bn_stats(st[s % 4][:, :], up[s % 3][:, :]).then_inc(stats_done, 1)
                        u = s - 1
                        if 0 <= u < U:
                            dve.wait_ge(rstd_ready, u + 1)
                            if u >= 2:
                                dve.wait_ge(turned, u - 1)
                            V.tensor_scalar(hn[u % 2][:, :], up[u % 3][:, :], mv[u % 4][:, 0:1], rs[u % 4][:, :], ALU.subtract, ALU.mult
                                            ).then_inc(normed, 1)
                        if s < U:
                            dve.wait_ge(stats_done, s + 1)
                            V.bn_aggr(mv[s % 4][:, :], st[s % 4][:, :]).then_inc(var_ready, 1)
                        u = s - 4
                        if u >= 0:
                            n, t = u // NT, u % NT
                            dve.wait_ge(y_ready, u + 1)
                            if t == 0 and n:
                                dve.wait_ge(y_added, NT * n)
                            V.scalar_tensor_tensor(k.h[:, t, :], k.ps[0:R, 5 + u % 3, 0:D], k.gate[:, t, bass.ds(first + n, 1)], k.h[:, t, :],
                                                   ALU.mult, ALU.add).then_inc(y_added, 1)

        with nc.Fori(0, ffn.n // GROUP - 1) as g:
            group(g * GROUP, False)
        group(ffn.n - GROUP, True)


def gelu_norm_layer(nc, k, a):
    ffn = FFN[3]
    normalise_columns(nc, k, k.h, k.xn, k.xt, 1e-5)
    router(nc, k, 3, ffn.n, 3)
    norm_experts(nc, k, a, ffn, k.gn_gain, k.gn_shift)
    gated_bias(nc, k, ffn.n, k.b2[3])


def program(nc, a, out):
    with ExitStack() as ctx:
        k = Chip(nc, ctx)
        weight_buffers(k)
        constants(nc, k)
        later_inputs(nc, k)
        slot_buffers(nc, k)
        with ExitStack() as c:
            ttt_inputs(nc, k, c)
            embed(nc, k, a)
            ttt_attention(nc, k, a)
        swiglu_layer(nc, k, a)
        channel_attention(nc, k, a)
        gelu_layer(nc, k, a)
        quantised_attention(nc, k, a)
        silu_layer(nc, k, a)
        ternary_attention(nc, k, a)
        gelu_norm_layer(nc, k, a)
        with stage(nc, "stored") as (block, stored):
            @block.sync
            def _(sp):
                sp.dma_start(out.rearrange("b (t p) d -> p (b t) d", p=R), k.h[:, :, :]).then_inc(stored, 16)
                sp.wait_ge(stored, 16)


def layout(inputs):
    out = {n: np.asarray(x) for n, x in inputs.items()}
    x = out.pop("x")
    for n, (p, _) in enumerate(LEVELS):
        e = x.shape[-1] // p
        out[f"pix{n}"] = x.reshape(B, 3, e, p, e, p).transpose(2, 4, 0, 3, 5, 1).reshape(e * e, -1)
        out[f"L0_tok_W{n}"] = out[f"L0_tok_W{n}"].T
        if n:
            out[f"inter{n}"] = interpolation(LEVELS[n][1], IMG_TOK)
    for n in ("x_txt", "mask_BS_i1_0"):
        out[n] = out[n].T
    out["L0_tok_bf"] = out["L0_tok_bf"].reshape(2, KC).T
    out["L0_tok_Wf"] = out["L0_tok_Wf"].T
    out["L0_txt_residual_weight"] = out["L0_txt_residual_weight"].reshape(1)
    w = np.concatenate([out.pop("L0_attn_" + n).reshape(D, NH0, -1) for n in ("Wk", "Wq", "Wv", "lr_w")], axis=2)
    row = np.zeros((KC + 1, 2, NH0, 3 * HD + 1), np.float32)
    row[0:KC] = w.reshape(2, KC, NH0, -1).transpose(1, 0, 2, 3)
    row[KC, 1, :, 3 * HD] = out.pop("L0_attn_lr_b")
    out["ttt_w_row"] = row
    gb = [out.pop("L0_attn_ttt_" + n) for n in "gb"]
    out["ttt_gb_col"] = np.concatenate([x.T for x in gb], axis=1)
    out["ttt_gb_row"] = np.repeat(np.tile(np.concatenate(gb, axis=1), (B, 1)), C, axis=0)
    out["ttt_state"] = np.tile(np.concatenate([out.pop("L0_attn_W1"), out.pop("L0_attn_b1")], axis=1), (B, 1, 1)).transpose(1, 0, 2)
    out["ttt_post"] = np.concatenate([out.pop("L0_attn_" + n) for n in ("post_g", "post_b", "norm_g", "norm_b")])
    out["L0_attn_b_down"] = out["L0_attn_b_down"].reshape(2, KC).T
    out.update(ttt_constants())
    out["L0_ffn_gate_w"] = out["L0_ffn_gate_w"].T
    w, v = out["L0_ffn_mlp1_w"], out["L0_ffn_mlp1_b"]
    out["L0_ffn_mlp1_w"] = np.concatenate([w[:, 0::2], w[:, 1::2]], axis=1).transpose(0, 2, 1)
    out["L0_ffn_mlp1_b"] = np.concatenate([v[:, 0::2], v[:, 1::2]], axis=1)
    out["L0_ffn_mlp2_w"] = out["L0_ffn_mlp2_w"].transpose(0, 2, 1)
    out["token_number"] = np.arange(B * S, dtype=np.float32).reshape(NT, R).T
    for n in ("L2_attn_qkv_w", "L2_attn_proj_w", "L3_attn_w_qkv"):
        out[n] = out[n].T
    out["qa_scales"] = np.stack([out.pop("L2_attn_" + n + "_scale") for n in ("w_qkv", "a1", "attn", "a2", "w_proj", "a3")])
    out["qa_bias"] = np.concatenate([out.pop("L2_attn_qkv_b"), out.pop("L2_attn_proj_b")])
    for n in ("L3_ffn_ln_w", "L3_ffn_ln_b"):
        out[n] = out[n].reshape(16, 3, 128).transpose(2, 0, 1)
    return {n: np.ascontiguousarray(v) for n, v in out.items()}


def kernel(**inputs):
    import concourse.bacc as bacc
    from concourse.bass_utils import run_bass_kernel_spmd

    nc = bacc.Bacc("TRN2", target_bir_lowering=False, num_devices=1)
    arrays, a = {}, {}
    for name, x in layout(inputs).items():
        arrays[f"in_{name}_dram"] = x
        a[name] = nc.dram_tensor(f"in_{name}_dram", x.shape, mybir.dt.from_np(x.dtype), kind="ExternalInput").ap()
    out = nc.dram_tensor("out_dram", (B, S, D), F32, kind="ExternalOutput").ap()
    program(nc, a, out)
    r = run_bass_kernel_spmd(nc, [arrays], core_ids=[0])
    return r.results[0]["out_dram"]
```
